# Optimizing a Trainium2 kernel written in Bass

```python
import numpy as np
import jax
import jax.numpy as jnp

def _softmax(x, axis=-1):
    return jax.nn.softmax(x, axis=axis)

def _gelu(x):
    return jax.nn.gelu(x, approximate=True)

def _silu(x):
    return jax.nn.silu(x)

def _sigmoid(x):
    return jax.nn.sigmoid(x)

def _layernorm(x, axis=-1, eps=1e-05):
    m = jnp.mean(x, axis=axis, keepdims=True)
    v = jnp.var(x, axis=axis, keepdims=True)
    return (x - m) / jnp.sqrt(v + eps)

def _scatter_add(tgt, idx, src, axis=0):
    return tgt.at[idx].add(src)

def _segment_sum(src, seg, n):
    return jax.ops.segment_sum(src, seg, n)
kernel_name = 'mk_early_fusion_embed_d2_tok_img768_r4_f2d255'

def setup_inputs(seed: int=0):
    np.random.seed(seed)
    _w = jnp.asarray

    def _rec_inputs():
        import jax
        import jax.numpy as jnp
        _rk = jax.random.key(seed)
        x = 1.64766e-05 + 1.00005 * jax.random.normal(jax.random.fold_in(_rk, 1), (4, 3, 512, 192), jnp.float32)
        x_txt = jax.random.randint(jax.random.fold_in(_rk, 51), (4, 128), 0, 31921, jnp.int32)
        return (x, x_txt)
    x, x_txt = _rec_inputs()

    def _L0_tok_setup():
        import jax, jax.numpy as jnp
        import numpy as np
        NUM_BANDS = 6
        D_MODEL = 192
        B, N = (2, 512)
        IN_FEATURES = 3 * NUM_BANDS * 2 * D_MODEL
        key = jax.random.key(seed)
        k_xyz, k_w = jax.random.split(key)
        xyz = jax.random.normal(k_xyz, (B, 3, N, D_MODEL), dtype=jnp.float32)
        freq_bands = 2.0 ** jnp.linspace(0.0, NUM_BANDS - 1, NUM_BANDS).astype(jnp.float32)
        bound = 1.0 / np.sqrt(IN_FEATURES)
        W = jax.random.uniform(k_w, (D_MODEL, IN_FEATURES), dtype=jnp.float32, minval=-bound, maxval=bound)
        return {'xyz': xyz, 'freq_bands': freq_bands, 'W': W}
    _L0_tok_all = _L0_tok_setup()
    _L0_tok_in = {k: v for k, v in _L0_tok_all.items() if k in ('freq_bands', 'W')}
    del _L0_tok_all

    def _L0_txt_setup():
        import jax, jax.numpy as jnp
        import numpy as np
        B, L, V, D_MODEL = (1, 512, 8000, 192)
        N_LAYER, D_STATE, EXPAND, D_CONV = (2, 16, 2, 4)
        D_INNER = EXPAND * D_MODEL
        DT_RANK = -(-D_MODEL // D_STATE)
        EPS = 1e-05

        def _rmsnorm(x, w):
            return x * jax.lax.rsqrt(jnp.mean(x * x, axis=-1, keepdims=True) + EPS) * w

        def _selective_scan(u, delta, A, Bm, Cm, D):
            deltaA = jnp.exp(delta[..., None] * A)
            dBu = delta[..., None] * Bm[:, :, None, :] * u[..., None]

            def comb(c1, c2):
                a1, b1 = c1
                a2, b2 = c2
                return (a2 * a1, a2 * b1 + b2)
            _, h = jax.lax.associative_scan(comb, (deltaA, dBu), axis=1)
            y = jnp.einsum('bldn,bln->bld', h, Cm)
            return y + u * D

        def _mamba_block(x, in_proj_w, conv_w, conv_b, x_proj_w, dt_proj_w, dt_proj_b, A_log, D, out_proj_w):
            xz = x @ in_proj_w
            xr, res = jnp.split(xz, 2, axis=-1)
            xc = jax.lax.conv_general_dilated(jnp.swapaxes(xr, 1, 2), conv_w, (1,), [(D_CONV - 1, 0)], feature_group_count=D_INNER, dimension_numbers=('NCH', 'OIH', 'NCH'))
            xr = jax.nn.silu(jnp.swapaxes(xc + conv_b[:, None], 1, 2))
            A = -jnp.exp(A_log)
            x_dbl = xr @ x_proj_w
            dt, Bm, Cm = jnp.split(x_dbl, [DT_RANK, DT_RANK + D_STATE], axis=-1)
            delta = jax.nn.softplus(dt @ dt_proj_w + dt_proj_b)
            y = _selective_scan(xr, delta, A, Bm, Cm, D)
            return y * jax.nn.silu(res) @ out_proj_w
        key = jax.random.key(seed)
        ks = jax.random.split(key, 12)
        s = 0.02
        inp = {'input_ids': jax.random.randint(ks[0], (B, L), 0, V), 'emb': jax.random.normal(ks[1], (V, D_MODEL), jnp.float32) * s, 'norm_w': jnp.ones((N_LAYER, D_MODEL), jnp.float32), 'in_proj_w': jax.random.normal(ks[2], (N_LAYER, D_MODEL, 2 * D_INNER), jnp.float32) * s, 'conv_w': jax.random.normal(ks[3], (N_LAYER, D_INNER, 1, D_CONV), jnp.float32) * s, 'conv_b': jnp.zeros((N_LAYER, D_INNER), jnp.float32), 'x_proj_w': jax.random.normal(ks[4], (N_LAYER, D_INNER, DT_RANK + 2 * D_STATE), jnp.float32) * s, 'dt_proj_w': jax.random.normal(ks[5], (N_LAYER, DT_RANK, D_INNER), jnp.float32) * s, 'dt_proj_b': jax.random.normal(ks[6], (N_LAYER, D_INNER), jnp.float32) * s, 'A_log': jnp.tile(jnp.log(jnp.arange(1, D_STATE + 1, dtype=jnp.float32)), (N_LAYER, D_INNER, 1)), 'D': jnp.ones((N_LAYER, D_INNER), jnp.float32), 'out_proj_w': jax.random.normal(ks[7], (N_LAYER, D_INNER, D_MODEL), jnp.float32) * s}
        return inp
    _L0_txt_all = _L0_txt_setup()
    _L0_txt_in = {k: v for k, v in _L0_txt_all.items() if k in ('emb', 'norm_w', 'in_proj_w', 'conv_w', 'conv_b', 'x_proj_w', 'dt_proj_w', 'dt_proj_b', 'A_log', 'D', 'out_proj_w')}
    del _L0_txt_all

    def _L0_attn_setup():
        import jax, jax.numpy as jnp
        import numpy as np
        NUM_HEADS = 12
        KERNEL_EPS = 0.001

        def _performer_relu_attention(q, k, v, projection):
            d = q.shape[-1]
            data_normalizer = 1.0 / jnp.sqrt(jnp.sqrt(jnp.asarray(d, q.dtype)))
            qp = jax.nn.relu(jnp.einsum('bhnd,md->bhnm', q * data_normalizer, projection)) + KERNEL_EPS
            kp = jax.nn.relu(jnp.einsum('bhnd,md->bhnm', k * data_normalizer, projection)) + KERNEL_EPS
            k_sum = kp.sum(axis=2)
            d_inv = 1.0 / jnp.einsum('bhnm,bhm->bhn', qp, k_sum)
            context = jnp.einsum('bhnm,bhnd->bhmd', kp, v)
            out = jnp.einsum('bhnm,bhmd->bhnd', qp, context) * d_inv[..., None]
            return out
        key = jax.random.key(seed)
        ks = jax.random.split(key, 6)
        B, N, C = (4, 1024, 192)
        H = NUM_HEADS
        d = C // H
        m = 64
        x = jax.random.normal(ks[0], (B, N, C), dtype=jnp.float32)
        w_qkv = jax.random.normal(ks[1], (3 * C, C), dtype=jnp.float32) * 0.02
        b_qkv = jnp.zeros((3 * C,), dtype=jnp.float32)
        w_proj = jax.random.normal(ks[2], (C, C), dtype=jnp.float32) * 0.02
        b_proj = jnp.zeros((C,), dtype=jnp.float32)
        projection = jax.random.normal(ks[3], (m, d), dtype=jnp.float32)
        return {'x': x, 'w_qkv': w_qkv, 'b_qkv': b_qkv, 'w_proj': w_proj, 'b_proj': b_proj, 'projection': projection}
    _L0_attn_all = _L0_attn_setup()
    _L0_attn_in = {k: v for k, v in _L0_attn_all.items() if k in ('w_qkv', 'b_qkv', 'w_proj', 'b_proj', 'projection')}
    del _L0_attn_all

    def _L0_ffn_setup():
        import jax, jax.numpy as jnp
        import numpy as np
        DIM = 192
        FF = 768
        E = 8
        K = 2
        H = 12
        HD = DIM // H
        LN_EPS = 1e-05

        def _layernorm(x, g, b):
            m = jnp.mean(x, axis=-1, keepdims=True)
            v = jnp.var(x, axis=-1, keepdims=True)
            return (x - m) * jax.lax.rsqrt(v + LN_EPS) * g + b

        def _attention(x, Wqkv, Wproj):
            B, T, D = x.shape
            qkv = (x @ Wqkv).reshape(B, T, 3, H, HD)
            q, k, v = (qkv[:, :, 0], qkv[:, :, 1], qkv[:, :, 2])
            scores = jnp.einsum('bqhd,bkhd->bhqk', q, k) * jnp.float32(HD) ** (-0.5)
            attn = jax.nn.softmax(scores, axis=-1)
            out = jnp.einsum('bhqk,bkhd->bqhd', attn, v).reshape(B, T, D)
            return out @ Wproj

        def _moe(x, Wrouter, W1, W2):
            B, T, D = x.shape
            xf = x.reshape(-1, D)
            N = xf.shape[0]
            logits = xf @ Wrouter
            topk_w, topk_idx = jax.lax.top_k(logits, K)
            topk_w = jax.nn.softmax(topk_w.astype(jnp.float32), axis=-1).astype(x.dtype)
            we = jnp.zeros((N, E), x.dtype).at[jnp.arange(N)[:, None], topk_idx].add(topk_w)

            def body(acc, expert):
                W1e, W2e, we_e = expert
                h = jax.nn.gelu(xf @ W1e, approximate=False)
                return (acc + we_e[:, None] * (h @ W2e), None)
            out, _ = jax.lax.scan(body, jnp.zeros_like(xf), (W1, W2, we.T))
            return out.reshape(B, T, D)
        key = jax.random.key(seed)
        ks = jax.random.split(key, 7)
        B, T = (4, 256)
        init = lambda k, shape, fan: jax.random.normal(k, shape, jnp.float32) * fan ** (-0.5)
        return {'x': jax.random.normal(ks[0], (B, T, DIM), jnp.float32), 'Wqkv': init(ks[1], (DIM, 3 * DIM), DIM), 'Wproj': init(ks[2], (DIM, DIM), DIM), 'Wrouter': init(ks[3], (DIM, E), DIM), 'W1': init(ks[4], (E, DIM, FF), DIM), 'W2': init(ks[5], (E, FF, DIM), FF), 'ln1_g': jnp.ones((DIM,), jnp.float32), 'ln1_b': jnp.zeros((DIM,), jnp.float32), 'ln2_g': jnp.ones((DIM,), jnp.float32), 'ln2_b': jnp.zeros((DIM,), jnp.float32)}
    _L0_ffn_all = _L0_ffn_setup()
    _L0_ffn_in = {k: v for k, v in _L0_ffn_all.items() if k in ('Wqkv', 'Wproj', 'Wrouter', 'W1', 'W2', 'ln1_g', 'ln1_b', 'ln2_g', 'ln2_b')}
    del _L0_ffn_all

    def _L1_attn_setup():
        import jax, jax.numpy as jnp
        import numpy as np
        CHUNK = 64

        def depthwise_fir(x, filt):
            B, N, H, D = x.shape
            K = filt.shape[-1]
            xc = x.reshape(B, N, H * D).transpose(0, 2, 1)
            xc = jnp.pad(xc, ((0, 0), (0, 0), (K - 1, 0)))
            w = filt.reshape(H * D, 1, K)
            y = jax.lax.conv_general_dilated(xc, w, (1,), 'VALID', feature_group_count=H * D, dimension_numbers=('NCH', 'OIH', 'NCH'))
            return y.transpose(0, 2, 1).reshape(B, N, H, D)

        def delta_rule_chunkwise(q, k, v, beta, chunk=CHUNK):
            B, H, L, D = q.shape
            q = q * D ** (-0.5)
            k = k / (jnp.linalg.norm(k, axis=-1, keepdims=True) + 1e-06)
            v = v * beta[..., None]
            k_beta = k * beta[..., None]
            n = L // chunk
            toc = lambda t: t.reshape(B, H, n, chunk, D)
            qc, kc, vc, kbc = (toc(q), toc(k), toc(v), toc(k_beta))
            A = jnp.tril(jnp.einsum('bhncd,bhnmd->bhncm', kbc, kc), -1)
            I = jnp.eye(chunk, dtype=q.dtype)
            T = jax.scipy.linalg.solve_triangular(I + A, jnp.broadcast_to(I, A.shape), lower=True)
            u = T @ vc
            w = T @ kbc

            def step(S, inp):
                q_i, k_i, u_i, w_i = inp
                u_t = u_i - w_i @ S
                attn_i = jnp.tril(jnp.einsum('bhcd,bhmd->bhcm', q_i, k_i))
                o_i = q_i @ S + attn_i @ u_t
                S = S + jnp.einsum('bhcd,bhce->bhde', k_i, u_t)
                return (S, o_i)
            xs = tuple((jnp.moveaxis(t, 2, 0) for t in (qc, kc, u, w)))
            S0 = jnp.zeros((B, H, D, D), dtype=q.dtype)
            S, o = jax.lax.scan(step, S0, xs)
            o = jnp.moveaxis(o, 0, 2).reshape(B, H, L, D)
            return (o, S)

        def _reference_tuple_inner(x, w_qkv, w_proj, b_proj, fir_short_w, fir_long_w, mix, w_prune, b_prune, w_g1, b_g1, w_g2, b_g2, w_id, id_static_logit, w_idgate, b_idgate):
            B, N, C = x.shape
            H = id_static_logit.shape[0]
            D = C // H
            qkv = (x @ w_qkv).reshape(B, N, 3, H, D).transpose(2, 0, 3, 1, 4)
            q, k, v = (qkv[0], qkv[1], qkv[2])
            scale = D ** (-0.5)
            scores = jnp.einsum('bhqd,bhkd->bhqk', q, k) * scale
            neg = jnp.finfo(scores.dtype).min
            causal = jnp.tril(jnp.ones((N, N), dtype=bool))
            attn = jax.nn.softmax(jnp.where(causal, scores, neg), axis=-1)
            attn_out = jnp.einsum('bhqk,bhkd->bnhd'.replace('n', 'q'), attn, v).transpose(0, 2, 1, 3)
            v_reshaped = v.transpose(0, 2, 1, 3)
            identity_out = (x @ w_id).reshape(B, N, H, D)
            dyn_gate = jax.nn.sigmoid(x @ w_idgate + b_idgate)
            static_gate = jax.nn.sigmoid(id_static_logit)
            identity_out = identity_out * (dyn_gate * static_gate)[..., None]
            beta = jax.nn.softmax(scores, axis=-1).sum(-1)
            delta_out = delta_rule_chunkwise(q, k, v, beta)[0].transpose(0, 2, 1, 3)
            fir_s = depthwise_fir(v_reshaped, fir_short_w)
            fir_l = depthwise_fir(v_reshaped, fir_long_w)
            mix_s = fir_s + jnp.einsum('bnhd,hg->bngd', fir_s, mix)
            mix_l = fir_l + jnp.einsum('bnhd,hg->bngd', fir_l, mix)
            paths = jnp.stack([mix_s, mix_l, delta_out, v_reshaped, identity_out], 0)
            P = paths.shape[0]
            wts = jax.nn.softmax((x @ w_prune + b_prune).reshape(B, N, H, P), axis=-1)
            pruned = jnp.einsum('pbnhd,bnhp->bnhd', paths, wts)
            ent1 = -jnp.mean(jnp.sum(wts * jnp.log(wts + 1e-08), -1))
            hdn = jax.nn.gelu(x @ w_g1 + b_g1)
            gate = jax.nn.sigmoid(hdn @ w_g2 + b_g2)
            context = pruned * gate[..., None]
            ent2 = -jnp.mean(gate * jnp.log(gate + 1e-08) + (1 - gate) * jnp.log(1 - gate + 1e-08))
            out = context.reshape(B, N, C) @ w_proj + b_proj
            return (out, ent1 + ent2)
        key = jax.random.key(seed)
        B, N, C, H = (4, 256, 192, 12)
        D = C // H
        P = 5
        ks = jax.random.split(key, 16)
        s = 0.02
        fir_s = jnp.zeros((H, D, 3)).at[..., -1].set(1.0) + 0.01 * jax.random.normal(ks[1], (H, D, 3))
        fir_l = jnp.zeros((H, D, 7)).at[..., -1].set(1.0) + 0.01 * jax.random.normal(ks[2], (H, D, 7))
        return {'x': jax.random.normal(ks[0], (B, N, C), jnp.float32), 'w_qkv': s * jax.random.normal(ks[3], (C, 3 * C)), 'w_proj': s * jax.random.normal(ks[4], (C, C)), 'b_proj': jnp.zeros((C,)), 'fir_short_w': fir_s, 'fir_long_w': fir_l, 'mix': 0.02 * jax.random.normal(ks[5], (H, H)), 'w_prune': s * jax.random.normal(ks[6], (C, H * P)), 'b_prune': jnp.zeros((H * P,)), 'w_g1': s * jax.random.normal(ks[7], (C, C)), 'b_g1': jnp.zeros((C,)), 'w_g2': s * jax.random.normal(ks[8], (C, H)), 'b_g2': jnp.zeros((H,)), 'w_id': s * jax.random.normal(ks[9], (C, C)), 'id_static_logit': jnp.full((H,), float(np.log(0.2 / 0.8)), jnp.float32), 'w_idgate': s * jax.random.normal(ks[10], (C, H)), 'b_idgate': jnp.full((H,), -1.5, jnp.float32)}
    _L1_attn_all = _L1_attn_setup()
    _L1_attn_in = {k: v for k, v in _L1_attn_all.items() if k in ('w_qkv', 'w_proj', 'b_proj', 'fir_short_w', 'fir_long_w', 'mix', 'w_prune', 'b_prune', 'w_g1', 'b_g1', 'w_g2', 'b_g2', 'w_id', 'id_static_logit', 'w_idgate', 'b_idgate')}
    del _L1_attn_all

    def _L1_ffn_setup():
        import jax, jax.numpy as jnp
        import numpy as np
        B, S, D, E = (8, 256, 192, 8)
        F = 4 * D
        key = jax.random.key(seed)
        ks = jax.random.split(key, 5)
        scale = 0.02
        x = jax.random.normal(ks[0], (B, S, D), jnp.float32)
        gate_w = jax.random.normal(ks[1], (D, E), jnp.float32) * scale
        gate_b = jnp.zeros((E,), jnp.float32)
        w1 = jax.random.normal(ks[2], (E, D, F), jnp.float32) * scale
        b1 = jnp.zeros((E, F), jnp.float32)
        w2 = jax.random.normal(ks[3], (E, F, D), jnp.float32) * scale
        b2 = jnp.zeros((E, D), jnp.float32)
        return {'x': x, 'gate_w': gate_w, 'gate_b': gate_b, 'w1': w1, 'b1': b1, 'w2': w2, 'b2': b2}
    _L1_ffn_all = _L1_ffn_setup()
    _L1_ffn_in = {k: v for k, v in _L1_ffn_all.items() if k in ('gate_w', 'gate_b', 'w1', 'b1', 'w2', 'b2')}
    del _L1_ffn_all
    return {'x': x, 'x_txt': x_txt, 'L0_tok_freq_bands': _L0_tok_in['freq_bands'], 'L0_tok_W': _L0_tok_in['W'], 'L0_txt_emb': _L0_txt_in['emb'], 'L0_txt_norm_w': _L0_txt_in['norm_w'], 'L0_txt_in_proj_w': _L0_txt_in['in_proj_w'], 'L0_txt_conv_w': _L0_txt_in['conv_w'], 'L0_txt_conv_b': _L0_txt_in['conv_b'], 'L0_txt_x_proj_w': _L0_txt_in['x_proj_w'], 'L0_txt_dt_proj_w': _L0_txt_in['dt_proj_w'], 'L0_txt_dt_proj_b': _L0_txt_in['dt_proj_b'], 'L0_txt_A_log': _L0_txt_in['A_log'], 'L0_txt_D': _L0_txt_in['D'], 'L0_txt_out_proj_w': _L0_txt_in['out_proj_w'], 'L0_attn_w_qkv': _L0_attn_in['w_qkv'], 'L0_attn_b_qkv': _L0_attn_in['b_qkv'], 'L0_attn_w_proj': _L0_attn_in['w_proj'], 'L0_attn_b_proj': _L0_attn_in['b_proj'], 'L0_attn_projection': _L0_attn_in['projection'], 'L0_ffn_Wqkv': _L0_ffn_in['Wqkv'], 'L0_ffn_Wproj': _L0_ffn_in['Wproj'], 'L0_ffn_Wrouter': _L0_ffn_in['Wrouter'], 'L0_ffn_W1': _L0_ffn_in['W1'], 'L0_ffn_W2': _L0_ffn_in['W2'], 'L0_ffn_ln1_g': _L0_ffn_in['ln1_g'], 'L0_ffn_ln1_b': _L0_ffn_in['ln1_b'], 'L0_ffn_ln2_g': _L0_ffn_in['ln2_g'], 'L0_ffn_ln2_b': _L0_ffn_in['ln2_b'], 'L1_attn_w_qkv': _L1_attn_in['w_qkv'], 'L1_attn_w_proj': _L1_attn_in['w_proj'], 'L1_attn_b_proj': _L1_attn_in['b_proj'], 'L1_attn_fir_short_w': _L1_attn_in['fir_short_w'], 'L1_attn_fir_long_w': _L1_attn_in['fir_long_w'], 'L1_attn_mix': _L1_attn_in['mix'], 'L1_attn_w_prune': _L1_attn_in['w_prune'], 'L1_attn_b_prune': _L1_attn_in['b_prune'], 'L1_attn_w_g1': _L1_attn_in['w_g1'], 'L1_attn_b_g1': _L1_attn_in['b_g1'], 'L1_attn_w_g2': _L1_attn_in['w_g2'], 'L1_attn_b_g2': _L1_attn_in['b_g2'], 'L1_attn_w_id': _L1_attn_in['w_id'], 'L1_attn_id_static_logit': _L1_attn_in['id_static_logit'], 'L1_attn_w_idgate': _L1_attn_in['w_idgate'], 'L1_attn_b_idgate': _L1_attn_in['b_idgate'], 'L1_ffn_gate_w': _L1_ffn_in['gate_w'], 'L1_ffn_gate_b': _L1_ffn_in['gate_b'], 'L1_ffn_w1': _L1_ffn_in['w1'], 'L1_ffn_b1': _L1_ffn_in['b1'], 'L1_ffn_w2': _L1_ffn_in['w2'], 'L1_ffn_b2': _L1_ffn_in['b2']}

def reference(x, x_txt, L0_tok_freq_bands, L0_tok_W, L0_txt_emb, L0_txt_norm_w, L0_txt_in_proj_w, L0_txt_conv_w, L0_txt_conv_b, L0_txt_x_proj_w, L0_txt_dt_proj_w, L0_txt_dt_proj_b, L0_txt_A_log, L0_txt_D, L0_txt_out_proj_w, L0_attn_w_qkv, L0_attn_b_qkv, L0_attn_w_proj, L0_attn_b_proj, L0_attn_projection, L0_ffn_Wqkv, L0_ffn_Wproj, L0_ffn_Wrouter, L0_ffn_W1, L0_ffn_W2, L0_ffn_ln1_g, L0_ffn_ln1_b, L0_ffn_ln2_g, L0_ffn_ln2_b, L1_attn_w_qkv, L1_attn_w_proj, L1_attn_b_proj, L1_attn_fir_short_w, L1_attn_fir_long_w, L1_attn_mix, L1_attn_w_prune, L1_attn_b_prune, L1_attn_w_g1, L1_attn_b_g1, L1_attn_w_g2, L1_attn_b_g2, L1_attn_w_id, L1_attn_id_static_logit, L1_attn_w_idgate, L1_attn_b_idgate, L1_ffn_gate_w, L1_ffn_gate_b, L1_ffn_w1, L1_ffn_b1, L1_ffn_w2, L1_ffn_b2):
    import jax
    import jax.numpy as jnp

    def _L0_tok_ref(xyz, freq_bands, W):
        import jax, jax.numpy as jnp
        import numpy as np
        NUM_BANDS = 6
        D_MODEL = 192
        B, N = (2, 512)
        IN_FEATURES = 3 * NUM_BANDS * 2 * D_MODEL
        b, c, n, d = xyz.shape
        xb = 2.0 * jnp.pi * xyz[..., None] * freq_bands
        feat = jnp.concatenate([jnp.sin(xb), jnp.cos(xb)], axis=-1)
        feat = feat.reshape(b, n, -1)
        return jnp.einsum('bnf,of->bno', feat, W)

    def _L0_txt_ref(input_ids, emb, norm_w, in_proj_w, conv_w, conv_b, x_proj_w, dt_proj_w, dt_proj_b, A_log, D, out_proj_w):
        import jax, jax.numpy as jnp
        import numpy as np
        B, L, V, D_MODEL = (1, 512, 8000, 192)
        N_LAYER, D_STATE, EXPAND, D_CONV = (2, 16, 2, 4)
        D_INNER = EXPAND * D_MODEL
        DT_RANK = -(-D_MODEL // D_STATE)
        EPS = 1e-05

        def _rmsnorm(x, w):
            return x * jax.lax.rsqrt(jnp.mean(x * x, axis=-1, keepdims=True) + EPS) * w

        def _selective_scan(u, delta, A, Bm, Cm, D):
            deltaA = jnp.exp(delta[..., None] * A)
            dBu = delta[..., None] * Bm[:, :, None, :] * u[..., None]

            def comb(c1, c2):
                a1, b1 = c1
                a2, b2 = c2
                return (a2 * a1, a2 * b1 + b2)
            _, h = jax.lax.associative_scan(comb, (deltaA, dBu), axis=1)
            y = jnp.einsum('bldn,bln->bld', h, Cm)
            return y + u * D

        def _mamba_block(x, in_proj_w, conv_w, conv_b, x_proj_w, dt_proj_w, dt_proj_b, A_log, D, out_proj_w):
            xz = x @ in_proj_w
            xr, res = jnp.split(xz, 2, axis=-1)
            xc = jax.lax.conv_general_dilated(jnp.swapaxes(xr, 1, 2), conv_w, (1,), [(D_CONV - 1, 0)], feature_group_count=D_INNER, dimension_numbers=('NCH', 'OIH', 'NCH'))
            xr = jax.nn.silu(jnp.swapaxes(xc + conv_b[:, None], 1, 2))
            A = -jnp.exp(A_log)
            x_dbl = xr @ x_proj_w
            dt, Bm, Cm = jnp.split(x_dbl, [DT_RANK, DT_RANK + D_STATE], axis=-1)
            delta = jax.nn.softplus(dt @ dt_proj_w + dt_proj_b)
            y = _selective_scan(xr, delta, A, Bm, Cm, D)
            return y * jax.nn.silu(res) @ out_proj_w
        x = emb[input_ids]
        for i in range(N_LAYER):
            x = x + _mamba_block(_rmsnorm(x, norm_w[i]), in_proj_w[i], conv_w[i], conv_b[i], x_proj_w[i], dt_proj_w[i], dt_proj_b[i], A_log[i], D[i], out_proj_w[i])
        return x

    def _L0_attn_ref(x, w_qkv, b_qkv, w_proj, b_proj, projection):
        import jax, jax.numpy as jnp
        import numpy as np
        NUM_HEADS = 12
        KERNEL_EPS = 0.001

        def _performer_relu_attention(q, k, v, projection):
            d = q.shape[-1]
            data_normalizer = 1.0 / jnp.sqrt(jnp.sqrt(jnp.asarray(d, q.dtype)))
            qp = jax.nn.relu(jnp.einsum('bhnd,md->bhnm', q * data_normalizer, projection)) + KERNEL_EPS
            kp = jax.nn.relu(jnp.einsum('bhnd,md->bhnm', k * data_normalizer, projection)) + KERNEL_EPS
            k_sum = kp.sum(axis=2)
            d_inv = 1.0 / jnp.einsum('bhnm,bhm->bhn', qp, k_sum)
            context = jnp.einsum('bhnm,bhnd->bhmd', kp, v)
            out = jnp.einsum('bhnm,bhmd->bhnd', qp, context) * d_inv[..., None]
            return out
        B, N, C = x.shape
        H = NUM_HEADS
        d = C // H
        qkv = x @ w_qkv.T + b_qkv
        qkv = qkv.reshape(B, N, 3, H, d).transpose(0, 3, 2, 1, 4)
        q, k, v = (qkv[:, :, 0], qkv[:, :, 1], qkv[:, :, 2])
        out = _performer_relu_attention(q, k, v, projection)
        out = out.transpose(0, 2, 1, 3).reshape(B, N, C)
        return out @ w_proj.T + b_proj

    def _L0_ffn_ref(x, Wqkv, Wproj, Wrouter, W1, W2, ln1_g, ln1_b, ln2_g, ln2_b):
        import jax, jax.numpy as jnp
        import numpy as np
        DIM = 192
        FF = 768
        E = 8
        K = 2
        H = 12
        HD = DIM // H
        LN_EPS = 1e-05

        def _layernorm(x, g, b):
            m = jnp.mean(x, axis=-1, keepdims=True)
            v = jnp.var(x, axis=-1, keepdims=True)
            return (x - m) * jax.lax.rsqrt(v + LN_EPS) * g + b

        def _attention(x, Wqkv, Wproj):
            B, T, D = x.shape
            qkv = (x @ Wqkv).reshape(B, T, 3, H, HD)
            q, k, v = (qkv[:, :, 0], qkv[:, :, 1], qkv[:, :, 2])
            scores = jnp.einsum('bqhd,bkhd->bhqk', q, k) * jnp.float32(HD) ** (-0.5)
            attn = jax.nn.softmax(scores, axis=-1)
            out = jnp.einsum('bhqk,bkhd->bqhd', attn, v).reshape(B, T, D)
            return out @ Wproj

        def _moe(x, Wrouter, W1, W2):
            B, T, D = x.shape
            xf = x.reshape(-1, D)
            N = xf.shape[0]
            logits = xf @ Wrouter
            topk_w, topk_idx = jax.lax.top_k(logits, K)
            topk_w = jax.nn.softmax(topk_w.astype(jnp.float32), axis=-1).astype(x.dtype)
            we = jnp.zeros((N, E), x.dtype).at[jnp.arange(N)[:, None], topk_idx].add(topk_w)

            def body(acc, expert):
                W1e, W2e, we_e = expert
                h = jax.nn.gelu(xf @ W1e, approximate=False)
                return (acc + we_e[:, None] * (h @ W2e), None)
            out, _ = jax.lax.scan(body, jnp.zeros_like(xf), (W1, W2, we.T))
            return out.reshape(B, T, D)
        x = x + _attention(_layernorm(x, ln1_g, ln1_b), Wqkv, Wproj)
        x = x + _moe(_layernorm(x, ln2_g, ln2_b), Wrouter, W1, W2)
        return x

    def _L1_attn_ref(x, w_qkv, w_proj, b_proj, fir_short_w, fir_long_w, mix, w_prune, b_prune, w_g1, b_g1, w_g2, b_g2, w_id, id_static_logit, w_idgate, b_idgate):
        import jax, jax.numpy as jnp
        import numpy as np
        CHUNK = 64

        def depthwise_fir(x, filt):
            B, N, H, D = x.shape
            K = filt.shape[-1]
            xc = x.reshape(B, N, H * D).transpose(0, 2, 1)
            xc = jnp.pad(xc, ((0, 0), (0, 0), (K - 1, 0)))
            w = filt.reshape(H * D, 1, K)
            y = jax.lax.conv_general_dilated(xc, w, (1,), 'VALID', feature_group_count=H * D, dimension_numbers=('NCH', 'OIH', 'NCH'))
            return y.transpose(0, 2, 1).reshape(B, N, H, D)

        def delta_rule_chunkwise(q, k, v, beta, chunk=CHUNK):
            B, H, L, D = q.shape
            q = q * D ** (-0.5)
            k = k / (jnp.linalg.norm(k, axis=-1, keepdims=True) + 1e-06)
            v = v * beta[..., None]
            k_beta = k * beta[..., None]
            n = L // chunk
            toc = lambda t: t.reshape(B, H, n, chunk, D)
            qc, kc, vc, kbc = (toc(q), toc(k), toc(v), toc(k_beta))
            A = jnp.tril(jnp.einsum('bhncd,bhnmd->bhncm', kbc, kc), -1)
            I = jnp.eye(chunk, dtype=q.dtype)
            T = jax.scipy.linalg.solve_triangular(I + A, jnp.broadcast_to(I, A.shape), lower=True)
            u = T @ vc
            w = T @ kbc

            def step(S, inp):
                q_i, k_i, u_i, w_i = inp
                u_t = u_i - w_i @ S
                attn_i = jnp.tril(jnp.einsum('bhcd,bhmd->bhcm', q_i, k_i))
                o_i = q_i @ S + attn_i @ u_t
                S = S + jnp.einsum('bhcd,bhce->bhde', k_i, u_t)
                return (S, o_i)
            xs = tuple((jnp.moveaxis(t, 2, 0) for t in (qc, kc, u, w)))
            S0 = jnp.zeros((B, H, D, D), dtype=q.dtype)
            S, o = jax.lax.scan(step, S0, xs)
            o = jnp.moveaxis(o, 0, 2).reshape(B, H, L, D)
            return (o, S)

        def _reference_tuple_inner(x, w_qkv, w_proj, b_proj, fir_short_w, fir_long_w, mix, w_prune, b_prune, w_g1, b_g1, w_g2, b_g2, w_id, id_static_logit, w_idgate, b_idgate):
            B, N, C = x.shape
            H = id_static_logit.shape[0]
            D = C // H
            qkv = (x @ w_qkv).reshape(B, N, 3, H, D).transpose(2, 0, 3, 1, 4)
            q, k, v = (qkv[0], qkv[1], qkv[2])
            scale = D ** (-0.5)
            scores = jnp.einsum('bhqd,bhkd->bhqk', q, k) * scale
            neg = jnp.finfo(scores.dtype).min
            causal = jnp.tril(jnp.ones((N, N), dtype=bool))
            attn = jax.nn.softmax(jnp.where(causal, scores, neg), axis=-1)
            attn_out = jnp.einsum('bhqk,bhkd->bnhd'.replace('n', 'q'), attn, v).transpose(0, 2, 1, 3)
            v_reshaped = v.transpose(0, 2, 1, 3)
            identity_out = (x @ w_id).reshape(B, N, H, D)
            dyn_gate = jax.nn.sigmoid(x @ w_idgate + b_idgate)
            static_gate = jax.nn.sigmoid(id_static_logit)
            identity_out = identity_out * (dyn_gate * static_gate)[..., None]
            beta = jax.nn.softmax(scores, axis=-1).sum(-1)
            delta_out = delta_rule_chunkwise(q, k, v, beta)[0].transpose(0, 2, 1, 3)
            fir_s = depthwise_fir(v_reshaped, fir_short_w)
            fir_l = depthwise_fir(v_reshaped, fir_long_w)
            mix_s = fir_s + jnp.einsum('bnhd,hg->bngd', fir_s, mix)
            mix_l = fir_l + jnp.einsum('bnhd,hg->bngd', fir_l, mix)
            paths = jnp.stack([mix_s, mix_l, delta_out, v_reshaped, identity_out], 0)
            P = paths.shape[0]
            wts = jax.nn.softmax((x @ w_prune + b_prune).reshape(B, N, H, P), axis=-1)
            pruned = jnp.einsum('pbnhd,bnhp->bnhd', paths, wts)
            ent1 = -jnp.mean(jnp.sum(wts * jnp.log(wts + 1e-08), -1))
            hdn = jax.nn.gelu(x @ w_g1 + b_g1)
            gate = jax.nn.sigmoid(hdn @ w_g2 + b_g2)
            context = pruned * gate[..., None]
            ent2 = -jnp.mean(gate * jnp.log(gate + 1e-08) + (1 - gate) * jnp.log(1 - gate + 1e-08))
            out = context.reshape(B, N, C) @ w_proj + b_proj
            return (out, ent1 + ent2)
        return _reference_tuple_inner(x, w_qkv, w_proj, b_proj, fir_short_w, fir_long_w, mix, w_prune, b_prune, w_g1, b_g1, w_g2, b_g2, w_id, id_static_logit, w_idgate, b_idgate)[0]

    def _L1_ffn_ref(x, gate_w, gate_b, w1, b1, w2, b2):
        import jax, jax.numpy as jnp
        import numpy as np
        B, S, D, E = (8, 256, 192, 8)
        F = 4 * D
        orig_shape = x.shape
        xt = x.reshape(-1, x.shape[-1])
        gates = jax.nn.softmax(xt @ gate_w + gate_b, axis=-1)
        expert_idx = jnp.argmax(gates, axis=-1)
        out = jnp.zeros_like(xt)
        n_experts = w1.shape[0]
        for e in range(n_experts):
            h = jax.nn.gelu(xt @ w1[e] + b1[e], approximate=False)
            y = h @ w2[e] + b2[e]
            out = jnp.where((expert_idx == e)[:, None], y, out)
        return out.reshape(orig_shape)
    h = _L0_tok_ref(x, L0_tok_freq_bands, L0_tok_W)
    h = jnp.concatenate([h, _L0_txt_ref(x_txt, L0_txt_emb, L0_txt_norm_w, L0_txt_in_proj_w, L0_txt_conv_w, L0_txt_conv_b, L0_txt_x_proj_w, L0_txt_dt_proj_w, L0_txt_dt_proj_b, L0_txt_A_log, L0_txt_D, L0_txt_out_proj_w)], axis=1)
    h = h + _L0_attn_ref(_layernorm(h, axis=-1), L0_attn_w_qkv, L0_attn_b_qkv, L0_attn_w_proj, L0_attn_b_proj, L0_attn_projection)
    h = h + _L0_ffn_ref(_layernorm(h, axis=-1), L0_ffn_Wqkv, L0_ffn_Wproj, L0_ffn_Wrouter, L0_ffn_W1, L0_ffn_W2, L0_ffn_ln1_g, L0_ffn_ln1_b, L0_ffn_ln2_g, L0_ffn_ln2_b)
    h = h + _L1_attn_ref(_layernorm(h, axis=-1), L1_attn_w_qkv, L1_attn_w_proj, L1_attn_b_proj, L1_attn_fir_short_w, L1_attn_fir_long_w, L1_attn_mix, L1_attn_w_prune, L1_attn_b_prune, L1_attn_w_g1, L1_attn_b_g1, L1_attn_w_g2, L1_attn_b_g2, L1_attn_w_id, L1_attn_id_static_logit, L1_attn_w_idgate, L1_attn_b_idgate)
    h = h + _L1_ffn_ref(_layernorm(h, axis=-1), L1_ffn_gate_w, L1_ffn_gate_b, L1_ffn_w1, L1_ffn_b1, L1_ffn_w2, L1_ffn_b2)
    return h

_drawn_inputs = setup_inputs


def setup_inputs(seed=0):
    import zlib

    import numpy as np

    out = dict(_drawn_inputs(seed))
    spreads = {'L0_txt_norm_w': (1.0, 0.6),
     'L0_txt_conv_b': (0.0, 0.1),
     'L0_txt_D': (1.0, 0.6),
     'L0_attn_b_qkv': (0.0, 0.1),
     'L0_attn_b_proj': (0.0, 0.1),
     'L0_ffn_ln1_g': (1.0, 0.2),
     'L0_ffn_ln1_b': (0.0, 0.1),
     'L0_ffn_ln2_g': (1.0, 0.2),
     'L0_ffn_ln2_b': (0.0, 0.1),
     'L1_attn_b_proj': (0.0, 0.1),
     'L1_attn_b_prune': (0.0, 0.8),
     'L1_attn_b_g1': (0.0, 0.8),
     'L1_attn_b_g2': (0.0, 0.8),
     'L1_attn_id_static_logit': (-1.3862943649291992, 0.6),
     'L1_attn_b_idgate': (-1.5, 0.6),
     'L1_ffn_gate_b': (0.0, 0.1),
     'L1_ffn_b1': (0.0, 0.408),
     'L1_ffn_b2': (0.0, 0.1)}
    factors = {'L0_txt_conv_w': 5.901,
     'L0_txt_x_proj_w': 22.055,
     'L0_txt_dt_proj_w': 64.0,
     'L0_txt_dt_proj_b': 64.0,
     'L0_txt_A_log': 64.0,
     'L1_attn_w_qkv': 3.009,
     'L1_attn_w_proj': 3.107,
     'L1_attn_fir_short_w': 7.333,
     'L1_attn_fir_long_w': 8.0,
     'L1_attn_mix': 8.0,
     'L1_attn_w_prune': 8.0,
     'L1_attn_w_g1': 8.0,
     'L1_attn_w_g2': 8.0,
     'L1_attn_w_id': 23.693,
     'L1_attn_w_idgate': 31.576}
    for name, (base, spread) in spreads.items():
        noise = np.random.default_rng([zlib.crc32(name.encode()), seed]).standard_normal(out[name].shape)
        drawn = base * np.exp(spread * noise) if base else spread * noise
        out[name] = jnp.asarray(drawn.astype(out[name].dtype))
    for name, factor in factors.items():
        out[name] = (out[name] * factor).astype(out[name].dtype)
    return out
```

```python
import math
from contextlib import ExitStack

import concourse.bass as bass
from concourse import mybir

F32 = mybir.dt.float32
I32 = mybir.dt.int32
ALU = mybir.AluOpType
ACT = mybir.ActivationFunctionType
AX = mybir.AxisListType

B = 4
NI = 512
NT = 128
N = NI + NT
P = 128
TB = N // P
TILES = B * TB
C = 192
CH = C // 2
H = 12
D = C // H
HALF = N // 2
EPS = 1e-5
ROUND = 1.5 * 2.0 ** 23
TWO_PI = 6.283185


class InOrder:

    def __init__(self, eng, own, per_turn=0):
        self.eng, self.own, self.per_turn, self.base, self.n = eng, own, per_turn, 0, 0

    def turn(self, i):
        self.base, self.n = i * self.per_turn, 0

    def step(self, ins):
        ins.then_inc(self.own, 1)
        self.n += 1
        self.eng.wait_ge(self.own, self.base + self.n)

    def announce(self, ins, sem, value):
        ins.then_inc(sem, 1)
        self.eng.wait_ge(sem, value)

    def count(self, ins):
        ins.then_inc(self.own, 1)
        self.n += 1

    def sem_step(self):
        self.eng.sem_inc(self.own, 1)
        self.n += 1

    def wait(self):
        self.eng.wait_ge(self.own, self.base + self.n)

    def ended(self):
        assert self.n == self.per_turn, (self.n, self.per_turn)


class Ring:

    def __init__(self, eng, banks, filled, taken, per_turn):
        self.eng, self.banks, self.filled, self.taken, self.per_turn = eng, banks, filled, taken, per_turn
        self.base, self.n = 0, 0

    def turn(self, i):
        assert self.n in (0, self.per_turn), (self.n, self.per_turn)
        self.base, self.n = i * self.per_turn, 0

    def bank(self):
        return self.banks[self.n % len(self.banks)]

    def free(self):
        self.eng.wait_ge(self.taken, self.base + self.n + 1)
        return self.bank()

    def fill(self, ins):
        ins.then_inc(self.filled, 1)
        self.n += 1

    def arrived(self, n=None):
        self.eng.wait_ge(self.taken, self.base + len(self.banks) + (self.n if n is None else n))

    def get(self):
        self.eng.wait_ge(self.filled, self.base + self.n + 1)
        return self.bank()

    def take(self, ins):
        ins.then_inc(self.taken, 1)
        self.n += 1

    def done(self):
        self.eng.wait_ge(self.taken, self.base + len(self.banks) + self.n)

    def ended(self):
        assert self.n == self.per_turn, (self.n, self.per_turn)


class Memory:

    def __init__(self, nc, stage):
        self.nc, self.stage, self.stack, self.semaphores = nc, stage, ExitStack(), []

    def __enter__(self):
        return self

    def __exit__(self, *exc):
        if self.semaphores and exc[0] is None:
            self.nc.clear_and_free_semaphores(self.semaphores)
            self.nc.all_engine_barrier()
        self.stack.close()

    def sbuf(self, name, shape, dt=F32):
        return self.stack.enter_context(self.nc.sbuf_tensor(f"{self.stage}_{name}", shape, dt))

    def psum(self, name, shape, dt=F32):
        return self.stack.enter_context(self.nc.psum_tensor(f"{self.stage}_{name}", shape, dt))

    def sem(self, name):
        self.semaphores.append(self.nc.alloc_semaphore(f"{self.stage}_{name}"))
        return self.semaphores[-1]

    def sems(self, *names):
        return [self.sem(n) for n in names]


BANDS = 6
JC = 5
UNITS = JC * BANDS
KTILES = 4 * 2 * BANDS + BANDS


def image_embedding(nc, h, io):
    with Memory(nc, "img") as m:
        w = m.sbuf("w", [P, KTILES, C])
        freq = m.sbuf("freq", [P, BANDS])
        shift = m.sbuf("shift", [P, 2])
        x = m.sbuf("x", [P, 2, NI])
        turns = m.sbuf("turns", [P, 2, NI])
        nearest = m.sbuf("nearest", [P, NI])
        rest = m.sbuf("rest", [P, 2, NI])
        folded = m.sbuf("folded", [P, 2, NI])
        feat = m.sbuf("feat", [P, 3, 2, NI])
        out = m.psum("out", [P, 4, 512])
        (w_in, x_in0, x_in1, x_free, turns_ready, turns_free, rest_ready, folded_ready, rest_free,
         feat_ready, feat_free, out_ready, out_free, dve_own, pool_own) = m.sems(
            "w_in", "x_in0", "x_in1", "x_free", "turns_ready", "turns_free", "rest_ready", "folded_ready",
            "rest_free", "feat_ready", "feat_free", "out_ready", "out_free", "dve_own", "pool_own")
        x_in = [x_in0, x_in1]
        with nc.Block() as block:

            @block.sync
            def _(sp):
                sp.dma_start(freq[:, :], io["freq"]).then_inc(w_in, 16)
                sp.dma_start(shift[:, :], io["sincos_shift"]).then_inc(w_in, 16)
                for part in range(3):
                    k0 = part * 18
                    sp.dma_start(w[:, k0:k0 + 18, :], io["tok_w"][:, k0:k0 + 18, :]).then_inc(w_in, 16)
                with sp.Fori(0, B // 2) as bb:
                    for half in range(2):
                        for c in range(JC):
                            n = half * JC + c
                            sp.wait_ge(x_free, bb * (2 * JC) + n + 1)
                            sp.dma_start(x[:, n % 2, :], io["x"][bass.ds(bb * (2 * JC) + n, 1)].rearrange("o p n -> p (o n)")).then_inc(x_in[n % 2], 16)

            @block.gpsimd
            def _(pool):
                pool.sem_inc(x_free, 2)
                pool.wait_ge(w_in, 5 * 16)
                with pool.Fori(0, B // 2) as bb:
                    for half in range(2):
                        for c in range(JC):
                            n = half * JC + c
                            pool.wait_ge(x_in[n % 2], bb * (16 * JC) + 16 * (n // 2 + 1))
                            for f in range(BANDS):
                                g = n * BANDS + f
                                pool.wait_ge(turns_free, bb * (2 * UNITS) + g + 1)
                                ins = nc.gpsimd.tensor_tensor(turns[:, g % 2, :], x[:, n % 2, :], freq[:, f:f + 1].to_broadcast([P, NI]), ALU.mult)
                                ins.then_inc(turns_ready, 1)
                            pool.wait_ge(turns_ready, bb * (2 * UNITS) + (n + 1) * BANDS)
                            pool.sem_inc(x_free, 1)

            @block.vector
            def _(dve):
                own = InOrder(dve, dve_own, UNITS)
                dve.sem_inc(turns_free, 2)
                with dve.Fori(0, B) as b:
                    own.turn(b)
                    for c in range(JC):
                        for f in range(BANDS):
                            g = c * BANDS + f
                            at = b * UNITS + g + 1
                            dve.wait_ge(turns_ready, at)
                            dve.wait_ge(rest_free, at)
                            own.step(nc.vector.tensor_scalar(nearest[:, :], turns[:, g % 2, :], ROUND, None, ALU.add))
                            own.announce(nc.vector.scalar_tensor_tensor(rest[:, g % 2, :], nearest[:, :], ROUND, turns[:, g % 2, :],
                                                                      ALU.subtract, ALU.subtract), rest_ready, at)
                            dve.sem_inc(turns_free, 1)
                            lo = 0 if c < JC - 1 else 64
                            dst = folded if c < JC - 1 else rest
                            nc.vector.scalar_tensor_tensor(dst[lo:P, g % 2, :], rest[lo:P, g % 2, :], -1.0, rest[lo:P, g % 2, :], ALU.mult, ALU.max).then_inc(folded_ready, 1)
                            dve.wait_ge(folded_ready, at)
                    own.ended()
                    dve.wait_ge(out_ready, b + 1)
                    for t in range(4):
                        nc.vector.tensor_copy(h[:, b * TB + t, :], out[:, t, 0:C]).then_inc(out_free, 1)

            @block.scalar
            def _(act):
                act.sem_inc(rest_free, 2)
                act.wait_ge(w_in, 5 * 16)
                with act.Fori(0, B) as b:
                    for c in range(JC):
                        for f in range(BANDS):
                            g = c * BANDS + f
                            at = b * UNITS + g + 1
                            act.wait_ge(folded_ready, at)
                            act.wait_ge(feat_free, at)
                            if c < JC - 1:
                                nc.scalar.activation(feat[:, g % 3, 0, :], rest[:, g % 2, :], ACT.Sin, scale=-TWO_PI)
                                ins = nc.scalar.activation(feat[:, g % 3, 1, :], folded[:, g % 2, :], ACT.Sin, scale=-TWO_PI,
                                                           bias=shift[:, 1:2])
                            else:
                                ins = nc.scalar.activation(feat[:, g % 3, 0, :], rest[:, g % 2, :], ACT.Sin, scale=-TWO_PI,
                                                           bias=shift[:, 0:1])
                            ins.then_inc(feat_ready, 1)
                            act.wait_ge(feat_ready, at)
                            act.sem_inc(rest_free, 1)

            @block.tensor
            def _(pe):
                pe.sem_inc(feat_free, 3)
                pe.sem_inc(out_free, 4)
                pe.wait_ge(w_in, 5 * 16)
                with pe.Fori(0, B) as b:
                    pe.wait_ge(out_free, b * 4 + 4)
                    for c in range(JC):
                        for f in range(BANDS):
                            g = c * BANDS + f
                            pe.wait_ge(feat_ready, b * UNITS + g + 1)
                            for part in range(2 if c < JC - 1 else 1):
                                k = c * 12 + part * BANDS + f
                                for t in range(4):
                                    ins = nc.tensor.matmul(out[:, t, 0:C], feat[:, g % 3, part, t * P:(t + 1) * P], w[:, k, :],
                                                           start=(k == 0), stop=(k == KTILES - 1))
                            ins.then_inc(feat_free, 1)
                    ins = None
                    pe.wait_ge(feat_free, b * UNITS + UNITS + 3)
                    pe.sem_inc(out_ready, 1)


LAYERS = 2
VOCAB = 8000
DI = 2 * C
FT = DI // P
STATES = 16
RANK = C // STATES
XD = RANK + 2 * STATES
TAPS = 4
CONV_W, CONV_B, DT_B, A_LOG, SKIP, PARAMS = 0, 4, 5, 6, 22, 23
TXT = B * NT
ATANH_TERMS = 8
NO_PAST = 200.0


def text_embedding(nc, h, ident, io):
    with Memory(nc, "txt") as m:
        ids = m.sbuf("ids", [P, B], I32)
        idf = m.sbuf("idf", [P, B])
        neg = m.sbuf("neg", [P, B])
        rows = m.sbuf("rows", [P, B], I32)
        in_w = m.sbuf("in_w", [CH, 2, 2 * DI])
        norm_w = m.sbuf("norm_w", [CH, 2])
        par = m.sbuf("par", [P, FT, PARAMS])
        xp_w = m.sbuf("xp_w", [P, FT, XD])
        dt_w = m.sbuf("dt_w", [RANK, DI])
        out_w = m.sbuf("out_w", [P, FT, C])
        pick = m.sbuf("pick", [XD, 2 * STATES, P])
        squares = m.sbuf("squares", [P, C])
        rms = m.sbuf("rms", [P, B])
        xn = m.sbuf("xn", [P, B, C])
        xnT = m.sbuf("xnT", [CH, 2, TXT])
        padded = m.sbuf("padded", [P, FT, B, TAPS - 1 + NT])
        conv = m.sbuf("conv", [P, FT, TXT])
        u = m.sbuf("u", [P, FT, TXT])
        gate = m.sbuf("gate", [P, FT, TXT])
        xdbl = m.sbuf("xdbl", [XD, TXT])
        delta = m.sbuf("delta", [P, FT, TXT])
        e = m.sbuf("e", [P, FT, TXT])
        ratio = m.sbuf("ratio", [P, FT, TXT])
        ratio2 = m.sbuf("ratio2", [P, FT, TXT])
        series = m.sbuf("series", [P, FT, TXT])
        du = m.sbuf("du", [P, FT, TXT])
        decay_rate = m.sbuf("decay_rate", [P, FT, STATES])
        decay = m.sbuf("decay", [P, 2, FT, TXT])
        exponent = m.sbuf("exponent", [P, 2, FT, TXT])
        drive = m.sbuf("drive", [P, FT, TXT])
        state = m.sbuf("state", [P, FT, TXT])
        read = m.sbuf("read", [P, 2, FT, TXT])
        bank = m.psum("bank", [P, 8, 512])
        XNT, XR, RES, XDB, DT, BN, CN, Y, OUT = 0, 2, 5, 0, 5, (0, 1), (5, 6), 2, 0
        (ids_in, fixed_in, weights_in, weights_free, rows_ready, x_in, padding, xn_ready, xnT_psum, xnT_ready, xz_psum,
         xz_taken, conv_ready, u_ready, xd_psum, xd_ready, dt_psum, e_ready, rate_ready, delta_ready, exponent_ready, exponent_free,
         decay_ready, decay_free, bc_psum, bc_free, read_ready, read_free, y_ready, out_psum, x_ready,
         dve_own, act_own, square_ready, root_ready, a_log_ready, z_ready, pool_turns) = m.sems(*(
            "ids_in fixed_in weights_in weights_free rows_ready x_in padding xn_ready xnT_psum xnT_ready xz_psum "
            "xz_taken conv_ready u_ready xd_psum xd_ready dt_psum e_ready rate_ready delta_ready exponent_ready exponent_free "
            "decay_ready decay_free bc_psum bc_free read_ready read_free y_ready out_psum x_ready "
            "dve_own act_own square_ready root_ready a_log_ready z_ready pool_turns").split())

        def wide(ap):
            return ap.rearrange("p (o n) -> p o n", o=1).to_broadcast([P, FT, TXT])

        with nc.Block() as block:

            @block.sync
            def _(sp):
                sp.dma_start(ids[:, :], io["ids"]).then_inc(ids_in, 16)
                sp.dma_start(pick[:, :, :], io["pick"]).then_inc(fixed_in, 16)
                with sp.Fori(0, LAYERS) as l:
                    sp.wait_ge(weights_free, l + 1)
                    for dst, name in ((in_w, "in_proj"), (norm_w, "norm_w"), (par, "txt_par"), (xp_w, "x_proj"),
                                      (dt_w, "dt_proj"), (out_w, "out_proj")):
                        src = io[name][bass.ds(l, 1)]
                        if len(src.shape) == 4:
                            sp.dma_start(dst[:, :, :], src.rearrange("o p a b -> p (o a) b")).then_inc(weights_in, 16)
                        else:
                            sp.dma_start(dst[:, :], src.rearrange("o p a -> p (o a)")).then_inc(weights_in, 16)

            @block.gpsimd
            def _(pool):
                nc.gpsimd.memset(padded[:, :, :, :], 0.0).then_inc(padding, 1)
                nc.gpsimd.memset(exponent[:, :, :, :], NO_PAST).then_inc(padding, 1)
                pool.wait_ge(padding, 2)
                pool.wait_ge(rows_ready, 1)
                for b in range(B):
                    nc.gpsimd.indirect_dma_start(out=h[:, b * TB + TB - 1, :], out_offset=None, in_=io["emb"],
                                                 in_offset=bass.IndirectOffsetOnAxis(ap=rows[:, b:b + 1], axis=0)).then_inc(x_in, 16)
                with pool.Fori(0, LAYERS) as l:
                    pool.wait_ge(delta_ready, l + 1)
                    pool.wait_ge(rate_ready, l + 1)
                    for n in range(STATES):
                        pool.wait_ge(exponent_free, l * STATES + n + 1)
                        pool.sem_inc(pool_turns, 1)
                        for f in range(FT):
                            later = [a[:, :].rearrange("p (b t) -> p b t", b=B)[:, :, 1:] for a in (exponent[:, n % 2, f], delta[:, f])]
                            ins = nc.gpsimd.tensor_scalar(later[0], later[1], decay_rate[:, f, n:n + 1], NO_PAST, ALU.mult, ALU.min)
                            ins.then_inc(exponent_ready, 1)

            @block.vector
            def _(dve):
                own = InOrder(dve, dve_own)
                dve.wait_ge(ids_in, 16)
                own.step(nc.vector.tensor_copy(idf[:, :], ids[:, :]))
                own.step(nc.vector.tensor_scalar(neg[:, :], idf[:, :], 0.0, float(VOCAB), ALU.is_lt, ALU.mult))
                own.step(nc.vector.tensor_tensor(idf[:, :], idf[:, :], neg[:, :], ALU.add))
                own.step(nc.vector.tensor_scalar(idf[:, :], idf[:, :], 0.0, float(VOCAB - 1), ALU.max, ALU.min))
                nc.vector.tensor_copy(rows[:, :], idf[:, :]).then_inc(rows_ready, 1)
                before = own.n
                own = InOrder(dve, dve_own, TXT_DVE_STEPS)
                dve.wait_ge(x_in, 16 * B)
                dve.sem_inc(bc_free, 2)
                with dve.Fori(0, LAYERS) as l:
                    own.turn(l)
                    own.base = own.base + before
                    dve.wait_ge(x_ready, l * B + 1)
                    for b in range(B):
                        x = h[:, b * TB + TB - 1, :]
                        own.step(nc.vector.tensor_tensor_reduce(out=squares[:, :], in0=x, in1=x, scale=1.0, scalar=0.0,
                                                                op0=ALU.mult, op1=ALU.add, accum_out=rms[:, b:b + 1]))
                    own.step(nc.vector.tensor_scalar(rms[:, :], rms[:, :], 1.0 / C, EPS, ALU.mult, ALU.add))
                    nc.vector.reciprocal(rms[:, :], rms[:, :]).then_inc(square_ready, 1)
                    dve.wait_ge(root_ready, l + 1)
                    for b in range(B):
                        nc.vector.tensor_scalar(xn[:, b, :], h[:, b * TB + TB - 1, :], rms[:, b:b + 1], None, ALU.mult).then_inc(xn_ready, 1)
                    dve.wait_ge(weights_in, l * 96 + 96)
                    nc.vector.tensor_scalar(par[:, :, A_LOG:A_LOG + STATES], par[:, :, A_LOG:A_LOG + STATES], 88.7, None,
                                            ALU.min).then_inc(a_log_ready, 1)
                    dve.wait_ge(xnT_psum, l + 1)
                    for k in range(2):
                        nc.vector.tensor_scalar(xnT[:, k, :], bank[0:CH, XNT + k, :], norm_w[:, k:k + 1], None, ALU.mult).then_inc(xnT_ready, 1)
                    dve.wait_ge(xz_taken, l * 2 * FT + FT)
                    for f in range(FT):
                        for k in range(TAPS):
                            src = padded[:, f, :, k:k + NT]
                            dst = conv[:, f, :].rearrange("p (b t) -> p b t", b=B)
                            tap = par[:, f, CONV_W + k:CONV_W + k + 1]
                            if k == 0:
                                own.step(nc.vector.tensor_scalar(dst, src, tap, None, ALU.mult))
                            elif k < TAPS - 1:
                                own.step(nc.vector.scalar_tensor_tensor(dst, src, tap, dst, ALU.mult, ALU.add))
                            else:
                                nc.vector.scalar_tensor_tensor(dst, src, tap, dst, ALU.mult, ALU.add).then_inc(conv_ready, 1)
                    dve.wait_ge(xd_psum, l + 1)
                    nc.vector.tensor_copy(xdbl[:, :], bank[0:XD, XDB, :]).then_inc(xd_ready, 1)
                    dve.wait_ge(dt_psum, l + 1)
                    for f in range(FT):
                        nc.vector.tensor_scalar(series[:, f, :], bank[:, DT + f, :], par[:, f, DT_B:DT_B + 1], None, ALU.add).then_inc(z_ready, 1)
                    dve.wait_ge(z_ready, l * FT + FT)
                    own.step(nc.vector.tensor_scalar(delta[:, :, :], series[:, :, :], 0.0, None, ALU.max))
                    dve.wait_ge(e_ready, l + 1)
                    own.step(nc.vector.tensor_scalar(ratio[:, :, :], e[:, :, :], 2.0, None, ALU.add))
                    own.step(nc.vector.reciprocal(ratio[:, :, :], ratio[:, :, :]))
                    own.step(nc.vector.tensor_tensor(ratio[:, :, :], ratio[:, :, :], e[:, :, :], ALU.mult))
                    own.step(nc.vector.tensor_tensor(ratio2[:, :, :], ratio[:, :, :], ratio[:, :, :], ALU.mult))
                    own.step(nc.vector.tensor_scalar(series[:, :, :], ratio2[:, :, :], 1.0 / (2 * ATANH_TERMS - 1), None, ALU.mult))
                    for t in range(ATANH_TERMS - 2, 0, -1):
                        own.step(nc.vector.scalar_tensor_tensor(series[:, :, :], series[:, :, :], 1.0 / (2 * t + 1), ratio2[:, :, :],
                                                                ALU.add, ALU.mult))
                    own.step(nc.vector.scalar_tensor_tensor(series[:, :, :], series[:, :, :], 1.0, ratio[:, :, :], ALU.add, ALU.mult))
                    own.announce(nc.vector.scalar_tensor_tensor(delta[:, :, :], series[:, :, :], 2.0, delta[:, :, :], ALU.mult, ALU.add),
                               delta_ready, l + 1)
                    dve.wait_ge(u_ready, l * FT + FT)
                    own.step(nc.vector.tensor_tensor(du[:, :, :], delta[:, :, :], u[:, :, :], ALU.mult))
                    for n in range(STATES):
                        at = l * STATES + n + 1
                        dve.wait_ge(bc_psum, at)
                        own.step(nc.vector.tensor_tensor(drive[:, :, :], du[:, :, :], wide(bank[:, BN[n % 2], :]), ALU.mult))
                        dve.wait_ge(decay_ready, at)
                        own.announce(nc.vector.tensor_tensor_scan(state[:, :, :].rearrange("p f n -> p (f n)"),
                                                                decay[:, n % 2, :, :].rearrange("p f n -> p (f n)"),
                                                                drive[:, :, :].rearrange("p f n -> p (f n)"), 0.0, ALU.mult, ALU.add),
                                   decay_free, at + 2)
                        dve.wait_ge(read_free, at)
                        own.announce(nc.vector.tensor_tensor(read[:, n % 2, :, :], state[:, :, :], wide(bank[:, CN[n % 2], :]), ALU.mult),
                                   read_ready, at)
                        dve.sem_inc(bc_free, 1)
                    dve.wait_ge(read_free, l * STATES + STATES + 2)
                    for f in range(FT):
                        own.step(nc.vector.scalar_tensor_tensor(conv[:, f, :], u[:, f, :], par[:, f, SKIP:SKIP + 1], bank[:, Y + f, :],
                                                                ALU.mult, ALU.add))
                    own.announce(nc.vector.tensor_tensor(conv[:, :, :], conv[:, :, :], gate[:, :, :], ALU.mult), y_ready, l + 1)
                    dve.wait_ge(out_psum, l + 1)
                    for b in range(B):
                        x = h[:, b * TB + TB - 1, :]
                        nc.vector.tensor_tensor(x, x, bank[:, OUT + b // 2, (b % 2) * C:(b % 2 + 1) * C], ALU.add).then_inc(x_ready, 1)
                    dve.wait_ge(x_ready, l * B + B + 1)
                    own.ended()

            @block.scalar
            def _(act):
                act.sem_inc(x_ready, 1)
                act.sem_inc(decay_free, 2)
                act.sem_inc(exponent_free, 2)
                own = InOrder(act, act_own, TXT_ACT_STEPS)
                act.wait_ge(padding, 1)
                with act.Fori(0, LAYERS) as l:
                    own.turn(l)
                    act.wait_ge(square_ready, l + 1)
                    nc.scalar.activation(rms[:, :], rms[:, :], ACT.Sqrt).then_inc(root_ready, 1)
                    for f in range(FT):
                        act.wait_ge(xz_psum, l * 2 * FT + f + 1)
                        nc.scalar.activation(padded[:, f, :, TAPS - 1:], bank[:, XR + f, :].rearrange("p (b t) -> p b t", b=B),
                                             ACT.Copy).then_inc(xz_taken, 1)
                    for f in range(FT):
                        act.wait_ge(xz_psum, l * 2 * FT + FT + f + 1)
                        nc.scalar.activation(gate[:, f, :], bank[:, RES + f, :], ACT.Silu).then_inc(xz_taken, 1)
                    for f in range(FT):
                        act.wait_ge(conv_ready, l * FT + f + 1)
                        nc.scalar.activation(u[:, f, :], conv[:, f, :], ACT.Silu, bias=par[:, f, CONV_B:CONV_B + 1]).then_inc(u_ready, 1)
                    act.wait_ge(a_log_ready, l + 1)
                    own.announce(nc.scalar.activation(decay_rate[:, :, :], par[:, :, A_LOG:A_LOG + STATES], ACT.Exp), rate_ready, l + 1)
                    act.wait_ge(z_ready, l * FT + FT)
                    own.step(nc.scalar.activation(e[:, :, :], series[:, :, :], ACT.Abs))
                    own.announce(nc.scalar.activation(e[:, :, :], e[:, :, :], ACT.Exp, scale=-1.0), e_ready, l + 1)
                    for n in range(STATES):
                        act.wait_ge(decay_free, l * STATES + n + 1)
                        act.wait_ge(exponent_ready, (l * STATES + n + 1) * FT)
                        nc.scalar.activation(decay[:, n % 2, :, :], exponent[:, n % 2, :, :], ACT.Exp, scale=-1.0).then_inc(decay_ready, 1)
                        act.wait_ge(decay_ready, l * STATES + n + 1)
                        act.sem_inc(exponent_free, 1)
                    own.ended()

            @block.tensor
            def _(pe):
                pe.sem_inc(read_free, 2)
                pe.sem_inc(weights_free, 1)
                pe.wait_ge(fixed_in, 16)
                with pe.Fori(0, LAYERS) as l:
                    pe.wait_ge(weights_in, l * 96 + 96)
                    for b in range(B):
                        pe.wait_ge(xn_ready, l * B + b + 1)
                        for k in range(2):
                            ins = nc.tensor.transpose(bank[0:CH, XNT + k, b * P:(b + 1) * P], xn[:, b, k * CH:(k + 1) * CH], ident[:, :])
                    ins.then_inc(xnT_psum, 1)
                    pe.wait_ge(xnT_ready, l * 2 + 2)
                    for f in range(2 * FT):
                        for k in range(2):
                            ins = nc.tensor.matmul(bank[:, XR + f, :], in_w[:, k, f * P:(f + 1) * P], xnT[:, k, :], start=(k == 0), stop=(k == 1))
                        ins.then_inc(xz_psum, 1)
                    for f in range(FT):
                        pe.wait_ge(u_ready, l * FT + f + 1)
                        ins = nc.tensor.matmul(bank[0:XD, XDB, :], xp_w[:, f, :], u[:, f, :], start=(f == 0), stop=(f == FT - 1))
                    ins.then_inc(xd_psum, 1)
                    pe.wait_ge(xd_ready, l + 1)
                    pe.wait_ge(xz_taken, l * 2 * FT + 2 * FT)
                    for f in range(FT):
                        ins = nc.tensor.matmul(bank[:, DT + f, :], dt_w[:, f * P:(f + 1) * P], xdbl[0:RANK, :], start=True, stop=True)
                    ins.then_inc(dt_psum, 1)
                    pe.wait_ge(delta_ready, l + 1)
                    for n in range(STATES):
                        at = l * STATES + n + 1
                        pe.wait_ge(bc_free, at)
                        nc.tensor.matmul(bank[:, BN[n % 2], :], pick[:, n, :], xdbl[:, :], start=True, stop=True)
                        nc.tensor.matmul(bank[:, CN[n % 2], :], pick[:, STATES + n, :], xdbl[:, :], start=True, stop=True).then_inc(bc_psum, 1)
                        if n >= 1:
                            pe.wait_ge(read_ready, at - 1)
                            for f in range(FT):
                                ins = nc.tensor.matmul(bank[:, Y + f, :], ident[:, :], read[:, (n - 1) % 2, f, :], start=(n == 1), stop=False)
                            ins.then_inc(read_free, 1)
                    pe.wait_ge(read_ready, l * STATES + STATES)
                    for f in range(FT):
                        ins = nc.tensor.matmul(bank[:, Y + f, :], ident[:, :], read[:, (STATES - 1) % 2, f, :], start=False, stop=True)
                    ins.then_inc(read_free, 1)
                    pe.wait_ge(y_ready, l + 1)
                    for b in range(B):
                        for f in range(FT):
                            ins = nc.tensor.matmul(bank[:, OUT + b // 2, (b % 2) * C:(b % 2 + 1) * C], conv[:, f, b * P:(b + 1) * P],
                                                   out_w[:, f, :], start=(f == 0), stop=(f == FT - 1))
                    ins.then_inc(out_psum, 1)
                    pe.wait_ge(out_psum, l + 1)
                    pe.sem_inc(weights_free, 1)


TXT_DVE_STEPS = 47
TXT_ACT_STEPS = 1


class Normed:

    def __init__(self, m, name):
        self.stats = m.sbuf(f"{name}_stats", [P, TB, 6])
        self.mv = m.sbuf(f"{name}_mv", [P, TB, 2])
        self.rstd = m.sbuf(f"{name}_rstd", [P, TB])
        self.xn = m.sbuf(f"{name}_xn", [P, TB, C])
        self.xT = m.sbuf(f"{name}_xT", [CH, 2, N])
        self.var_ready = m.sem(f"{name}_var")
        self.rstd_ready = m.sem(f"{name}_rstd")
        self.xn_ready = m.sem(f"{name}_xn")
        self.psum_ready = m.sem(f"{name}_psum")
        self.xT_ready = m.sem(f"{name}_xT")


NORM_STEPS = 2 * TB + 2


def norm_rows(nc, dve, own, z, src, b, dst=None):
    dst = dst or (lambda s: z.xn[:, s, :])
    for s in range(TB):
        own.count(nc.vector.bn_stats(z.stats[:, s, :], src(s)))
    own.wait()
    own.sem_step()
    for s in range(TB):
        own.count(nc.vector.bn_aggr(z.mv[:, s, :], z.stats[:, s, :]))
    own.wait()
    own.step(nc.vector.tensor_scalar(z.rstd[:, :], z.mv[:, :, 1], EPS, None, ALU.add))
    nc.vector.reciprocal(z.rstd[:, :], z.rstd[:, :]).then_inc(z.var_ready, 1)
    dve.wait_ge(z.rstd_ready, b + 1)
    for s in range(TB):
        nc.vector.tensor_scalar(dst(s), src(s), z.mv[:, s, 0:1], z.rstd[:, s:s + 1], ALU.subtract, ALU.mult).then_inc(z.xn_ready, 1)


def root(nc, act, z, b):
    act.wait_ge(z.var_ready, b + 1)
    nc.scalar.activation(z.rstd[:, :], z.rstd[:, :], ACT.Sqrt).then_inc(z.rstd_ready, 1)


def transpose_rows(nc, pe, src, ident, bank, ready):
    for s in range(TB):
        for k in range(2):
            out = bank[0:CH, k, s * P:(s + 1) * P] if s < 4 else bank[0:CH, 2, k * P:(k + 1) * P]
            ins = nc.tensor.transpose(out, src(s, k), ident[:, :])
    ins.then_inc(ready, 1)


def copy_transposed(nc, bank, xT, ready, scale=None, shift=None):
    for k in range(2):
        for src, dst in ((bank[0:CH, k, :], xT[:, k, 0:4 * P]), (bank[0:CH, 2, k * P:(k + 1) * P], xT[:, k, 4 * P:])):
            if scale is None:
                ins = nc.scalar.activation(dst, src, ACT.Copy)
            else:
                ins = nc.scalar.activation(dst, src, ACT.Identity, scale=scale[:, k:k + 1], bias=shift[:, k:k + 1])
            ins.then_inc(ready, 1)


COPIES = 4


def load(sp, pairs, sem):
    for dst, src in pairs:
        idx = tuple(slice(None) for _ in dst.shape)
        sp.dma_start(dst[idx], src).then_inc(sem, 16)
    return 16 * len(pairs)


M = 64
GH = H // 2
PAIRS = H // 2
DV = D + 1
KERNEL_EPS = 1e-3
QK_SCALE = 1.0 / math.sqrt(math.sqrt(D))
PERF_ITEMS = 4 + 4 + 2 * TB + TB + 12 + 1 + TB + TB


def performer(nc, h, ident, io):
    with Memory(nc, "perf") as m:
        z = Normed(m, "ln")
        w = m.sbuf("w", [CH, 2, 3 * C])
        bqk = m.sbuf("bqk", [CH, 2, 2])
        bv = m.sbuf("bv", [1, C])
        wp = m.sbuf("wp", [CH, 2, C])
        bp = m.sbuf("bp", [1, C])
        feat = m.sbuf("feat", [CH, GH * M])
        ones = m.sbuf("ones", [1, P])
        qT = m.sbuf("qT", [CH, 2, N])
        kT = m.sbuf("kT", [CH, 2, N])
        kp = m.sbuf("kp", [P, TB, H * M])
        v = m.sbuf("v", [P, TB, H, DV])
        qpT = m.sbuf("qpT", [P, PAIRS, N])
        ctx = m.sbuf("ctx", [P, PAIRS, 2 * DV])
        recip = m.sbuf("recip", [P, H])
        attn = m.sbuf("attn", [P, TB, C])
        aT = m.sbuf("aT", [CH, 2, N])
        bank = m.psum("bank", [P, 8, 512])
        banks = (3, 4, 5, 6, 7)
        (loaded, set_up, filled, taken, attn_ready, aT_psum, aT_ready, h_ready, dve_own) = m.sems(
            *"loaded set_up filled taken attn_ready aT_psum aT_ready h_ready dve_own".split())
        pairs = ((w, io["perf_w"]), (bqk, io["perf_bqk"]), (bv, io["perf_bv"]), (wp, io["perf_wp"]), (bp, io["perf_bp"]),
                 (feat, io["perf_feat"]))
        LOADED = 16 * len(pairs)
        with nc.Block() as block:

            @block.sync
            def _(sp):
                load(sp, pairs, loaded)

            @block.gpsimd
            def _(pool):
                nc.gpsimd.memset(v[:, :, :, :], 1.0).then_inc(set_up, 1)
                nc.gpsimd.memset(ctx[:, :, :], 0.0).then_inc(set_up, 1)
                nc.gpsimd.memset(ones[:, :], 1.0).then_inc(set_up, 1)

            @block.vector
            def _(dve):
                own = InOrder(dve, dve_own, NORM_STEPS + TB)
                ring = Ring(dve, banks, filled, taken, PERF_ITEMS)
                dve.sem_inc(taken, len(banks))
                dve.wait_ge(loaded, LOADED)
                dve.wait_ge(set_up, 3)
                with dve.Fori(0, B) as b:
                    own.turn(b)
                    ring.turn(b)
                    norm_rows(nc, dve, own, z, lambda s: h[:, b * TB + s, :], b)
                    for i, dst in enumerate((qT, kT)):
                        for half in range(2):
                            for c in range(2):
                                src = ring.get()
                                ring.take(nc.vector.tensor_scalar(dst[:, half, c * HALF:(c + 1) * HALF], bank[0:CH, src, 0:HALF],
                                                                  bqk[:, half, i:i + 1], QK_SCALE, ALU.add, ALU.mult))
                    for s in range(TB):
                        for half in range(2):
                            src = ring.get()
                            ring.take(nc.vector.tensor_scalar(kp[:, s, half * GH * M:(half + 1) * GH * M], bank[:, src, 0:GH * M], 0.0,
                                                              KERNEL_EPS, ALU.max, ALU.add))
                        src = ring.get()
                        ring.take(nc.vector.tensor_copy(v[:, s, :, 0:D], bank[:, src, 0:C].rearrange("p (h d) -> p h d", h=H)))
                    for j in range(PAIRS):
                        for c in range(2):
                            src = ring.get()
                            ring.take(nc.vector.tensor_scalar(qpT[:, j, c * HALF:(c + 1) * HALF], bank[:, src, 0:HALF], 0.0, KERNEL_EPS,
                                                              ALU.max, ALU.add))
                    src = ring.get()
                    got = bank[:, src, 0:PAIRS * 2 * DV].rearrange("p (j c) -> p j c", j=PAIRS)
                    nc.vector.tensor_copy(ctx[0:M, :, 0:DV], got[0:M, :, 0:DV])
                    ring.take(nc.vector.tensor_copy(ctx[M:P, :, DV:], got[M:P, :, DV:]))
                    for s in range(TB):
                        src = ring.get()
                        got = bank[:, src, 0:H * DV].rearrange("p (h c) -> p h c", h=H)
                        own.step(nc.vector.reciprocal(recip[:, :], got[:, :, D]))
                        ring.take(nc.vector.tensor_tensor(attn[:, s, :].rearrange("p (h d) -> p h d", h=H), got[:, :, 0:D],
                                                          recip[:, :].unsqueeze(2).to_broadcast([P, H, D]), ALU.mult))
                        ring.done()
                    for s in range(TB):
                        src = ring.get()
                        row = h[:, b * TB + s, :]
                        ring.take(nc.vector.tensor_tensor(row, row, bank[:, src, 0:C], ALU.add))
                    ring.done()
                    ring.ended()
                    own.ended()

            @block.scalar
            def _(act):
                with act.Fori(0, B) as b:
                    root(nc, act, z, b)
                    act.wait_ge(z.psum_ready, b + 1)
                    copy_transposed(nc, bank, z.xT, z.xT_ready)
                    act.wait_ge(aT_psum, b + 1)
                    copy_transposed(nc, bank, aT, aT_ready)

            @block.tensor
            def _(pe):
                ring = Ring(pe, banks, filled, taken, PERF_ITEMS)
                pe.wait_ge(loaded, LOADED)
                pe.wait_ge(set_up, 3)
                with pe.Fori(0, B) as b:
                    ring.turn(b)
                    pe.wait_ge(z.xn_ready, b * TB + TB)
                    transpose_rows(nc, pe, lambda s, k: z.xn[:, s, k * CH:(k + 1) * CH], ident, bank, z.psum_ready)
                    pe.wait_ge(z.xT_ready, b * COPIES + COPIES)
                    for i in range(2):
                        for half in range(2):
                            for c in range(2):
                                dst = ring.free()
                                for k in range(2):
                                    at = i * C + half * CH
                                    ins = nc.tensor.matmul(bank[0:CH, dst, 0:HALF], w[:, k, at:at + CH], z.xT[:, k, c * HALF:(c + 1) * HALF],
                                                           start=(k == 0), stop=(k == 1))
                                ring.fill(ins)
                    ring.arrived(8)
                    for s in range(TB):
                        for half in range(2):
                            dst = ring.free()
                            ring.fill(nc.tensor.matmul(bank[:, dst, 0:GH * M], kT[:, half, s * P:(s + 1) * P], feat[:, :], start=True, stop=True))
                        dst = ring.free()
                        for k in range(2):
                            nc.tensor.matmul(bank[:, dst, 0:C], z.xT[:, k, s * P:(s + 1) * P], w[:, k, 2 * C:], start=(k == 0), stop=False)
                        ring.fill(nc.tensor.matmul(bank[:, dst, 0:C], ones[:, :], bv[:, :], start=False, stop=True))
                    for j in range(PAIRS):
                        at = (j % 3) * P
                        for c in range(2):
                            dst = ring.free()
                            ring.fill(nc.tensor.matmul(bank[:, dst, 0:HALF], feat[:, at:at + P], qT[:, j // 3, c * HALF:(c + 1) * HALF],
                                                       start=True, stop=True))
                    ring.arrived(8 + 3 * TB)
                    dst = ring.free()
                    for j in range(PAIRS):
                        for s in range(TB):
                            ins = nc.tensor.matmul(bank[:, dst, j * 2 * DV:(j + 1) * 2 * DV], kp[:, s, j * P:(j + 1) * P],
                                                   v[:, s, 2 * j:2 * j + 2, :].rearrange("p h c -> p (h c)"), start=(s == 0), stop=(s == TB - 1))
                    ring.fill(ins)
                    ring.arrived()
                    for s in range(TB):
                        dst = ring.free()
                        for j in range(PAIRS):
                            ins = nc.tensor.matmul(bank[:, dst, j * 2 * DV:(j + 1) * 2 * DV], qpT[:, j, s * P:(s + 1) * P], ctx[:, j, :],
                                                   start=True, stop=True)
                        ring.fill(ins)
                    ring.arrived()
                    transpose_rows(nc, pe, lambda s, k: attn[:, s, k * CH:(k + 1) * CH], ident, bank, aT_psum)
                    pe.wait_ge(aT_ready, b * COPIES + COPIES)
                    for s in range(TB):
                        dst = ring.free()
                        for k in range(2):
                            nc.tensor.matmul(bank[:, dst, 0:C], aT[:, k, s * P:(s + 1) * P], wp[:, k, :], start=(k == 0), stop=False)
                        ring.fill(nc.tensor.matmul(bank[:, dst, 0:C], ones[:, :], bp[:, :], start=False, stop=True))
                    ring.ended()


BF16 = mybir.dt.bfloat16
PARTS = 3
STACK = ((0, 0), (0, 1), (1, 0), (1, 1), (0, 2), (2, 0))
ROWS = len(STACK) * D
ALL_ROWS = ROWS + PARTS
LOT = 4
LOTS = H // LOT
QK_ITEMS = 2 * 2 * 2 + TB


def split_bf16(nc, own, x, parts, rest):
    own.step(nc.vector.tensor_copy(parts[0], x))
    own.step(nc.vector.tensor_tensor(rest, x, parts[0], ALU.subtract))
    own.step(nc.vector.tensor_copy(parts[1], rest))
    return nc.vector.tensor_tensor(parts[2], rest, parts[1], ALU.subtract)


def attention_operands(nc, h, x1, v, qk_rows, ident, io):
    with Memory(nc, "qk") as m:
        z0 = Normed(m, "ln0")
        z = Normed(m, "ln1")
        wqk = m.sbuf("wqk", [CH, 2, 2 * C])
        wv = m.sbuf("wv", [CH, 2, C])
        ln = m.sbuf("ln", [CH, 2, 2])
        parts = m.sbuf("parts", [CH, 2, 2, PARTS, N], BF16)
        rest = m.sbuf("rest", [CH, HALF])
        bank = m.psum("bank", [P, 8, 512])
        banks = (3, 4, 5, 6, 7)
        (loaded, set_up, filled, taken, stored, dve_own) = m.sems(*"loaded set_up filled taken stored dve_own".split())
        pairs = ((wqk, io["att_wqk"]), (wv, io["att_wv"]), (ln, io["att_ln"]))
        LOADED = 16 * len(pairs)
        with nc.Block() as block:

            @block.sync
            def _(sp):
                load(sp, pairs, loaded)
                with sp.Fori(0, B) as b:
                    sp.wait_ge(taken, b * QK_ITEMS + len(banks) + 8)
                    for half in range(2):
                        dst = qk_rows[bass.ds(b * 2 * PARTS, 2 * PARTS), half * CH:(half + 1) * CH, :]
                        sp.dma_start(dst.rearrange("i c n -> c i n"), parts[:, half].rearrange("c i s n -> c (i s) n")).then_inc(stored, 16)
                sp.wait_ge(stored, 32 * B + 32)

            @block.gpsimd
            def _(pool):
                nc.gpsimd.memset(v[:, :, :, :], 1.0).then_inc(set_up, 1)

            @block.vector
            def _(dve):
                own = InOrder(dve, dve_own, 2 * NORM_STEPS + 1 + 8 * 3)
                ring = Ring(dve, banks, filled, taken, QK_ITEMS)
                dve.sem_inc(taken, len(banks))
                dve.sem_inc(stored, 32)
                dve.wait_ge(loaded, LOADED)
                dve.wait_ge(set_up, 1)
                with dve.Fori(0, B) as b:
                    own.turn(b)
                    ring.turn(b)
                    norm_rows(nc, dve, own, z0, lambda s: h[:, b * TB + s, :], b, lambda s: x1[:, b * TB + s, :])
                    dve.wait_ge(z0.xn_ready, b * TB + TB)
                    own.sem_step()
                    norm_rows(nc, dve, own, z, lambda s: x1[:, b * TB + s, :], b)
                    dve.wait_ge(stored, b * 32 + 32)
                    for i in range(2):
                        for half in range(2):
                            for c in range(2):
                                slot = ring.get()
                                cols = slice(c * HALF, (c + 1) * HALF)
                                ring.take(split_bf16(nc, own, bank[0:CH, slot, 0:HALF], [parts[:, half, i, p, cols] for p in range(PARTS)],
                                                     rest[:, :]))
                                ring.done()
                    for s in range(TB):
                        slot = ring.get()
                        ring.take(nc.vector.tensor_scalar(v[:, b * TB + s, :, 0:D], bank[:, slot, 0:C].rearrange("p (h d) -> p h d", h=H),
                                                          1.0, None, ALU.mult))
                    ring.ended()
                    own.ended()

            @block.scalar
            def _(act):
                act.wait_ge(loaded, LOADED)
                with act.Fori(0, B) as b:
                    root(nc, act, z0, b)
                    root(nc, act, z, b)
                    act.wait_ge(z.psum_ready, b + 1)
                    copy_transposed(nc, bank, z.xT, z.xT_ready, ln[:, 0, :], ln[:, 1, :])

            @block.tensor
            def _(pe):
                ring = Ring(pe, banks, filled, taken, QK_ITEMS)
                pe.wait_ge(loaded, LOADED)
                with pe.Fori(0, B) as b:
                    ring.turn(b)
                    pe.wait_ge(z.xn_ready, b * TB + TB)
                    transpose_rows(nc, pe, lambda s, k: z.xn[:, s, k * CH:(k + 1) * CH], ident, bank, z.psum_ready)
                    pe.wait_ge(z.xT_ready, b * COPIES + COPIES)
                    for i in range(2):
                        for half in range(2):
                            for c in range(2):
                                slot = ring.free()
                                at = i * C + half * CH
                                for k in range(2):
                                    ins = nc.tensor.matmul(bank[0:CH, slot, 0:HALF], wqk[:, k, at:at + CH], z.xT[:, k, c * HALF:(c + 1) * HALF],
                                                           start=(k == 0), stop=(k == 1))
                                ring.fill(ins)
                    for s in range(TB):
                        slot = ring.free()
                        for k in range(2):
                            ins = nc.tensor.matmul(bank[:, slot, 0:C], z.xT[:, k, s * P:(s + 1) * P], wv[:, k, :], start=(k == 0), stop=(k == 1))
                        ring.fill(ins)
                    ring.ended()


WINDOW = 96
MAX_ITEMS = H * TB + H + TB
EXP_ITEMS = H + H * TB + 2
MAX_LAG, PV_LAG = 2, 3


def softmax_attention(nc, x1, v, qk_rows, ident, io):
    with Memory(nc, "att") as m:
        q = m.sbuf("q", [ALL_ROWS, H, N], BF16)
        k = m.sbuf("k", [ALL_ROWS, H, N], BF16)
        wp = m.sbuf("wp", [CH, 2, C])
        ident16 = m.sbuf("ident16", [P, P], BF16)
        vb = m.sbuf("vb", [P, TB, H * DV])
        negmax = m.sbuf("negmax", [P, H, TB])
        rest = m.sbuf("rest", [P, TB])
        placed = m.sbuf("placed", [P, 2, TB, ALL_ROWS], BF16)
        probs = m.sbuf("probs", [P, 2, TB, N])
        recip = m.sbuf("recip", [P, TB])
        attn = m.sbuf("attn", [P, TB, C])
        aT = m.sbuf("aT", [CH, 2, N])
        bank = m.psum("bank", [P, 8, 512])
        exp_banks, banks = (0, 2), (4, 6)
        (loaded, set_up, filled, taken, exp_filled, exp_taken, placed_ready, v_ready, lot_used, ones_ready, dve_own) = m.sems(
            *"loaded set_up filled taken exp_filled exp_taken placed_ready v_ready lot_used ones_ready dve_own".split())
        lot_in = m.sems(*(f"lot_in{i}" for i in range(LOTS)))
        LOT_IN = 16 * 2 * len(STACK)

        def two(slot, rows=P):
            return bank[0:rows, slot:slot + 2, 0:HALF]

        def halves(ap):
            return ap.rearrange("p (c n) -> p c n", c=2)

        with nc.Block() as block:

            @block.sync
            def _(sp):
                load(sp, ((wp, io["att_wp"]),), loaded)
                with sp.Fori(0, B) as b:
                    for lot in range(LOTS):
                        heads = slice(lot * LOT, (lot + 1) * LOT)
                        sp.wait_ge(lot_used, b * LOTS + lot + 1)
                        for i, buf in enumerate((q, k)):
                            for at, pair in enumerate(STACK):
                                src = qk_rows[bass.ds((b * 2 + i) * PARTS + pair[i], 1), lot * LOT * D:(lot + 1) * LOT * D, :]
                                sp.dma_start(buf[at * D:(at + 1) * D, heads, :], src.rearrange("o (h d) n -> d (o h) n", d=D)).then_inc(lot_in[lot], 16)

            @block.gpsimd
            def _(pool):
                nc.gpsimd.memset(k[ROWS:ALL_ROWS, :, :], 1.0).then_inc(ones_ready, 1)
                pool.wait_ge(ones_ready, 1)
                nc.gpsimd.memset(placed[:, :, :, :], 0.0).then_inc(set_up, 1)

            @block.vector
            def _(dve):
                own = InOrder(dve, dve_own, H * 4)
                ring = Ring(dve, banks, filled, taken, MAX_ITEMS)
                dve.sem_inc(taken, len(banks))
                dve.wait_ge(loaded, 16)
                nc.vector.tensor_copy(ident16[:, :], ident[:, :]).then_inc(set_up, 1)
                dve.wait_ge(set_up, 2)

                def maxima(head, s):
                    slot = ring.get()
                    ring.take(nc.vector.tensor_reduce(negmax[:, head, s:s + 1], two(slot), AX.XY, ALU.max, negate=True))

                def place(head):
                    ring.done()
                    cols = [placed[:, head % 2, :, ROWS + p] for p in range(PARTS)]
                    split_bf16(nc, own, negmax[:, head, :], cols, rest[:, :]).then_inc(placed_ready, 1)

                def normalize(head):
                    ring.done()
                    slot = ring.get()
                    at = head * DV - min(head * DV, H * DV - WINDOW)
                    got = bank[:, slot, 0:TB * WINDOW].rearrange("p (s c) -> p s c", s=TB)
                    own.step(nc.vector.reciprocal(recip[:, :], got[:, :, at + D]))
                    ring.take(nc.vector.tensor_tensor(attn[:, :, head * D:(head + 1) * D], got[:, :, at:at + D],
                                                      recip[:, :].unsqueeze(2).to_broadcast([P, TB, D]), ALU.mult))

                with dve.Fori(0, B) as b:
                    own.turn(b)
                    ring.turn(b)
                    nc.vector.tensor_scalar(vb[:, :, :], v[:, bass.ds(b * TB, TB), :, :].rearrange("p s h c -> p s (h c)"), 1.0, None,
                                            ALU.mult).then_inc(v_ready, 1)
                    for i in range(H + PV_LAG):
                        if i < H:
                            for s in range(TB):
                                maxima(i, s)
                            place(i)
                        if i >= PV_LAG:
                            normalize(i - PV_LAG)
                    for s in range(TB):
                        slot = ring.get()
                        row = x1[:, b * TB + s, :]
                        ring.take(nc.vector.tensor_tensor(row, row, bank[:, slot, 0:C], ALU.add))
                    ring.ended()
                    own.ended()

            @block.scalar
            def _(act):
                ring = Ring(act, exp_banks, exp_filled, exp_taken, EXP_ITEMS)
                act.sem_inc(exp_taken, len(exp_banks))
                with act.Fori(0, B) as b:
                    ring.turn(b)
                    for i in range(H + MAX_LAG):
                        if 1 <= i <= H:
                            slot = ring.get()
                            got = bank[ROWS:ALL_ROWS, slot:slot + 2, :]
                            nc.scalar.activation(q[ROWS:ALL_ROWS, i - 1, 0:4 * P], got[:, 0, :], ACT.Copy)
                            ring.take(nc.scalar.activation(q[ROWS:ALL_ROWS, i - 1, 4 * P:], got[:, 1, 0:P], ACT.Copy))
                        if i >= MAX_LAG:
                            head = i - MAX_LAG
                            for t in range(TB):
                                slot = ring.get()
                                ring.take(nc.scalar.activation(halves(probs[:, head % 2, t, :]), two(slot), ACT.Exp, scale=float(D) ** -0.5))
                    for half in range(2):
                        slot = ring.get()
                        nc.scalar.activation(aT[:, half, 0:4 * P], bank[0:CH, slot, :], ACT.Copy)
                        ring.take(nc.scalar.activation(aT[:, half, 4 * P:], bank[0:CH, slot + 1, 0:P], ACT.Copy))
                    ring.ended()

            @block.tensor
            def _(pe):
                ring = Ring(pe, banks, filled, taken, MAX_ITEMS)
                exps = Ring(pe, exp_banks, exp_filled, exp_taken, EXP_ITEMS)
                pe.sem_inc(lot_used, LOTS)
                pe.wait_ge(loaded, 16)
                pe.wait_ge(ones_ready, 1)
                pe.wait_ge(set_up, 2)

                def queries_first(head, s):
                    slot = ring.free()
                    for c in range(2):
                        ins = nc.tensor.matmul(bank[:, slot + c, 0:HALF], q[0:ROWS, head, s * P:(s + 1) * P], k[0:ROWS, head, c * HALF:(c + 1) * HALF],
                                               start=True, stop=True)
                    ring.fill(ins)

                def keys_first(head, t):
                    slot = exps.free()
                    for c in range(2):
                        ins = nc.tensor.matmul(bank[:, slot + c, 0:HALF], k[:, head, t * P:(t + 1) * P], q[:, head, c * HALF:(c + 1) * HALF],
                                               start=True, stop=True)
                    exps.fill(ins)

                def max_rows(b, head):
                    pe.wait_ge(placed_ready, b * H + head + 1)
                    slot = exps.free()
                    for s in range(TB):
                        ins = nc.tensor.matmul(bank[0:ALL_ROWS, slot + s // 4, (s % 4) * P:(s % 4 + 1) * P], placed[:, head % 2, s, :], ident16[:, :],
                                               start=True, stop=True)
                    exps.fill(ins)

                def times_v(head):
                    slot = ring.free()
                    at = min(head * DV, H * DV - WINDOW)
                    for s in range(TB):
                        for t in range(TB):
                            ins = nc.tensor.matmul(bank[:, slot, s * WINDOW:(s + 1) * WINDOW], probs[:, head % 2, t, s * P:(s + 1) * P],
                                                   vb[:, t, at:at + WINDOW], start=(t == 0), stop=(t == TB - 1))
                    ring.fill(ins)

                with pe.Fori(0, B) as b:
                    ring.turn(b)
                    exps.turn(b)
                    pe.wait_ge(v_ready, b + 1)
                    for i in range(H + PV_LAG):
                        if i < H and i % LOT == 0:
                            pe.wait_ge(lot_in[i // LOT], (b + 1) * LOT_IN)
                        if 1 <= i <= H:
                            max_rows(b, i - 1)
                        if i < H + MAX_LAG and i >= MAX_LAG:
                            exps.arrived(items_before(i))
                        for s in range(TB):
                            if i < H:
                                queries_first(i, s)
                            if MAX_LAG <= i < H + MAX_LAG:
                                keys_first(i - MAX_LAG, s)
                        if i >= PV_LAG:
                            head = i - PV_LAG
                            exps.arrived(items_before(head + MAX_LAG) + TB)
                            times_v(head)
                            if head % LOT == LOT - 1:
                                pe.wait_ge(filled, ring.base + ring.n)
                                pe.sem_inc(lot_used, 1)
                    ring.arrived()
                    for half in range(2):
                        slot = exps.free()
                        for s in range(TB):
                            ins = nc.tensor.transpose(bank[0:CH, slot + s // 4, (s % 4) * P:(s % 4 + 1) * P], attn[:, s, half * CH:(half + 1) * CH],
                                                      ident[:, :])
                        exps.fill(ins)
                    exps.arrived()
                    for s in range(TB):
                        slot = ring.free()
                        for half in range(2):
                            ins = nc.tensor.matmul(bank[:, slot, 0:C], aT[:, half, s * P:(s + 1) * P], wp[:, half, :], start=(half == 0), stop=(half == 1))
                        ring.fill(ins)
                    ring.ended()
                    exps.ended()


def items_before(i):
    return sum((1 <= j <= H) + TB * (MAX_LAG <= j < H + MAX_LAG) for j in range(i)) + (1 <= i <= H)


E = 8
FF = 4 * C
FFT = FF // P
HIDDEN_ITEMS = E * 2 * FFT


def experts(nc, h, x1, ident, io, top2):
    name = "moe" if top2 else "ffn"
    src = x1 if top2 else h
    with Memory(nc, name) as m:
        z = Normed(m, "ln")
        w1 = m.sbuf("w1", [CH, E, 2, FF])
        w2 = m.sbuf("w2", [P, E, FFT, C])
        wr = m.sbuf("wr", [CH, 2, E])
        before = m.sbuf("before", [P, E, E])
        ln = m.sbuf("ln_gb", [CH, 2, 2])
        b1 = m.sbuf("b1", [P, E, FFT])
        b2 = m.sbuf("b2", [1, E, C])
        br = m.sbuf("br", [1, E])
        ones = m.sbuf("ones", [1, P])
        hidden = m.sbuf("hidden", [P, 2, FFT, N])
        logits = m.sbuf("logits", [P, TB, E])
        above = m.sbuf("above", [P, TB, E, E])
        ties = m.sbuf("ties", [P, TB, E, E])
        rank = m.sbuf("rank", [P, TB, E])
        first = m.sbuf("first", [P, TB, E])
        second = m.sbuf("second", [P, TB, E])
        best = m.sbuf("best", [P, 2, TB])
        share = m.sbuf("share", [P, TB])
        weight = m.sbuf("weight", [P, TB, E])
        acc = m.sbuf("acc", [P, TB, C])
        bank = m.psum("bank", [P, 8, 512])
        act_banks, banks = (0, 1, 2, 3), (4, 5, 6, 7)
        ITEMS = 1 + E * TB
        STEPS = NORM_STEPS + (16 if top2 else 4)
        (loaded, weights_in, set_up, filled, taken, act_filled, act_taken, gap_ready, share_ready, h_ready, dve_own) = m.sems(
            *"loaded weights_in set_up filled taken act_filled act_taken gap_ready share_ready h_ready dve_own".split())
        pairs = ((wr, io[f"{name}_wr"]), (before, io["before"]))
        pairs += ((ln, io["moe_ln"]),) if top2 else ((b1, io["ffn_b1"]), (b2, io["ffn_b2"]), (br, io["ffn_br"]))
        LOADED = 16 * len(pairs)

        def other(ap):
            return ap.unsqueeze(2).to_broadcast([P, TB, E, E])

        def this(ap):
            return ap.unsqueeze(3).to_broadcast([P, TB, E, E])

        with nc.Block() as block:

            @block.sync
            def _(sp):
                load(sp, pairs, loaded)
                for e in range(E):
                    sp.dma_start(w1[:, e, :, :], io[f"{name}_w1"][e]).then_inc(weights_in, 16)
                    sp.dma_start(w2[:, e, :, :], io[f"{name}_w2"][e]).then_inc(weights_in, 16)

            @block.gpsimd
            def _(pool):
                nc.gpsimd.memset(ones[:, :], 1.0).then_inc(set_up, 1)

            @block.vector
            def _(dve):
                own = InOrder(dve, dve_own, STEPS)
                ring = Ring(dve, banks, filled, taken, ITEMS)
                dve.sem_inc(taken, len(banks))
                dve.sem_inc(h_ready, 1)
                dve.wait_ge(loaded, LOADED)
                with dve.Fori(0, B) as b:
                    own.turn(b)
                    ring.turn(b)
                    dve.wait_ge(h_ready, b * TB + 1)
                    norm_rows(nc, dve, own, z, lambda s: src[:, b * TB + s, :], b)
                    slot = ring.get()
                    ring.take(nc.vector.tensor_copy(logits[:, :, :], bank[:, slot, 0:TB * E].rearrange("p (s e) -> p s e", s=TB)))
                    ring.done()
                    own.count(nc.vector.tensor_tensor(above[:, :, :, :], other(logits[:, :, :]), this(logits[:, :, :]), ALU.is_gt))
                    own.step(nc.vector.tensor_tensor(ties[:, :, :, :], other(logits[:, :, :]), this(logits[:, :, :]), ALU.is_equal))
                    own.step(nc.vector.tensor_tensor(ties[:, :, :, :], ties[:, :, :, :],
                                                     before[:, :, :].unsqueeze(1).to_broadcast([P, TB, E, E]), ALU.mult))
                    own.step(nc.vector.tensor_tensor(above[:, :, :, :], above[:, :, :, :], ties[:, :, :, :], ALU.add))
                    own_rank = nc.vector.tensor_reduce(rank[:, :, :], above[:, :, :, :], AX.X, ALU.add)
                    if top2:
                        own.step(own_rank)
                        own.count(nc.vector.tensor_scalar(first[:, :, :], rank[:, :, :], 0.0, None, ALU.is_equal))
                        own.step(nc.vector.tensor_scalar(second[:, :, :], rank[:, :, :], 1.0, None, ALU.is_equal))
                        own.count(nc.vector.tensor_reduce(best[:, 0, :], logits[:, :, :], AX.X, ALU.max))
                        own.step(nc.vector.tensor_tensor(weight[:, :, :], logits[:, :, :], second[:, :, :], ALU.mult))
                        own.step(nc.vector.tensor_reduce(best[:, 1, :], weight[:, :, :], AX.X, ALU.add))
                        nc.vector.tensor_tensor(share[:, :], best[:, 1, :], best[:, 0, :], ALU.subtract).then_inc(gap_ready, 1)
                        dve.wait_ge(share_ready, b + 1)
                        own.step(nc.vector.tensor_scalar(best[:, 0, :], share[:, :], 1.0, None, ALU.add))
                        own.step(nc.vector.reciprocal(best[:, 0, :], best[:, 0, :]))
                        own.step(nc.vector.tensor_tensor(best[:, 1, :], best[:, 0, :], share[:, :], ALU.mult))
                        own.count(nc.vector.tensor_tensor(first[:, :, :], first[:, :, :], best[:, 0, :].unsqueeze(2).to_broadcast([P, TB, E]), ALU.mult))
                        own.step(nc.vector.tensor_tensor(second[:, :, :], second[:, :, :], best[:, 1, :].unsqueeze(2).to_broadcast([P, TB, E]), ALU.mult))
                        own.step(nc.vector.tensor_tensor(weight[:, :, :], first[:, :, :], second[:, :, :], ALU.add))
                        base = lambda s: x1[:, b * TB + s, :]
                    else:
                        own_rank.then_inc(gap_ready, 1)
                        dve.wait_ge(gap_ready, b + 1)
                        nc.vector.tensor_scalar(weight[:, :, :], rank[:, :, :], 0.0, None, ALU.is_equal).then_inc(share_ready, 1)
                        dve.wait_ge(share_ready, b + 1)
                    for e in range(E):
                        for s in range(TB):
                            slot = ring.get()
                            if e == 0:
                                start = x1[:, b * TB + s, :] if top2 else h[:, b * TB + s, :]
                            else:
                                start = acc[:, s, :]
                                dve.wait_ge(taken, ring.base + len(banks) + ring.n - TB + 1)
                            ring.take(nc.vector.scalar_tensor_tensor(acc[:, s, :], bank[:, slot, 0:C], weight[:, s, e:e + 1], start,
                                                                     ALU.mult, ALU.add))
                    ring.done()
                    for s in range(TB):
                        row = h[:, b * TB + s, :]
                        if top2:
                            ins = nc.vector.tensor_tensor(row, row, acc[:, s, :], ALU.add)
                        else:
                            ins = nc.vector.tensor_scalar(row, acc[:, s, :], 1.0, None, ALU.mult)
                        ins.then_inc(h_ready, 1)
                    ring.ended()
                    own.ended()

            @block.scalar
            def _(act):
                ring = Ring(act, act_banks, act_filled, act_taken, HIDDEN_ITEMS)
                act.sem_inc(act_taken, len(act_banks))
                act.wait_ge(loaded, LOADED)
                with act.Fori(0, B) as b:
                    ring.turn(b)
                    root(nc, act, z, b)
                    act.wait_ge(z.psum_ready, b + 1)
                    copy_transposed(nc, bank, z.xT, z.xT_ready, *((ln[:, 0, :], ln[:, 1, :]) if top2 else ()))
                    if top2:
                        act.wait_ge(gap_ready, b + 1)
                        nc.scalar.activation(share[:, :], share[:, :], ACT.Exp).then_inc(share_ready, 1)
                    for e in range(E):
                        for f in range(FFT):
                            for c in range(2):
                                slot = ring.get()
                                dst = hidden[:, e % 2, f, c * HALF:(c + 1) * HALF]
                                bias = {} if top2 else {"bias": b1[:, e, f:f + 1]}
                                ring.take(nc.scalar.activation(dst, bank[:, slot, 0:HALF], ACT.Gelu, **bias))
                    ring.ended()

            @block.tensor
            def _(pe):
                ring = Ring(pe, banks, filled, taken, ITEMS)
                up = Ring(pe, act_banks, act_filled, act_taken, HIDDEN_ITEMS)
                pe.wait_ge(loaded, LOADED)
                pe.wait_ge(set_up, 1)

                def widen(e):
                    for f in range(FFT):
                        for c in range(2):
                            slot = up.free()
                            for k in range(2):
                                ins = nc.tensor.matmul(bank[:, slot, 0:HALF], w1[:, e, k, f * P:(f + 1) * P], z.xT[:, k, c * HALF:(c + 1) * HALF],
                                                       start=(k == 0), stop=(k == 1))
                            up.fill(ins)

                with pe.Fori(0, B) as b:
                    ring.turn(b)
                    up.turn(b)
                    pe.wait_ge(z.xn_ready, b * TB + TB)
                    transpose_rows(nc, pe, lambda s, k: z.xn[:, s, k * CH:(k + 1) * CH], ident, bank, z.psum_ready)
                    pe.wait_ge(z.xT_ready, b * COPIES + COPIES)
                    slot = ring.free()
                    for s in range(TB):
                        for k in range(2):
                            ins = nc.tensor.matmul(bank[:, slot, s * E:(s + 1) * E], z.xT[:, k, s * P:(s + 1) * P], wr[:, k, :], start=(k == 0),
                                                   stop=(top2 and k == 1))
                        if not top2:
                            ins = nc.tensor.matmul(bank[:, slot, s * E:(s + 1) * E], ones[:, :], br[:, :], start=False, stop=True)
                    ring.fill(ins)
                    for e in range(E):
                        if e == 0:
                            pe.wait_ge(weights_in, 16 * 2 * E)
                            widen(0)
                        if e + 1 < E:
                            widen(e + 1)
                        up.arrived((e + 1) * 2 * FFT)
                        for s in range(TB):
                            slot = ring.free()
                            for f in range(FFT):
                                ins = nc.tensor.matmul(bank[:, slot, 0:C], hidden[:, e % 2, f, s * P:(s + 1) * P], w2[:, e, f, :], start=(f == 0),
                                                       stop=(top2 and f == FFT - 1))
                            if not top2:
                                ins = nc.tensor.matmul(bank[:, slot, 0:C], ones[:, :], b2[:, e, :], start=False, stop=True)
                            ring.fill(ins)
                    ring.ended()
                    up.ended()


CK = 16
NC = N // CK
CB = GH * CK
STREAMS = 2 * B
PATHS = 5
SIDE = C + H + H * PATHS
SHORT, LONG = 3, 7
PAD = LONG - 1
MIX_ITEMS = 4 + TB + TB + 4 + TB + TB + 1


def mix_paths(nc, h, part, delta_weight, kq, k_rows, v_rows, ident, io):
    with Memory(nc, "mix") as m:
        z = Normed(m, "ln")
        wq = m.sbuf("wq", [CH, 2, C])
        wkv = m.sbuf("wkv", [CH, 2, 2 * C])
        wside = m.sbuf("wside", [CH, 2, SIDE])
        bside = m.sbuf("bside", [1, SIDE])
        wg1 = m.sbuf("wg1", [CH, 2, C])
        bg1 = m.sbuf("bg1", [CH, 2])
        wg2 = m.sbuf("wg2", [CH, 2, H])
        bg2 = m.sbuf("bg2", [1, H])
        static = m.sbuf("static", [P, H])
        taps = m.sbuf("taps", [CH, 2, SHORT + LONG])
        mixer = m.sbuf("mixer", [CH, 2, C])
        same_dim = m.sbuf("same_dim", [CH, 2, C])
        same = m.sbuf("same", [CH, 2, C])
        ones = m.sbuf("ones", [1, P])
        kv = m.sbuf("kv", [P, TB, 2 * C])
        squares = m.sbuf("squares", [P, TB, C])
        norm = m.sbuf("norm", [P, TB, H])
        unit = m.sbuf("unit", [P, TB, C])
        side = m.sbuf("side", [P, TB, SIDE])
        vT = m.sbuf("vT", [CH, 2, PAD + N])
        fir = m.sbuf("fir", [CH, 2, 2, N])
        mixed = m.sbuf("mixed", [P, TB, 2, C])
        hidden = m.sbuf("hidden", [CH, 2, N])
        top = m.sbuf("top", [P, TB, H])
        weights = m.sbuf("weights", [P, TB, H, PATHS])
        total = m.sbuf("total", [P, TB, H])
        dyn = m.sbuf("dyn", [P, TB, H])
        gate = m.sbuf("gate", [P, TB, H])
        term = m.sbuf("term", [P, TB, C])
        sum_ = m.sbuf("sum", [P, TB, C])
        bank = m.psum("bank", [P, 8, 512])
        act_banks, banks = (0, 1, 2), (3, 4, 5, 6, 7)
        (loaded, set_up, mixer_ready, static_ready, filled, taken, act_filled, act_taken, norm2_ready, norm_ready, unit_ready,
         side_ready, dyn_ready, gap_ready, exp_ready, fir_ready, gate_raw, gate_ready, rows_stored, part_ready,
         dve_own) = m.sems(*(
             "loaded set_up mixer_ready static_ready filled taken act_filled act_taken norm2_ready norm_ready unit_ready "
             "side_ready dyn_ready gap_ready exp_ready fir_ready gate_raw gate_ready rows_stored part_ready dve_own").split())
        pairs = ((wq, io["mix_wq"]), (wkv, io["mix_wkv"]), (wside, io["mix_wside"]), (bside, io["mix_bside"]), (wg1, io["mix_wg1"]),
                 (bg1, io["mix_bg1"]), (wg2, io["mix_wg2"]), (bg2, io["mix_bg2"]), (static, io["mix_static"]), (taps, io["mix_taps"]),
                 (mixer, io["mix_mixer"]), (same_dim, io["same_dim"]), (same, io["same"]))
        LOADED = 16 * len(pairs)

        def heads(ap):
            return ap.rearrange("p s (h d) -> p s h d", h=H)

        def per_head(ap):
            return ap.unsqueeze(3).to_broadcast([P, TB, H, D])

        def weight(p):
            return weights[:, :, :, p]

        with nc.Block() as block:

            @block.sync
            def _(sp):
                load(sp, pairs, loaded)
                with sp.Fori(0, B) as b:
                    sp.wait_ge(unit_ready, b + 1)
                    sp.wait_ge(taken, b * MIX_ITEMS + len(banks) + 4 + TB)
                    for dram, buf in ((k_rows, unit[:, :, :]), (v_rows, kv[:, :, C:])):
                        sp.dma_start(dram[bass.ds(b * N, N), :].rearrange("(s p) c -> p s c", p=P), buf).then_inc(rows_stored, 16)
                sp.wait_ge(rows_stored, 32 * B + 32)

            @block.gpsimd
            def _(pool):
                pool.sem_inc(rows_stored, 32)
                nc.gpsimd.memset(vT[:, :, 0:PAD], 0.0).then_inc(set_up, 1)
                nc.gpsimd.memset(ones[:, :], 1.0).then_inc(set_up, 1)

            @block.vector
            def _(dve):
                setup = InOrder(dve, mixer_ready)
                dve.sem_inc(taken, len(banks))
                dve.sem_inc(part_ready, 1)
                dve.wait_ge(loaded, LOADED)
                setup.step(nc.vector.tensor_tensor(mixer[:, :, :], mixer[:, :, :], same_dim[:, :, :], ALU.mult))
                setup.step(nc.vector.tensor_tensor(mixer[:, :, :], mixer[:, :, :], same[:, :, :], ALU.add))
                dve.wait_ge(set_up, 2)
                dve.wait_ge(static_ready, 1)
                own = InOrder(dve, dve_own, MIX_DVE_STEPS)
                ring = Ring(dve, banks, filled, taken, MIX_ITEMS)
                with dve.Fori(0, B) as b:
                    own.turn(b)
                    ring.turn(b)
                    norm_rows(nc, dve, own, z, lambda s: h[:, b * TB + s, :], b)
                    for half in range(2):
                        for c in range(2):
                            slot = ring.get()
                            dst = kq[:, half, b, c * NC // 2:(c + 1) * NC // 2, CK:]
                            ring.take(nc.vector.tensor_scalar(dst, bank[0:CH, slot, 0:HALF].rearrange("p (c t) -> p c t", t=CK),
                                                              float(D) ** -0.5, None, ALU.mult))
                    dve.wait_ge(rows_stored, b * 32 + 32)
                    for s in range(TB):
                        slot = ring.get()
                        ring.take(nc.vector.tensor_copy(kv[:, s, :], bank[:, slot, 0:2 * C]))
                    ring.done()
                    own.step(nc.vector.tensor_tensor(squares[:, :, :], kv[:, :, 0:C], kv[:, :, 0:C], ALU.mult))
                    nc.vector.tensor_reduce(norm[:, :, :], heads(squares[:, :, :]), AX.X, ALU.add).then_inc(norm2_ready, 1)
                    for s in range(TB):
                        slot = ring.get()
                        ring.take(nc.vector.tensor_copy(side[:, s, :], bank[:, slot, 0:SIDE]))
                    ring.done()
                    dve.wait_ge(norm_ready, b + 1)
                    own.step(nc.vector.tensor_scalar(norm[:, :, :], norm[:, :, :], 1e-6, None, ALU.add))
                    own.step(nc.vector.reciprocal(norm[:, :, :], norm[:, :, :]))
                    nc.vector.tensor_tensor(heads(unit[:, :, :]), heads(kv[:, :, 0:C]), per_head(norm[:, :, :]),
                                            ALU.mult).then_inc(unit_ready, 1)
                    logits = side[:, :, C + H:].rearrange("p s (h q) -> p s h q", q=PATHS)
                    own.step(nc.vector.tensor_reduce(top[:, :, :], logits, AX.X, ALU.max))
                    nc.vector.tensor_tensor(weights[:, :, :, :], logits, top[:, :, :].unsqueeze(3).to_broadcast([P, TB, H, PATHS]),
                                            ALU.subtract).then_inc(gap_ready, 1)
                    for half in range(2):
                        for c in range(2):
                            slot = ring.get()
                            ring.take(nc.vector.tensor_copy(vT[:, half, PAD + c * HALF:PAD + (c + 1) * HALF], bank[0:CH, slot, 0:HALF]))
                    ring.done()
                    for half in range(2):
                        for which, first, n_taps in ((0, 0, SHORT), (1, SHORT, LONG)):
                            dst = fir[:, which, half, :]
                            for k in range(n_taps):
                                at = PAD - (n_taps - 1) + k
                                src, tap = vT[:, half, at:at + N], taps[:, half, first + k:first + k + 1]
                                if k == 0:
                                    own.step(nc.vector.tensor_scalar(dst, src, tap, None, ALU.mult))
                                elif k < n_taps - 1:
                                    own.step(nc.vector.scalar_tensor_tensor(dst, src, tap, dst, ALU.mult, ALU.add))
                                else:
                                    nc.vector.scalar_tensor_tensor(dst, src, tap, dst, ALU.mult, ALU.add).then_inc(fir_ready, 1)
                    for s in range(TB):
                        slot = ring.get()
                        ring.take(nc.vector.tensor_copy(kq[:, :, b, s * P // CK:(s + 1) * P // CK, 0:CK],
                                                        bank[0:CH, slot, 0:2 * P].rearrange("p (z c t) -> p z c t", z=2, t=CK)))
                    slot = ring.get()
                    ring.take(nc.vector.tensor_copy(gate[:, :, :], bank[:, slot, 0:TB * H].rearrange("p (s h) -> p s h", s=TB)))
                    dve.wait_ge(exp_ready, b + 1)
                    own.step(nc.vector.tensor_reduce(total[:, :, :], weights[:, :, :, :], AX.X, ALU.add))
                    own.step(nc.vector.reciprocal(total[:, :, :], total[:, :, :]))
                    dve.wait_ge(gate_ready, b + 1)
                    own.step(nc.vector.tensor_tensor(total[:, :, :], total[:, :, :], gate[:, :, :], ALU.mult))
                    own.step(nc.vector.tensor_tensor(weights[:, :, :, :], weights[:, :, :, :],
                                                     total[:, :, :].unsqueeze(3).to_broadcast([P, TB, H, PATHS]), ALU.mult))
                    own.count(nc.vector.tensor_copy(delta_weight[:, bass.ds(b * TB, TB), :], weight(2)))
                    dve.wait_ge(dyn_ready, b + 1)
                    own.step(nc.vector.tensor_tensor(dyn[:, :, :], dyn[:, :, :], static[:, :].unsqueeze(1).to_broadcast([P, TB, H]), ALU.mult))
                    own.step(nc.vector.tensor_tensor(dyn[:, :, :], dyn[:, :, :], weight(4), ALU.mult))
                    own.count(nc.vector.tensor_tensor(heads(sum_[:, :, :]), heads(kv[:, :, C:]), per_head(weight(3)), ALU.mult))
                    own.step(nc.vector.tensor_tensor(heads(term[:, :, :]), heads(side[:, :, 0:C]), per_head(dyn[:, :, :]), ALU.mult))
                    own.step(nc.vector.tensor_tensor(sum_[:, :, :], sum_[:, :, :], term[:, :, :], ALU.add))
                    for s in range(TB):
                        slot = ring.get()
                        ring.take(nc.vector.tensor_copy(mixed[:, s, :, :], bank[:, slot, 0:2 * C].rearrange("p (w c) -> p w c", w=2)))
                    ring.done()
                    for which in range(2):
                        own.step(nc.vector.tensor_tensor(heads(term[:, :, :]), heads(mixed[:, :, which, :]), per_head(weight(which)), ALU.mult))
                        if which == 0:
                            own.step(nc.vector.tensor_tensor(sum_[:, :, :], sum_[:, :, :], term[:, :, :], ALU.add))
                    own.step(nc.vector.tensor_tensor(part[:, bass.ds(b * TB, TB), :], sum_[:, :, :], term[:, :, :], ALU.add))
                    ring.ended()
                    own.ended()

            @block.scalar
            def _(act):
                ring = Ring(act, act_banks, act_filled, act_taken, 4)
                act.sem_inc(act_taken, len(act_banks))
                act.wait_ge(loaded, LOADED)
                nc.scalar.activation(static[:, :], static[:, :], ACT.Sigmoid).then_inc(static_ready, 1)
                with act.Fori(0, B) as b:
                    ring.turn(b)
                    root(nc, act, z, b)
                    act.wait_ge(z.psum_ready, b + 1)
                    copy_transposed(nc, bank, z.xT, z.xT_ready)
                    act.wait_ge(norm2_ready, b + 1)
                    nc.scalar.activation(norm[:, :, :], norm[:, :, :], ACT.Sqrt).then_inc(norm_ready, 1)
                    for half in range(2):
                        for c in range(2):
                            slot = ring.get()
                            ring.take(nc.scalar.activation(hidden[:, half, c * HALF:(c + 1) * HALF], bank[0:CH, slot, 0:HALF],
                                                           ACT.Gelu_apprx_tanh, bias=bg1[:, half:half + 1]))
                    act.wait_ge(gap_ready, b + 1)
                    nc.scalar.activation(weights[:, :, :, :], weights[:, :, :, :], ACT.Exp).then_inc(exp_ready, 1)
                    nc.scalar.activation(dyn[:, :, :], side[:, :, C:C + H], ACT.Sigmoid).then_inc(dyn_ready, 1)
                    act.wait_ge(taken, b * MIX_ITEMS + len(banks) + 4 + TB + TB + 4 + TB + 1)
                    nc.scalar.activation(gate[:, :, :], gate[:, :, :], ACT.Sigmoid).then_inc(gate_ready, 1)
                    ring.ended()

            @block.tensor
            def _(pe):
                ring = Ring(pe, banks, filled, taken, MIX_ITEMS)
                up = Ring(pe, act_banks, act_filled, act_taken, 4)
                pe.wait_ge(loaded, LOADED)
                pe.wait_ge(set_up, 2)
                pe.wait_ge(mixer_ready, 2)

                def columns(ring, w, at, rows, half_tokens):
                    slot = ring.free()
                    for k in range(2):
                        ins = nc.tensor.matmul(bank[0:rows, slot, 0:HALF], w[:, k, at:at + rows],
                                               z.xT[:, k, half_tokens * HALF:(half_tokens + 1) * HALF], start=(k == 0), stop=(k == 1))
                    ring.fill(ins)

                with pe.Fori(0, B) as b:
                    ring.turn(b)
                    up.turn(b)
                    pe.wait_ge(z.xn_ready, b * TB + TB)
                    transpose_rows(nc, pe, lambda s, k: z.xn[:, s, k * CH:(k + 1) * CH], ident, bank, z.psum_ready)
                    pe.wait_ge(z.xT_ready, b * COPIES + COPIES)
                    for half in range(2):
                        for c in range(2):
                            columns(ring, wq, half * CH, CH, c)
                    for s in range(TB):
                        slot = ring.free()
                        for k in range(2):
                            ins = nc.tensor.matmul(bank[:, slot, 0:2 * C], z.xT[:, k, s * P:(s + 1) * P], wkv[:, k, :], start=(k == 0), stop=(k == 1))
                        ring.fill(ins)
                    for s in range(TB):
                        slot = ring.free()
                        for k in range(2):
                            nc.tensor.matmul(bank[:, slot, 0:SIDE], z.xT[:, k, s * P:(s + 1) * P], wside[:, k, :], start=(k == 0), stop=False)
                        ring.fill(nc.tensor.matmul(bank[:, slot, 0:SIDE], ones[:, :], bside[:, :], start=False, stop=True))
                    for half in range(2):
                        for c in range(2):
                            columns(up, wg1, half * CH, CH, c)
                    for half in range(2):
                        for c in range(2):
                            columns(ring, wkv, C + half * CH, CH, c)
                    pe.wait_ge(unit_ready, b + 1)
                    for s in range(TB):
                        slot = ring.free()
                        for k in range(2):
                            ins = nc.tensor.transpose(bank[0:CH, slot, k * P:(k + 1) * P], unit[:, s, k * CH:(k + 1) * CH], ident[:, :])
                        ring.fill(ins)
                    up.arrived()
                    slot = ring.free()
                    for s in range(TB):
                        for k in range(2):
                            nc.tensor.matmul(bank[:, slot, s * H:(s + 1) * H], hidden[:, k, s * P:(s + 1) * P], wg2[:, k, :], start=(k == 0), stop=False)
                        ins = nc.tensor.matmul(bank[:, slot, s * H:(s + 1) * H], ones[:, :], bg2[:, :], start=False, stop=True)
                    ring.fill(ins)
                    pe.wait_ge(fir_ready, b * 4 + 4)
                    for s in range(TB):
                        slot = ring.free()
                        for which in range(2):
                            for k in range(2):
                                ins = nc.tensor.matmul(bank[:, slot, which * C:(which + 1) * C], fir[:, which, k, s * P:(s + 1) * P],
                                                       mixer[:, k, :], start=(k == 0), stop=(k == 1))
                        ring.fill(ins)
                    ring.ended()
                    up.ended()


MIX_DVE_STEPS = 46


def chunk_products(nc, kq, grams, reads, mask, upto, g_dram, tt_dram):
    each = H // 2 * STREAMS * NC // P
    with Memory(nc, "gram") as m:
        k_block = m.sbuf("k_block", [CB, 2, STREAMS, GH, CK])
        a = m.sbuf("a", [P, each, CK, CK])
        tt = m.sbuf("tt", [P, each, CK, CK])
        product = m.sbuf("product", [P, each, CK, CK])
        bank = m.psum("bank", [CB, 2, 512])
        (block_ready, block_free, filled, taken, stored, a_in, zeroed, solved, back, dve_own) = m.sems(
            *"block_ready block_free filled taken stored a_in zeroed solved back dve_own".split())
        with nc.Block() as block:

            def by_chunk(dram):
                return dram.rearrange("(h n i) j -> h i n j", h=GH, i=CK)

            @block.vector
            def _(dve):
                dve.sem_inc(taken, 2)
                with dve.Fori(0, NC // 2) as cc:
                    for c in range(2):
                        slot = c
                        dve.wait_ge(filled, cc * 2 + c + 1)
                        got = bank[:, slot, 0:STREAMS * 2 * CK].rearrange("p (n c) -> p n c", n=STREAMS)
                        view = lambda ap: ap[:, :, cc * 2 + c, :]
                        nc.vector.tensor_copy(view(grams), got[:, :, 0:CK])
                        nc.vector.tensor_tensor(view(reads), got[:, :, CK:], upto[:, :].unsqueeze(1).to_broadcast([CB, STREAMS, CK]),
                                                ALU.mult).then_inc(taken, 1)
                own = InOrder(dve, dve_own)
                own.count(nc.vector.memset(tt[:, :, :, :], 0.0))
                own.wait()
                diagonal = tt[:, :, :, :].rearrange("p n i j -> p n (i j)")[:, :, 0:CK * CK:CK + 1]
                own.step(nc.vector.memset(diagonal, 1.0))
                dve.wait_ge(a_in, 16)
                for i in range(1, CK):
                    own.step(nc.vector.tensor_tensor(product[:, :, 0:i, 0:i], a[:, :, i, 0:i].unsqueeze(2).to_broadcast([P, each, i, i]),
                                                     tt[:, :, 0:i, 0:i], ALU.mult))
                    last = nc.vector.tensor_reduce(tt[:, :, 0:i, i], product[:, :, 0:i, 0:i], AX.X, ALU.add, negate=True)
                    if i < CK - 1:
                        own.step(last)
                    else:
                        last.then_inc(solved, 1)

            @block.gpsimd
            def _(pool):
                pool.sem_inc(block_free, 2)
                with pool.Fori(0, NC // 2) as cc:
                    for c in range(2):
                        pool.wait_ge(block_free, cc * 2 + c + 1)
                        nc.gpsimd.tensor_tensor(k_block[:, c, :, :, :],
                                                kq[:, :, cc * 2 + c, 0:CK].unsqueeze(2).to_broadcast([CB, STREAMS, GH, CK]),
                                                mask[:, :].unsqueeze(2).unsqueeze(1).to_broadcast([CB, STREAMS, GH, CK]), ALU.mult).then_inc(block_ready, 1)

            @block.tensor
            def _(pe):
                with pe.Fori(0, NC // 2) as cc:
                    for c in range(2):
                        pe.wait_ge(block_ready, cc * 2 + c + 1)
                        pe.wait_ge(taken, cc * 2 + c + 1)
                        for n in range(STREAMS):
                            ins = nc.tensor.matmul(bank[:, c, n * 2 * CK:(n + 1) * 2 * CK], k_block[:, c, n, :, :].rearrange("p h t -> p (h t)"),
                                                   kq[:, n, cc * 2 + c, :], start=True, stop=True)
                        ins.then_inc(filled, 1)
                        pe.wait_ge(filled, cc * 2 + c + 1)
                        pe.sem_inc(block_free, 1)

            @block.sync
            def _(sp):
                sp.wait_ge(taken, NC + 2)
                for g in range(GH):
                    sp.dma_start(by_chunk(g_dram)[g], grams[g * CK:(g + 1) * CK].rearrange("p n c j -> p (n c) j")).then_inc(stored, 16)
                sp.wait_ge(stored, 16 * GH)
                sp.dma_start(a[:, :, :, :].rearrange("p n i j -> p (n i j)"), g_dram.rearrange("(p r) j -> p (r j)", p=P)).then_inc(a_in, 16)
                sp.wait_ge(solved, 1)
                sp.dma_start(tt_dram.rearrange("(p r) j -> p (r j)", p=P), tt[:, :, :, :].rearrange("p n i j -> p (n i j)")).then_inc(stored, 16)
                sp.wait_ge(stored, 16 * GH + 16)
                for g in range(GH):
                    sp.dma_start(grams[g * CK:(g + 1) * CK].rearrange("p n c j -> p (n c) j"), by_chunk(tt_dram)[g]).then_inc(back, 16)
                sp.wait_ge(back, 16 * GH)


def delta_rule(nc, kq, tt, reads, k_rows, v_rows, o_rows, mask):
    with Memory(nc, "delta") as m:
        keys = m.sbuf("keys", [CB, STREAMS, NC, CK])
        values = m.sbuf("values", [CB, STREAMS, NC, CK])
        state = m.sbuf("state", [CB, STREAMS, CK])
        resid = m.sbuf("resid", [CB, STREAMS, CK])
        update = m.sbuf("update", [CB, STREAMS, CK])
        K_T, T_T, Q_T, R_T, K = range(5)
        blocks = [m.sbuf(f"block{i}", [CB, 2, STREAMS, GH, CK]) for i in range(5)]
        bank = m.psum("bank", [CB, 8, 512])
        (rows_in, blocks_dve, blocks_pool, blocks_free, zeroed, ks_psum, resid_ready, u_psum, u_ready, s_psum, s_ready, o_psum, o_taken,
         o_stored) = m.sems(*("rows_in blocks_dve blocks_pool blocks_free zeroed ks_psum resid_ready u_psum u_ready s_psum s_ready "
                              "o_psum o_taken o_stored").split())
        KS, U, SB, O = 0, 2, 4, 6

        def part(z):
            return slice(z * B, (z + 1) * B)

        def spread(ap):
            return ap.unsqueeze(2).to_broadcast([CB, STREAMS, GH, CK])

        masks = mask[:, :].unsqueeze(2).unsqueeze(1).to_broadcast([CB, STREAMS, GH, CK])

        def rows(dram, half, g):
            at = half * CH + g * D
            return dram.rearrange("(n t) c -> t n c", t=CK)[:, :, at:at + D]

        def operands(i, c):
            return {K_T: kq[:, :, c, 0:CK], T_T: tt[:, :, c, :], Q_T: kq[:, :, c, CK:], R_T: reads[:, :, c, :], K: keys[:, :, c, :]}[i]

        with nc.Block() as block:

            @block.sync
            def _(sp):
                for dram, buf in ((k_rows, keys), (v_rows, values)):
                    for half in range(2):
                        for g in range(GH):
                            sp.dma_start(buf[g * CK:(g + 1) * CK, part(half), :, :].rearrange("p b c e -> p (b c) e"),
                                         rows(dram, half, g)).then_inc(rows_in, 16)
                sp.wait_ge(o_taken, 2 * NC + 2)
                for half in range(2):
                    for g in range(GH):
                        sp.dma_start(rows(o_rows, half, g),
                                     values[g * CK:(g + 1) * CK, part(half), :, :].rearrange("p b c e -> p (b c) e")).then_inc(o_stored, 16)
                sp.wait_ge(o_stored, 16 * H)

            @block.gpsimd
            def _(pool):
                pool.sem_inc(blocks_free, 2)
                pool.wait_ge(rows_in, 16 * 2 * H)
                with pool.Fori(0, NC // 2) as cc:
                    for c in range(2):
                        pool.wait_ge(blocks_free, cc * 2 + c + 1)
                        for i in (R_T, K):
                            nc.gpsimd.tensor_tensor(blocks[i][:, c], spread(operands(i, cc * 2 + c)), masks, ALU.mult).then_inc(blocks_pool, 1)

            @block.vector
            def _(dve):
                nc.vector.memset(state[:, :, :], 0.0).then_inc(s_ready, 2)
                dve.wait_ge(rows_in, 16 * 2 * H)

                def make_blocks(step, c):
                    dve.wait_ge(blocks_free, step + 1)
                    for i in (K_T, T_T, Q_T):
                        nc.vector.tensor_tensor(blocks[i][:, c], spread(operands(i, step)), masks, ALU.mult).then_inc(blocks_dve, 1)

                with dve.Fori(0, NC // 2) as cc:
                    for c in range(2):
                        step = cc * 2 + c
                        make_blocks(step, c)
                        for z in range(2):
                            at = step * 2 + z + 1
                            dve.wait_ge(ks_psum, at)
                            nc.vector.tensor_tensor(resid[:, part(z), :], values[:, part(z), step, :],
                                                    bank[:, KS + z, 0:B * CK].rearrange("p (b e) -> p b e", b=B), ALU.subtract).then_inc(resid_ready, 1)
                        for z in range(2):
                            at = step * 2 + z + 1
                            dve.wait_ge(u_psum, at)
                            nc.vector.tensor_copy(update[:, part(z), :], bank[:, U + z, 0:B * CK].rearrange("p (b e) -> p b e", b=B)).then_inc(u_ready, 1)
                        for z in range(2):
                            at = step * 2 + z + 1
                            dve.wait_ge(s_psum, at)
                            dve.wait_ge(s_ready, at)
                            nc.vector.tensor_tensor(state[:, part(z), :], state[:, part(z), :],
                                                    bank[:, SB + z, 0:B * CK].rearrange("p (b e) -> p b e", b=B), ALU.add).then_inc(s_ready, 1)

            @block.scalar
            def _(act):
                act.sem_inc(o_taken, 2)
                with act.Fori(0, NC // 2) as cc:
                    for c in range(2):
                        step = cc * 2 + c
                        for z in range(2):
                            at = step * 2 + z + 1
                            act.wait_ge(o_psum, at)
                            nc.scalar.activation(values[:, part(z), step, :], bank[:, O + z, 0:B * CK].rearrange("p (b e) -> p b e", b=B),
                                                 ACT.Copy).then_inc(o_taken, 1)

            @block.tensor
            def _(pe):
                def product(z, dst, i, c, rhs, start, stop):
                    for n in range(B):
                        ins = nc.tensor.matmul(bank[:, dst + z, n * CK:(n + 1) * CK], blocks[i][:, c, z * B + n].rearrange("p h t -> p (h t)"),
                                               rhs[:, z * B + n, :], start=start, stop=stop)
                    return ins

                with pe.Fori(0, NC // 2) as cc:
                    for c in range(2):
                        step = cc * 2 + c
                        pe.wait_ge(blocks_dve, step * 3 + 3)
                        for z in range(2):
                            pe.wait_ge(s_ready, step * 2 + z + 1)
                            product(z, KS, K_T, c, state, True, True).then_inc(ks_psum, 1)
                        for z in range(2):
                            pe.wait_ge(resid_ready, step * 2 + z + 1)
                            product(z, U, T_T, c, resid, True, True).then_inc(u_psum, 1)
                        pe.wait_ge(blocks_pool, step * 2 + 2)
                        for z in range(2):
                            at = step * 2 + z + 1
                            pe.wait_ge(u_ready, at)
                            pe.wait_ge(o_taken, at)
                            for n in range(B):
                                out = bank[:, O + z, n * CK:(n + 1) * CK]
                                at_n = z * B + n
                                nc.tensor.matmul(out, blocks[Q_T][:, c, at_n].rearrange("p h t -> p (h t)"), state[:, at_n, :], start=True, stop=False)
                                ins = nc.tensor.matmul(out, blocks[R_T][:, c, at_n].rearrange("p h t -> p (h t)"), update[:, at_n, :], start=False, stop=True)
                            ins.then_inc(o_psum, 1)
                            product(z, SB, K, c, update, True, True).then_inc(s_psum, 1)
                        pe.wait_ge(s_psum, step * 2 + 2)
                        pe.sem_inc(blocks_free, 1)


def project_paths(nc, h, part, delta_weight, o_rows, ident, io):
    with Memory(nc, "proj") as m:
        delta = m.sbuf("delta", [P, TILES, C])
        context = m.sbuf("context", [P, TB, C])
        cT = m.sbuf("cT", [CH, 2, N])
        wp = m.sbuf("wp", [CH, 2, C])
        bp = m.sbuf("bp", [1, C])
        ones = m.sbuf("ones", [1, P])
        bank = m.psum("bank", [P, 8, 512])
        banks = (3, 4, 5, 6, 7)
        (loaded, set_up, scaled, context_ready, cT_psum, cT_ready, filled, taken) = m.sems(
            *"loaded set_up scaled context_ready cT_psum cT_ready filled taken".split())
        pairs = ((wp, io["proj_w"]), (bp, io["proj_b"]))
        LOADED = 16 * (len(pairs) + B)
        with nc.Block() as block:

            @block.sync
            def _(sp):
                load(sp, pairs, loaded)
                for b in range(B):
                    sp.dma_start(delta[:, b * TB:(b + 1) * TB, :],
                                 o_rows[b * N:(b + 1) * N, :].rearrange("(s p) c -> p s c", p=P)).then_inc(loaded, 16)

            @block.gpsimd
            def _(pool):
                nc.gpsimd.memset(ones[:, :], 1.0).then_inc(set_up, 1)

            @block.vector
            def _(dve):
                ring = Ring(dve, banks, filled, taken, TB)
                dve.sem_inc(taken, len(banks))
                dve.wait_ge(loaded, LOADED)
                with dve.Fori(0, B) as b:
                    ring.turn(b)
                    here = bass.ds(b * TB, TB)
                    nc.vector.tensor_tensor(context[:, :, :].rearrange("p s (h d) -> p (s h) d", h=H),
                                            delta[:, here, :].rearrange("p s (h d) -> p (s h) d", h=H),
                                            delta_weight[:, here, :].rearrange("p s h -> p (s h)").unsqueeze(2).to_broadcast([P, TB * H, D]),
                                            ALU.mult).then_inc(scaled, 1)
                    dve.wait_ge(scaled, b + 1)
                    nc.vector.tensor_tensor(context[:, :, :], context[:, :, :], part[:, here, :], ALU.add).then_inc(context_ready, 1)
                    for s in range(TB):
                        slot = ring.get()
                        row = h[:, b * TB + s, :]
                        ring.take(nc.vector.tensor_tensor(row, row, bank[:, slot, 0:C], ALU.add))
                    ring.ended()

            @block.scalar
            def _(act):
                with act.Fori(0, B) as b:
                    act.wait_ge(cT_psum, b + 1)
                    copy_transposed(nc, bank, cT, cT_ready)

            @block.tensor
            def _(pe):
                ring = Ring(pe, banks, filled, taken, TB)
                pe.wait_ge(loaded, LOADED)
                pe.wait_ge(set_up, 1)
                with pe.Fori(0, B) as b:
                    ring.turn(b)
                    pe.wait_ge(context_ready, b + 1)
                    transpose_rows(nc, pe, lambda s, k: context[:, s, k * CH:(k + 1) * CH], ident, bank, cT_psum)
                    pe.wait_ge(cT_ready, b * COPIES + COPIES)
                    for s in range(TB):
                        slot = ring.free()
                        for k in range(2):
                            nc.tensor.matmul(bank[:, slot, 0:C], cT[:, k, s * P:(s + 1) * P], wp[:, k, :], start=(k == 0), stop=False)
                        ring.fill(nc.tensor.matmul(bank[:, slot, 0:C], ones[:, :], bp[:, :], start=False, stop=True))
                    ring.ended()


def delta_attention(nc, h, part, ident, io):
    scratch = {k: nc.dram_tensor(k, (B * N, C), F32, kind="Internal").ap() for k in ("k_rows", "v_rows", "o_rows")}
    systems = {k: nc.dram_tensor(k, (GH * STREAMS * NC * CK, CK), F32, kind="Internal").ap() for k in ("g_rows", "t_rows")}
    with Memory(nc, "l1") as m:
        delta_weight = m.sbuf("delta_weight", [P, TILES, H])
        kq = m.sbuf("kq", [CH, 2, B, NC, 2 * CK])
        mask = m.sbuf("mask", [CB, GH])
        upto = m.sbuf("upto", [CB, CK])
        masks_in = m.sem("masks_in")
        with nc.Block() as block:

            @block.sync
            def _(sp):
                sp.wait_ge(masks_in, load(sp, ((mask, io["head_mask"]), (upto, io["upto"])), masks_in))
        mix_paths(nc, h, part, delta_weight, kq, scratch["k_rows"], scratch["v_rows"], ident, io)
        by_stream = kq[:, :, :, :, :].rearrange("p z b c t -> p (z b) c t")
        with Memory(nc, "chunks") as n:
            grams = n.sbuf("grams", [CB, STREAMS, NC, CK])
            reads = n.sbuf("reads", [CB, STREAMS, NC, CK])
            chunk_products(nc, by_stream, grams, reads, mask, upto, systems["g_rows"], systems["t_rows"])
            delta_rule(nc, by_stream, grams, reads, scratch["k_rows"], scratch["v_rows"], scratch["o_rows"], mask)
        project_paths(nc, h, part, delta_weight, scratch["o_rows"], ident, io)


def store(nc, h, out):
    with Memory(nc, "store") as m:
        stored = m.sem("stored")
        with nc.Block() as block:

            @block.sync
            def _(sp):
                rows = out.rearrange("b (s p) c -> p (b s) c", p=P)
                for b in range(B):
                    sp.dma_start(rows[:, b * TB:(b + 1) * TB, :], h[:, b * TB:(b + 1) * TB, :]).then_inc(stored, 16)
                sp.wait_ge(stored, 16 * B)


def program(nc, io, out):
    with Memory(nc, "all") as m:
        h = m.sbuf("h", [P, TILES, C])
        ident = m.sbuf("ident", [P, P])
        ident_in = m.sem("ident_in")
        with nc.Block() as block:

            @block.sync
            def _(sp):
                sp.dma_start(ident[:, :], io["ident"]).then_inc(ident_in, 16)
                sp.wait_ge(ident_in, 16)
        image_embedding(nc, h, io)
        text_embedding(nc, h, ident, io)
        performer(nc, h, ident, io)
        x1 = m.sbuf("x1", [P, TILES, C])
        with Memory(nc, "values") as n:
            v = n.sbuf("v", [P, TILES, H, DV])
            qk_rows = nc.dram_tensor("qk_rows", (B * 2 * PARTS, C, N), BF16, kind="Internal").ap()
            attention_operands(nc, h, x1, v, qk_rows, ident, io)
            softmax_attention(nc, x1, v, qk_rows, ident, io)
        experts(nc, h, x1, ident, io, True)
        delta_attention(nc, h, x1, ident, io)
        experts(nc, h, x1, ident, io, False)
        store(nc, h, out)


def layouts(i, np):
    a = {}
    flat = i["x"].reshape(B, NI, 3 * C).transpose(0, 2, 1)
    a["x"] = np.concatenate([flat[:, :512].reshape(B, 4, P, NI),
                             np.concatenate([flat[:, 512:], flat[:, 512:]], 1)[:, None]], 1).reshape(B * JC, P, NI)
    wt = i["L0_tok_W"].T.reshape(3 * C, 2 * BANDS, C)
    main = wt[:512].reshape(4, P, 2 * BANDS, C).transpose(1, 0, 2, 3).reshape(P, 8 * BANDS, C)
    last = np.concatenate([wt[512:, :BANDS], wt[512:, BANDS:]], 0)
    a["tok_w"] = np.concatenate([main, last], 1)
    a["freq"] = np.broadcast_to(i["L0_tok_freq_bands"], (P, BANDS))
    a["sincos_shift"] = np.stack([np.where(np.arange(P) < 64, 0.0, math.pi / 2), np.full(P, math.pi / 2)], 1).astype(np.float32)
    a["ident"] = np.eye(P, dtype=np.float32)
    a["ids"] = i["x_txt"].T
    a["emb"] = i["L0_txt_emb"]

    def halves(w):
        return w.reshape(w.shape[:-2] + (2, CH, w.shape[-1])).swapaxes(-3, -2)

    def tiles(w):
        return w.reshape(LAYERS, FT, P, -1).swapaxes(1, 2)

    a["in_proj"] = halves(i["L0_txt_in_proj_w"])
    a["norm_w"] = i["L0_txt_norm_w"].reshape(LAYERS, 2, CH).swapaxes(1, 2)
    a["txt_par"] = tiles(np.concatenate([i["L0_txt_conv_w"][:, :, 0], i["L0_txt_conv_b"][..., None], i["L0_txt_dt_proj_b"][..., None],
                                         i["L0_txt_A_log"], i["L0_txt_D"][..., None]], -1))
    a["x_proj"] = tiles(i["L0_txt_x_proj_w"])
    a["dt_proj"] = i["L0_txt_dt_proj_w"]
    a["out_proj"] = tiles(i["L0_txt_out_proj_w"])
    pick = np.zeros((XD, 2 * STATES, P), np.float32)
    pick[RANK + np.arange(2 * STATES), np.arange(2 * STATES)] = 1
    a["pick"] = pick

    def vector(v):
        return v.reshape(2, CH).T

    def blocks(w):
        out = np.zeros((GH, D, GH, w.shape[0]), w.dtype)
        for g in range(GH):
            out[g, :, g] = w.T
        return out.reshape(CH, GH * w.shape[0])

    a["perf_w"] = halves(i["L0_attn_w_qkv"].T)
    bias = i["L0_attn_b_qkv"].reshape(3, 2, CH)
    a["perf_bqk"] = bias[0:2].transpose(2, 1, 0)
    a["perf_bv"] = i["L0_attn_b_qkv"][None, 2 * C:]
    a["perf_wp"] = halves(i["L0_attn_w_proj"].T)
    a["perf_bp"] = i["L0_attn_b_proj"][None]
    a["perf_feat"] = blocks(i["L0_attn_projection"])
    qkv = i["L0_ffn_Wqkv"].reshape(C, 3, H, D)
    a["att_wqk"] = halves(i["L0_ffn_Wqkv"][:, :2 * C])
    a["att_wv"] = halves(qkv[:, 2].reshape(C, C))
    a["att_wp"] = halves(i["L0_ffn_Wproj"])
    a["att_ln"] = np.stack([vector(i["L0_ffn_ln1_g"]), vector(i["L0_ffn_ln1_b"])], 1)
    a["before"] = np.broadcast_to(np.tril(np.ones((E, E), np.float32), -1), (P, E, E))
    a["moe_ln"] = np.stack([vector(i["L0_ffn_ln2_g"]), vector(i["L0_ffn_ln2_b"])], 1)
    a["moe_wr"] = halves(i["L0_ffn_Wrouter"])
    a["moe_w1"] = halves(i["L0_ffn_W1"])
    a["moe_w2"] = i["L0_ffn_W2"].reshape(E, FFT, P, C).swapaxes(1, 2)
    a["ffn_wr"] = halves(i["L1_ffn_gate_w"])
    a["ffn_br"] = i["L1_ffn_gate_b"][None]
    a["ffn_w1"] = halves(i["L1_ffn_w1"])
    a["ffn_b1"] = i["L1_ffn_b1"].reshape(E, FFT, P).transpose(2, 0, 1)
    a["ffn_w2"] = i["L1_ffn_w2"].reshape(E, FFT, P, C).swapaxes(1, 2)
    a["ffn_b2"] = i["L1_ffn_b2"][None]
    w = i["L1_attn_w_qkv"]
    a["mix_wq"] = halves(w[:, :C])
    a["mix_wkv"] = halves(w[:, C:])
    a["mix_wside"] = halves(np.concatenate([i["L1_attn_w_id"], i["L1_attn_w_idgate"], i["L1_attn_w_prune"]], 1))
    a["mix_bside"] = np.concatenate([np.zeros(C, np.float32), i["L1_attn_b_idgate"], i["L1_attn_b_prune"]])[None]
    a["mix_wg1"] = halves(i["L1_attn_w_g1"])
    a["mix_bg1"] = vector(i["L1_attn_b_g1"])
    a["mix_wg2"] = halves(i["L1_attn_w_g2"])
    a["mix_bg2"] = i["L1_attn_b_g2"][None]
    a["mix_static"] = np.broadcast_to(i["L1_attn_id_static_logit"], (P, H))
    a["mix_taps"] = halves(np.concatenate([i["L1_attn_fir_short_w"].reshape(C, SHORT), i["L1_attn_fir_long_w"].reshape(C, LONG)], 1))
    a["mix_mixer"] = halves(np.repeat(np.repeat(i["L1_attn_mix"], D, 0), D, 1))
    a["same_dim"] = halves(np.tile(np.eye(D, dtype=np.float32), (H, H)))
    a["same"] = halves(np.eye(C, dtype=np.float32))
    a["head_mask"] = np.repeat(np.eye(GH, dtype=np.float32), CK, 0)
    a["upto"] = np.tile(np.triu(np.ones((CK, CK), np.float32)), (GH, 1))
    a["proj_w"] = halves(i["L1_attn_w_proj"])
    a["proj_b"] = i["L1_attn_b_proj"][None]
    return {k: np.ascontiguousarray(v) for k, v in a.items()}


def kernel(**inputs):
    import numpy as np
    import concourse.bacc as bacc
    from concourse.bass_utils import run_bass_kernel_spmd

    arrays = layouts({k: np.asarray(v) for k, v in inputs.items()}, np)
    nc = bacc.Bacc("TRN2", target_bir_lowering=False, num_devices=1)
    io = {k: nc.dram_tensor(f"in_{k}", v.shape, mybir.dt.from_np(v.dtype), kind="ExternalInput").ap()
          for k, v in arrays.items()}
    out = nc.dram_tensor("out", (B, N, C), F32, kind="ExternalOutput").ap()
    program(nc, io, out)
    r = run_bass_kernel_spmd(nc, [{f"in_{k}": v for k, v in arrays.items()}], core_ids=[0])
    return r.results[0]["out"]
```

```python
import math
from contextlib import ExitStack

import concourse.bass as bass
from concourse import mybir

F32 = mybir.dt.float32
I32 = mybir.dt.int32
BF16 = mybir.dt.bfloat16
ALU = mybir.AluOpType
ACT = mybir.ActivationFunctionType
AX = mybir.AxisListType

B = 4
NI = 512
NT = 128
N = NI + NT
P = 128
TB = N // P
TILES = B * TB
C = 192
CH = C // 2
H = 12
D = C // H
HALF = N // 2
EPS = 1e-5
ROUND = 1.5 * 2.0 ** 23
TWO_PI = 6.283185


class InOrder:

    def __init__(self, eng, own, per_turn=0):
        self.eng, self.own, self.per_turn, self.base, self.n = eng, own, per_turn, 0, 0

    def turn(self, i):
        self.base, self.n = i * self.per_turn, 0

    def step(self, ins):
        ins.then_inc(self.own, 1)
        self.n += 1
        self.eng.wait_ge(self.own, self.base + self.n)

    def announce(self, ins, sem, value):
        ins.then_inc(sem, 1)
        self.eng.wait_ge(sem, value)

    def count(self, ins):
        ins.then_inc(self.own, 1)
        self.n += 1

    def sem_step(self):
        self.eng.sem_inc(self.own, 1)
        self.n += 1

    def wait(self):
        self.eng.wait_ge(self.own, self.base + self.n)

    def ended(self):
        assert self.n == self.per_turn, (self.n, self.per_turn)


class Ring:

    def __init__(self, eng, banks, filled, taken, per_turn):
        self.eng, self.banks, self.filled, self.taken, self.per_turn = eng, banks, filled, taken, per_turn
        self.base, self.n = 0, 0

    def turn(self, i):
        assert self.n in (0, self.per_turn), (self.n, self.per_turn)
        self.base, self.n = i * self.per_turn, 0

    def bank(self):
        return self.banks[self.n % len(self.banks)]

    def free(self):
        self.eng.wait_ge(self.taken, self.base + self.n + 1)
        return self.bank()

    def fill(self, ins):
        ins.then_inc(self.filled, 1)
        self.n += 1

    def arrived(self, n=None):
        self.eng.wait_ge(self.taken, self.base + len(self.banks) + (self.n if n is None else n))

    def get(self):
        self.eng.wait_ge(self.filled, self.base + self.n + 1)
        return self.bank()

    def take(self, ins):
        ins.then_inc(self.taken, 1)
        self.n += 1

    def done(self):
        self.eng.wait_ge(self.taken, self.base + len(self.banks) + self.n)

    def ended(self):
        assert self.n == self.per_turn, (self.n, self.per_turn)


class Memory:

    def __init__(self, nc, stage):
        self.nc, self.stage, self.stack, self.semaphores = nc, stage, ExitStack(), []

    def __enter__(self):
        return self

    def __exit__(self, *exc):
        if self.semaphores and exc[0] is None:
            self.nc.clear_and_free_semaphores(self.semaphores)
            self.nc.all_engine_barrier()
        self.stack.close()

    def sbuf(self, name, shape, dt=F32):
        return self.stack.enter_context(self.nc.sbuf_tensor(f"{self.stage}_{name}", shape, dt))

    def psum(self, name, shape, dt=F32):
        return self.stack.enter_context(self.nc.psum_tensor(f"{self.stage}_{name}", shape, dt))

    def sem(self, name):
        self.semaphores.append(self.nc.alloc_semaphore(f"{self.stage}_{name}"))
        return self.semaphores[-1]

    def sems(self, *names):
        return [self.sem(n) for n in names]


def split_bf16(nc, own, x, parts, rest):
    own.step(nc.vector.tensor_copy(parts[0], x))
    own.step(nc.vector.tensor_tensor(rest, x, parts[0], ALU.subtract))
    own.step(nc.vector.tensor_copy(parts[1], rest))
    return nc.vector.tensor_tensor(parts[2], rest, parts[1], ALU.subtract)


BANDS = 6
JC = 5
UNITS = JC * BANDS
KTILES = 4 * 2 * BANDS + BANDS


def image_embedding(nc, h, io):
    with Memory(nc, "img") as m:
        w = m.sbuf("w", [P, KTILES, C])
        freq = m.sbuf("freq", [P, BANDS])
        shift = m.sbuf("shift", [P, 2])
        x = m.sbuf("x", [P, 2, NI])
        turns = m.sbuf("turns", [P, 2, NI])
        nearest = m.sbuf("nearest", [P, NI])
        rest = m.sbuf("rest", [P, 2, NI])
        folded = m.sbuf("folded", [P, 2, NI])
        feat = m.sbuf("feat", [P, 3, 2, NI])
        out = m.psum("out", [P, 4, 512])
        (w_in, x_in0, x_in1, x_free, turns_ready, turns_free, rest_ready, folded_ready, rest_free,
         feat_ready, feat_free, out_ready, out_free, dve_own, pool_own) = m.sems(
            "w_in", "x_in0", "x_in1", "x_free", "turns_ready", "turns_free", "rest_ready", "folded_ready",
            "rest_free", "feat_ready", "feat_free", "out_ready", "out_free", "dve_own", "pool_own")
        x_in = [x_in0, x_in1]
        with nc.Block() as block:

            @block.sync
            def _(sp):
                sp.dma_start(freq[:, :], io["freq"]).then_inc(w_in, 16)
                sp.dma_start(shift[:, :], io["sincos_shift"]).then_inc(w_in, 16)
                for part in range(3):
                    k0 = part * 18
                    sp.dma_start(w[:, k0:k0 + 18, :], io["tok_w"][:, k0:k0 + 18, :]).then_inc(w_in, 16)
                with sp.Fori(0, B // 2) as bb:
                    for half in range(2):
                        for c in range(JC):
                            n = half * JC + c
                            sp.wait_ge(x_free, bb * (2 * JC) + n + 1)
                            sp.dma_start(x[:, n % 2, :], io["x"][bass.ds(bb * (2 * JC) + n, 1)].rearrange("o p n -> p (o n)")).then_inc(x_in[n % 2], 16)

            @block.gpsimd
            def _(pool):
                pool.sem_inc(x_free, 2)
                pool.wait_ge(w_in, 5 * 16)
                with pool.Fori(0, B // 2) as bb:
                    for half in range(2):
                        for c in range(JC):
                            n = half * JC + c
                            pool.wait_ge(x_in[n % 2], bb * (16 * JC) + 16 * (n // 2 + 1))
                            for f in range(BANDS):
                                g = n * BANDS + f
                                pool.wait_ge(turns_free, bb * (2 * UNITS) + g + 1)
                                ins = nc.gpsimd.tensor_tensor(turns[:, g % 2, :], x[:, n % 2, :], freq[:, f:f + 1].to_broadcast([P, NI]), ALU.mult)
                                ins.then_inc(turns_ready, 1)
                            pool.wait_ge(turns_ready, bb * (2 * UNITS) + (n + 1) * BANDS)
                            pool.sem_inc(x_free, 1)

            @block.vector
            def _(dve):
                own = InOrder(dve, dve_own, UNITS)
                dve.sem_inc(turns_free, 2)
                with dve.Fori(0, B) as b:
                    own.turn(b)
                    for c in range(JC):
                        for f in range(BANDS):
                            g = c * BANDS + f
                            at = b * UNITS + g + 1
                            dve.wait_ge(turns_ready, at)
                            dve.wait_ge(rest_free, at)
                            own.step(nc.vector.tensor_scalar(nearest[:, :], turns[:, g % 2, :], ROUND, None, ALU.add))
                            own.announce(nc.vector.scalar_tensor_tensor(rest[:, g % 2, :], nearest[:, :], ROUND, turns[:, g % 2, :],
                                                                      ALU.subtract, ALU.subtract), rest_ready, at)
                            dve.sem_inc(turns_free, 1)
                            lo = 0 if c < JC - 1 else 64
                            dst = folded if c < JC - 1 else rest
                            nc.vector.scalar_tensor_tensor(dst[lo:P, g % 2, :], rest[lo:P, g % 2, :], -1.0, rest[lo:P, g % 2, :], ALU.mult, ALU.max).then_inc(folded_ready, 1)
                            dve.wait_ge(folded_ready, at)
                    own.ended()
                    dve.wait_ge(out_ready, b + 1)
                    for t in range(4):
                        nc.vector.tensor_copy(h[:, b * TB + t, :], out[:, t, 0:C]).then_inc(out_free, 1)

            @block.scalar
            def _(act):
                act.sem_inc(rest_free, 2)
                act.wait_ge(w_in, 5 * 16)
                with act.Fori(0, B) as b:
                    for c in range(JC):
                        for f in range(BANDS):
                            g = c * BANDS + f
                            at = b * UNITS + g + 1
                            act.wait_ge(folded_ready, at)
                            act.wait_ge(feat_free, at)
                            if c < JC - 1:
                                nc.scalar.activation(feat[:, g % 3, 0, :], rest[:, g % 2, :], ACT.Sin, scale=-TWO_PI)
                                ins = nc.scalar.activation(feat[:, g % 3, 1, :], folded[:, g % 2, :], ACT.Sin, scale=-TWO_PI,
                                                           bias=shift[:, 1:2])
                            else:
                                ins = nc.scalar.activation(feat[:, g % 3, 0, :], rest[:, g % 2, :], ACT.Sin, scale=-TWO_PI,
                                                           bias=shift[:, 0:1])
                            ins.then_inc(feat_ready, 1)
                            act.wait_ge(feat_ready, at)
                            act.sem_inc(rest_free, 1)

            @block.tensor
            def _(pe):
                pe.sem_inc(feat_free, 3)
                pe.sem_inc(out_free, 4)
                pe.wait_ge(w_in, 5 * 16)
                with pe.Fori(0, B) as b:
                    pe.wait_ge(out_free, b * 4 + 4)
                    for c in range(JC):
                        for f in range(BANDS):
                            g = c * BANDS + f
                            pe.wait_ge(feat_ready, b * UNITS + g + 1)
                            for part in range(2 if c < JC - 1 else 1):
                                k = c * 12 + part * BANDS + f
                                for t in range(4):
                                    ins = nc.tensor.matmul(out[:, t, 0:C], feat[:, g % 3, part, t * P:(t + 1) * P], w[:, k, :],
                                                           start=(k == 0), stop=(k == KTILES - 1))
                            ins.then_inc(feat_free, 1)
                    ins = None
                    pe.wait_ge(feat_free, b * UNITS + UNITS + 3)
                    pe.sem_inc(out_ready, 1)


LAYERS = 2
VOCAB = 8000
DI = 2 * C
FT = DI // P
STATES = 16
RANK = C // STATES
BC = 2 * STATES
COPIED = 3 * BC
XD = COPIED + RANK
TAPS = 4
CONV_W, CONV_B, DT_B, A_LOG, SKIP, PARAMS = 0, 4, 5, 6, 22, 23
TXT = B * NT
ATANH_TERMS = 8
NO_PAST = 200.0


def text_embedding(nc, h, ident, io):
    with Memory(nc, "txt") as m:
        ids = m.sbuf("ids", [P, B], I32)
        idf = m.sbuf("idf", [P, B])
        neg = m.sbuf("neg", [P, B])
        rows = m.sbuf("rows", [P, B], I32)
        in_w = m.sbuf("in_w", [CH, 2, 2 * DI])
        norm_w = m.sbuf("norm_w", [CH, 2])
        par = m.sbuf("par", [P, FT, PARAMS])
        xp_w = m.sbuf("xp_w", [P, FT, XD])
        dt_w = m.sbuf("dt_w", [XD, DI])
        out_w = m.sbuf("out_w", [P, FT, C])
        pick = m.sbuf("pick", [COPIED, BC, P])
        pick16 = m.sbuf("pick16", [COPIED, BC, P], BF16)
        squares = m.sbuf("squares", [P, C])
        rms = m.sbuf("rms", [P, B])
        xn = m.sbuf("xn", [P, B, C])
        xnT = m.sbuf("xnT", [CH, 2, TXT])
        padded = m.sbuf("padded", [P, FT, B, TAPS - 1 + NT])
        conv = m.sbuf("conv", [P, FT, TXT])
        u = m.sbuf("u", [P, FT, TXT])
        gate = m.sbuf("gate", [P, FT, TXT])
        xdbl = m.sbuf("xdbl", [XD, TXT])
        stack = m.sbuf("stack", [COPIED, TXT], BF16)
        part1 = m.sbuf("part1", [COPIED, TXT], BF16)
        part2 = m.sbuf("part2", [COPIED, TXT], BF16)
        part_rest = m.sbuf("part_rest", [COPIED, TXT])
        delta = m.sbuf("delta", [P, FT, TXT])
        e = m.sbuf("e", [P, FT, TXT])
        ratio = m.sbuf("ratio", [P, FT, TXT])
        ratio2 = m.sbuf("ratio2", [P, FT, TXT])
        series = m.sbuf("series", [P, FT, TXT])
        du = m.sbuf("du", [P, FT, TXT])
        decay_rate = m.sbuf("decay_rate", [P, FT, STATES])
        decay = m.sbuf("decay", [P, 2, FT, TXT])
        exponent = m.sbuf("exponent", [P, 2, FT, TXT])
        drive = m.sbuf("drive", [P, FT, TXT])
        state = m.sbuf("state", [P, 2, FT, TXT])
        read = m.sbuf("read", [P, 2, FT, TXT])
        c_row = m.sbuf("c_row", [P, 2, TXT])
        bank = m.psum("bank", [P, 8, 512])
        XNT, XR, RES, XDB, DT, BN, CN, Y, OUT = 0, 2, 5, 0, 5, (0, 1), (5, 6), 2, 0
        (ids_in, fixed_in, weights_in, weights_free, rows_ready, x_in, padding, xn_ready, xnT_psum, xnT_ready, xz_psum,
         xz_taken, conv_ready, u_ready, xd_psum, xd_ready, dt_psum, e_ready, rate_ready, delta_ready, exponent_ready,
         decay_ready, scanned, c_ready, bc_psum, stack_ready, pick_ready, read_ready, read_free, y_ready, out_psum, x_ready,
         dve_own, act_own, square_ready, root_ready, a_log_ready, z_ready) = m.sems(*(
            "ids_in fixed_in weights_in weights_free rows_ready x_in padding xn_ready xnT_psum xnT_ready xz_psum "
            "xz_taken conv_ready u_ready xd_psum xd_ready dt_psum e_ready rate_ready delta_ready exponent_ready "
            "decay_ready scanned c_ready bc_psum stack_ready pick_ready read_ready read_free y_ready out_psum x_ready "
            "dve_own act_own square_ready root_ready a_log_ready z_ready").split())

        def wide(ap):
            return ap.rearrange("p (o n) -> p o n", o=1).to_broadcast([P, FT, TXT])

        with nc.Block() as block:

            @block.sync
            def _(sp):
                sp.dma_start(ids[:, :], io["ids"]).then_inc(ids_in, 16)
                sp.dma_start(pick[:, :, :], io["pick"]).then_inc(fixed_in, 16)
                with sp.Fori(0, LAYERS) as l:
                    sp.wait_ge(weights_free, l + 1)
                    for dst, name in ((in_w, "in_proj"), (norm_w, "norm_w"), (par, "txt_par"), (xp_w, "x_proj"),
                                      (dt_w, "dt_proj"), (out_w, "out_proj")):
                        src = io[name][bass.ds(l, 1)]
                        if len(src.shape) == 4:
                            sp.dma_start(dst[:, :, :], src.rearrange("o p a b -> p (o a) b")).then_inc(weights_in, 16)
                        else:
                            dst = dst[COPIED:, :] if name == "dt_proj" else dst[:, :]
                            sp.dma_start(dst, src.rearrange("o p a -> p (o a)")).then_inc(weights_in, 16)

            @block.gpsimd
            def _(pool):
                nc.gpsimd.memset(padded[:, :, :, :], 0.0).then_inc(padding, 1)
                nc.gpsimd.memset(exponent[:, :, :, :], NO_PAST).then_inc(padding, 1)
                pool.sem_inc(read_ready, 2)
                pool.wait_ge(padding, 2)
                pool.wait_ge(rows_ready, 1)
                for b in range(B):
                    nc.gpsimd.indirect_dma_start(out=h[:, b * TB + TB - 1, :], out_offset=None, in_=io["emb"],
                                                 in_offset=bass.IndirectOffsetOnAxis(ap=rows[:, b:b + 1], axis=0)).then_inc(x_in, 16)
                with pool.Fori(0, LAYERS) as l:
                    for n in range(STATES):
                        at = l * STATES + n + 1
                        pool.wait_ge(scanned, at + 2)
                        pool.wait_ge(read_free, at)
                        pool.wait_ge(c_ready, at)
                        nc.gpsimd.tensor_tensor(read[:, n % 2, :, :], state[:, n % 2, :, :], wide(c_row[:, n % 2, :]),
                                                ALU.mult).then_inc(read_ready, 1)

            @block.vector
            def _(dve):
                own = InOrder(dve, dve_own)
                dve.wait_ge(ids_in, 16)
                own.step(nc.vector.tensor_copy(idf[:, :], ids[:, :]))
                own.step(nc.vector.tensor_scalar(neg[:, :], idf[:, :], 0.0, float(VOCAB), ALU.is_lt, ALU.mult))
                own.step(nc.vector.tensor_tensor(idf[:, :], idf[:, :], neg[:, :], ALU.add))
                own.step(nc.vector.tensor_scalar(idf[:, :], idf[:, :], 0.0, float(VOCAB - 1), ALU.max, ALU.min))
                nc.vector.tensor_copy(rows[:, :], idf[:, :]).then_inc(rows_ready, 1)
                before = own.n
                own = InOrder(dve, dve_own, TXT_DVE_STEPS)
                dve.wait_ge(x_in, 16 * B)
                with dve.Fori(0, LAYERS) as l:
                    own.turn(l)
                    own.base = own.base + before
                    dve.wait_ge(x_ready, l * B + 1)
                    for b in range(B):
                        x = h[:, b * TB + TB - 1, :]
                        own.step(nc.vector.tensor_tensor_reduce(out=squares[:, :], in0=x, in1=x, scale=1.0, scalar=0.0,
                                                                op0=ALU.mult, op1=ALU.add, accum_out=rms[:, b:b + 1]))
                    own.step(nc.vector.tensor_scalar(rms[:, :], rms[:, :], 1.0 / C, EPS, ALU.mult, ALU.add))
                    nc.vector.reciprocal(rms[:, :], rms[:, :]).then_inc(square_ready, 1)
                    dve.wait_ge(root_ready, l + 1)
                    for b in range(B):
                        nc.vector.tensor_scalar(xn[:, b, :], h[:, b * TB + TB - 1, :], rms[:, b:b + 1], None, ALU.mult).then_inc(xn_ready, 1)
                    dve.wait_ge(weights_in, l * 96 + 96)
                    nc.vector.tensor_scalar(par[:, :, A_LOG:A_LOG + STATES], par[:, :, A_LOG:A_LOG + STATES], 88.7, None,
                                            ALU.min).then_inc(a_log_ready, 1)
                    dve.wait_ge(xnT_psum, l + 1)
                    for k in range(2):
                        nc.vector.tensor_scalar(xnT[:, k, :], bank[0:CH, XNT + k, :], norm_w[:, k:k + 1], None, ALU.mult).then_inc(xnT_ready, 1)
                    dve.wait_ge(xz_taken, l * 2 * FT + FT)
                    for f in range(FT):
                        for k in range(TAPS):
                            src = padded[:, f, :, k:k + NT]
                            dst = conv[:, f, :].rearrange("p (b t) -> p b t", b=B)
                            tap = par[:, f, CONV_W + k:CONV_W + k + 1]
                            if k == 0:
                                own.step(nc.vector.tensor_scalar(dst, src, tap, None, ALU.mult))
                            elif k < TAPS - 1:
                                own.step(nc.vector.scalar_tensor_tensor(dst, src, tap, dst, ALU.mult, ALU.add))
                            else:
                                nc.vector.scalar_tensor_tensor(dst, src, tap, dst, ALU.mult, ALU.add).then_inc(conv_ready, 1)
                    dve.wait_ge(xd_psum, l + 1)
                    nc.vector.tensor_copy(xdbl[:, :], bank[0:XD, XDB, :]).then_inc(xd_ready, 1)
                    dve.wait_ge(xd_ready, l + 1)
                    parts = [stack[:, :], part1[:, :], part2[:, :]]
                    own.step(split_bf16(nc, own, xdbl[0:COPIED, :], parts, part_rest[:, :]))
                    for p in (1, 2):
                        rows_of = slice(p * BC, (p + 1) * BC)
                        nc.vector.tensor_copy(stack[rows_of, :], parts[p][rows_of, :]).then_inc(stack_ready, 1)
                    dve.wait_ge(dt_psum, l + 1)
                    for f in range(FT):
                        nc.vector.tensor_scalar(series[:, f, :], bank[:, DT + f, :], par[:, f, DT_B:DT_B + 1], None, ALU.add).then_inc(z_ready, 1)
                    dve.wait_ge(z_ready, l * FT + FT)
                    own.step(nc.vector.tensor_scalar(delta[:, :, :], series[:, :, :], 0.0, None, ALU.max))
                    dve.wait_ge(e_ready, l + 1)
                    own.step(nc.vector.tensor_scalar(ratio[:, :, :], e[:, :, :], 2.0, None, ALU.add))
                    own.step(nc.vector.reciprocal(ratio[:, :, :], ratio[:, :, :]))
                    own.step(nc.vector.tensor_tensor(ratio[:, :, :], ratio[:, :, :], e[:, :, :], ALU.mult))
                    own.step(nc.vector.tensor_tensor(ratio2[:, :, :], ratio[:, :, :], ratio[:, :, :], ALU.mult))
                    own.step(nc.vector.tensor_scalar(series[:, :, :], ratio2[:, :, :], 1.0 / (2 * ATANH_TERMS - 1), None, ALU.mult))
                    for t in range(ATANH_TERMS - 2, 0, -1):
                        own.step(nc.vector.scalar_tensor_tensor(series[:, :, :], series[:, :, :], 1.0 / (2 * t + 1), ratio2[:, :, :],
                                                                ALU.add, ALU.mult))
                    own.step(nc.vector.scalar_tensor_tensor(series[:, :, :], series[:, :, :], 1.0, ratio[:, :, :], ALU.add, ALU.mult))
                    own.announce(nc.vector.scalar_tensor_tensor(delta[:, :, :], series[:, :, :], 2.0, delta[:, :, :], ALU.mult, ALU.add),
                               delta_ready, l + 1)
                    dve.wait_ge(u_ready, l * FT + FT)
                    own.step(nc.vector.tensor_tensor(du[:, :, :], delta[:, :, :], u[:, :, :], ALU.mult))

                    def exponents(n):
                        if n >= 2:
                            dve.wait_ge(decay_ready, l * STATES + n - 1)
                        for f in range(FT):
                            later = [a.rearrange("p (b t) -> p b t", b=B)[:, :, 1:] for a in (exponent[:, n % 2, f, :], delta[:, f, :])]
                            nc.vector.tensor_scalar(later[0], later[1], decay_rate[:, f, n:n + 1], NO_PAST, ALU.mult, ALU.min).then_inc(exponent_ready, 1)

                    dve.wait_ge(rate_ready, l + 1)
                    exponents(0)
                    for n in range(STATES):
                        at = l * STATES + n + 1
                        dve.wait_ge(bc_psum, at)
                        own.step(nc.vector.tensor_tensor(drive[:, :, :], du[:, :, :], wide(bank[:, BN[n % 2], :]), ALU.mult))
                        if n + 1 < STATES:
                            exponents(n + 1)
                        dve.wait_ge(decay_ready, at)
                        dve.wait_ge(read_ready, at)
                        own.announce(nc.vector.tensor_tensor_scan(state[:, n % 2, :, :].rearrange("p f n -> p (f n)"),
                                                                decay[:, n % 2, :, :].rearrange("p f n -> p (f n)"),
                                                                drive[:, :, :].rearrange("p f n -> p (f n)"), 0.0, ALU.mult, ALU.add),
                                   scanned, at + 2)
                    dve.wait_ge(read_free, l * STATES + STATES + 2)
                    for f in range(FT):
                        own.step(nc.vector.scalar_tensor_tensor(conv[:, f, :], u[:, f, :], par[:, f, SKIP:SKIP + 1], bank[:, Y + f, :],
                                                                ALU.mult, ALU.add))
                    own.announce(nc.vector.tensor_tensor(conv[:, :, :], conv[:, :, :], gate[:, :, :], ALU.mult), y_ready, l + 1)
                    dve.wait_ge(out_psum, l + 1)
                    for b in range(B):
                        x = h[:, b * TB + TB - 1, :]
                        nc.vector.tensor_tensor(x, x, bank[:, OUT + b // 2, (b % 2) * C:(b % 2 + 1) * C], ALU.add).then_inc(x_ready, 1)
                    dve.wait_ge(x_ready, l * B + B + 1)
                    own.ended()

            @block.scalar
            def _(act):
                act.sem_inc(x_ready, 1)
                act.sem_inc(scanned, 2)
                own = InOrder(act, act_own, TXT_ACT_STEPS)
                act.wait_ge(padding, 2)
                act.wait_ge(fixed_in, 16)
                nc.scalar.activation(pick16[:, :, :], pick[:, :, :], ACT.Copy).then_inc(pick_ready, 1)
                with act.Fori(0, LAYERS) as l:
                    own.turn(l)
                    act.wait_ge(square_ready, l + 1)
                    nc.scalar.activation(rms[:, :], rms[:, :], ACT.Sqrt).then_inc(root_ready, 1)
                    for f in range(FT):
                        act.wait_ge(xz_psum, l * 2 * FT + f + 1)
                        nc.scalar.activation(padded[:, f, :, TAPS - 1:], bank[:, XR + f, :].rearrange("p (b t) -> p b t", b=B),
                                             ACT.Copy).then_inc(xz_taken, 1)
                    for f in range(FT):
                        act.wait_ge(xz_psum, l * 2 * FT + FT + f + 1)
                        nc.scalar.activation(gate[:, f, :], bank[:, RES + f, :], ACT.Silu).then_inc(xz_taken, 1)
                    for f in range(FT):
                        act.wait_ge(conv_ready, l * FT + f + 1)
                        nc.scalar.activation(u[:, f, :], conv[:, f, :], ACT.Silu, bias=par[:, f, CONV_B:CONV_B + 1]).then_inc(u_ready, 1)
                    act.wait_ge(a_log_ready, l + 1)
                    own.announce(nc.scalar.activation(decay_rate[:, :, :], par[:, :, A_LOG:A_LOG + STATES], ACT.Exp), rate_ready, l + 1)
                    act.wait_ge(z_ready, l * FT + FT)
                    own.step(nc.scalar.activation(e[:, :, :], series[:, :, :], ACT.Abs))
                    own.announce(nc.scalar.activation(e[:, :, :], e[:, :, :], ACT.Exp, scale=-1.0), e_ready, l + 1)
                    for n in range(STATES):
                        act.wait_ge(scanned, l * STATES + n + 1)
                        act.wait_ge(exponent_ready, (l * STATES + n + 1) * FT)
                        nc.scalar.activation(decay[:, n % 2, :, :], exponent[:, n % 2, :, :], ACT.Exp, scale=-1.0).then_inc(decay_ready, 1)
                        act.wait_ge(bc_psum, l * STATES + n + 1)
                        act.wait_ge(read_ready, l * STATES + n + 1)
                        nc.scalar.activation(c_row[:, n % 2, :], bank[:, CN[n % 2], :], ACT.Copy).then_inc(c_ready, 1)
                    own.ended()

            @block.tensor
            def _(pe):
                pe.sem_inc(read_free, 2)
                pe.sem_inc(weights_free, 1)
                pe.wait_ge(pick_ready, 1)
                with pe.Fori(0, LAYERS) as l:
                    pe.wait_ge(weights_in, l * 96 + 96)
                    for b in range(B):
                        pe.wait_ge(xn_ready, l * B + b + 1)
                        for k in range(2):
                            ins = nc.tensor.transpose(bank[0:CH, XNT + k, b * P:(b + 1) * P], xn[:, b, k * CH:(k + 1) * CH], ident[:, :])
                    ins.then_inc(xnT_psum, 1)
                    pe.wait_ge(xnT_ready, l * 2 + 2)
                    for f in range(2 * FT):
                        for k in range(2):
                            ins = nc.tensor.matmul(bank[:, XR + f, :], in_w[:, k, f * P:(f + 1) * P], xnT[:, k, :], start=(k == 0), stop=(k == 1))
                        ins.then_inc(xz_psum, 1)
                    for f in range(FT):
                        pe.wait_ge(u_ready, l * FT + f + 1)
                        ins = nc.tensor.matmul(bank[0:XD, XDB, :], xp_w[:, f, :], u[:, f, :], start=(f == 0), stop=(f == FT - 1))
                    ins.then_inc(xd_psum, 1)
                    pe.wait_ge(xd_ready, l + 1)
                    pe.wait_ge(xz_taken, l * 2 * FT + 2 * FT)
                    for f in range(FT):
                        ins = nc.tensor.matmul(bank[:, DT + f, :], dt_w[COPIED:, f * P:(f + 1) * P], xdbl[COPIED:, :], start=True, stop=True)
                    ins.then_inc(dt_psum, 1)
                    pe.wait_ge(stack_ready, l * 2 + 2)
                    pe.wait_ge(delta_ready, l + 1)
                    for n in range(STATES):
                        at = l * STATES + n + 1
                        pe.wait_ge(read_ready, at)
                        nc.tensor.matmul(bank[:, BN[n % 2], :], pick16[:, n, :], stack[:, :], start=True, stop=True)
                        nc.tensor.matmul(bank[:, CN[n % 2], :], pick16[:, STATES + n, :], stack[:, :], start=True, stop=True).then_inc(bc_psum, 1)
                        if n >= 1:
                            pe.wait_ge(read_ready, at + 1)
                            for f in range(FT):
                                ins = nc.tensor.matmul(bank[:, Y + f, :], ident[:, :], read[:, (n - 1) % 2, f, :], start=(n == 1), stop=False)
                            ins.then_inc(read_free, 1)
                    pe.wait_ge(read_ready, l * STATES + STATES + 2)
                    for f in range(FT):
                        ins = nc.tensor.matmul(bank[:, Y + f, :], ident[:, :], read[:, (STATES - 1) % 2, f, :], start=False, stop=True)
                    ins.then_inc(read_free, 1)
                    pe.wait_ge(y_ready, l + 1)
                    for b in range(B):
                        for f in range(FT):
                            ins = nc.tensor.matmul(bank[:, OUT + b // 2, (b % 2) * C:(b % 2 + 1) * C], conv[:, f, b * P:(b + 1) * P],
                                                   out_w[:, f, :], start=(f == 0), stop=(f == FT - 1))
                    ins.then_inc(out_psum, 1)
                    pe.wait_ge(out_psum, l + 1)
                    pe.sem_inc(weights_free, 1)


TXT_DVE_STEPS = 51
TXT_ACT_STEPS = 1


class Normed:

    def __init__(self, m, name):
        self.stats = m.sbuf(f"{name}_stats", [P, TB, 6])
        self.mv = m.sbuf(f"{name}_mv", [P, TB, 2])
        self.rstd = m.sbuf(f"{name}_rstd", [P, TB])
        self.xn = m.sbuf(f"{name}_xn", [P, TB, C])
        self.xT = m.sbuf(f"{name}_xT", [CH, 2, N])
        self.var_ready = m.sem(f"{name}_var")
        self.rstd_ready = m.sem(f"{name}_rstd")
        self.xn_ready = m.sem(f"{name}_xn")
        self.psum_ready = m.sem(f"{name}_psum")
        self.xT_ready = m.sem(f"{name}_xT")


NORM_STEPS = 2 * TB + 2


def norm_rows(nc, dve, own, z, src, b, dst=None):
    dst = dst or (lambda s: z.xn[:, s, :])
    for s in range(TB):
        own.count(nc.vector.bn_stats(z.stats[:, s, :], src(s)))
    own.wait()
    own.sem_step()
    for s in range(TB):
        own.count(nc.vector.bn_aggr(z.mv[:, s, :], z.stats[:, s, :]))
    own.wait()
    own.step(nc.vector.tensor_scalar(z.rstd[:, :], z.mv[:, :, 1], EPS, None, ALU.add))
    nc.vector.reciprocal(z.rstd[:, :], z.rstd[:, :]).then_inc(z.var_ready, 1)
    dve.wait_ge(z.rstd_ready, b + 1)
    for s in range(TB):
        nc.vector.tensor_scalar(dst(s), src(s), z.mv[:, s, 0:1], z.rstd[:, s:s + 1], ALU.subtract, ALU.mult).then_inc(z.xn_ready, 1)


def root(nc, act, z, b):
    act.wait_ge(z.var_ready, b + 1)
    nc.scalar.activation(z.rstd[:, :], z.rstd[:, :], ACT.Sqrt).then_inc(z.rstd_ready, 1)


def transpose_rows(nc, pe, src, ident, bank, ready):
    for s in range(TB):
        for k in range(2):
            out = bank[0:CH, k, s * P:(s + 1) * P] if s < 4 else bank[0:CH, 2, k * P:(k + 1) * P]
            ins = nc.tensor.transpose(out, src(s, k), ident[:, :])
    ins.then_inc(ready, 1)


def copy_transposed(nc, bank, xT, ready, scale=None, shift=None):
    for k in range(2):
        for src, dst in ((bank[0:CH, k, :], xT[:, k, 0:4 * P]), (bank[0:CH, 2, k * P:(k + 1) * P], xT[:, k, 4 * P:])):
            if scale is None:
                ins = nc.scalar.activation(dst, src, ACT.Copy)
            else:
                ins = nc.scalar.activation(dst, src, ACT.Identity, scale=scale[:, k:k + 1], bias=shift[:, k:k + 1])
            ins.then_inc(ready, 1)


COPIES = 4


def load(sp, pairs, sem):
    for dst, src in pairs:
        idx = tuple(slice(None) for _ in dst.shape)
        sp.dma_start(dst[idx], src).then_inc(sem, 16)
    return 16 * len(pairs)


M = 64
GH = H // 2
PAIRS = H // 2
DV = D + 1
KERNEL_EPS = 1e-3
QK_SCALE = 1.0 / math.sqrt(math.sqrt(D))
PERF_ITEMS = 4 + 4 + 2 * TB + TB + 12 + 1 + TB + TB


def performer(nc, h, ident, io):
    with Memory(nc, "perf") as m:
        z = Normed(m, "ln")
        w = m.sbuf("w", [CH, 2, 3 * C])
        bqk = m.sbuf("bqk", [CH, 2, 2])
        bv = m.sbuf("bv", [1, C])
        wp = m.sbuf("wp", [CH, 2, C])
        bp = m.sbuf("bp", [1, C])
        feat = m.sbuf("feat", [CH, GH * M])
        ones = m.sbuf("ones", [1, P])
        qT = m.sbuf("qT", [CH, 2, N])
        kT = m.sbuf("kT", [CH, 2, N])
        kp = m.sbuf("kp", [P, TB, H * M])
        v = m.sbuf("v", [P, TB, H, DV])
        qpT = m.sbuf("qpT", [P, PAIRS, N])
        ctx = m.sbuf("ctx", [P, PAIRS, 2 * DV])
        recip = m.sbuf("recip", [P, H])
        attn = m.sbuf("attn", [P, TB, C])
        aT = m.sbuf("aT", [CH, 2, N])
        bank = m.psum("bank", [P, 8, 512])
        banks = (3, 4, 5, 6, 7)
        (loaded, set_up, filled, taken, attn_ready, aT_psum, aT_ready, h_ready, dve_own) = m.sems(
            *"loaded set_up filled taken attn_ready aT_psum aT_ready h_ready dve_own".split())
        pairs = ((w, io["perf_w"]), (bqk, io["perf_bqk"]), (bv, io["perf_bv"]), (wp, io["perf_wp"]), (bp, io["perf_bp"]),
                 (feat, io["perf_feat"]))
        LOADED = 16 * len(pairs)
        with nc.Block() as block:

            @block.sync
            def _(sp):
                load(sp, pairs, loaded)

            @block.gpsimd
            def _(pool):
                nc.gpsimd.memset(v[:, :, :, :], 1.0).then_inc(set_up, 1)
                nc.gpsimd.memset(ctx[:, :, :], 0.0).then_inc(set_up, 1)
                nc.gpsimd.memset(ones[:, :], 1.0).then_inc(set_up, 1)

            @block.vector
            def _(dve):
                own = InOrder(dve, dve_own, NORM_STEPS + TB)
                ring = Ring(dve, banks, filled, taken, PERF_ITEMS)
                dve.sem_inc(taken, len(banks))
                dve.wait_ge(loaded, LOADED)
                dve.wait_ge(set_up, 3)
                with dve.Fori(0, B) as b:
                    own.turn(b)
                    ring.turn(b)
                    norm_rows(nc, dve, own, z, lambda s: h[:, b * TB + s, :], b)
                    for i, dst in enumerate((qT, kT)):
                        for half in range(2):
                            for c in range(2):
                                src = ring.get()
                                ring.take(nc.vector.tensor_scalar(dst[:, half, c * HALF:(c + 1) * HALF], bank[0:CH, src, 0:HALF],
                                                                  bqk[:, half, i:i + 1], QK_SCALE, ALU.add, ALU.mult))
                    for s in range(TB):
                        for half in range(2):
                            src = ring.get()
                            ring.take(nc.vector.tensor_scalar(kp[:, s, half * GH * M:(half + 1) * GH * M], bank[:, src, 0:GH * M], 0.0,
                                                              KERNEL_EPS, ALU.max, ALU.add))
                        src = ring.get()
                        ring.take(nc.vector.tensor_copy(v[:, s, :, 0:D], bank[:, src, 0:C].rearrange("p (h d) -> p h d", h=H)))
                    for j in range(PAIRS):
                        for c in range(2):
                            src = ring.get()
                            ring.take(nc.vector.tensor_scalar(qpT[:, j, c * HALF:(c + 1) * HALF], bank[:, src, 0:HALF], 0.0, KERNEL_EPS,
                                                              ALU.max, ALU.add))
                    src = ring.get()
                    got = bank[:, src, 0:PAIRS * 2 * DV].rearrange("p (j c) -> p j c", j=PAIRS)
                    nc.vector.tensor_copy(ctx[0:M, :, 0:DV], got[0:M, :, 0:DV])
                    ring.take(nc.vector.tensor_copy(ctx[M:P, :, DV:], got[M:P, :, DV:]))
                    for s in range(TB):
                        src = ring.get()
                        got = bank[:, src, 0:H * DV].rearrange("p (h c) -> p h c", h=H)
                        own.step(nc.vector.reciprocal(recip[:, :], got[:, :, D]))
                        ring.take(nc.vector.tensor_tensor(attn[:, s, :].rearrange("p (h d) -> p h d", h=H), got[:, :, 0:D],
                                                          recip[:, :].unsqueeze(2).to_broadcast([P, H, D]), ALU.mult))
                        ring.done()
                    for s in range(TB):
                        src = ring.get()
                        row = h[:, b * TB + s, :]
                        ring.take(nc.vector.tensor_tensor(row, row, bank[:, src, 0:C], ALU.add))
                    ring.done()
                    ring.ended()
                    own.ended()

            @block.scalar
            def _(act):
                with act.Fori(0, B) as b:
                    root(nc, act, z, b)
                    act.wait_ge(z.psum_ready, b + 1)
                    copy_transposed(nc, bank, z.xT, z.xT_ready)
                    act.wait_ge(aT_psum, b + 1)
                    copy_transposed(nc, bank, aT, aT_ready)

            @block.tensor
            def _(pe):
                ring = Ring(pe, banks, filled, taken, PERF_ITEMS)
                pe.wait_ge(loaded, LOADED)
                pe.wait_ge(set_up, 3)
                with pe.Fori(0, B) as b:
                    ring.turn(b)
                    pe.wait_ge(z.xn_ready, b * TB + TB)
                    transpose_rows(nc, pe, lambda s, k: z.xn[:, s, k * CH:(k + 1) * CH], ident, bank, z.psum_ready)
                    pe.wait_ge(z.xT_ready, b * COPIES + COPIES)
                    for i in range(2):
                        for half in range(2):
                            for c in range(2):
                                dst = ring.free()
                                for k in range(2):
                                    at = i * C + half * CH
                                    ins = nc.tensor.matmul(bank[0:CH, dst, 0:HALF], w[:, k, at:at + CH], z.xT[:, k, c * HALF:(c + 1) * HALF],
                                                           start=(k == 0), stop=(k == 1))
                                ring.fill(ins)
                    ring.arrived(8)
                    for s in range(TB):
                        for half in range(2):
                            dst = ring.free()
                            ring.fill(nc.tensor.matmul(bank[:, dst, 0:GH * M], kT[:, half, s * P:(s + 1) * P], feat[:, :], start=True, stop=True))
                        dst = ring.free()
                        for k in range(2):
                            nc.tensor.matmul(bank[:, dst, 0:C], z.xT[:, k, s * P:(s + 1) * P], w[:, k, 2 * C:], start=(k == 0), stop=False)
                        ring.fill(nc.tensor.matmul(bank[:, dst, 0:C], ones[:, :], bv[:, :], start=False, stop=True))
                    for j in range(PAIRS):
                        at = (j % 3) * P
                        for c in range(2):
                            dst = ring.free()
                            ring.fill(nc.tensor.matmul(bank[:, dst, 0:HALF], feat[:, at:at + P], qT[:, j // 3, c * HALF:(c + 1) * HALF],
                                                       start=True, stop=True))
                    ring.arrived(8 + 3 * TB)
                    dst = ring.free()
                    for j in range(PAIRS):
                        for s in range(TB):
                            ins = nc.tensor.matmul(bank[:, dst, j * 2 * DV:(j + 1) * 2 * DV], kp[:, s, j * P:(j + 1) * P],
                                                   v[:, s, 2 * j:2 * j + 2, :].rearrange("p h c -> p (h c)"), start=(s == 0), stop=(s == TB - 1))
                    ring.fill(ins)
                    ring.arrived()
                    for s in range(TB):
                        dst = ring.free()
                        for j in range(PAIRS):
                            ins = nc.tensor.matmul(bank[:, dst, j * 2 * DV:(j + 1) * 2 * DV], qpT[:, j, s * P:(s + 1) * P], ctx[:, j, :],
                                                   start=True, stop=True)
                        ring.fill(ins)
                    ring.arrived()
                    transpose_rows(nc, pe, lambda s, k: attn[:, s, k * CH:(k + 1) * CH], ident, bank, aT_psum)
                    pe.wait_ge(aT_ready, b * COPIES + COPIES)
                    for s in range(TB):
                        dst = ring.free()
                        for k in range(2):
                            nc.tensor.matmul(bank[:, dst, 0:C], aT[:, k, s * P:(s + 1) * P], wp[:, k, :], start=(k == 0), stop=False)
                        ring.fill(nc.tensor.matmul(bank[:, dst, 0:C], ones[:, :], bp[:, :], start=False, stop=True))
                    ring.ended()


PARTS = 3
STACK = ((0, 0), (0, 1), (1, 0), (1, 1), (0, 2), (2, 0))
ROWS = len(STACK) * D
ALL_ROWS = ROWS + PARTS
LOT = 4
LOTS = H // LOT
QK_ITEMS = 2 * 2 * 2 + TB


def attention_operands(nc, h, x1, v, qk_rows, ident, io):
    with Memory(nc, "qk") as m:
        z0 = Normed(m, "ln0")
        z = Normed(m, "ln1")
        wqk = m.sbuf("wqk", [CH, 2, 2 * C])
        wv = m.sbuf("wv", [CH, 2, C])
        ln = m.sbuf("ln", [CH, 2, 2])
        parts = m.sbuf("parts", [CH, 2, 2, PARTS, N], BF16)
        rest = m.sbuf("rest", [CH, HALF])
        bank = m.psum("bank", [P, 8, 512])
        banks = (3, 4, 5, 6, 7)
        (loaded, set_up, filled, taken, stored, dve_own) = m.sems(*"loaded set_up filled taken stored dve_own".split())
        pairs = ((wqk, io["att_wqk"]), (wv, io["att_wv"]), (ln, io["att_ln"]))
        LOADED = 16 * len(pairs)
        with nc.Block() as block:

            @block.sync
            def _(sp):
                load(sp, pairs, loaded)
                with sp.Fori(0, B) as b:
                    sp.wait_ge(taken, b * QK_ITEMS + len(banks) + 8)
                    for half in range(2):
                        dst = qk_rows[bass.ds(b * 2 * PARTS, 2 * PARTS), half * CH:(half + 1) * CH, :]
                        sp.dma_start(dst.rearrange("i c n -> c i n"), parts[:, half].rearrange("c i s n -> c (i s) n")).then_inc(stored, 16)
                sp.wait_ge(stored, 32 * B + 32)

            @block.gpsimd
            def _(pool):
                nc.gpsimd.memset(v[:, :, :, :], 1.0).then_inc(set_up, 1)

            @block.vector
            def _(dve):
                own = InOrder(dve, dve_own, 2 * NORM_STEPS + 1 + 8 * 3)
                ring = Ring(dve, banks, filled, taken, QK_ITEMS)
                dve.sem_inc(taken, len(banks))
                dve.sem_inc(stored, 32)
                dve.wait_ge(loaded, LOADED)
                dve.wait_ge(set_up, 1)
                with dve.Fori(0, B) as b:
                    own.turn(b)
                    ring.turn(b)
                    norm_rows(nc, dve, own, z0, lambda s: h[:, b * TB + s, :], b, lambda s: x1[:, b * TB + s, :])
                    dve.wait_ge(z0.xn_ready, b * TB + TB)
                    own.sem_step()
                    norm_rows(nc, dve, own, z, lambda s: x1[:, b * TB + s, :], b)
                    dve.wait_ge(stored, b * 32 + 32)
                    for i in range(2):
                        for half in range(2):
                            for c in range(2):
                                slot = ring.get()
                                cols = slice(c * HALF, (c + 1) * HALF)
                                ring.take(split_bf16(nc, own, bank[0:CH, slot, 0:HALF], [parts[:, half, i, p, cols] for p in range(PARTS)],
                                                     rest[:, :]))
                                ring.done()
                    for s in range(TB):
                        slot = ring.get()
                        ring.take(nc.vector.tensor_scalar(v[:, b * TB + s, :, 0:D], bank[:, slot, 0:C].rearrange("p (h d) -> p h d", h=H),
                                                          1.0, None, ALU.mult))
                    ring.ended()
                    own.ended()

            @block.scalar
            def _(act):
                act.wait_ge(loaded, LOADED)
                with act.Fori(0, B) as b:
                    root(nc, act, z0, b)
                    root(nc, act, z, b)
                    act.wait_ge(z.psum_ready, b + 1)
                    copy_transposed(nc, bank, z.xT, z.xT_ready, ln[:, 0, :], ln[:, 1, :])

            @block.tensor
            def _(pe):
                ring = Ring(pe, banks, filled, taken, QK_ITEMS)
                pe.wait_ge(loaded, LOADED)
                with pe.Fori(0, B) as b:
                    ring.turn(b)
                    pe.wait_ge(z.xn_ready, b * TB + TB)
                    transpose_rows(nc, pe, lambda s, k: z.xn[:, s, k * CH:(k + 1) * CH], ident, bank, z.psum_ready)
                    pe.wait_ge(z.xT_ready, b * COPIES + COPIES)
                    for i in range(2):
                        for half in range(2):
                            for c in range(2):
                                slot = ring.free()
                                at = i * C + half * CH
                                for k in range(2):
                                    ins = nc.tensor.matmul(bank[0:CH, slot, 0:HALF], wqk[:, k, at:at + CH], z.xT[:, k, c * HALF:(c + 1) * HALF],
                                                           start=(k == 0), stop=(k == 1))
                                ring.fill(ins)
                    for s in range(TB):
                        slot = ring.free()
                        for k in range(2):
                            ins = nc.tensor.matmul(bank[:, slot, 0:C], z.xT[:, k, s * P:(s + 1) * P], wv[:, k, :], start=(k == 0), stop=(k == 1))
                        ring.fill(ins)
                    ring.ended()


WINDOW = 96
MAX_ITEMS = H * TB + H + TB
EXP_ITEMS = H + H * TB + 2
MAX_LAG, PV_LAG = 2, 3


def softmax_attention(nc, x1, v, qk_rows, ident, io):
    with Memory(nc, "att") as m:
        q = m.sbuf("q", [ALL_ROWS, H, N], BF16)
        k = m.sbuf("k", [ALL_ROWS, H, N], BF16)
        wp = m.sbuf("wp", [CH, 2, C])
        ident16 = m.sbuf("ident16", [P, P], BF16)
        vb = m.sbuf("vb", [P, TB, H * DV])
        negmax = m.sbuf("negmax", [P, H, TB])
        rest = m.sbuf("rest", [P, TB])
        placed = m.sbuf("placed", [P, 2, TB, ALL_ROWS], BF16)
        probs = m.sbuf("probs", [P, 2, TB, N])
        recip = m.sbuf("recip", [P, TB])
        attn = m.sbuf("attn", [P, TB, C])
        aT = m.sbuf("aT", [CH, 2, N])
        bank = m.psum("bank", [P, 8, 512])
        exp_banks, banks = (0, 2), (4, 6)
        (loaded, set_up, filled, taken, exp_filled, exp_taken, placed_ready, v_ready, lot_used, ones_ready, dve_own) = m.sems(
            *"loaded set_up filled taken exp_filled exp_taken placed_ready v_ready lot_used ones_ready dve_own".split())
        lot_in = m.sems(*(f"lot_in{i}" for i in range(LOTS)))
        LOT_IN = 16 * 2 * len(STACK)

        def two(slot, rows=P):
            return bank[0:rows, slot:slot + 2, 0:HALF]

        def halves(ap):
            return ap.rearrange("p (c n) -> p c n", c=2)

        with nc.Block() as block:

            @block.sync
            def _(sp):
                load(sp, ((wp, io["att_wp"]),), loaded)
                with sp.Fori(0, B) as b:
                    for lot in range(LOTS):
                        heads = slice(lot * LOT, (lot + 1) * LOT)
                        sp.wait_ge(lot_used, b * LOTS + lot + 1)
                        for i, buf in enumerate((q, k)):
                            for at, pair in enumerate(STACK):
                                src = qk_rows[bass.ds((b * 2 + i) * PARTS + pair[i], 1), lot * LOT * D:(lot + 1) * LOT * D, :]
                                sp.dma_start(buf[at * D:(at + 1) * D, heads, :], src.rearrange("o (h d) n -> d (o h) n", d=D)).then_inc(lot_in[lot], 16)

            @block.gpsimd
            def _(pool):
                nc.gpsimd.memset(k[ROWS:ALL_ROWS, :, :], 1.0).then_inc(ones_ready, 1)
                pool.wait_ge(ones_ready, 1)
                nc.gpsimd.memset(placed[:, :, :, :], 0.0).then_inc(set_up, 1)

            @block.vector
            def _(dve):
                own = InOrder(dve, dve_own, H * 4)
                ring = Ring(dve, banks, filled, taken, MAX_ITEMS)
                dve.sem_inc(taken, len(banks))
                dve.wait_ge(loaded, 16)
                nc.vector.tensor_copy(ident16[:, :], ident[:, :]).then_inc(set_up, 1)
                dve.wait_ge(set_up, 2)

                def maxima(head, s):
                    slot = ring.get()
                    ring.take(nc.vector.tensor_reduce(negmax[:, head, s:s + 1], two(slot), AX.XY, ALU.max, negate=True))

                def place(head):
                    ring.done()
                    cols = [placed[:, head % 2, :, ROWS + p] for p in range(PARTS)]
                    split_bf16(nc, own, negmax[:, head, :], cols, rest[:, :]).then_inc(placed_ready, 1)

                def normalize(head):
                    ring.done()
                    slot = ring.get()
                    at = head * DV - min(head * DV, H * DV - WINDOW)
                    got = bank[:, slot, 0:TB * WINDOW].rearrange("p (s c) -> p s c", s=TB)
                    own.step(nc.vector.reciprocal(recip[:, :], got[:, :, at + D]))
                    ring.take(nc.vector.tensor_tensor(attn[:, :, head * D:(head + 1) * D], got[:, :, at:at + D],
                                                      recip[:, :].unsqueeze(2).to_broadcast([P, TB, D]), ALU.mult))

                with dve.Fori(0, B) as b:
                    own.turn(b)
                    ring.turn(b)
                    nc.vector.tensor_scalar(vb[:, :, :], v[:, bass.ds(b * TB, TB), :, :].rearrange("p s h c -> p s (h c)"), 1.0, None,
                                            ALU.mult).then_inc(v_ready, 1)
                    for i in range(H + PV_LAG):
                        if i < H:
                            for s in range(TB):
                                maxima(i, s)
                            place(i)
                        if i >= PV_LAG:
                            normalize(i - PV_LAG)
                    for s in range(TB):
                        slot = ring.get()
                        row = x1[:, b * TB + s, :]
                        ring.take(nc.vector.tensor_tensor(row, row, bank[:, slot, 0:C], ALU.add))
                    ring.ended()
                    own.ended()

            @block.scalar
            def _(act):
                ring = Ring(act, exp_banks, exp_filled, exp_taken, EXP_ITEMS)
                act.sem_inc(exp_taken, len(exp_banks))
                with act.Fori(0, B) as b:
                    ring.turn(b)
                    for i in range(H + MAX_LAG):
                        if 1 <= i <= H:
                            slot = ring.get()
                            got = bank[ROWS:ALL_ROWS, slot:slot + 2, :]
                            nc.scalar.activation(q[ROWS:ALL_ROWS, i - 1, 0:4 * P], got[:, 0, :], ACT.Copy)
                            ring.take(nc.scalar.activation(q[ROWS:ALL_ROWS, i - 1, 4 * P:], got[:, 1, 0:P], ACT.Copy))
                        if i >= MAX_LAG:
                            head = i - MAX_LAG
                            for t in range(TB):
                                slot = ring.get()
                                ring.take(nc.scalar.activation(halves(probs[:, head % 2, t, :]), two(slot), ACT.Exp, scale=float(D) ** -0.5))
                    for half in range(2):
                        slot = ring.get()
                        nc.scalar.activation(aT[:, half, 0:4 * P], bank[0:CH, slot, :], ACT.Copy)
                        ring.take(nc.scalar.activation(aT[:, half, 4 * P:], bank[0:CH, slot + 1, 0:P], ACT.Copy))
                    ring.ended()

            @block.tensor
            def _(pe):
                ring = Ring(pe, banks, filled, taken, MAX_ITEMS)
                exps = Ring(pe, exp_banks, exp_filled, exp_taken, EXP_ITEMS)
                pe.sem_inc(lot_used, LOTS)
                pe.wait_ge(loaded, 16)
                pe.wait_ge(ones_ready, 1)
                pe.wait_ge(set_up, 2)

                def queries_first(head, s):
                    slot = ring.free()
                    for c in range(2):
                        ins = nc.tensor.matmul(bank[:, slot + c, 0:HALF], q[0:ROWS, head, s * P:(s + 1) * P], k[0:ROWS, head, c * HALF:(c + 1) * HALF],
                                               start=True, stop=True)
                    ring.fill(ins)

                def keys_first(head, t):
                    slot = exps.free()
                    for c in range(2):
                        ins = nc.tensor.matmul(bank[:, slot + c, 0:HALF], k[:, head, t * P:(t + 1) * P], q[:, head, c * HALF:(c + 1) * HALF],
                                               start=True, stop=True)
                    exps.fill(ins)

                def max_rows(b, head):
                    pe.wait_ge(placed_ready, b * H + head + 1)
                    slot = exps.free()
                    for s in range(TB):
                        ins = nc.tensor.matmul(bank[0:ALL_ROWS, slot + s // 4, (s % 4) * P:(s % 4 + 1) * P], placed[:, head % 2, s, :], ident16[:, :],
                                               start=True, stop=True)
                    exps.fill(ins)

                def times_v(head):
                    slot = ring.free()
                    at = min(head * DV, H * DV - WINDOW)
                    for s in range(TB):
                        for t in range(TB):
                            ins = nc.tensor.matmul(bank[:, slot, s * WINDOW:(s + 1) * WINDOW], probs[:, head % 2, t, s * P:(s + 1) * P],
                                                   vb[:, t, at:at + WINDOW], start=(t == 0), stop=(t == TB - 1))
                    ring.fill(ins)

                with pe.Fori(0, B) as b:
                    ring.turn(b)
                    exps.turn(b)
                    pe.wait_ge(v_ready, b + 1)
                    for i in range(H + PV_LAG):
                        if i < H and i % LOT == 0:
                            pe.wait_ge(lot_in[i // LOT], (b + 1) * LOT_IN)
                        if 1 <= i <= H:
                            max_rows(b, i - 1)
                        if i < H + MAX_LAG and i >= MAX_LAG:
                            exps.arrived(items_before(i))
                        for s in range(TB):
                            if i < H:
                                queries_first(i, s)
                            if MAX_LAG <= i < H + MAX_LAG:
                                keys_first(i - MAX_LAG, s)
                        if i >= PV_LAG:
                            head = i - PV_LAG
                            exps.arrived(items_before(head + MAX_LAG) + TB)
                            times_v(head)
                            if head % LOT == LOT - 1:
                                pe.wait_ge(filled, ring.base + ring.n)
                                pe.sem_inc(lot_used, 1)
                    ring.arrived()
                    for half in range(2):
                        slot = exps.free()
                        for s in range(TB):
                            ins = nc.tensor.transpose(bank[0:CH, slot + s // 4, (s % 4) * P:(s % 4 + 1) * P], attn[:, s, half * CH:(half + 1) * CH],
                                                      ident[:, :])
                        exps.fill(ins)
                    exps.arrived()
                    for s in range(TB):
                        slot = ring.free()
                        for half in range(2):
                            ins = nc.tensor.matmul(bank[:, slot, 0:C], aT[:, half, s * P:(s + 1) * P], wp[:, half, :], start=(half == 0), stop=(half == 1))
                        ring.fill(ins)
                    ring.ended()
                    exps.ended()


def items_before(i):
    return sum((1 <= j <= H) + TB * (MAX_LAG <= j < H + MAX_LAG) for j in range(i)) + (1 <= i <= H)


E = 8
FF = 4 * C
FFT = FF // P
WIDE = FF // 2


def slots_for(k):
    n = k * TILES + E - 1
    return n + n % 2


def route_tokens(nc, name, k, src, xn, where, share, table, x_rows, weights, weights_in, ident, ln, io):
    slots = slots_for(k)
    with Memory(nc, f"{name}_route") as m:
        z = Normed(m, "ln")
        wr = m.sbuf("wr", [CH, 2, E])
        br = m.sbuf("br", [1, E])
        ones = m.sbuf("ones", [P, P])
        earlier = m.sbuf("earlier", [P, P])
        before = m.sbuf("before", [P, E, E])
        slot_no = m.sbuf("slot_no", [1, slots])
        zeros = m.sbuf("zeros", [P, C])
        logits = m.sbuf("logits", [P, TILES, E])
        above = m.sbuf("above", [P, TILES, E, E])
        ties = m.sbuf("ties", [P, TILES, E, E])
        rank = m.sbuf("rank", [P, TILES, E])
        chosen = m.sbuf("chosen", [P, k, TILES, E])
        either = m.sbuf("either", [P, TILES, E])
        best = m.sbuf("best", [P, 2, TILES])
        ahead = m.sbuf("ahead", [P, TILES + 1, E])
        used = m.sbuf("used", [P, E])
        first_slot = m.sbuf("first_slot", [P, E + 1])
        row = m.sbuf("row", [P, TILES, E])
        picked = m.sbuf("picked", [P, k, TILES, E])
        row_f = m.sbuf("row_f", [P, k, TILES])
        passed = m.sbuf("passed", [1, slots, E])
        expert_f = m.sbuf("expert_f", [1, slots + 2])
        bank = m.psum("bank", [P, 8, 512])
        LOGITS, EARLIER, TOTAL = 3, 4, 5
        (loaded, set_up, zero_ready, zero_filled, logits_psum, logits_ready, gap_ready, exp_ready, chosen_ready, counted, where_ready,
         kept, pool_own, scattered, dve_own, router_step) = m.sems(*(
             "loaded set_up zero_ready zero_filled logits_psum logits_ready gap_ready exp_ready chosen_ready counted where_ready kept pool_own scattered "
             "dve_own router_step").split())
        pairs = ((wr, io[f"{name}_wr"]), (before, io["before"]), (earlier, io["earlier"]), (slot_no, io["slot_no"][:, 0:slots]))
        if k == 1:
            pairs += ((br, io["ffn_br"]),)
        LOADED = 16 * len(pairs)

        def other(ap):
            return ap.unsqueeze(2).to_broadcast([P, TILES, E, E])

        def this(ap):
            return ap.unsqueeze(3).to_broadcast([P, TILES, E, E])

        with nc.Block() as block:

            @block.sync
            def _(sp):
                load(sp, pairs, loaded)
                sp.wait_ge(zero_ready, 1)
                sp.dma_start(x_rows.rearrange("(s p) c -> p s c", p=P), zeros[:, :].unsqueeze(1).to_broadcast([P, slots, C])).then_inc(zero_filled, 16)

            @block.gpsimd
            def _(pool):
                nc.gpsimd.memset(zeros[:, :], 0.0).then_inc(zero_ready, 1)
                nc.gpsimd.memset(ones[:, :], 1.0).then_inc(set_up, 1)
                pool.sem_inc(kept, 1)
                with pool.Fori(0, B) as b:
                    pool.wait_ge(z.xn_ready, b * TB + TB)
                    pool.sem_inc(pool_own, 1)
                    nc.gpsimd.tensor_copy(xn[:, bass.ds(b * TB, TB), :], z.xn[:, :, :]).then_inc(kept, 1)
                pool.wait_ge(kept, B + 1)
                pool.wait_ge(zero_filled, 16)
                pool.wait_ge(where_ready, 1)
                pool.sem_inc(pool_own, 1)
                for j in range(k):
                    for t in range(TILES):
                        nc.gpsimd.indirect_dma_start(out=x_rows, out_offset=bass.IndirectOffsetOnAxis(ap=where[:, j, t:t + 1], axis=0),
                                                     in_=xn[:, t, :], in_offset=None).then_inc(scattered, 16)
                pool.wait_ge(scattered, 16 * k * TILES)

            @block.vector
            def _(dve):
                own = InOrder(dve, dve_own, NORM_STEPS + 1)
                dve.sem_inc(logits_ready, 1)
                dve.wait_ge(loaded, LOADED)
                with dve.Fori(0, B) as b:
                    own.turn(b)
                    here = bass.ds(b * TB, TB)
                    dve.wait_ge(kept, b + 1)
                    own.sem_step()
                    norm_rows(nc, dve, own, z, lambda s: src[:, b * TB + s, :], b)
                    dve.wait_ge(logits_psum, b + 1)
                    nc.vector.tensor_scalar(logits[:, here, :], bank[:, LOGITS, 0:TB * E].rearrange("p (s e) -> p s e", s=TB),
                                            1.0, None, ALU.mult).then_inc(logits_ready, 1)
                    own.ended()
                step = InOrder(dve, router_step)
                dve.wait_ge(logits_ready, B + 1)
                step.count(nc.vector.tensor_tensor(above[:, :, :, :], other(logits[:, :, :]), this(logits[:, :, :]), ALU.is_gt))
                step.step(nc.vector.tensor_tensor(ties[:, :, :, :], other(logits[:, :, :]), this(logits[:, :, :]), ALU.is_equal))
                step.step(nc.vector.tensor_tensor(ties[:, :, :, :], ties[:, :, :, :],
                                                  before[:, :, :].unsqueeze(1).to_broadcast([P, TILES, E, E]), ALU.mult))
                step.step(nc.vector.tensor_tensor(above[:, :, :, :], above[:, :, :, :], ties[:, :, :, :], ALU.add))
                step.step(nc.vector.tensor_reduce(rank[:, :, :], above[:, :, :, :], AX.X, ALU.add))
                for j in range(k):
                    step.count(nc.vector.tensor_scalar(chosen[:, j, :, :], rank[:, :, :], float(j), None, ALU.is_equal))
                step.wait()
                if k == 2:
                    nc.vector.tensor_tensor(either[:, :, :], chosen[:, 0, :, :], chosen[:, 1, :, :], ALU.add).then_inc(chosen_ready, 1)
                    step.count(nc.vector.tensor_reduce(best[:, 0, :], logits[:, :, :], AX.X, ALU.max))
                    step.step(nc.vector.tensor_tensor(row[:, :, :], logits[:, :, :], chosen[:, 1, :, :], ALU.mult))
                    step.step(nc.vector.tensor_reduce(best[:, 1, :], row[:, :, :], AX.X, ALU.add))
                    nc.vector.tensor_tensor(share[:, 1, :], best[:, 1, :], best[:, 0, :], ALU.subtract).then_inc(gap_ready, 1)
                    dve.wait_ge(exp_ready, 1)
                    step.step(nc.vector.tensor_scalar(share[:, 0, :], share[:, 1, :], 1.0, None, ALU.add))
                    step.step(nc.vector.reciprocal(share[:, 0, :], share[:, 0, :]))
                    step.count(nc.vector.tensor_tensor(share[:, 1, :], share[:, 0, :], share[:, 1, :], ALU.mult))
                else:
                    nc.vector.tensor_copy(either[:, :, :], chosen[:, 0, :, :]).then_inc(chosen_ready, 1)
                step.step(nc.vector.memset(ahead[:, 0, :], 0.0))
                dve.wait_ge(counted, 1)
                total = bank[:, TOTAL, 0:TILES * E].rearrange("p (t e) -> p t e", t=TILES)
                for t in range(TILES):
                    step.step(nc.vector.tensor_tensor(ahead[:, t + 1, :], ahead[:, t, :], total[:, t, :], ALU.add))
                step.step(nc.vector.tensor_scalar(used[:, :], ahead[:, TILES, :], (P - 1) / 2, 1.0 / P, ALU.add, ALU.mult))
                step.step(nc.vector.tensor_scalar(used[:, :], used[:, :], ROUND, None, ALU.add))
                step.step(nc.vector.tensor_scalar(used[:, :], used[:, :], ROUND, None, ALU.subtract))
                step.step(nc.vector.memset(first_slot[:, 0:1], 0.0))
                for e in range(E):
                    step.step(nc.vector.tensor_tensor(first_slot[:, e + 1:e + 2], first_slot[:, e:e + 1], used[:, e:e + 1], ALU.add))
                step.step(nc.vector.tensor_scalar(used[:, :], first_slot[:, 0:E], float(P), None, ALU.mult))
                step.step(nc.vector.tensor_tensor(row[:, :, :], bank[:, EARLIER, 0:TILES * E].rearrange("p (t e) -> p t e", t=TILES),
                                                  ahead[:, 0:TILES, :], ALU.add))
                step.step(nc.vector.tensor_tensor(row[:, :, :], row[:, :, :], used[:, :].unsqueeze(1).to_broadcast([P, TILES, E]), ALU.add))
                step.step(nc.vector.tensor_tensor(picked[:, :, :, :], chosen[:, :, :, :],
                                                  row[:, :, :].unsqueeze(1).to_broadcast([P, k, TILES, E]), ALU.mult))
                step.step(nc.vector.tensor_reduce(row_f[:, :, :], picked[:, :, :, :], AX.X, ALU.add))
                nc.vector.tensor_copy(where[:, :, :], row_f[:, :, :]).then_inc(where_ready, 1)
                step.count(nc.vector.memset(expert_f[:, :], 0.0))
                step.step(nc.vector.tensor_tensor(passed[:, :, :], first_slot[0:1, 1:E + 1].unsqueeze(1).to_broadcast([1, slots, E]),
                                                  slot_no[:, :].unsqueeze(2).to_broadcast([1, slots, E]), ALU.is_le))
                step.step(nc.vector.tensor_reduce(expert_f[:, 2:], passed[:, :, :], AX.X, ALU.add))
                step.step(nc.vector.tensor_scalar(expert_f[:, :], expert_f[:, :], float(E - 1), None, ALU.min))
                step.step(nc.vector.tensor_copy(table[:, :], expert_f[:, :]))

            @block.scalar
            def _(act):
                act.wait_ge(loaded, LOADED)
                for dst, src in weights:
                    act.dma_start(dst, src).then_inc(weights_in, 16)
                with act.Fori(0, B) as b:
                    root(nc, act, z, b)
                    act.wait_ge(z.psum_ready, b + 1)
                    copy_transposed(nc, bank, z.xT, z.xT_ready, *((ln[:, 0, :], ln[:, 1, :]) if k == 2 else ()))
                if k == 2:
                    act.wait_ge(gap_ready, 1)
                    nc.scalar.activation(share[:, 1, :], share[:, 1, :], ACT.Exp).then_inc(exp_ready, 1)

            @block.tensor
            def _(pe):
                pe.wait_ge(loaded, LOADED)
                pe.wait_ge(set_up, 1)
                with pe.Fori(0, B) as b:
                    pe.wait_ge(z.xn_ready, b * TB + TB)
                    transpose_rows(nc, pe, lambda s, c: z.xn[:, s, c * CH:(c + 1) * CH], ident, bank, z.psum_ready)
                    pe.wait_ge(z.xT_ready, b * COPIES + COPIES)
                    pe.wait_ge(logits_ready, b + 1)
                    for s in range(TB):
                        out = bank[:, LOGITS, s * E:(s + 1) * E]
                        for c in range(2):
                            ins = nc.tensor.matmul(out, z.xT[:, c, s * P:(s + 1) * P], wr[:, c, :], start=(c == 0), stop=(k == 2 and c == 1))
                        if k == 1:
                            ins = nc.tensor.matmul(out, ones[0:1, :], br[:, :], start=False, stop=True)
                    ins.then_inc(logits_psum, 1)
                pe.wait_ge(chosen_ready, 1)
                mask = either[:, :, :].rearrange("p t e -> p (t e)")
                nc.tensor.matmul(bank[:, EARLIER, 0:TILES * E], earlier[:, :], mask, start=True, stop=True)
                nc.tensor.matmul(bank[:, TOTAL, 0:TILES * E], ones[:, :], mask, start=True, stop=True).then_inc(counted, 1)


def always(d):
    return True


def run_slots(nc, name, k, table, x_rows, y_rows, w1, w2, b2, ones_row, weights_in, ident, ln):
    slots = slots_for(k)
    rows = CH if k == 2 else CH + 1
    with Memory(nc, f"{name}_slots") as m:
        x = m.sbuf("x", [P, 2, C])
        xT = m.sbuf("xT", [CH + 1, 2, 2, P])
        hidden = m.sbuf("hidden", [P, 2, FF])
        hT = m.sbuf("hT", [P, 2, FFT, P])
        y = m.sbuf("y", [P, 2, C])
        bank = m.psum("bank", [P, 8, 512])
        UP, HT, OUT, XT = (0, 2), 4, 6, 7
        (ones_ready, xT_psum, xT_ready, up_psum, hidden_ready, hT_psum, hT_ready, y_psum, y_ready) = m.sems(
            *"ones_ready xT_psum xT_ready up_psum hidden_ready hT_psum hT_ready y_psum y_ready".split())
        x_in = m.sems("x_in0", "x_in1")
        y_stored = m.sems("y_stored0", "y_stored1")

        def by_slot(dram, i):
            return dram[bass.ds(i * P, P), :]

        def turns(eng, turn):
            def pair(p):
                for c in range(2):
                    i = p * 2 + c
                    turn(i, c, p, lambda d: 0 <= i + d < slots)

            pair(0)
            with eng.Fori(1, slots // 2 - 1) as p:
                for c in range(2):
                    turn(p * 2 + c, c, p, always)
            pair(slots // 2 - 1)
            pair(slots // 2)

        with nc.Block() as block:

            @block.sync
            def _(sp):
                def turn(i, c, p, exists):
                    if exists(0) and exists(2):
                        sp.wait_ge(xT_psum, i + 1)
                        sp.dma_start(x[:, c, :], by_slot(x_rows, i + 2)).then_inc(x_in[c], 16)
                    if exists(-2):
                        sp.wait_ge(y_ready, i)
                        sp.dma_start(by_slot(y_rows, i - 2), y[:, c, :]).then_inc(y_stored[c], 16)

                for c in range(2):
                    sp.dma_start(x[:, c, :], by_slot(x_rows, c)).then_inc(x_in[c], 16)
                turns(sp, turn)
                for c in range(2):
                    sp.wait_ge(y_stored[c], 16 * (slots // 2) + 16)

            @block.gpsimd
            def _(pool):
                nc.gpsimd.memset(xT[CH:CH + 1, :, :, :], 1.0).then_inc(ones_ready, 1)

            @block.vector
            def _(dve):
                for c in range(2):
                    dve.sem_inc(y_stored[c], 16)
                dve.sem_inc(y_ready, 1)

                def turn(i, c, p, exists):
                    if exists(-1):
                        dve.wait_ge(hT_psum, i)
                        for at, n in ((0, 4), (4, FFT - 4)):
                            nc.vector.tensor_copy(hT[:, 1 - c, at:at + n, :],
                                                  bank[:, HT + at // 4, 0:n * P].rearrange("p (f t) -> p f t", t=P)).then_inc(hT_ready, 1)
                    if exists(-2):
                        dve.wait_ge(y_psum, i - 1)
                        dve.wait_ge(y_stored[c], p * 16)
                        nc.vector.tensor_copy(y[:, c, :], bank[:, OUT, 0:C]).then_inc(y_ready, 1)

                turns(dve, turn)

            @block.scalar
            def _(act):
                def rows_in(i, c):
                    act.wait_ge(xT_psum, i + 1)
                    for half in range(2):
                        src, dst = bank[0:CH, XT, half * P:(half + 1) * P], xT[0:CH, c, half, :]
                        if k == 2:
                            ins = nc.scalar.activation(dst, src, ACT.Identity, scale=ln[:, 0, half:half + 1], bias=ln[:, 1, half:half + 1])
                        else:
                            ins = nc.scalar.activation(dst, src, ACT.Copy)
                        ins.then_inc(xT_ready, 1)

                def turn(i, c, p, exists):
                    if exists(0):
                        for part in range(2):
                            act.wait_ge(up_psum, i * 2 + part + 1)
                            nc.scalar.activation(hidden[:, c, part * WIDE:(part + 1) * WIDE], bank[:, UP[c] + part, 0:WIDE],
                                                 ACT.Gelu).then_inc(hidden_ready, 1)
                    if exists(1):
                        rows_in(i + 1, 1 - c)

                rows_in(0, 0)
                turns(act, turn)

            @block.tensor
            def _(pe):
                def transpose_x(i, c, p):
                    pe.wait_ge(x_in[c], p * 16 + 16)
                    for half in range(2):
                        ins = nc.tensor.transpose(bank[0:CH, XT, half * P:(half + 1) * P], x[:, c, half * CH:(half + 1) * CH], ident[:, :])
                    ins.then_inc(xT_psum, 1)

                def widen(i, c, e):
                    pe.wait_ge(xT_ready, i * 2 + 2)
                    for part in range(2):
                        for half in range(2):
                            n = rows if half else CH
                            weights = w1[0:n, bass.ds(e, 1), half, part * WIDE:(part + 1) * WIDE].rearrange("p o f -> p (o f)")
                            ins = nc.tensor.matmul(bank[:, UP[c] + part, 0:WIDE], xT[0:n, c, half, :], weights, start=(half == 0), stop=(half == 1))
                        ins.then_inc(up_psum, 1)

                def transpose_hidden(c):
                    for f in range(FFT):
                        ins = nc.tensor.transpose(bank[:, HT + f // 4, (f % 4) * P:(f % 4 + 1) * P], hidden[:, c, f * P:(f + 1) * P], ident[:, :])
                    ins.then_inc(hT_psum, 1)

                def narrow(c, e):
                    for f in range(FFT):
                        ins = nc.tensor.matmul(bank[:, OUT, 0:C], hT[:, c, f, :], w2[:, bass.ds(e, 1), f, :].rearrange("p o c -> p (o c)"),
                                               start=(f == 0), stop=(k == 2 and f == FFT - 1))
                    if k == 1:
                        ins = nc.tensor.matmul(bank[:, OUT, 0:C], ones_row[:, :], b2[:, bass.ds(e, 1), :].rearrange("p o c -> p (o c)"),
                                               start=False, stop=True)
                    ins.then_inc(y_psum, 1)

                experts = []

                def turn(i, c, p, exists):
                    if c == 0:
                        n = 4 if exists(0) else 2
                        entries = table[0:1, bass.ds(i, n)] if exists is always else table[0:1, i:i + n]
                        _, experts[:] = nc.values_load_multi_w_load_instructions(entries, engines=[mybir.EngineType.PE], min_val=0, max_val=E - 1)
                    if exists(0):
                        widen(i, c, experts[2 + c])
                        if exists(1):
                            transpose_x(i + 1, 1 - c, p + c)
                    if exists(-1):
                        if exists(-2):
                            pe.wait_ge(hT_ready, i * 2 - 2)
                        pe.wait_ge(hidden_ready, i * 2)
                        transpose_hidden(1 - c)
                    if exists(-2):
                        if not exists(-1):
                            pe.wait_ge(hT_ready, i * 2 - 2)
                        pe.wait_ge(y_ready, i - 1)
                        narrow(c, experts[c])

                pe.wait_ge(*weights_in)
                pe.wait_ge(ones_ready, 1)
                transpose_x(0, 0, 0)
                turns(pe, turn)


def combine(nc, name, k, h, x1, where, share, y_rows):
    with Memory(nc, f"{name}_combine") as m:
        found = m.sbuf("found", [P, B, k, TB, C])
        base_ready, added = m.sems("base_ready", "added")
        found_in = m.sems(*(f"found_in{b}" for b in range(B)))
        with nc.Block() as block:

            @block.gpsimd
            def _(pool):
                for b in range(B):
                    for j in range(k):
                        for s in range(TB):
                            nc.gpsimd.indirect_dma_start(out=found[:, b, j, s, :], out_offset=None, in_=y_rows,
                                                         in_offset=bass.IndirectOffsetOnAxis(ap=where[:, j, b * TB + s:b * TB + s + 1], axis=0),
                                                         ).then_inc(found_in[b], 16)

            @block.vector
            def _(dve):
                done = InOrder(dve, added)
                for b in range(B):
                    rows = h[:, b * TB:(b + 1) * TB, :]
                    if k == 2:
                        done.step(nc.vector.tensor_tensor(rows, rows, x1[:, b * TB:(b + 1) * TB, :], ALU.add))
                    dve.wait_ge(found_in[b], 16 * k * TB)
                    if k == 1:
                        done.step(nc.vector.tensor_tensor(rows, rows, found[:, b, 0, :, :], ALU.add))
                        continue
                    for j in range(k):
                        for s in range(TB):
                            t = b * TB + s
                            done.count(nc.vector.scalar_tensor_tensor(h[:, t, :], found[:, b, j, s, :], share[:, j, t:t + 1], h[:, t, :],
                                                                      ALU.mult, ALU.add))
                        done.wait()


def experts(nc, h, x1, ident, io, top2):
    name, k = ("moe", 2) if top2 else ("ffn", 1)
    slots = slots_for(k)
    x_rows, y_rows = (nc.dram_tensor(f"{name}_{r}_rows", (slots * P, C), F32, kind="Internal").ap() for r in ("x", "y"))
    with Memory(nc, name) as m:
        where = m.sbuf("where", [P, k, TILES], I32)
        share = m.sbuf("share", [P, k, TILES])
        table = m.sbuf("table", [1, slots + 2], I32)
        w1 = m.sbuf("w1", [CH + 1, E, 2, FF])
        w2 = m.sbuf("w2", [P, E, FFT, C])
        b2 = m.sbuf("b2", [1, E, C])
        ones_row = m.sbuf("ones_row", [1, P])
        ln = m.sbuf("ln_gb", [CH, 2, 2])
        weights_in, ones_set = m.sems("weights_in", "ones_set")
        weights = [(w1[0:CH, e, :, :], io[f"{name}_w1"][e]) for e in range(E)] + [(w2[:, e, :, :], io[f"{name}_w2"][e]) for e in range(E)]
        if k == 1:
            weights += [(w1[CH:CH + 1, :, 1, :], io["ffn_b1"]), (b2[:, :, :], io["ffn_b2"])]
        with nc.Block() as block:

            @block.sync
            def _(sp):
                if k == 2:
                    sp.dma_start(ln[:, :, :], io["moe_ln"]).then_inc(ones_set, 16)
                    sp.wait_ge(ones_set, 16)

            @block.vector
            def _(dve):
                nc.vector.memset(ones_row[:, :], 1.0)
        with Memory(nc, f"{name}_rows") as n:
            xn = n.sbuf("xn", [P, TILES, C])
            route_tokens(nc, name, k, x1 if top2 else h, xn, where, share, table, x_rows, weights, weights_in, ident, ln, io)
        run_slots(nc, name, k, table, x_rows, y_rows, w1, w2, b2, ones_row, (weights_in, 16 * len(weights)), ident, ln)
        combine(nc, name, k, h, x1, where, share, y_rows)


CK = 16
NC = N // CK
CB = GH * CK
WIDTH = 6
EACH = 16
STREAMS = 2 * B
PATHS = 5
SIDE = C + H + H * PATHS
SHORT, LONG = 3, 7
PAD = LONG - 1
MIX_ITEMS = 4 + TB + TB + 4 + TB + TB + 1


def mix_paths(nc, h, part, delta_weight, kq, k_rows, v_rows, ident, io):
    with Memory(nc, "mix") as m:
        z = Normed(m, "ln")
        wq = m.sbuf("wq", [CH, 2, C])
        wkv = m.sbuf("wkv", [CH, 2, 2 * C])
        wside = m.sbuf("wside", [CH, 2, SIDE])
        bside = m.sbuf("bside", [1, SIDE])
        wg1 = m.sbuf("wg1", [CH, 2, C])
        bg1 = m.sbuf("bg1", [CH, 2])
        wg2 = m.sbuf("wg2", [CH, 2, H])
        bg2 = m.sbuf("bg2", [1, H])
        static = m.sbuf("static", [P, H])
        taps = m.sbuf("taps", [CH, 2, SHORT + LONG])
        mixer = m.sbuf("mixer", [CH, 2, C])
        same_dim = m.sbuf("same_dim", [CH, 2, C])
        same = m.sbuf("same", [CH, 2, C])
        ones = m.sbuf("ones", [1, P])
        kv = m.sbuf("kv", [P, TB, 2 * C])
        squares = m.sbuf("squares", [P, TB, C])
        norm = m.sbuf("norm", [P, TB, H])
        unit = m.sbuf("unit", [P, TB, C])
        side = m.sbuf("side", [P, TB, SIDE])
        vT = m.sbuf("vT", [CH, 2, PAD + N])
        fir = m.sbuf("fir", [CH, 2, 2, N])
        mixed = m.sbuf("mixed", [P, TB, 2, C])
        hidden = m.sbuf("hidden", [CH, 2, N])
        top = m.sbuf("top", [P, TB, H])
        weights = m.sbuf("weights", [P, TB, H, PATHS])
        total = m.sbuf("total", [P, TB, H])
        dyn = m.sbuf("dyn", [P, TB, H])
        gate = m.sbuf("gate", [P, TB, H])
        term = m.sbuf("term", [P, TB, C])
        sum_ = m.sbuf("sum", [P, TB, C])
        bank = m.psum("bank", [P, 8, 512])
        act_banks, banks = (0, 1, 2), (3, 4, 5, 6, 7)
        (loaded, set_up, mixer_ready, static_ready, filled, taken, act_filled, act_taken, norm2_ready, norm_ready, unit_ready,
         side_ready, dyn_ready, gap_ready, exp_ready, fir_ready, gate_raw, gate_ready, rows_stored, part_ready,
         dve_own) = m.sems(*(
             "loaded set_up mixer_ready static_ready filled taken act_filled act_taken norm2_ready norm_ready unit_ready "
             "side_ready dyn_ready gap_ready exp_ready fir_ready gate_raw gate_ready rows_stored part_ready dve_own").split())
        pairs = ((wq, io["mix_wq"]), (wkv, io["mix_wkv"]), (wside, io["mix_wside"]), (bside, io["mix_bside"]), (wg1, io["mix_wg1"]),
                 (bg1, io["mix_bg1"]), (wg2, io["mix_wg2"]), (bg2, io["mix_bg2"]), (static, io["mix_static"]), (taps, io["mix_taps"]),
                 (mixer, io["mix_mixer"]), (same_dim, io["same_dim"]), (same, io["same"]))
        LOADED = 16 * len(pairs)

        def heads(ap):
            return ap.rearrange("p s (h d) -> p s h d", h=H)

        def per_head(ap):
            return ap.unsqueeze(3).to_broadcast([P, TB, H, D])

        def weight(p):
            return weights[:, :, :, p]

        with nc.Block() as block:

            @block.sync
            def _(sp):
                load(sp, pairs, loaded)
                with sp.Fori(0, B) as b:
                    sp.wait_ge(unit_ready, b + 1)
                    sp.wait_ge(taken, b * MIX_ITEMS + len(banks) + 4 + TB)
                    for dram, buf in ((k_rows, unit[:, :, :]), (v_rows, kv[:, :, C:])):
                        sp.dma_start(dram[bass.ds(b * N, N), :].rearrange("(s p) c -> p s c", p=P), buf).then_inc(rows_stored, 16)
                sp.wait_ge(rows_stored, 32 * B + 32)

            @block.gpsimd
            def _(pool):
                pool.sem_inc(rows_stored, 32)
                nc.gpsimd.memset(vT[:, :, 0:PAD], 0.0).then_inc(set_up, 1)
                nc.gpsimd.memset(ones[:, :], 1.0).then_inc(set_up, 1)

            @block.vector
            def _(dve):
                setup = InOrder(dve, mixer_ready)
                dve.sem_inc(taken, len(banks))
                dve.sem_inc(part_ready, 1)
                dve.wait_ge(loaded, LOADED)
                setup.step(nc.vector.tensor_tensor(mixer[:, :, :], mixer[:, :, :], same_dim[:, :, :], ALU.mult))
                setup.step(nc.vector.tensor_tensor(mixer[:, :, :], mixer[:, :, :], same[:, :, :], ALU.add))
                dve.wait_ge(set_up, 2)
                dve.wait_ge(static_ready, 1)
                own = InOrder(dve, dve_own, MIX_DVE_STEPS)
                ring = Ring(dve, banks, filled, taken, MIX_ITEMS)
                with dve.Fori(0, B) as b:
                    own.turn(b)
                    ring.turn(b)
                    norm_rows(nc, dve, own, z, lambda s: h[:, b * TB + s, :], b)
                    for half in range(2):
                        for c in range(2):
                            slot = ring.get()
                            dst = kq[:, half, b, c * NC // 2:(c + 1) * NC // 2, CK:]
                            ring.take(nc.vector.tensor_scalar(dst, bank[0:CH, slot, 0:HALF].rearrange("p (c t) -> p c t", t=CK),
                                                              float(D) ** -0.5, None, ALU.mult))
                    dve.wait_ge(rows_stored, b * 32 + 32)
                    for s in range(TB):
                        slot = ring.get()
                        ring.take(nc.vector.tensor_copy(kv[:, s, :], bank[:, slot, 0:2 * C]))
                    ring.done()
                    own.step(nc.vector.tensor_tensor(squares[:, :, :], kv[:, :, 0:C], kv[:, :, 0:C], ALU.mult))
                    nc.vector.tensor_reduce(norm[:, :, :], heads(squares[:, :, :]), AX.X, ALU.add).then_inc(norm2_ready, 1)
                    for s in range(TB):
                        slot = ring.get()
                        ring.take(nc.vector.tensor_copy(side[:, s, :], bank[:, slot, 0:SIDE]))
                    ring.done()
                    dve.wait_ge(norm_ready, b + 1)
                    own.step(nc.vector.tensor_scalar(norm[:, :, :], norm[:, :, :], 1e-6, None, ALU.add))
                    own.step(nc.vector.reciprocal(norm[:, :, :], norm[:, :, :]))
                    nc.vector.tensor_tensor(heads(unit[:, :, :]), heads(kv[:, :, 0:C]), per_head(norm[:, :, :]),
                                            ALU.mult).then_inc(unit_ready, 1)
                    logits = side[:, :, C + H:].rearrange("p s (h q) -> p s h q", q=PATHS)
                    own.step(nc.vector.tensor_reduce(top[:, :, :], logits, AX.X, ALU.max))
                    nc.vector.tensor_tensor(weights[:, :, :, :], logits, top[:, :, :].unsqueeze(3).to_broadcast([P, TB, H, PATHS]),
                                            ALU.subtract).then_inc(gap_ready, 1)
                    for half in range(2):
                        for c in range(2):
                            slot = ring.get()
                            ring.take(nc.vector.tensor_copy(vT[:, half, PAD + c * HALF:PAD + (c + 1) * HALF], bank[0:CH, slot, 0:HALF]))
                    ring.done()
                    for half in range(2):
                        for which, first, n_taps in ((0, 0, SHORT), (1, SHORT, LONG)):
                            dst = fir[:, which, half, :]
                            for k in range(n_taps):
                                at = PAD - (n_taps - 1) + k
                                src, tap = vT[:, half, at:at + N], taps[:, half, first + k:first + k + 1]
                                if k == 0:
                                    own.step(nc.vector.tensor_scalar(dst, src, tap, None, ALU.mult))
                                elif k < n_taps - 1:
                                    own.step(nc.vector.scalar_tensor_tensor(dst, src, tap, dst, ALU.mult, ALU.add))
                                else:
                                    nc.vector.scalar_tensor_tensor(dst, src, tap, dst, ALU.mult, ALU.add).then_inc(fir_ready, 1)
                    for s in range(TB):
                        slot = ring.get()
                        ring.take(nc.vector.tensor_copy(kq[:, :, b, s * P // CK:(s + 1) * P // CK, 0:CK],
                                                        bank[0:CH, slot, 0:2 * P].rearrange("p (z c t) -> p z c t", z=2, t=CK)))
                    slot = ring.get()
                    ring.take(nc.vector.tensor_copy(gate[:, :, :], bank[:, slot, 0:TB * H].rearrange("p (s h) -> p s h", s=TB)))
                    dve.wait_ge(exp_ready, b + 1)
                    own.step(nc.vector.tensor_reduce(total[:, :, :], weights[:, :, :, :], AX.X, ALU.add))
                    own.step(nc.vector.reciprocal(total[:, :, :], total[:, :, :]))
                    dve.wait_ge(gate_ready, b + 1)
                    own.step(nc.vector.tensor_tensor(total[:, :, :], total[:, :, :], gate[:, :, :], ALU.mult))
                    own.step(nc.vector.tensor_tensor(weights[:, :, :, :], weights[:, :, :, :],
                                                     total[:, :, :].unsqueeze(3).to_broadcast([P, TB, H, PATHS]), ALU.mult))
                    own.count(nc.vector.tensor_copy(delta_weight[:, bass.ds(b * TB, TB), :], weight(2)))
                    dve.wait_ge(dyn_ready, b + 1)
                    own.step(nc.vector.tensor_tensor(dyn[:, :, :], dyn[:, :, :], static[:, :].unsqueeze(1).to_broadcast([P, TB, H]), ALU.mult))
                    own.step(nc.vector.tensor_tensor(dyn[:, :, :], dyn[:, :, :], weight(4), ALU.mult))
                    own.count(nc.vector.tensor_tensor(heads(sum_[:, :, :]), heads(kv[:, :, C:]), per_head(weight(3)), ALU.mult))
                    own.step(nc.vector.tensor_tensor(heads(term[:, :, :]), heads(side[:, :, 0:C]), per_head(dyn[:, :, :]), ALU.mult))
                    own.step(nc.vector.tensor_tensor(sum_[:, :, :], sum_[:, :, :], term[:, :, :], ALU.add))
                    for s in range(TB):
                        slot = ring.get()
                        ring.take(nc.vector.tensor_copy(mixed[:, s, :, :], bank[:, slot, 0:2 * C].rearrange("p (w c) -> p w c", w=2)))
                    ring.done()
                    for which in range(2):
                        own.step(nc.vector.tensor_tensor(heads(term[:, :, :]), heads(mixed[:, :, which, :]), per_head(weight(which)), ALU.mult))
                        if which == 0:
                            own.step(nc.vector.tensor_tensor(sum_[:, :, :], sum_[:, :, :], term[:, :, :], ALU.add))
                    own.step(nc.vector.tensor_tensor(part[:, bass.ds(b * TB, TB), :], sum_[:, :, :], term[:, :, :], ALU.add))
                    ring.ended()
                    own.ended()

            @block.scalar
            def _(act):
                ring = Ring(act, act_banks, act_filled, act_taken, 4)
                act.sem_inc(act_taken, len(act_banks))
                act.wait_ge(loaded, LOADED)
                nc.scalar.activation(static[:, :], static[:, :], ACT.Sigmoid).then_inc(static_ready, 1)
                with act.Fori(0, B) as b:
                    ring.turn(b)
                    root(nc, act, z, b)
                    act.wait_ge(z.psum_ready, b + 1)
                    copy_transposed(nc, bank, z.xT, z.xT_ready)
                    act.wait_ge(norm2_ready, b + 1)
                    nc.scalar.activation(norm[:, :, :], norm[:, :, :], ACT.Sqrt).then_inc(norm_ready, 1)
                    for half in range(2):
                        for c in range(2):
                            slot = ring.get()
                            ring.take(nc.scalar.activation(hidden[:, half, c * HALF:(c + 1) * HALF], bank[0:CH, slot, 0:HALF],
                                                           ACT.Gelu_apprx_tanh, bias=bg1[:, half:half + 1]))
                    act.wait_ge(gap_ready, b + 1)
                    nc.scalar.activation(weights[:, :, :, :], weights[:, :, :, :], ACT.Exp).then_inc(exp_ready, 1)
                    nc.scalar.activation(dyn[:, :, :], side[:, :, C:C + H], ACT.Sigmoid).then_inc(dyn_ready, 1)
                    act.wait_ge(taken, b * MIX_ITEMS + len(banks) + 4 + TB + TB + 4 + TB + 1)
                    nc.scalar.activation(gate[:, :, :], gate[:, :, :], ACT.Sigmoid).then_inc(gate_ready, 1)
                    ring.ended()

            @block.tensor
            def _(pe):
                ring = Ring(pe, banks, filled, taken, MIX_ITEMS)
                up = Ring(pe, act_banks, act_filled, act_taken, 4)
                pe.wait_ge(loaded, LOADED)
                pe.wait_ge(set_up, 2)
                pe.wait_ge(mixer_ready, 2)

                def columns(ring, w, at, rows, half_tokens):
                    slot = ring.free()
                    for k in range(2):
                        ins = nc.tensor.matmul(bank[0:rows, slot, 0:HALF], w[:, k, at:at + rows],
                                               z.xT[:, k, half_tokens * HALF:(half_tokens + 1) * HALF], start=(k == 0), stop=(k == 1))
                    ring.fill(ins)

                with pe.Fori(0, B) as b:
                    ring.turn(b)
                    up.turn(b)
                    pe.wait_ge(z.xn_ready, b * TB + TB)
                    transpose_rows(nc, pe, lambda s, k: z.xn[:, s, k * CH:(k + 1) * CH], ident, bank, z.psum_ready)
                    pe.wait_ge(z.xT_ready, b * COPIES + COPIES)
                    for half in range(2):
                        for c in range(2):
                            columns(ring, wq, half * CH, CH, c)
                    for s in range(TB):
                        slot = ring.free()
                        for k in range(2):
                            ins = nc.tensor.matmul(bank[:, slot, 0:2 * C], z.xT[:, k, s * P:(s + 1) * P], wkv[:, k, :], start=(k == 0), stop=(k == 1))
                        ring.fill(ins)
                    for s in range(TB):
                        slot = ring.free()
                        for k in range(2):
                            nc.tensor.matmul(bank[:, slot, 0:SIDE], z.xT[:, k, s * P:(s + 1) * P], wside[:, k, :], start=(k == 0), stop=False)
                        ring.fill(nc.tensor.matmul(bank[:, slot, 0:SIDE], ones[:, :], bside[:, :], start=False, stop=True))
                    for half in range(2):
                        for c in range(2):
                            columns(up, wg1, half * CH, CH, c)
                    for half in range(2):
                        for c in range(2):
                            columns(ring, wkv, C + half * CH, CH, c)
                    pe.wait_ge(unit_ready, b + 1)
                    for s in range(TB):
                        slot = ring.free()
                        for k in range(2):
                            ins = nc.tensor.transpose(bank[0:CH, slot, k * P:(k + 1) * P], unit[:, s, k * CH:(k + 1) * CH], ident[:, :])
                        ring.fill(ins)
                    up.arrived()
                    slot = ring.free()
                    for s in range(TB):
                        for k in range(2):
                            nc.tensor.matmul(bank[:, slot, s * H:(s + 1) * H], hidden[:, k, s * P:(s + 1) * P], wg2[:, k, :], start=(k == 0), stop=False)
                        ins = nc.tensor.matmul(bank[:, slot, s * H:(s + 1) * H], ones[:, :], bg2[:, :], start=False, stop=True)
                    ring.fill(ins)
                    pe.wait_ge(fir_ready, b * 4 + 4)
                    for s in range(TB):
                        slot = ring.free()
                        for which in range(2):
                            for k in range(2):
                                ins = nc.tensor.matmul(bank[:, slot, which * C:(which + 1) * C], fir[:, which, k, s * P:(s + 1) * P],
                                                       mixer[:, k, :], start=(k == 0), stop=(k == 1))
                        ring.fill(ins)
                    ring.ended()
                    up.ended()


MIX_DVE_STEPS = 46


def chunk_products(nc, kq, grams, reads, keys, values, k_rows, v_rows, mask, upto, g_dram, tt_dram):
    GROUPS = STREAMS * NC // EACH
    with Memory(nc, "gram") as m:
        k_block = m.sbuf("k_block", [CB, 2, STREAMS, GH, CK])
        a = m.sbuf("a", [GH * GROUPS, CK, EACH, CK])
        tt = m.sbuf("tt", [GH * GROUPS, CK, EACH, CK])
        product = m.sbuf("product", [GH * GROUPS, EACH, CK, CK])
        bank = m.psum("bank", [CB, 4, 512])
        (rows_in, even_ready, odd_ready, filled, taken, stored, a_in, zeroed, solved, back, dve_own) = m.sems(
            *"rows_in even_ready odd_ready filled taken stored a_in zeroed solved back dve_own".split())
        with nc.Block() as block:

            def of_step(step, at):
                return bank[:, step * 2:step * 2 + 2, 0:B * 6 * CK].rearrange("p z (n c) -> p z n c", n=B)[:, :, :, at * 2 * CK:(at + 1) * 2 * CK]

            def k_blocks(eng, step, c):
                return eng.tensor_tensor(k_block[:, c, :, :, :], kq[:, :, step, 0:CK].unsqueeze(2).to_broadcast([CB, STREAMS, GH, CK]),
                                         mask[:, :].unsqueeze(2).unsqueeze(1).to_broadcast([CB, STREAMS, GH, CK]), ALU.mult)

            def halves(ap):
                return ap.rearrange("p (z n) c -> p z n c", z=2)

            @block.vector
            def _(dve):
                def copy_out(step, c, at):
                    dve.wait_ge(filled, step + 1)
                    got = of_step(c, at)
                    nc.vector.tensor_copy(halves(grams[:, :, step, :]), got[:, :, :, 0:CK]).then_inc(taken, 1)
                    nc.vector.tensor_tensor(halves(reads[:, :, step, :]), got[:, :, :, CK:],
                                            upto[:, :].unsqueeze(1).unsqueeze(1).to_broadcast([CB, 2, B, CK]), ALU.mult).then_inc(taken, 1)

                k_blocks(nc.vector, 1, 1).then_inc(odd_ready, 1)
                copy_out(0, 0, 0)
                copy_out(1, 1, 1)
                with dve.Fori(1, NC // 2) as cc:
                    k_blocks(nc.vector, cc * 2 + 1, 1).then_inc(odd_ready, 1)
                    for c in range(2):
                        copy_out(cc * 2 + c, c, 2)
                own = InOrder(dve, dve_own)
                own.step(nc.vector.memset(tt[:, :, :, :], 0.0))
                for i in range(CK):
                    own.count(nc.vector.memset(tt[:, i, :, i], 1.0))
                own.wait()
                dve.wait_ge(a_in, 16 * GH)
                by_system = tt[:, :, :, :].rearrange("p m e t -> p e m t")
                for i in range(1, CK):
                    own.step(nc.vector.tensor_tensor(product[:, :, 0:i, 0:i], a[:, i, :, 0:i].unsqueeze(2).to_broadcast([GH * GROUPS, EACH, i, i]),
                                                     by_system[:, :, 0:i, 0:i], ALU.mult))
                    last = nc.vector.tensor_reduce(by_system[:, :, 0:i, i], product[:, :, 0:i, 0:i], AX.X, ALU.add, negate=True)
                    if i < CK - 1:
                        own.step(last)
                    else:
                        last.then_inc(solved, 1)

            @block.gpsimd
            def _(pool):
                k_blocks(nc.gpsimd, 0, 0).then_inc(even_ready, 1)
                with pool.Fori(1, NC // 2) as cc:
                    pool.wait_ge(filled, cc * 2 - 1)
                    k_blocks(nc.gpsimd, cc * 2, 0).then_inc(even_ready, 1)

            @block.tensor
            def _(pe):
                def products(step, c, first):
                    for n in range(STREAMS):
                        ins = nc.tensor.matmul(bank[:, c * 2 + n // B, (n % B) * 6 * CK:(n % B + 1) * 6 * CK],
                                               k_block[:, c, n, :, :].rearrange("p h t -> p (h t)"),
                                               kq[:, n, bass.ds(first, 3), :].rearrange("p c t -> p (c t)"), start=True, stop=True)
                    ins.then_inc(filled, 1)

                pe.wait_ge(even_ready, 1)
                products(0, 0, 0)
                pe.wait_ge(odd_ready, 1)
                products(1, 1, 0)
                with pe.Fori(1, NC // 2) as cc:
                    for c, ready in ((0, even_ready), (1, odd_ready)):
                        pe.wait_ge(ready, cc + 1)
                        pe.wait_ge(taken, cc * 4 + c * 2 - 2)
                        products(cc * 2 + c, c, cc * 2 + c - 2)

            @block.sync
            def _(sp):
                def by_row(dram):
                    return dram.rearrange("h i s j -> (h i) (s j)")

                def by_system(buf, dram, g):
                    return buf[g * GROUPS:(g + 1) * GROUPS].rearrange("p i e j -> p i (e j)"), dram[g].rearrange("i (p e) j -> p i (e j)", p=GROUPS)

                sp.wait_ge(taken, NC * 2)
                flat = grams[:, :, :, :].rearrange("p n c j -> p (n c j)")
                sp.dma_start(by_row(g_dram), flat).then_inc(stored, 16)
                sp.wait_ge(stored, 16)
                for g in range(GH):
                    dst, src = by_system(a, g_dram, g)
                    sp.dma_start(dst, src).then_inc(a_in, 16)
                sp.wait_ge(solved, 1)
                for g in range(GH):
                    src, dst = by_system(tt, tt_dram, g)
                    sp.dma_start(dst, src).then_inc(stored, 16)
                sp.wait_ge(stored, 16 * GH + 16)
                sp.dma_start(flat, by_row(tt_dram)).then_inc(back, 16)
                sp.wait_ge(back, 16)

            @block.scalar
            def _(act):
                for dram, buf in ((k_rows, keys), (v_rows, values)):
                    for half in range(2):
                        for g in range(GH):
                            act.dma_start(buf[g * CK:(g + 1) * CK, half * B:(half + 1) * B, :, :].rearrange("p b c e -> p (b c) e"),
                                          chunk_rows(dram, half, g)).then_inc(rows_in, 16)
                act.wait_ge(rows_in, 16 * 2 * H)


def chunk_rows(dram, half, g):
    at = half * CH + g * D
    return dram.rearrange("(n t) c -> t n c", t=CK)[:, :, at:at + D]


def delta_rule(nc, kq, tt, reads, keys, values, o_rows, mask):
    with Memory(nc, "delta") as m:
        state = m.sbuf("state", [CB, 2, WIDTH, CK])
        resid = m.sbuf("resid", [CB, 2, WIDTH, CK])
        update = m.sbuf("update", [CB, 2, WIDTH, CK])
        K_T, T_T, Q_T, R_T, K = range(5)
        blocks = [m.sbuf(f"block{i}", [CB, 2, STREAMS, GH, CK]) for i in range(5)]
        bank = m.psum("bank", [CB, 8, 512])
        (blocks_dve, blocks_pool, zeroed, ks_psum, resid_ready, u_psum, u_ready, s_psum, s_ready, o_psum, o_taken,
         o_stored) = m.sems(*("blocks_dve blocks_pool zeroed ks_psum resid_ready u_psum u_ready s_psum s_ready "
                              "o_psum o_taken o_stored").split())
        KS, U, SB, O = 0, 2, 4, 6

        def part(z):
            return slice(z * B, (z + 1) * B)

        def own_columns(slot):
            return bank[:, slot, 0:B * (WIDTH + 1) * CK].rearrange("p (b e) -> p b e", b=B)[:, :, 0:CK]

        def spread(ap):
            return ap.unsqueeze(2).to_broadcast([CB, STREAMS, GH, CK])

        masks = mask[:, :].unsqueeze(2).unsqueeze(1).to_broadcast([CB, STREAMS, GH, CK])

        def operands(i, c):
            return {K_T: kq[:, :, c, 0:CK], T_T: tt[:, :, c, :], Q_T: kq[:, :, c, CK:], R_T: reads[:, :, c, :], K: keys[:, :, c, :]}[i]

        with nc.Block() as block:

            @block.sync
            def _(sp):
                sp.wait_ge(o_taken, 2 * NC + 2)
                for half in range(2):
                    for g in range(GH):
                        sp.dma_start(chunk_rows(o_rows, half, g),
                                     values[g * CK:(g + 1) * CK, part(half), :, :].rearrange("p b c e -> p (b c) e")).then_inc(o_stored, 16)
                sp.wait_ge(o_stored, 16 * H)

            @block.gpsimd
            def _(pool):
                for buf in (resid, update):
                    nc.gpsimd.memset(buf[:, :, :, :], 0.0).then_inc(zeroed, 1)

                def make_blocks(step, c):
                    for i in (R_T, K):
                        nc.gpsimd.tensor_tensor(blocks[i][:, c], spread(operands(i, step)), masks, ALU.mult).then_inc(blocks_pool, 1)

                for c in range(2):
                    make_blocks(c, c)
                with pool.Fori(1, NC // 2) as cc:
                    for c in range(2):
                        pool.wait_ge(s_psum, cc * 4 + c * 2 - 2)
                        make_blocks(cc * 2 + c, c)

            @block.vector
            def _(dve):
                nc.vector.memset(state[:, :, :, :], 0.0).then_inc(s_ready, 2)
                dve.wait_ge(zeroed, 2)

                def make_block(i, step, c):
                    nc.vector.tensor_tensor(blocks[i][:, c], spread(operands(i, step)), masks, ALU.mult).then_inc(blocks_dve, 1)

                def chunk(step, c, more):
                    for z in range(2):
                        dve.wait_ge(ks_psum, step * 2 + z + 1)
                        nc.vector.tensor_tensor(resid[:, z, 0:B, :], values[:, part(z), step, :], own_columns(KS + z), ALU.subtract).then_inc(resid_ready, 1)
                    for z in range(2):
                        dve.wait_ge(u_psum, step * 2 + z + 1)
                        nc.vector.tensor_copy(update[:, z, 0:B, :], own_columns(U + z)).then_inc(u_ready, 1)
                    if more:
                        make_block(K_T, step + 1, 1 - c)
                        make_block(T_T, step + 1, 1 - c)
                    for z in range(2):
                        at = step * 2 + z + 1
                        dve.wait_ge(s_psum, at)
                        dve.wait_ge(s_ready, at)
                        nc.vector.tensor_tensor(state[:, z, 0:B, :], state[:, z, 0:B, :], own_columns(SB + z), ALU.add).then_inc(s_ready, 1)
                        if z == 0 and more:
                            make_block(Q_T, step + 1, 1 - c)

                for i in (K_T, T_T, Q_T):
                    make_block(i, 0, 0)
                with dve.Fori(0, NC // 2 - 1) as cc:
                    for c in range(2):
                        chunk(cc * 2 + c, c, True)
                chunk(NC - 2, 0, True)
                chunk(NC - 1, 1, False)

            @block.scalar
            def _(act):
                act.sem_inc(o_taken, 2)
                with act.Fori(0, NC // 2) as cc:
                    for c in range(2):
                        step = cc * 2 + c
                        for z in range(2):
                            at = step * 2 + z + 1
                            act.wait_ge(o_psum, at)
                            nc.scalar.activation(values[:, part(z), step, :], own_columns(O + z), ACT.Copy).then_inc(o_taken, 1)

            @block.tensor
            def _(pe):
                def columns(buf, z):
                    return buf[:, z, :, :].rearrange("p w e -> p (w e)")

                def product(z, dst, i, c, rhs, start, stop):
                    for n in range(B):
                        ins = nc.tensor.matmul(bank[:, dst + z, n * WIDTH * CK:(n + 1) * WIDTH * CK],
                                               blocks[i][:, c, z * B + n].rearrange("p h t -> p (h t)"), columns(rhs, z), start=start, stop=stop)
                    return ins

                with pe.Fori(0, NC // 2) as cc:
                    for c in range(2):
                        step = cc * 2 + c
                        pe.wait_ge(blocks_dve, step * 3 + 3)
                        for z in range(2):
                            pe.wait_ge(s_ready, step * 2 + z + 1)
                            product(z, KS, K_T, c, state, True, True).then_inc(ks_psum, 1)
                        for z in range(2):
                            pe.wait_ge(resid_ready, step * 2 + z + 1)
                            product(z, U, T_T, c, resid, True, True).then_inc(u_psum, 1)
                        pe.wait_ge(blocks_pool, step * 2 + 2)
                        for z in range(2):
                            at = step * 2 + z + 1
                            pe.wait_ge(u_ready, at)
                            pe.wait_ge(o_taken, at)
                            for n in range(B):
                                out = bank[:, O + z, n * WIDTH * CK:(n + 1) * WIDTH * CK]
                                at_n = z * B + n
                                nc.tensor.matmul(out, blocks[Q_T][:, c, at_n].rearrange("p h t -> p (h t)"), columns(state, z), start=True, stop=False)
                                ins = nc.tensor.matmul(out, blocks[R_T][:, c, at_n].rearrange("p h t -> p (h t)"), columns(update, z), start=False, stop=True)
                            ins.then_inc(o_psum, 1)
                            product(z, SB, K, c, update, True, True).then_inc(s_psum, 1)


def project_paths(nc, h, part, delta_weight, o_rows, ident, io):
    with Memory(nc, "proj") as m:
        delta = m.sbuf("delta", [P, TILES, C])
        context = m.sbuf("context", [P, TB, C])
        cT = m.sbuf("cT", [CH, 2, N])
        wp = m.sbuf("wp", [CH, 2, C])
        bp = m.sbuf("bp", [1, C])
        ones = m.sbuf("ones", [1, P])
        bank = m.psum("bank", [P, 8, 512])
        banks = (3, 4, 5, 6, 7)
        (loaded, set_up, scaled, context_ready, cT_psum, cT_ready, filled, taken) = m.sems(
            *"loaded set_up scaled context_ready cT_psum cT_ready filled taken".split())
        pairs = ((wp, io["proj_w"]), (bp, io["proj_b"]))
        LOADED = 16 * (len(pairs) + B)
        with nc.Block() as block:

            @block.sync
            def _(sp):
                load(sp, pairs, loaded)
                for b in range(B):
                    sp.dma_start(delta[:, b * TB:(b + 1) * TB, :],
                                 o_rows[b * N:(b + 1) * N, :].rearrange("(s p) c -> p s c", p=P)).then_inc(loaded, 16)

            @block.gpsimd
            def _(pool):
                nc.gpsimd.memset(ones[:, :], 1.0).then_inc(set_up, 1)

            @block.vector
            def _(dve):
                ring = Ring(dve, banks, filled, taken, TB)
                dve.sem_inc(taken, len(banks))
                dve.wait_ge(loaded, LOADED)
                with dve.Fori(0, B) as b:
                    ring.turn(b)
                    here = bass.ds(b * TB, TB)
                    nc.vector.tensor_tensor(context[:, :, :].rearrange("p s (h d) -> p (s h) d", h=H),
                                            delta[:, here, :].rearrange("p s (h d) -> p (s h) d", h=H),
                                            delta_weight[:, here, :].rearrange("p s h -> p (s h)").unsqueeze(2).to_broadcast([P, TB * H, D]),
                                            ALU.mult).then_inc(scaled, 1)
                    dve.wait_ge(scaled, b + 1)
                    nc.vector.tensor_tensor(context[:, :, :], context[:, :, :], part[:, here, :], ALU.add).then_inc(context_ready, 1)
                    for s in range(TB):
                        slot = ring.get()
                        row = h[:, b * TB + s, :]
                        ring.take(nc.vector.tensor_tensor(row, row, bank[:, slot, 0:C], ALU.add))
                    ring.ended()

            @block.scalar
            def _(act):
                with act.Fori(0, B) as b:
                    act.wait_ge(cT_psum, b + 1)
                    copy_transposed(nc, bank, cT, cT_ready)

            @block.tensor
            def _(pe):
                ring = Ring(pe, banks, filled, taken, TB)
                pe.wait_ge(loaded, LOADED)
                pe.wait_ge(set_up, 1)
                with pe.Fori(0, B) as b:
                    ring.turn(b)
                    pe.wait_ge(context_ready, b + 1)
                    transpose_rows(nc, pe, lambda s, k: context[:, s, k * CH:(k + 1) * CH], ident, bank, cT_psum)
                    pe.wait_ge(cT_ready, b * COPIES + COPIES)
                    for s in range(TB):
                        slot = ring.free()
                        for k in range(2):
                            nc.tensor.matmul(bank[:, slot, 0:C], cT[:, k, s * P:(s + 1) * P], wp[:, k, :], start=(k == 0), stop=False)
                        ring.fill(nc.tensor.matmul(bank[:, slot, 0:C], ones[:, :], bp[:, :], start=False, stop=True))
                    ring.ended()


def delta_attention(nc, h, part, ident, io):
    scratch = {k: nc.dram_tensor(k, (B * N, C), F32, kind="Internal").ap() for k in ("k_rows", "v_rows", "o_rows")}
    systems = {k: nc.dram_tensor(k, (GH, CK, STREAMS * NC, CK), F32, kind="Internal").ap() for k in ("g_rows", "t_rows")}
    with Memory(nc, "l1") as m:
        delta_weight = m.sbuf("delta_weight", [P, TILES, H])
        kq = m.sbuf("kq", [CH, 2, B, NC, 2 * CK])
        mask = m.sbuf("mask", [CB, GH])
        upto = m.sbuf("upto", [CB, CK])
        masks_in = m.sem("masks_in")
        with nc.Block() as block:

            @block.sync
            def _(sp):
                sp.wait_ge(masks_in, load(sp, ((mask, io["head_mask"]), (upto, io["upto"])), masks_in))
        mix_paths(nc, h, part, delta_weight, kq, scratch["k_rows"], scratch["v_rows"], ident, io)
        by_stream = kq[:, :, :, :, :].rearrange("p z b c t -> p (z b) c t")
        with Memory(nc, "chunks") as n:
            grams = n.sbuf("grams", [CB, STREAMS, NC, CK])
            reads = n.sbuf("reads", [CB, STREAMS, NC, CK])
            keys = n.sbuf("keys", [CB, STREAMS, NC, CK])
            values = n.sbuf("values", [CB, STREAMS, NC, CK])
            chunk_products(nc, by_stream, grams, reads, keys, values, scratch["k_rows"], scratch["v_rows"], mask, upto,
                           systems["g_rows"], systems["t_rows"])
            delta_rule(nc, by_stream, grams, reads, keys, values, scratch["o_rows"], mask)
        project_paths(nc, h, part, delta_weight, scratch["o_rows"], ident, io)


def store(nc, h, out):
    with Memory(nc, "store") as m:
        stored = m.sem("stored")
        with nc.Block() as block:

            @block.sync
            def _(sp):
                rows = out.rearrange("b (s p) c -> p (b s) c", p=P)
                for b in range(B):
                    sp.dma_start(rows[:, b * TB:(b + 1) * TB, :], h[:, b * TB:(b + 1) * TB, :]).then_inc(stored, 16)
                sp.wait_ge(stored, 16 * B)


def program(nc, io, out):
    with Memory(nc, "all") as m:
        h = m.sbuf("h", [P, TILES, C])
        ident = m.sbuf("ident", [P, P])
        ident_in = m.sem("ident_in")
        with nc.Block() as block:

            @block.sync
            def _(sp):
                sp.dma_start(ident[:, :], io["ident"]).then_inc(ident_in, 16)
                sp.wait_ge(ident_in, 16)
        image_embedding(nc, h, io)
        text_embedding(nc, h, ident, io)
        performer(nc, h, ident, io)
        x1 = m.sbuf("x1", [P, TILES, C])
        with Memory(nc, "values") as n:
            v = n.sbuf("v", [P, TILES, H, DV])
            qk_rows = nc.dram_tensor("qk_rows", (B * 2 * PARTS, C, N), BF16, kind="Internal").ap()
            attention_operands(nc, h, x1, v, qk_rows, ident, io)
            softmax_attention(nc, x1, v, qk_rows, ident, io)
        experts(nc, h, x1, ident, io, True)
        delta_attention(nc, h, x1, ident, io)
        experts(nc, h, x1, ident, io, False)
        store(nc, h, out)


def layouts(i, np):
    a = {}
    flat = i["x"].reshape(B, NI, 3 * C).transpose(0, 2, 1)
    a["x"] = np.concatenate([flat[:, :512].reshape(B, 4, P, NI),
                             np.concatenate([flat[:, 512:], flat[:, 512:]], 1)[:, None]], 1).reshape(B * JC, P, NI)
    wt = i["L0_tok_W"].T.reshape(3 * C, 2 * BANDS, C)
    main = wt[:512].reshape(4, P, 2 * BANDS, C).transpose(1, 0, 2, 3).reshape(P, 8 * BANDS, C)
    last = np.concatenate([wt[512:, :BANDS], wt[512:, BANDS:]], 0)
    a["tok_w"] = np.concatenate([main, last], 1)
    a["freq"] = np.broadcast_to(i["L0_tok_freq_bands"], (P, BANDS))
    a["sincos_shift"] = np.stack([np.where(np.arange(P) < 64, 0.0, math.pi / 2), np.full(P, math.pi / 2)], 1).astype(np.float32)
    a["ident"] = np.eye(P, dtype=np.float32)
    a["ids"] = i["x_txt"].T
    a["emb"] = i["L0_txt_emb"]

    def halves(w):
        return w.reshape(w.shape[:-2] + (2, CH, w.shape[-1])).swapaxes(-3, -2)

    def tiles(w):
        return w.reshape(LAYERS, FT, P, -1).swapaxes(1, 2)

    a["in_proj"] = halves(i["L0_txt_in_proj_w"])
    a["norm_w"] = i["L0_txt_norm_w"].reshape(LAYERS, 2, CH).swapaxes(1, 2)
    a["txt_par"] = tiles(np.concatenate([i["L0_txt_conv_w"][:, :, 0], i["L0_txt_conv_b"][..., None], i["L0_txt_dt_proj_b"][..., None],
                                         i["L0_txt_A_log"], i["L0_txt_D"][..., None]], -1))
    w = i["L0_txt_x_proj_w"]
    a["x_proj"] = tiles(np.concatenate([w[..., RANK:]] * 3 + [w[..., :RANK]], -1))
    a["dt_proj"] = i["L0_txt_dt_proj_w"]
    a["out_proj"] = tiles(i["L0_txt_out_proj_w"])
    pick = np.zeros((3, BC, BC, P), np.float32)
    pick[:, np.arange(BC), np.arange(BC)] = 1
    pick = pick.reshape(COPIED, BC, P)
    a["pick"] = pick

    def vector(v):
        return v.reshape(2, CH).T

    def blocks(w):
        out = np.zeros((GH, D, GH, w.shape[0]), w.dtype)
        for g in range(GH):
            out[g, :, g] = w.T
        return out.reshape(CH, GH * w.shape[0])

    a["perf_w"] = halves(i["L0_attn_w_qkv"].T)
    bias = i["L0_attn_b_qkv"].reshape(3, 2, CH)
    a["perf_bqk"] = bias[0:2].transpose(2, 1, 0)
    a["perf_bv"] = i["L0_attn_b_qkv"][None, 2 * C:]
    a["perf_wp"] = halves(i["L0_attn_w_proj"].T)
    a["perf_bp"] = i["L0_attn_b_proj"][None]
    a["perf_feat"] = blocks(i["L0_attn_projection"])
    qkv = i["L0_ffn_Wqkv"].reshape(C, 3, H, D)
    a["att_wqk"] = halves(i["L0_ffn_Wqkv"][:, :2 * C])
    a["att_wv"] = halves(qkv[:, 2].reshape(C, C))
    a["att_wp"] = halves(i["L0_ffn_Wproj"])
    a["att_ln"] = np.stack([vector(i["L0_ffn_ln1_g"]), vector(i["L0_ffn_ln1_b"])], 1)
    a["earlier"] = np.triu(np.ones((P, P), np.float32), 1)
    a["slot_no"] = np.arange(slots_for(2), dtype=np.float32)[None]
    a["before"] = np.broadcast_to(np.tril(np.ones((E, E), np.float32), -1), (P, E, E))
    a["moe_ln"] = np.stack([vector(i["L0_ffn_ln2_g"]), vector(i["L0_ffn_ln2_b"])], 1)
    a["moe_wr"] = halves(i["L0_ffn_Wrouter"])
    a["moe_w1"] = halves(i["L0_ffn_W1"])
    a["moe_w2"] = i["L0_ffn_W2"].reshape(E, FFT, P, C).swapaxes(1, 2)
    a["ffn_wr"] = halves(i["L1_ffn_gate_w"])
    a["ffn_br"] = i["L1_ffn_gate_b"][None]
    a["ffn_w1"] = halves(i["L1_ffn_w1"])
    a["ffn_b1"] = i["L1_ffn_b1"][None]
    a["ffn_w2"] = i["L1_ffn_w2"].reshape(E, FFT, P, C).swapaxes(1, 2)
    a["ffn_b2"] = i["L1_ffn_b2"][None]
    w = i["L1_attn_w_qkv"]
    a["mix_wq"] = halves(w[:, :C])
    a["mix_wkv"] = halves(w[:, C:])
    a["mix_wside"] = halves(np.concatenate([i["L1_attn_w_id"], i["L1_attn_w_idgate"], i["L1_attn_w_prune"]], 1))
    a["mix_bside"] = np.concatenate([np.zeros(C, np.float32), i["L1_attn_b_idgate"], i["L1_attn_b_prune"]])[None]
    a["mix_wg1"] = halves(i["L1_attn_w_g1"])
    a["mix_bg1"] = vector(i["L1_attn_b_g1"])
    a["mix_wg2"] = halves(i["L1_attn_w_g2"])
    a["mix_bg2"] = i["L1_attn_b_g2"][None]
    a["mix_static"] = np.broadcast_to(i["L1_attn_id_static_logit"], (P, H))
    a["mix_taps"] = halves(np.concatenate([i["L1_attn_fir_short_w"].reshape(C, SHORT), i["L1_attn_fir_long_w"].reshape(C, LONG)], 1))
    a["mix_mixer"] = halves(np.repeat(np.repeat(i["L1_attn_mix"], D, 0), D, 1))
    a["same_dim"] = halves(np.tile(np.eye(D, dtype=np.float32), (H, H)))
    a["same"] = halves(np.eye(C, dtype=np.float32))
    a["head_mask"] = np.repeat(np.eye(GH, dtype=np.float32), CK, 0)
    a["upto"] = np.tile(np.triu(np.ones((CK, CK), np.float32)), (GH, 1))
    a["proj_w"] = halves(i["L1_attn_w_proj"])
    a["proj_b"] = i["L1_attn_b_proj"][None]
    return {k: np.ascontiguousarray(v) for k, v in a.items()}


def kernel(**inputs):
    import numpy as np
    import concourse.bacc as bacc
    from concourse.bass_utils import run_bass_kernel_spmd

    arrays = layouts({k: np.asarray(v) for k, v in inputs.items()}, np)
    nc = bacc.Bacc("TRN2", target_bir_lowering=False, num_devices=1)
    io = {k: nc.dram_tensor(f"in_{k}", v.shape, mybir.dt.from_np(v.dtype), kind="ExternalInput").ap()
          for k, v in arrays.items()}
    out = nc.dram_tensor("out", (B, N, C), F32, kind="ExternalOutput").ap()
    program(nc, io, out)
    r = run_bass_kernel_spmd(nc, [{f"in_{k}": v for k, v in arrays.items()}], core_ids=[0])
    return r.results[0]["out"]
```

```python
import math
from contextlib import ExitStack

import concourse.bass as bass
from concourse import mybir

F32 = mybir.dt.float32
I32 = mybir.dt.int32
BF16 = mybir.dt.bfloat16
ALU = mybir.AluOpType
ACT = mybir.ActivationFunctionType
AX = mybir.AxisListType

B = 4
NI = 512
NT = 128
N = NI + NT
P = 128
TB = N // P
TILES = B * TB
C = 192
CH = C // 2
H = 12
D = C // H
HALF = N // 2
EPS = 1e-5
ROUND = 1.5 * 2.0 ** 23
TWO_PI = 6.283185


class InOrder:

    def __init__(self, eng, own, per_turn=0):
        self.eng, self.own, self.per_turn, self.base, self.n = eng, own, per_turn, 0, 0

    def turn(self, i, before=0):
        self.base, self.n = i * self.per_turn + before, 0

    def step(self, ins):
        ins.then_inc(self.own, 1)
        self.n += 1
        self.eng.wait_ge(self.own, self.base + self.n)

    def announce(self, ins, sem, value):
        ins.then_inc(sem, 1)
        self.eng.wait_ge(sem, value)

    def count(self, ins):
        ins.then_inc(self.own, 1)
        self.n += 1

    def sem_step(self):
        self.eng.sem_inc(self.own, 1)
        self.n += 1

    def wait(self):
        self.eng.wait_ge(self.own, self.base + self.n)

    def ended(self):
        assert self.n == self.per_turn, (self.n, self.per_turn)


class Ring:

    def __init__(self, eng, banks, filled, taken, per_turn):
        self.eng, self.banks, self.filled, self.taken, self.per_turn = eng, banks, filled, taken, per_turn
        self.base, self.n = 0, 0

    def turn(self, i, before=0):
        assert before or self.n in (0, self.per_turn), (self.n, self.per_turn)
        self.base, self.n = i * self.per_turn + before, 0

    def restart(self, i, before=0):
        self.turn(i, before)
        self.eng.wait_ge(self.taken, self.base + len(self.banks))

    def bank(self):
        return self.banks[self.n % len(self.banks)]

    def free(self):
        self.eng.wait_ge(self.taken, self.base + self.n + 1)
        return self.bank()

    def fill(self, ins):
        ins.then_inc(self.filled, 1)
        self.n += 1

    def arrived(self, n=None):
        self.eng.wait_ge(self.taken, self.base + len(self.banks) + (self.n if n is None else n))

    def get(self):
        self.eng.wait_ge(self.filled, self.base + self.n + 1)
        return self.bank()

    def take(self, ins):
        ins.then_inc(self.taken, 1)
        self.n += 1

    def done(self):
        self.eng.wait_ge(self.taken, self.base + len(self.banks) + self.n)

    def ended(self):
        assert self.n == self.per_turn, (self.n, self.per_turn)


class Memory:

    def __init__(self, nc, stage):
        self.nc, self.stage, self.stack, self.semaphores = nc, stage, ExitStack(), []

    def __enter__(self):
        return self

    def __exit__(self, *exc):
        if self.semaphores and exc[0] is None:
            self.nc.clear_and_free_semaphores(self.semaphores)
            self.nc.all_engine_barrier()
        self.stack.close()

    def sbuf(self, name, shape, dt=F32):
        return self.stack.enter_context(self.nc.sbuf_tensor(f"{self.stage}_{name}", shape, dt))

    def psum(self, name, shape, dt=F32):
        return self.stack.enter_context(self.nc.psum_tensor(f"{self.stage}_{name}", shape, dt))

    def sem(self, name):
        self.semaphores.append(self.nc.alloc_semaphore(f"{self.stage}_{name}"))
        return self.semaphores[-1]

    def sems(self, *names):
        return [self.sem(n) for n in names]


def split_bf16(nc, own, x, parts, rest):
    own.step(nc.vector.tensor_copy(parts[0], x))
    own.step(nc.vector.tensor_tensor(rest, x, parts[0], ALU.subtract))
    own.step(nc.vector.tensor_copy(parts[1], rest))
    return nc.vector.tensor_tensor(parts[2], rest, parts[1], ALU.subtract)


BANDS = 6
JC = 5
UNITS = JC * BANDS
KTILES = 4 * 2 * BANDS + BANDS


def image_embedding(nc, h, io):
    with Memory(nc, "img") as m:
        w = m.sbuf("w", [P, KTILES, C])
        freq = m.sbuf("freq", [P, BANDS])
        shift = m.sbuf("shift", [P, 2])
        x = m.sbuf("x", [P, 2, NI])
        turns = m.sbuf("turns", [P, 2, NI])
        nearest = m.sbuf("nearest", [P, NI])
        rest = m.sbuf("rest", [P, 2, NI])
        folded = m.sbuf("folded", [P, 2, NI])
        feat = m.sbuf("feat", [P, 3, 2, NI])
        out = m.psum("out", [P, 8, 512])
        (w_in, x_in0, x_in1, x_free, turns_ready, turns_free, rest_ready, folded_ready, rest_free,
         feat_ready, feat_free, out_ready, out_free, dve_own, pool_own) = m.sems(
            "w_in", "x_in0", "x_in1", "x_free", "turns_ready", "turns_free", "rest_ready", "folded_ready",
            "rest_free", "feat_ready", "feat_free", "out_ready", "out_free", "dve_own", "pool_own")
        x_in = [x_in0, x_in1]
        w_parts = m.sems("w_part0", "w_part1", "w_part2")
        KPART = KTILES // len(w_parts)
        with nc.Block() as block:

            @block.sync
            def _(sp):
                sp.dma_start(freq[:, :], io["freq"]).then_inc(w_in, 16)
                sp.dma_start(shift[:, :], io["sincos_shift"]).then_inc(w_in, 16)
                with sp.Fori(0, B // 2) as bb:
                    for half in range(2):
                        for c in range(JC):
                            n = half * JC + c
                            sp.wait_ge(x_free, bb * (2 * JC) + n + 1)
                            sp.dma_start(x[:, n % 2, :], io["x"][bass.ds(bb * (2 * JC) + n, 1)].rearrange("o p n -> p (o n)")).then_inc(x_in[n % 2], 16)

            @block.gpsimd
            def _(pool):
                pool.sem_inc(x_free, 2)
                pool.wait_ge(w_in, 2 * 16)
                with pool.Fori(0, B // 2) as bb:
                    for half in range(2):
                        for c in range(JC):
                            n = half * JC + c
                            pool.wait_ge(x_in[n % 2], bb * (16 * JC) + 16 * (n // 2 + 1))
                            for f in range(BANDS):
                                g = n * BANDS + f
                                pool.wait_ge(turns_free, bb * (2 * UNITS) + g + 1)
                                ins = nc.gpsimd.tensor_tensor(turns[:, g % 2, :], x[:, n % 2, :], freq[:, f:f + 1].to_broadcast([P, NI]), ALU.mult)
                                ins.then_inc(turns_ready, 1)
                            pool.wait_ge(turns_ready, bb * (2 * UNITS) + (n + 1) * BANDS)
                            pool.sem_inc(x_free, 1)

            @block.vector
            def _(dve):
                own = InOrder(dve, dve_own, 2 * UNITS)
                dve.sem_inc(turns_free, 2)

                def sums_out(b, half):
                    dve.wait_ge(out_ready, b + 1)
                    for t in range(4):
                        nc.vector.tensor_copy(h[:, b * TB + t, :], out[:, half * 4 + t, 0:C]).then_inc(out_free, 1)

                with dve.Fori(0, B // 2) as bb:
                    own.turn(bb)
                    for half in range(2):
                        b = bb * 2 + half
                        for g in range(UNITS):
                            at = b * UNITS + g + 1
                            dve.wait_ge(turns_ready, at)
                            dve.wait_ge(rest_free, at)
                            own.step(nc.vector.tensor_scalar(nearest[:, :], turns[:, g % 2, :], ROUND, None, ALU.add))
                            own.announce(nc.vector.scalar_tensor_tensor(rest[:, g % 2, :], nearest[:, :], ROUND, turns[:, g % 2, :],
                                                                      ALU.subtract, ALU.subtract), rest_ready, at)
                            dve.sem_inc(turns_free, 1)
                            last = g >= (JC - 1) * BANDS
                            lo = 64 if last else 0
                            dst = rest if last else folded
                            nc.vector.scalar_tensor_tensor(dst[lo:P, g % 2, :], rest[lo:P, g % 2, :], -1.0, rest[lo:P, g % 2, :], ALU.mult, ALU.max).then_inc(folded_ready, 1)
                            dve.wait_ge(folded_ready, at)
                            if half == 1 and g == BANDS:
                                sums_out(bb * 2, 0)
                    own.ended()
                    sums_out(bb * 2 + 1, 1)

            @block.scalar
            def _(act):
                act.sem_inc(rest_free, 2)
                for part, arrived in enumerate(w_parts):
                    act.dma_start(w[:, part * KPART:(part + 1) * KPART, :], io["tok_w"][:, part * KPART:(part + 1) * KPART, :]).then_inc(arrived, 16)
                act.wait_ge(w_in, 2 * 16)
                with act.Fori(0, B) as b:
                    for c in range(JC):
                        for f in range(BANDS):
                            g = c * BANDS + f
                            at = b * UNITS + g + 1
                            act.wait_ge(folded_ready, at)
                            act.wait_ge(feat_free, at)
                            if c < JC - 1:
                                nc.scalar.activation(feat[:, g % 3, 0, :], rest[:, g % 2, :], ACT.Sin, scale=-TWO_PI)
                                ins = nc.scalar.activation(feat[:, g % 3, 1, :], folded[:, g % 2, :], ACT.Sin, scale=-TWO_PI,
                                                           bias=shift[:, 1:2])
                            else:
                                ins = nc.scalar.activation(feat[:, g % 3, 0, :], rest[:, g % 2, :], ACT.Sin, scale=-TWO_PI,
                                                           bias=shift[:, 0:1])
                            ins.then_inc(feat_ready, 1)
                            act.wait_ge(feat_ready, at)
                            act.sem_inc(rest_free, 1)

            @block.tensor
            def _(pe):
                pe.sem_inc(feat_free, 3)
                pe.sem_inc(out_free, 8)

                def batch(b, half):
                    pe.wait_ge(out_free, b * 4 + 4)
                    for c in range(JC):
                        for f in range(BANDS):
                            g = c * BANDS + f
                            pe.wait_ge(feat_ready, b * UNITS + g + 1)
                            for part in range(2 if c < JC - 1 else 1):
                                k = c * 12 + part * BANDS + f
                                if half == 0 and (f == 0 or k % KPART == 0):
                                    pe.wait_ge(w_parts[k // KPART], 16)
                                for t in range(4):
                                    ins = nc.tensor.matmul(out[:, half * 4 + t, 0:C], feat[:, g % 3, part, t * P:(t + 1) * P], w[:, k, :],
                                                           start=(k == 0), stop=(k == KTILES - 1))
                            ins.then_inc(feat_free, 1)
                    pe.wait_ge(feat_free, b * UNITS + UNITS + 3)
                    pe.sem_inc(out_ready, 1)

                with pe.Fori(0, B // 2) as bb:
                    for half in range(2):
                        batch(bb * 2 + half, half)


LAYERS = 2
VOCAB = 8000
DI = 2 * C
FT = DI // P
STATES = 16
RANK = C // STATES
BC = 2 * STATES
COPIED = 3 * BC
XD = COPIED + RANK
TAPS = 4
CONV_W, CONV_B, DT_B, A_LOG, SKIP, PARAMS = 0, 4, 5, 6, 22, 23
TXT = B * NT
NO_PAST = 200.0


def text_embedding(nc, h, ident, io):
    with Memory(nc, "txt") as m:
        ids = m.sbuf("ids", [P, B], I32)
        idf = m.sbuf("idf", [P, B])
        neg = m.sbuf("neg", [P, B])
        rows = m.sbuf("rows", [P, B], I32)
        in_w = m.sbuf("in_w", [CH, 2, 2 * DI])
        norm_w = m.sbuf("norm_w", [CH, 2])
        par = m.sbuf("par", [P, FT, PARAMS])
        xp_w = m.sbuf("xp_w", [P, FT, XD])
        dt_w = m.sbuf("dt_w", [XD, DI])
        out_w = m.sbuf("out_w", [P, FT, C])
        pick = m.sbuf("pick", [COPIED, BC, P])
        pick16 = m.sbuf("pick16", [COPIED, BC, P], BF16)
        squares = m.sbuf("squares", [P, C])
        rms = m.sbuf("rms", [P, B])
        xn = m.sbuf("xn", [P, B, C])
        xnT = m.sbuf("xnT", [CH, 2, TXT])
        padded = m.sbuf("padded", [P, FT, B, TAPS - 1 + NT])
        conv = m.sbuf("conv", [P, FT, TXT])
        u = m.sbuf("u", [P, FT, TXT])
        gate = m.sbuf("gate", [P, FT, TXT])
        xdbl = m.sbuf("xdbl", [XD, TXT])
        stack = m.sbuf("stack", [COPIED, TXT], BF16)
        part1 = m.sbuf("part1", [COPIED, TXT], BF16)
        part2 = m.sbuf("part2", [COPIED, TXT], BF16)
        part_rest = m.sbuf("part_rest", [COPIED, TXT])
        delta = m.sbuf("delta", [P, FT, TXT])
        e = m.sbuf("e", [P, FT, TXT])
        w = m.sbuf("w", [P, FT, TXT])
        ln_w = m.sbuf("ln_w", [P, FT, TXT])
        lost = m.sbuf("lost", [P, FT, TXT])
        raw_delta = m.sbuf("raw_delta", [P, FT, TXT])
        du = m.sbuf("du", [P, FT, TXT])
        decay_rate = m.sbuf("decay_rate", [P, FT, STATES])
        decay = m.sbuf("decay", [P, 2, FT, TXT])
        exponent = m.sbuf("exponent", [P, 2, FT, TXT])
        drive = m.sbuf("drive", [P, FT, TXT])
        state = m.sbuf("state", [P, 2, FT, TXT])
        read = m.sbuf("read", [P, 2, FT, TXT])
        c_row = m.sbuf("c_row", [P, 2, TXT])
        bank = m.psum("bank", [P, 8, 512])
        XNT, XR, RES, XDB, DT, BN, CN, Y, OUT = 0, 2, 5, 0, 5, (0, 1), (5, 6), 2, 0
        (ids_in, fixed_in, weights_in, weights_free, rows_ready, x_in, padding, xn_ready, xnT_psum, xnT_ready, xz_psum,
         xz_taken, conv_ready, u_ready, xd_psum, xd_ready, dt_psum, e_ready, rate_ready, delta_ready, exponent_ready,
         decay_ready, scanned, c_ready, bc_psum, stack_ready, pick_ready, read_ready, read_free, y_ready, out_psum, x_ready,
         dve_own, act_own, square_ready, root_ready, a_log_ready, z_ready, w_ready, ln_ready) = m.sems(*(
            "ids_in fixed_in weights_in weights_free rows_ready x_in padding xn_ready xnT_psum xnT_ready xz_psum "
            "xz_taken conv_ready u_ready xd_psum xd_ready dt_psum e_ready rate_ready delta_ready exponent_ready "
            "decay_ready scanned c_ready bc_psum stack_ready pick_ready read_ready read_free y_ready out_psum x_ready "
            "dve_own act_own square_ready root_ready a_log_ready z_ready w_ready ln_ready").split())

        def wide(ap):
            return ap.rearrange("p (o n) -> p o n", o=1).to_broadcast([P, FT, TXT])

        with nc.Block() as block:

            @block.sync
            def _(sp):
                sp.dma_start(ids[:, :], io["ids"]).then_inc(ids_in, 16)
                sp.dma_start(pick[:, :, :], io["pick"]).then_inc(fixed_in, 16)
                with sp.Fori(0, LAYERS) as l:
                    sp.wait_ge(weights_free, l + 1)
                    for dst, name in ((in_w, "in_proj"), (norm_w, "norm_w"), (par, "txt_par"), (xp_w, "x_proj"),
                                      (dt_w, "dt_proj"), (out_w, "out_proj")):
                        src = io[name][bass.ds(l, 1)]
                        if len(src.shape) == 4:
                            sp.dma_start(dst[:, :, :], src.rearrange("o p a b -> p (o a) b")).then_inc(weights_in, 16)
                        else:
                            dst = dst[COPIED:, :] if name == "dt_proj" else dst[:, :]
                            sp.dma_start(dst, src.rearrange("o p a -> p (o a)")).then_inc(weights_in, 16)

            @block.gpsimd
            def _(pool):
                nc.gpsimd.memset(padded[:, :, :, :], 0.0).then_inc(padding, 1)
                nc.gpsimd.memset(exponent[:, :, :, :], NO_PAST).then_inc(padding, 1)
                pool.sem_inc(read_ready, 2)
                pool.wait_ge(padding, 2)
                pool.wait_ge(rows_ready, 1)
                for b in range(B):
                    nc.gpsimd.indirect_dma_start(out=h[:, b * TB + TB - 1, :], out_offset=None, in_=io["emb"],
                                                 in_offset=bass.IndirectOffsetOnAxis(ap=rows[:, b:b + 1], axis=0)).then_inc(x_in, 16)
                with pool.Fori(0, LAYERS) as l:
                    for n in range(STATES):
                        at = l * STATES + n + 1
                        pool.wait_ge(scanned, at + 2)
                        pool.wait_ge(read_free, at)
                        pool.wait_ge(c_ready, at)
                        nc.gpsimd.tensor_tensor(read[:, n % 2, :, :], state[:, n % 2, :, :], wide(c_row[:, n % 2, :]),
                                                ALU.mult).then_inc(read_ready, 1)

            @block.vector
            def _(dve):
                own = InOrder(dve, dve_own)
                dve.wait_ge(ids_in, 16)
                own.step(nc.vector.tensor_copy(idf[:, :], ids[:, :]))
                own.step(nc.vector.tensor_scalar(neg[:, :], idf[:, :], 0.0, float(VOCAB), ALU.is_lt, ALU.mult))
                own.step(nc.vector.tensor_tensor(idf[:, :], idf[:, :], neg[:, :], ALU.add))
                own.step(nc.vector.tensor_scalar(idf[:, :], idf[:, :], 0.0, float(VOCAB - 1), ALU.max, ALU.min))
                nc.vector.tensor_copy(rows[:, :], idf[:, :]).then_inc(rows_ready, 1)
                before = own.n
                own = InOrder(dve, dve_own, TXT_DVE_STEPS)
                dve.wait_ge(x_in, 16 * B)
                with dve.Fori(0, LAYERS) as l:
                    own.turn(l)
                    own.base = own.base + before
                    dve.wait_ge(x_ready, l * B + 1)
                    for b in range(B):
                        x = h[:, b * TB + TB - 1, :]
                        own.step(nc.vector.tensor_tensor_reduce(out=squares[:, :], in0=x, in1=x, scale=1.0, scalar=0.0,
                                                                op0=ALU.mult, op1=ALU.add, accum_out=rms[:, b:b + 1]))
                    own.step(nc.vector.tensor_scalar(rms[:, :], rms[:, :], 1.0 / C, EPS, ALU.mult, ALU.add))
                    nc.vector.reciprocal(rms[:, :], rms[:, :]).then_inc(square_ready, 1)
                    dve.wait_ge(root_ready, l + 1)
                    for b in range(B):
                        nc.vector.tensor_scalar(xn[:, b, :], h[:, b * TB + TB - 1, :], rms[:, b:b + 1], None, ALU.mult).then_inc(xn_ready, 1)
                    dve.wait_ge(weights_in, l * 96 + 96)
                    nc.vector.tensor_scalar(par[:, :, A_LOG:A_LOG + STATES], par[:, :, A_LOG:A_LOG + STATES], 88.7, None,
                                            ALU.min).then_inc(a_log_ready, 1)
                    dve.wait_ge(xnT_psum, l + 1)
                    for k in range(2):
                        nc.vector.tensor_scalar(xnT[:, k, :], bank[0:CH, XNT + k, :], norm_w[:, k:k + 1], None, ALU.mult).then_inc(xnT_ready, 1)
                    dve.wait_ge(xz_taken, l * 2 * FT + FT)
                    for f in range(FT):
                        for k in range(TAPS):
                            src = padded[:, f, :, k:k + NT]
                            dst = conv[:, f, :].rearrange("p (b t) -> p b t", b=B)
                            tap = par[:, f, CONV_W + k:CONV_W + k + 1]
                            if k == 0:
                                own.step(nc.vector.tensor_scalar(dst, src, tap, None, ALU.mult))
                            elif k < TAPS - 1:
                                own.step(nc.vector.scalar_tensor_tensor(dst, src, tap, dst, ALU.mult, ALU.add))
                            else:
                                nc.vector.scalar_tensor_tensor(dst, src, tap, dst, ALU.mult, ALU.add).then_inc(conv_ready, 1)
                    dve.wait_ge(xd_psum, l + 1)
                    nc.vector.tensor_copy(xdbl[:, :], bank[0:XD, XDB, :]).then_inc(xd_ready, 1)
                    dve.wait_ge(xd_ready, l + 1)
                    parts = [stack[:, :], part1[:, :], part2[:, :]]
                    own.step(split_bf16(nc, own, xdbl[0:COPIED, :], parts, part_rest[:, :]))
                    for p in (1, 2):
                        rows_of = slice(p * BC, (p + 1) * BC)
                        nc.vector.tensor_copy(stack[rows_of, :], parts[p][rows_of, :]).then_inc(stack_ready, 1)
                    dve.wait_ge(dt_psum, l + 1)
                    for f in range(FT):
                        nc.vector.tensor_scalar(raw_delta[:, f, :], bank[:, DT + f, :], par[:, f, DT_B:DT_B + 1], None, ALU.add).then_inc(z_ready, 1)
                    dve.wait_ge(z_ready, l * FT + FT)
                    own.step(nc.vector.tensor_scalar(delta[:, :, :], raw_delta[:, :, :], 0.0, None, ALU.max))
                    dve.wait_ge(e_ready, l + 1)
                    own.announce(nc.vector.tensor_scalar(w[:, :, :], e[:, :, :], 1.0, None, ALU.add), w_ready, l + 1)
                    own.step(nc.vector.scalar_tensor_tensor(lost[:, :, :], w[:, :, :], -1.0, e[:, :, :], ALU.add, ALU.subtract))
                    own.step(nc.vector.tensor_tensor(delta[:, :, :], delta[:, :, :], lost[:, :, :], ALU.subtract))
                    dve.wait_ge(ln_ready, l + 1)
                    own.announce(nc.vector.tensor_tensor(delta[:, :, :], delta[:, :, :], ln_w[:, :, :], ALU.add), delta_ready, l + 1)
                    dve.wait_ge(u_ready, l * FT + FT)
                    own.step(nc.vector.tensor_tensor(du[:, :, :], delta[:, :, :], u[:, :, :], ALU.mult))

                    def exponents(n):
                        if n >= 2:
                            dve.wait_ge(decay_ready, l * STATES + n - 1)
                        for f in range(FT):
                            later = [a.rearrange("p (b t) -> p b t", b=B)[:, :, 1:] for a in (exponent[:, n % 2, f, :], delta[:, f, :])]
                            nc.vector.tensor_scalar(later[0], later[1], decay_rate[:, f, n:n + 1], NO_PAST, ALU.mult, ALU.min).then_inc(exponent_ready, 1)

                    dve.wait_ge(rate_ready, l + 1)
                    exponents(0)
                    for n in range(STATES):
                        at = l * STATES + n + 1
                        dve.wait_ge(bc_psum, at)
                        own.step(nc.vector.tensor_tensor(drive[:, :, :], du[:, :, :], wide(bank[:, BN[n % 2], :]), ALU.mult))
                        if n + 1 < STATES:
                            exponents(n + 1)
                        dve.wait_ge(decay_ready, at)
                        dve.wait_ge(read_ready, at)
                        own.announce(nc.vector.tensor_tensor_scan(state[:, n % 2, :, :].rearrange("p f n -> p (f n)"),
                                                                decay[:, n % 2, :, :].rearrange("p f n -> p (f n)"),
                                                                drive[:, :, :].rearrange("p f n -> p (f n)"), 0.0, ALU.mult, ALU.add),
                                   scanned, at + 2)
                    dve.wait_ge(read_free, l * STATES + STATES + 2)
                    for f in range(FT):
                        own.step(nc.vector.scalar_tensor_tensor(conv[:, f, :], u[:, f, :], par[:, f, SKIP:SKIP + 1], bank[:, Y + f, :],
                                                                ALU.mult, ALU.add))
                    own.announce(nc.vector.tensor_tensor(conv[:, :, :], conv[:, :, :], gate[:, :, :], ALU.mult), y_ready, l + 1)
                    dve.wait_ge(out_psum, l + 1)
                    for b in range(B):
                        x = h[:, b * TB + TB - 1, :]
                        nc.vector.tensor_tensor(x, x, bank[:, OUT + b // 2, (b % 2) * C:(b % 2 + 1) * C], ALU.add).then_inc(x_ready, 1)
                    dve.wait_ge(x_ready, l * B + B + 1)
                    own.ended()

            @block.scalar
            def _(act):
                act.sem_inc(x_ready, 1)
                act.sem_inc(scanned, 2)
                own = InOrder(act, act_own, TXT_ACT_STEPS)
                act.wait_ge(padding, 2)
                act.wait_ge(fixed_in, 16)
                nc.scalar.activation(pick16[:, :, :], pick[:, :, :], ACT.Copy).then_inc(pick_ready, 1)
                with act.Fori(0, LAYERS) as l:
                    own.turn(l)
                    act.wait_ge(square_ready, l + 1)
                    nc.scalar.activation(rms[:, :], rms[:, :], ACT.Sqrt).then_inc(root_ready, 1)
                    for f in range(FT):
                        act.wait_ge(xz_psum, l * 2 * FT + f + 1)
                        nc.scalar.activation(padded[:, f, :, TAPS - 1:], bank[:, XR + f, :].rearrange("p (b t) -> p b t", b=B),
                                             ACT.Copy).then_inc(xz_taken, 1)
                    for f in range(FT):
                        act.wait_ge(xz_psum, l * 2 * FT + FT + f + 1)
                        nc.scalar.activation(gate[:, f, :], bank[:, RES + f, :], ACT.Silu).then_inc(xz_taken, 1)
                    for f in range(FT):
                        act.wait_ge(conv_ready, l * FT + f + 1)
                        nc.scalar.activation(u[:, f, :], conv[:, f, :], ACT.Silu, bias=par[:, f, CONV_B:CONV_B + 1]).then_inc(u_ready, 1)
                    act.wait_ge(a_log_ready, l + 1)
                    own.announce(nc.scalar.activation(decay_rate[:, :, :], par[:, :, A_LOG:A_LOG + STATES], ACT.Exp), rate_ready, l + 1)
                    act.wait_ge(z_ready, l * FT + FT)
                    own.step(nc.scalar.activation(e[:, :, :], raw_delta[:, :, :], ACT.Abs))
                    own.announce(nc.scalar.activation(e[:, :, :], e[:, :, :], ACT.Exp, scale=-1.0), e_ready, l + 1)
                    act.wait_ge(w_ready, l + 1)
                    nc.scalar.activation(ln_w[:, :, :], w[:, :, :], ACT.Ln).then_inc(ln_ready, 1)
                    for n in range(STATES):
                        act.wait_ge(scanned, l * STATES + n + 1)
                        act.wait_ge(exponent_ready, (l * STATES + n + 1) * FT)
                        nc.scalar.activation(decay[:, n % 2, :, :], exponent[:, n % 2, :, :], ACT.Exp, scale=-1.0).then_inc(decay_ready, 1)
                        act.wait_ge(bc_psum, l * STATES + n + 1)
                        act.wait_ge(read_ready, l * STATES + n + 1)
                        nc.scalar.activation(c_row[:, n % 2, :], bank[:, CN[n % 2], :], ACT.Copy).then_inc(c_ready, 1)
                    own.ended()

            @block.tensor
            def _(pe):
                pe.sem_inc(read_free, 2)
                pe.sem_inc(weights_free, 1)
                pe.wait_ge(pick_ready, 1)
                with pe.Fori(0, LAYERS) as l:
                    pe.wait_ge(weights_in, l * 96 + 96)
                    for b in range(B):
                        pe.wait_ge(xn_ready, l * B + b + 1)
                        for k in range(2):
                            ins = nc.tensor.transpose(bank[0:CH, XNT + k, b * P:(b + 1) * P], xn[:, b, k * CH:(k + 1) * CH], ident[:, :])
                    ins.then_inc(xnT_psum, 1)
                    pe.wait_ge(xnT_ready, l * 2 + 2)
                    for f in range(2 * FT):
                        for k in range(2):
                            ins = nc.tensor.matmul(bank[:, XR + f, :], in_w[:, k, f * P:(f + 1) * P], xnT[:, k, :], start=(k == 0), stop=(k == 1))
                        ins.then_inc(xz_psum, 1)
                    for f in range(FT):
                        pe.wait_ge(u_ready, l * FT + f + 1)
                        ins = nc.tensor.matmul(bank[0:XD, XDB, :], xp_w[:, f, :], u[:, f, :], start=(f == 0), stop=(f == FT - 1))
                    ins.then_inc(xd_psum, 1)
                    pe.wait_ge(xd_ready, l + 1)
                    pe.wait_ge(xz_taken, l * 2 * FT + 2 * FT)
                    for f in range(FT):
                        ins = nc.tensor.matmul(bank[:, DT + f, :], dt_w[COPIED:, f * P:(f + 1) * P], xdbl[COPIED:, :], start=True, stop=True)
                    ins.then_inc(dt_psum, 1)
                    pe.wait_ge(stack_ready, l * 2 + 2)
                    pe.wait_ge(delta_ready, l + 1)

                    def b_and_c(n):
                        nc.tensor.matmul(bank[:, BN[n % 2], :], pick16[:, n, :], stack[:, :], start=True, stop=True)
                        nc.tensor.matmul(bank[:, CN[n % 2], :], pick16[:, STATES + n, :], stack[:, :], start=True, stop=True).then_inc(bc_psum, 1)

                    for n in range(2):
                        b_and_c(n)
                    for n in range(STATES):
                        pe.wait_ge(read_ready, l * STATES + n + 3)
                        if n + 2 < STATES:
                            b_and_c(n + 2)
                        for f in range(FT):
                            ins = nc.tensor.matmul(bank[:, Y + f, :], ident[:, :], read[:, n % 2, f, :], start=(n == 0), stop=(n == STATES - 1))
                        ins.then_inc(read_free, 1)
                    pe.wait_ge(y_ready, l + 1)
                    for b in range(B):
                        for f in range(FT):
                            ins = nc.tensor.matmul(bank[:, OUT + b // 2, (b % 2) * C:(b % 2 + 1) * C], conv[:, f, b * P:(b + 1) * P],
                                                   out_w[:, f, :], start=(f == 0), stop=(f == FT - 1))
                    ins.then_inc(out_psum, 1)
                    pe.wait_ge(out_psum, l + 1)
                    pe.sem_inc(weights_free, 1)


TXT_DVE_STEPS = 41
TXT_ACT_STEPS = 1


class Normed:

    def __init__(self, m, name):
        self.stats = m.sbuf(f"{name}_stats", [P, TB, 6])
        self.mv = m.sbuf(f"{name}_mv", [P, TB, 2])
        self.rstd = m.sbuf(f"{name}_rstd", [P, TB])
        self.xn = m.sbuf(f"{name}_xn", [P, TB, C])
        self.xT = m.sbuf(f"{name}_xT", [CH + 1, 2, N])
        self.var_ready = m.sem(f"{name}_var")
        self.rstd_ready = m.sem(f"{name}_rstd")
        self.xn_ready = m.sem(f"{name}_xn")
        self.psum_ready = m.sem(f"{name}_psum")
        self.xT_ready = m.sem(f"{name}_xT")


def rows_of(k, bias=True):
    return slice(0, CH + 1 if bias and k == 1 else CH)


NARROW = 96
NORM_STEPS = 2 * TB + 2


def norm_rows(nc, dve, own, z, src, b, dst=None):
    dst = dst or (lambda s: z.xn[:, s, :])
    for s in range(TB):
        own.count(nc.vector.bn_stats(z.stats[:, s, :], src(s)))
    own.wait()
    own.sem_step()
    for s in range(TB):
        own.count(nc.vector.bn_aggr(z.mv[:, s, :], z.stats[:, s, :]))
    own.wait()
    own.step(nc.vector.tensor_scalar(z.rstd[:, :], z.mv[:, :, 1], EPS, None, ALU.add))
    nc.vector.reciprocal(z.rstd[:, :], z.rstd[:, :]).then_inc(z.var_ready, 1)
    dve.wait_ge(z.rstd_ready, b + 1)
    for s in range(TB):
        nc.vector.tensor_scalar(dst(s), src(s), z.mv[:, s, 0:1], z.rstd[:, s:s + 1], ALU.subtract, ALU.mult).then_inc(z.xn_ready, 1)


def following(b):
    return (b + 1) % B


def root(nc, act, z, b):
    act.wait_ge(z.var_ready, b + 1)
    nc.scalar.activation(z.rstd[:, :], z.rstd[:, :], ACT.Sqrt).then_inc(z.rstd_ready, 1)


def transpose_rows(nc, pe, src, ident, bank, ready):
    for s in range(TB):
        for k in range(2):
            out = bank[0:CH, k, s * P:(s + 1) * P] if s < 4 else bank[0:CH, 2, k * P:(k + 1) * P]
            ins = nc.tensor.transpose(out, src(s, k), ident[:, :])
    ins.then_inc(ready, 1)


def copy_transposed(nc, bank, xT, ready, scale=None, shift=None):
    for k in range(2):
        for src, dst in ((bank[0:CH, k, :], xT[0:CH, k, 0:4 * P]), (bank[0:CH, 2, k * P:(k + 1) * P], xT[0:CH, k, 4 * P:])):
            if scale is None:
                ins = nc.scalar.activation(dst, src, ACT.Copy)
            else:
                ins = nc.scalar.activation(dst, src, ACT.Identity, scale=scale[:, k:k + 1], bias=shift[:, k:k + 1])
            ins.then_inc(ready, 1)


def fill(nc, pool, sem, pairs):
    for n, (view, value) in enumerate(pairs):
        nc.gpsimd.memset(view, value).then_inc(sem, 1)
        pool.wait_ge(sem, n + 1)


COPIES = 4


def load(sp, pairs, sem):
    for dst, src in pairs:
        idx = tuple(slice(None) for _ in dst.shape)
        sp.dma_start(dst[idx], src).then_inc(sem, 16)
    return 16 * len(pairs)


M = 64
GH = H // 2
PAIRS = H // 2
DV = D + 1
PAIR = 2 * DV
KERNEL_EPS = 1e-3
QK_SCALE = 1.0 / math.sqrt(math.sqrt(D))
PERF_ITEMS = 4 + 4 + 2 * TB + TB + 12 + 2 + 2 * TB + TB


def performer(nc, h, ident, io):
    with Memory(nc, "perf") as m:
        z = Normed(m, "ln")
        w = m.sbuf("w", [CH + 1, 2, 3 * C])
        wp = m.sbuf("wp", [CH + 1, 2, C])
        feat = m.sbuf("feat", [CH, GH * M])
        qT = m.sbuf("qT", [CH, 2, N])
        kT = m.sbuf("kT", [CH, 2, N])
        kp = m.sbuf("kp", [P, TB, H * M])
        v = m.sbuf("v", [P, TB, PAIRS * PAIR + NARROW - PAIR])
        qpT = m.sbuf("qpT", [P, PAIRS, N])
        ctx = m.sbuf("ctx", [P, PAIRS * PAIR + NARROW - PAIR])
        recip = m.sbuf("recip", [P, 3, 2])
        attn = m.sbuf("attn", [P, TB, C])
        aT = m.sbuf("aT", [CH + 1, 2, N])
        bank = m.psum("bank", [P, 8, 512])
        banks = (3, 4, 5, 6, 7)
        (loaded, set_up, filled, taken, attn_ready, aT_psum, aT_ready, h_ready, dve_own) = m.sems(
            *"loaded set_up filled taken attn_ready aT_psum aT_ready h_ready dve_own".split())
        pairs = ((w, io["perf_w"]), (wp, io["perf_wp"]), (feat, io["perf_feat"]))
        LOADED = 16 * len(pairs)

        def of_three(slot):
            return bank[:, slot, 0:3 * NARROW].rearrange("p (j c) -> p j c", j=3)

        with nc.Block() as block:

            @block.sync
            def _(sp):
                load(sp, pairs, loaded)

            @block.gpsimd
            def _(pool):
                fill(nc, pool, set_up, ((v[:, :, :], 1.0), (ctx[:, :], 0.0), (z.xT[CH:CH + 1, :, :], 1.0), (aT[CH:CH + 1, :, :], 1.0)))

            @block.vector
            def _(dve):
                own = InOrder(dve, dve_own, NORM_STEPS + 2 * TB)
                ring = Ring(dve, banks, filled, taken, PERF_ITEMS)
                dve.sem_inc(taken, len(banks))
                dve.wait_ge(loaded, LOADED)
                dve.wait_ge(set_up, 4)
                norm_rows(nc, dve, own, z, lambda s: h[:, s, :], 0)
                with dve.Fori(0, B) as b:
                    own.turn(b, NORM_STEPS)
                    ring.turn(b)
                    for i, dst in enumerate((qT, kT)):
                        for half in range(2):
                            for c in range(2):
                                src = ring.get()
                                ring.take(nc.vector.tensor_scalar(dst[:, half, c * HALF:(c + 1) * HALF], bank[0:CH, src, 0:HALF],
                                                                  QK_SCALE, None, ALU.mult))
                    for s in range(TB):
                        for half in range(2):
                            src = ring.get()
                            ring.take(nc.vector.tensor_scalar(kp[:, s, half * GH * M:(half + 1) * GH * M], bank[:, src, 0:GH * M], 0.0,
                                                              KERNEL_EPS, ALU.max, ALU.add))
                        src = ring.get()
                        ring.take(nc.vector.tensor_copy(v[:, s, 0:H * DV].rearrange("p (h c) -> p h c", h=H)[:, :, 0:D], bank[:, src, 0:C].rearrange("p (h d) -> p h d", h=H)))
                    for j in range(PAIRS):
                        for c in range(2):
                            src = ring.get()
                            ring.take(nc.vector.tensor_scalar(qpT[:, j, c * HALF:(c + 1) * HALF], bank[:, src, 0:HALF], 0.0, KERNEL_EPS,
                                                              ALU.max, ALU.add))
                    for part in range(2):
                        src = ring.get()
                        got = of_three(src)
                        dst = ctx[:, part * 3 * PAIR:(part + 1) * 3 * PAIR].rearrange("p (j c) -> p j c", j=3)
                        nc.vector.tensor_copy(dst[0:M, :, 0:DV], got[0:M, :, 0:DV])
                        ring.take(nc.vector.tensor_copy(dst[M:P, :, DV:], got[M:P, :, DV:PAIR]))
                    norm_rows(nc, dve, own, z, lambda s: h[:, following(b) * TB + s, :], b + 1)
                    for s in range(TB):
                        for part in range(2):
                            src = ring.get()
                            got = of_three(src)[:, :, 0:PAIR].rearrange("p j (g c) -> p j g c", g=2)
                            own.step(nc.vector.reciprocal(recip[:, :, :], got[:, :, :, D]))
                            dst = attn[:, s, part * CH:(part + 1) * CH].rearrange("p (j g d) -> p j g d", j=3, g=2)
                            ring.take(nc.vector.tensor_tensor(dst, got[:, :, :, 0:D], recip[:, :, :].unsqueeze(3).to_broadcast([P, 3, 2, D]),
                                                              ALU.mult))
                            ring.done()
                    for s in range(TB):
                        src = ring.get()
                        row = h[:, b * TB + s, :]
                        ring.take(nc.vector.tensor_tensor(row, row, bank[:, src, 0:C], ALU.add))
                    ring.done()
                    ring.ended()
                    own.ended()

            @block.scalar
            def _(act):
                root(nc, act, z, 0)
                act.wait_ge(z.psum_ready, 1)
                copy_transposed(nc, bank, z.xT, z.xT_ready)
                with act.Fori(0, B) as b:
                    root(nc, act, z, b + 1)
                    act.wait_ge(aT_psum, b + 1)
                    copy_transposed(nc, bank, aT, aT_ready)
                    act.wait_ge(z.psum_ready, b + 2)
                    copy_transposed(nc, bank, z.xT, z.xT_ready)

            @block.tensor
            def _(pe):
                ring = Ring(pe, banks, filled, taken, PERF_ITEMS)
                pe.wait_ge(loaded, LOADED)
                pe.wait_ge(set_up, 4)
                pe.wait_ge(z.xn_ready, TB)
                transpose_rows(nc, pe, lambda s, k: z.xn[:, s, k * CH:(k + 1) * CH], ident, bank, z.psum_ready)
                with pe.Fori(0, B) as b:
                    ring.restart(b)
                    pe.wait_ge(z.xT_ready, b * COPIES + COPIES)
                    for i in range(2):
                        for half in range(2):
                            for c in range(2):
                                dst = ring.free()
                                for k in range(2):
                                    at = i * C + half * CH
                                    ins = nc.tensor.matmul(bank[0:CH, dst, 0:HALF], w[rows_of(k), k, at:at + CH], z.xT[rows_of(k), k, c * HALF:(c + 1) * HALF],
                                                           start=(k == 0), stop=(k == 1))
                                ring.fill(ins)
                    ring.arrived(8)
                    for s in range(TB):
                        for half in range(2):
                            dst = ring.free()
                            ring.fill(nc.tensor.matmul(bank[:, dst, 0:GH * M], kT[:, half, s * P:(s + 1) * P], feat[:, :], start=True, stop=True))
                        dst = ring.free()
                        for k in range(2):
                            ins = nc.tensor.matmul(bank[:, dst, 0:C], z.xT[rows_of(k), k, s * P:(s + 1) * P], w[rows_of(k), k, 2 * C:],
                                                   start=(k == 0), stop=(k == 1))
                        ring.fill(ins)
                    for j in range(PAIRS):
                        at = (j % 3) * P
                        for c in range(2):
                            dst = ring.free()
                            ring.fill(nc.tensor.matmul(bank[:, dst, 0:HALF], feat[:, at:at + P], qT[:, j // 3, c * HALF:(c + 1) * HALF],
                                                       start=True, stop=True))
                    ring.arrived(8 + 3 * TB)
                    for part in range(2):
                        dst = ring.free()
                        for j in range(part * 3, part * 3 + 3):
                            for s in range(TB):
                                ins = nc.tensor.matmul(bank[:, dst, j % 3 * NARROW:(j % 3 + 1) * NARROW], kp[:, s, j * P:(j + 1) * P],
                                                       v[:, s, j * PAIR:j * PAIR + NARROW], start=(s == 0), stop=(s == TB - 1))
                        ring.fill(ins)
                    ring.arrived()
                    for s in range(TB):
                        for part in range(2):
                            dst = ring.free()
                            for j in range(part * 3, part * 3 + 3):
                                ins = nc.tensor.matmul(bank[:, dst, j % 3 * NARROW:(j % 3 + 1) * NARROW], qpT[:, j, s * P:(s + 1) * P],
                                                       ctx[:, j * PAIR:j * PAIR + NARROW], start=True, stop=True)
                            ring.fill(ins)
                    ring.arrived()
                    transpose_rows(nc, pe, lambda s, k: attn[:, s, k * CH:(k + 1) * CH], ident, bank, aT_psum)
                    pe.wait_ge(aT_ready, b * COPIES + COPIES)
                    pe.wait_ge(z.xn_ready, b * TB + 2 * TB)
                    transpose_rows(nc, pe, lambda s, k: z.xn[:, s, k * CH:(k + 1) * CH], ident, bank, z.psum_ready)
                    for s in range(TB):
                        dst = ring.free()
                        for k in range(2):
                            ins = nc.tensor.matmul(bank[:, dst, 0:C], aT[rows_of(k), k, s * P:(s + 1) * P], wp[rows_of(k), k, :],
                                                   start=(k == 0), stop=(k == 1))
                        ring.fill(ins)
                    ring.ended()


PARTS = 3
STACK = ((0, 0), (0, 1), (1, 0), (1, 1), (0, 2), (2, 0))
ROWS = len(STACK) * D
ALL_ROWS = ROWS + PARTS
LOT = 4
LOTS = H // LOT
QK_ITEMS = 2 * 2 * 2 + TB


def attention_operands(nc, h, x1, v, qk_rows, ident, io):
    with Memory(nc, "qk") as m:
        z0 = Normed(m, "ln0")
        z = Normed(m, "ln1")
        wqk = m.sbuf("wqk", [CH, 2, 2 * C])
        wv = m.sbuf("wv", [CH, 2, C])
        ln = m.sbuf("ln", [CH, 2, 2])
        parts = m.sbuf("parts", [CH, 2, 2, PARTS, N], BF16)
        rest = m.sbuf("rest", [CH, HALF])
        bank = m.psum("bank", [P, 8, 512])
        banks = (3, 4, 5, 6, 7)
        (loaded, set_up, filled, taken, stored, dve_own) = m.sems(*"loaded set_up filled taken stored dve_own".split())
        pairs = ((wqk, io["att_wqk"]), (wv, io["att_wv"]), (ln, io["att_ln"]))
        LOADED = 16 * len(pairs)
        with nc.Block() as block:

            @block.sync
            def _(sp):
                load(sp, pairs, loaded)
                with sp.Fori(0, B) as b:
                    sp.wait_ge(taken, b * QK_ITEMS + len(banks) + 8)
                    for half in range(2):
                        dst = qk_rows[bass.ds(b * 2 * PARTS, 2 * PARTS), half * CH:(half + 1) * CH, :]
                        sp.dma_start(dst.rearrange("i c n -> c i n"), parts[:, half].rearrange("c i s n -> c (i s) n")).then_inc(stored, 16)
                sp.wait_ge(stored, 32 * B + 32)

            @block.gpsimd
            def _(pool):
                nc.gpsimd.memset(v[:, :, :, :], 1.0).then_inc(set_up, 1)

            @block.vector
            def _(dve):
                own = InOrder(dve, dve_own, 2 * NORM_STEPS + 1 + 8 * 3)
                ring = Ring(dve, banks, filled, taken, QK_ITEMS)
                dve.sem_inc(taken, len(banks))
                dve.sem_inc(stored, 32)
                dve.wait_ge(loaded, LOADED)
                dve.wait_ge(set_up, 1)

                def norms(b, n):
                    norm_rows(nc, dve, own, z0, lambda s: h[:, b * TB + s, :], n, lambda s: x1[:, b * TB + s, :])
                    dve.wait_ge(z0.xn_ready, n * TB + TB)
                    own.sem_step()
                    norm_rows(nc, dve, own, z, lambda s: x1[:, b * TB + s, :], n)

                norms(0, 0)
                with dve.Fori(0, B) as b:
                    own.turn(b, 2 * NORM_STEPS + 1)
                    ring.turn(b)
                    dve.wait_ge(stored, b * 32 + 32)
                    for i in range(2):
                        for half in range(2):
                            for c in range(2):
                                slot = ring.get()
                                cols = slice(c * HALF, (c + 1) * HALF)
                                ring.take(split_bf16(nc, own, bank[0:CH, slot, 0:HALF], [parts[:, half, i, p, cols] for p in range(PARTS)],
                                                     rest[:, :]))
                                ring.done()
                    norms(following(b), b + 1)
                    for s in range(TB):
                        slot = ring.get()
                        ring.take(nc.vector.tensor_scalar(v[:, b * TB + s, :, 0:D], bank[:, slot, 0:C].rearrange("p (h d) -> p h d", h=H),
                                                          1.0, None, ALU.mult))
                    ring.ended()
                    own.ended()

            @block.scalar
            def _(act):
                act.wait_ge(loaded, LOADED)
                with act.Fori(0, B + 1) as n:
                    root(nc, act, z0, n)
                    root(nc, act, z, n)
                    act.wait_ge(z.psum_ready, n + 1)
                    copy_transposed(nc, bank, z.xT, z.xT_ready, ln[:, 0, :], ln[:, 1, :])

            @block.tensor
            def _(pe):
                ring = Ring(pe, banks, filled, taken, QK_ITEMS)
                pe.wait_ge(loaded, LOADED)
                pe.wait_ge(z.xn_ready, TB)
                transpose_rows(nc, pe, lambda s, k: z.xn[:, s, k * CH:(k + 1) * CH], ident, bank, z.psum_ready)
                with pe.Fori(0, B) as b:
                    ring.restart(b)
                    pe.wait_ge(z.xT_ready, b * COPIES + COPIES)
                    for i in range(2):
                        for half in range(2):
                            for c in range(2):
                                slot = ring.free()
                                at = i * C + half * CH
                                for k in range(2):
                                    ins = nc.tensor.matmul(bank[0:CH, slot, 0:HALF], wqk[:, k, at:at + CH], z.xT[0:CH, k, c * HALF:(c + 1) * HALF],
                                                           start=(k == 0), stop=(k == 1))
                                ring.fill(ins)
                    for s in range(TB):
                        slot = ring.free()
                        for k in range(2):
                            ins = nc.tensor.matmul(bank[:, slot, 0:C], z.xT[0:CH, k, s * P:(s + 1) * P], wv[:, k, :], start=(k == 0), stop=(k == 1))
                        ring.fill(ins)
                    pe.wait_ge(z.xn_ready, b * TB + 2 * TB)
                    transpose_rows(nc, pe, lambda s, k: z.xn[:, s, k * CH:(k + 1) * CH], ident, bank, z.psum_ready)
                    ring.ended()


WINDOW = 96
MAX_ITEMS = H * TB
OUT_ITEMS = H + TB
EXP_ITEMS = H + H * TB + 2
EARLY = 3
ROWS_AT = 2
MAX_LAG, PV_LAG = 2, 3


def softmax_attention(nc, x1, v, qk_rows, ident, io):
    with Memory(nc, "att") as m:
        q = m.sbuf("q", [ALL_ROWS, H, N], BF16)
        k = m.sbuf("k", [ALL_ROWS, H, N], BF16)
        wp = m.sbuf("wp", [CH, 2, C])
        ident16 = m.sbuf("ident16", [P, P], BF16)
        vb = m.sbuf("vb", [P, TB, H * DV])
        negmax = m.sbuf("negmax", [P, H, TB])
        rest = m.sbuf("rest", [P, TB])
        placed = m.sbuf("placed", [P, 2, TB, ALL_ROWS], BF16)
        probs = m.sbuf("probs", [P, 2, TB, N])
        recip = m.sbuf("recip", [P, TB])
        attn = m.sbuf("attn", [P, TB, C])
        aT = m.sbuf("aT", [CH, 2, N])
        bank = m.psum("bank", [P, 8, 512])
        exp_banks, banks, out_banks = (0, 2), (4,), (6, 7)
        (loaded, set_up, filled, taken, exp_filled, exp_taken, out_filled, out_taken, placed_ready, v_ready, lot_used, ones_ready, dve_own) = m.sems(
            *"loaded set_up filled taken exp_filled exp_taken out_filled out_taken placed_ready v_ready lot_used ones_ready dve_own".split())
        lot_in = m.sems(*(f"lot_in{i}" for i in range(LOTS)))
        LOT_IN = 16 * 2 * len(STACK)

        def two(slot, rows=P):
            return bank[0:rows, slot:slot + 2, 0:HALF]

        def halves(ap):
            return ap.rearrange("p (c n) -> p c n", c=2)

        with nc.Block() as block:

            @block.sync
            def _(sp):
                load(sp, ((wp, io["att_wp"]),), loaded)
                with sp.Fori(0, B) as b:
                    for lot in range(LOTS):
                        heads = slice(lot * LOT, (lot + 1) * LOT)
                        sp.wait_ge(lot_used, b * LOTS + lot + 1)
                        for i, buf in enumerate((q, k)):
                            for at, pair in enumerate(STACK):
                                src = qk_rows[bass.ds((b * 2 + i) * PARTS + pair[i], 1), lot * LOT * D:(lot + 1) * LOT * D, :]
                                sp.dma_start(buf[at * D:(at + 1) * D, heads, :], src.rearrange("o (h d) n -> d (o h) n", d=D)).then_inc(lot_in[lot], 16)

            @block.gpsimd
            def _(pool):
                nc.gpsimd.memset(k[ROWS:ALL_ROWS, :, :], 1.0).then_inc(ones_ready, 1)
                pool.wait_ge(ones_ready, 1)
                nc.gpsimd.memset(placed[:, :, :, :], 0.0).then_inc(set_up, 1)

            @block.vector
            def _(dve):
                own = InOrder(dve, dve_own, H * 4)
                ring = Ring(dve, banks, filled, taken, MAX_ITEMS)
                outs = Ring(dve, out_banks, out_filled, out_taken, OUT_ITEMS)
                dve.sem_inc(taken, len(banks))
                dve.sem_inc(out_taken, len(out_banks))
                dve.wait_ge(loaded, 16)
                nc.vector.tensor_copy(ident16[:, :], ident[:, :]).then_inc(set_up, 1)
                dve.wait_ge(set_up, 2)

                def maxima(head, s):
                    slot = ring.get()
                    ring.take(nc.vector.tensor_reduce(negmax[:, head, s:s + 1], two(slot), AX.XY, ALU.max, negate=True))

                def place(head):
                    ring.done()
                    cols = [placed[:, head % 2, :, ROWS + p] for p in range(PARTS)]
                    split_bf16(nc, own, negmax[:, head, :], cols, rest[:, :]).then_inc(placed_ready, 1)

                def normalize(head):
                    outs.done()
                    slot = outs.get()
                    at = head * DV - min(head * DV, H * DV - WINDOW)
                    got = bank[:, slot, 0:TB * WINDOW].rearrange("p (s c) -> p s c", s=TB)
                    own.step(nc.vector.reciprocal(recip[:, :], got[:, :, at + D]))
                    outs.take(nc.vector.tensor_tensor(attn[:, :, head * D:(head + 1) * D], got[:, :, at:at + D],
                                                      recip[:, :].unsqueeze(2).to_broadcast([P, TB, D]), ALU.mult))

                def take_values(b):
                    nc.vector.tensor_scalar(vb[:, :, :], v[:, bass.ds(b * TB, TB), :, :].rearrange("p s h c -> p s (h c)"), 1.0, None,
                                            ALU.mult).then_inc(v_ready, 1)

                def turn(b, i, old, new):
                    if new:
                        for s in range(TB):
                            maxima(i, s)
                        place(i)
                    if exists(i, PV_LAG, old, new):
                        normalize((i - PV_LAG) % H)

                def add(b):
                    for s in range(TB):
                        slot = outs.get()
                        row = x1[:, b * TB + s, :]
                        outs.take(nc.vector.tensor_tensor(row, row, bank[:, slot, 0:C], ALU.add))

                take_values(0)
                for i in range(EARLY):
                    turn(0, i, False, True)
                before = [r.n for r in (own, ring, outs)]
                with dve.Fori(0, B - 1) as b:
                    for r, n in zip((own, ring, outs), before):
                        r.turn(b, n)
                    batch(turn, b, True)
                    add(b)
                    take_values(b + 1)
                    for r in (ring, outs, own):
                        r.ended()
                for r, n in zip((own, ring, outs), before):
                    r.turn(B - 1, n)
                batch(turn, B - 1, False)
                add(B - 1)

            @block.scalar
            def _(act):
                ring = Ring(act, exp_banks, exp_filled, exp_taken, EXP_ITEMS)
                act.sem_inc(exp_taken, len(exp_banks))

                def turn(b, i, old, new):
                    for t in range(TB):
                        if t == ROWS_AT and exists(i, 1, old, new):
                            head = (i - 1) % H
                            slot = ring.get()
                            got = bank[ROWS:ALL_ROWS, slot:slot + 2, :]
                            nc.scalar.activation(q[ROWS:ALL_ROWS, head, 0:4 * P], got[:, 0, :], ACT.Copy)
                            ring.take(nc.scalar.activation(q[ROWS:ALL_ROWS, head, 4 * P:], got[:, 1, 0:P], ACT.Copy))
                        if exists(i, MAX_LAG, old, new):
                            head = (i - MAX_LAG) % H
                            slot = ring.get()
                            ring.take(nc.scalar.activation(halves(probs[:, head % 2, t, :]), two(slot), ACT.Exp, scale=float(D) ** -0.5))

                def transposed():
                    for half in range(2):
                        slot = ring.get()
                        nc.scalar.activation(aT[:, half, 0:4 * P], bank[0:CH, slot, :], ACT.Copy)
                        ring.take(nc.scalar.activation(aT[:, half, 4 * P:], bank[0:CH, slot + 1, 0:P], ACT.Copy))

                for i in range(EARLY):
                    turn(0, i, False, True)
                before = ring.n
                with act.Fori(0, B - 1) as b:
                    ring.turn(b, before)
                    batch(turn, b, True)
                    transposed()
                    ring.ended()
                ring.turn(B - 1, before)
                batch(turn, B - 1, False)
                transposed()

            @block.tensor
            def _(pe):
                ring = Ring(pe, banks, filled, taken, MAX_ITEMS)
                exps = Ring(pe, exp_banks, exp_filled, exp_taken, EXP_ITEMS)
                outs = Ring(pe, out_banks, out_filled, out_taken, OUT_ITEMS)
                pe.sem_inc(lot_used, LOTS)
                pe.wait_ge(loaded, 16)
                pe.wait_ge(ones_ready, 1)
                pe.wait_ge(set_up, 2)

                def queries_first(head, s):
                    slot = ring.free()
                    for c in range(2):
                        ins = nc.tensor.matmul(bank[:, slot + c, 0:HALF], q[0:ROWS, head, s * P:(s + 1) * P], k[0:ROWS, head, c * HALF:(c + 1) * HALF],
                                               start=True, stop=True)
                    ring.fill(ins)

                def keys_first(head, t):
                    slot = exps.free()
                    for c in range(2):
                        ins = nc.tensor.matmul(bank[:, slot + c, 0:HALF], k[:, head, t * P:(t + 1) * P], q[:, head, c * HALF:(c + 1) * HALF],
                                               start=True, stop=True)
                    exps.fill(ins)

                def max_rows(placed_before, head):
                    pe.wait_ge(placed_ready, placed_before)
                    slot = exps.free()
                    for s in range(TB):
                        ins = nc.tensor.matmul(bank[0:ALL_ROWS, slot + s // 4, (s % 4) * P:(s % 4 + 1) * P], placed[:, head % 2, s, :], ident16[:, :],
                                               start=True, stop=True)
                    exps.fill(ins)

                def times_v(head, s):
                    slot = outs.free() if s == 0 else outs.bank()
                    at = min(head * DV, H * DV - WINDOW)
                    for t in range(TB):
                        ins = nc.tensor.matmul(bank[:, slot, s * WINDOW:(s + 1) * WINDOW], probs[:, head % 2, t, s * P:(s + 1) * P],
                                               vb[:, t, at:at + WINDOW], start=(t == 0), stop=(t == TB - 1))
                    if s == TB - 1:
                        outs.fill(ins)

                in_at = {}

                def turn(b, i, old, new):
                    if new and i % LOT == 0:
                        pe.wait_ge(lot_in[i // LOT], (b + 1) * LOT_IN)
                    rows_head, exp_head, v_head = [(i - lag) % H if exists(i, lag, old, new) else None for lag in (1, MAX_LAG, PV_LAG)]
                    for what in (("rows", exp_head), ("probs", v_head)):
                        if what in in_at:
                            exps.arrived(in_at[what])
                    for s in range(TB):
                        if s == ROWS_AT and rows_head is not None:
                            max_rows(b * H + i, rows_head)
                            in_at["rows", rows_head] = exps.n
                        if new:
                            queries_first(i, s)
                        if exp_head is not None:
                            keys_first(exp_head, s)
                            in_at["probs", exp_head] = exps.n
                        if v_head is not None:
                            times_v(v_head, s)
                    if v_head is not None and v_head % LOT == LOT - 1:
                        pe.wait_ge(out_filled, outs.base + outs.n)
                        pe.sem_inc(lot_used, 1)

                def project():
                    outs.arrived()
                    for half in range(2):
                        slot = exps.free()
                        for s in range(TB):
                            ins = nc.tensor.transpose(bank[0:CH, slot + s // 4, (s % 4) * P:(s % 4 + 1) * P], attn[:, s, half * CH:(half + 1) * CH],
                                                      ident[:, :])
                        exps.fill(ins)
                    exps.arrived()
                    for s in range(TB):
                        slot = outs.free()
                        for half in range(2):
                            ins = nc.tensor.matmul(bank[:, slot, 0:C], aT[:, half, s * P:(s + 1) * P], wp[:, half, :], start=(half == 0), stop=(half == 1))
                        outs.fill(ins)

                def one_batch(b, more):
                    for r, n in zip((ring, exps, outs), before):
                        r.restart(b, n)
                    in_at.clear()
                    pe.wait_ge(v_ready, b + 1)
                    batch(turn, b, more)
                    project()

                for i in range(EARLY):
                    turn(0, i, False, True)
                before = [r.n for r in (ring, exps, outs)]
                with pe.Fori(0, B - 1) as b:
                    one_batch(b, True)
                    for r in (ring, exps, outs):
                        r.ended()
                one_batch(B - 1, False)


def exists(i, lag, old, new):
    return new if i >= lag else old


def batch(turn, b, more):
    for i in range(EARLY, H):
        turn(b, i, False, True)
    for i in range(EARLY):
        turn(b + 1, i, True, more)


E = 8
FF = 4 * C
FFT = FF // P


def slots_for(k):
    n = k * TILES + E - 1
    return n + n % 2


def route_tokens(nc, name, k, src, share, table, x_rows, weights, weights_in, ident, ln, io):
    slots = slots_for(k)
    with Memory(nc, f"{name}_route") as m:
        z = Normed(m, "ln")
        wr = m.sbuf("wr", [CH + 1, 2, NARROW])
        ones = m.sbuf("ones", [P, P])
        earlier = m.sbuf("earlier", [P, P])
        before = m.sbuf("before", [P, E, E])
        slot_no = m.sbuf("slot_no", [1, slots])
        xn = m.sbuf("xn", [P, TILES, C + 1])
        where = m.sbuf("where", [P, k, TILES], I32)
        home = m.sbuf("home", [P, TILES])
        logits = m.sbuf("logits", [P, TILES, E])
        above = m.sbuf("above", [P, TILES, E, E])
        ties = m.sbuf("ties", [P, TILES, E, E])
        rank = m.sbuf("rank", [P, TILES, E])
        chosen = m.sbuf("chosen", [P, k, TILES, E])
        either = m.sbuf("either", [P, TILES, E])
        best = m.sbuf("best", [P, 2, TILES])
        last_tile = m.sbuf("last_tile", [P, E, TILES + 1])
        keep = m.sbuf("keep", [P, E, TILES + 1])
        ahead = m.sbuf("ahead", [P, E, TILES + 1])
        used = m.sbuf("used", [P, E])
        first_slot = m.sbuf("first_slot", [P, E + 1])
        keep_slots = m.sbuf("keep_slots", [P, E])
        row = m.sbuf("row", [P, TILES, E])
        picked = m.sbuf("picked", [P, k, TILES, E])
        row_f = m.sbuf("row_f", [P, k, TILES])
        passed = m.sbuf("passed", [1, slots, E])
        expert_f = m.sbuf("expert_f", [1, slots + 2])
        bank = m.psum("bank", [P, 8, 512])
        LOGITS, EARLIER, TOTAL = 3, 0, 1
        (loaded, set_up, blank_in, home_ready, logits_psum, gap_ready, exp_ready, chosen_ready, counted, where_ready,
         kept, copied, pool_own, scattered, dve_own, router_step) = m.sems(*(
             "loaded set_up blank_in home_ready logits_psum gap_ready exp_ready chosen_ready counted where_ready kept copied pool_own scattered "
             "dve_own router_step").split())
        pairs = ((wr, io[f"{name}_wr"]), (before, io["before"]), (earlier, io["earlier"]), (slot_no, io["slot_no"][:, 0:slots]), (home, io["home"]))
        LOADED = 16 * len(pairs)

        def other(ap):
            return ap.unsqueeze(2).to_broadcast([P, TILES, E, E])

        def this(ap):
            return ap.unsqueeze(3).to_broadcast([P, TILES, E, E])

        with nc.Block() as block:

            @block.sync
            def _(sp):
                load(sp, pairs, loaded)
                sp.dma_start(x_rows, io[f"{name}_blank"]).then_inc(blank_in, 16)
                for dst, src in weights:
                    sp.dma_start(dst, src).then_inc(weights_in, 16)

            @block.gpsimd
            def _(pool):
                fill(nc, pool, set_up, ((ones[:, :], 1.0), (z.xT[CH:CH + 1, :, :], 1.0)))
                pool.sem_inc(kept, 1)
                with pool.Fori(0, B) as b:
                    pool.wait_ge(z.xn_ready, b * TB + TB)
                    pool.sem_inc(pool_own, 1)
                    nc.gpsimd.tensor_copy(xn[:, bass.ds(b * TB, TB), 0:C], z.xn[:, :, :]).then_inc(copied, 1)
                    pool.wait_ge(copied, b + 1)
                    pool.wait_ge(z.psum_ready, b + 1)
                    pool.sem_inc(kept, 1)
                pool.wait_ge(blank_in, 16)
                pool.wait_ge(where_ready, 1)
                for j in range(k):
                    pool.wait_ge(home_ready, j + 1)
                    pool.sem_inc(pool_own, 1)
                    for t in range(TILES):
                        nc.gpsimd.indirect_dma_start(out=x_rows, out_offset=bass.IndirectOffsetOnAxis(ap=where[:, j, t:t + 1], axis=0),
                                                     in_=xn[:, t, :], in_offset=None).then_inc(scattered, 16)
                    pool.wait_ge(scattered, 16 * (j + 1) * TILES)

            @block.vector
            def _(dve):
                own = InOrder(dve, dve_own, NORM_STEPS + 1)
                dve.wait_ge(loaded, LOADED)
                with dve.Fori(0, B) as b:
                    own.turn(b)
                    dve.wait_ge(kept, b + 1)
                    own.sem_step()
                    norm_rows(nc, dve, own, z, lambda s: src[:, b * TB + s, :], b)
                    own.ended()
                step = InOrder(dve, router_step)
                nc.vector.tensor_copy(xn[:, :, C], home[:, :]).then_inc(home_ready, 1)
                step.count(nc.vector.memset(last_tile[:, :, 0:1], 0.0))
                step.step(nc.vector.memset(keep[:, :, :], 1.0))
                step.count(nc.vector.memset(keep[:, :, 0:1], 0.0))
                step.count(nc.vector.memset(keep_slots[:, :], 1.0))
                step.step(nc.vector.memset(first_slot[:, 0:1], 0.0))
                dve.wait_ge(logits_psum, B)
                step.step(nc.vector.tensor_copy(logits[:, :, :].rearrange("p (b s) e -> p b s e", b=B),
                                                bank[:, LOGITS:LOGITS + B, 0:TB * NARROW].rearrange("p b (s e) -> p b s e", s=TB)[:, :, :, 0:E]))
                step.count(nc.vector.tensor_tensor(above[:, :, :, :], other(logits[:, :, :]), this(logits[:, :, :]), ALU.is_gt))
                step.step(nc.vector.tensor_tensor(ties[:, :, :, :], other(logits[:, :, :]), this(logits[:, :, :]), ALU.is_equal))
                step.step(nc.vector.tensor_tensor(ties[:, :, :, :], ties[:, :, :, :],
                                                  before[:, :, :].unsqueeze(1).to_broadcast([P, TILES, E, E]), ALU.mult))
                step.step(nc.vector.tensor_tensor(above[:, :, :, :], above[:, :, :, :], ties[:, :, :, :], ALU.add))
                step.step(nc.vector.tensor_reduce(rank[:, :, :], above[:, :, :, :], AX.X, ALU.add))
                for j in range(k):
                    step.count(nc.vector.tensor_scalar(chosen[:, j, :, :], rank[:, :, :], float(j), None, ALU.is_equal))
                step.wait()
                if k == 2:
                    nc.vector.tensor_tensor(either[:, :, :], chosen[:, 0, :, :], chosen[:, 1, :, :], ALU.add).then_inc(chosen_ready, 1)
                    step.count(nc.vector.tensor_reduce(best[:, 0, :], logits[:, :, :], AX.X, ALU.max))
                    step.step(nc.vector.tensor_tensor(row[:, :, :], logits[:, :, :], chosen[:, 1, :, :], ALU.mult))
                    step.step(nc.vector.tensor_reduce(best[:, 1, :], row[:, :, :], AX.X, ALU.add))
                    nc.vector.tensor_tensor(share[:, 1, :], best[:, 1, :], best[:, 0, :], ALU.subtract).then_inc(gap_ready, 1)
                    dve.wait_ge(exp_ready, 1)
                    step.step(nc.vector.tensor_scalar(share[:, 0, :], share[:, 1, :], 1.0, None, ALU.add))
                    step.step(nc.vector.reciprocal(share[:, 0, :], share[:, 0, :]))
                    step.count(nc.vector.tensor_tensor(share[:, 1, :], share[:, 0, :], share[:, 1, :], ALU.mult))
                else:
                    nc.vector.tensor_copy(either[:, :, :], chosen[:, 0, :, :]).then_inc(chosen_ready, 1)
                dve.wait_ge(counted, 1)
                step.step(nc.vector.tensor_copy(last_tile[:, :, 1:].rearrange("p e t -> p t e"),
                                                bank[:, TOTAL, 0:TILES * E].rearrange("p (t e) -> p t e", t=TILES)))
                step.step(nc.vector.tensor_tensor_scan(ahead[:, :, :].rearrange("p e t -> p (e t)"), keep[:, :, :].rearrange("p e t -> p (e t)"),
                                                       last_tile[:, :, :].rearrange("p e t -> p (e t)"), 0.0, ALU.mult, ALU.add))
                step.step(nc.vector.tensor_scalar(used[:, :], ahead[:, :, TILES], (P - 1) / 2, 1.0 / P, ALU.add, ALU.mult))
                step.step(nc.vector.tensor_scalar(used[:, :], used[:, :], ROUND, None, ALU.add))
                step.step(nc.vector.tensor_scalar(used[:, :], used[:, :], ROUND, None, ALU.subtract))
                step.step(nc.vector.tensor_tensor_scan(first_slot[:, 1:], keep_slots[:, :], used[:, :], 0.0, ALU.mult, ALU.add))
                step.step(nc.vector.tensor_scalar(used[:, :], first_slot[:, 0:E], float(P), None, ALU.mult))
                step.step(nc.vector.tensor_tensor(row[:, :, :], bank[:, EARLIER, 0:TILES * E].rearrange("p (t e) -> p t e", t=TILES),
                                                  ahead[:, :, 0:TILES].rearrange("p e t -> p t e"), ALU.add))
                step.step(nc.vector.tensor_tensor(row[:, :, :], row[:, :, :], used[:, :].unsqueeze(1).to_broadcast([P, TILES, E]), ALU.add))
                step.step(nc.vector.tensor_tensor(picked[:, :, :, :], chosen[:, :, :, :],
                                                  row[:, :, :].unsqueeze(1).to_broadcast([P, k, TILES, E]), ALU.mult))
                step.step(nc.vector.tensor_reduce(row_f[:, :, :], picked[:, :, :, :], AX.X, ALU.add))
                nc.vector.tensor_copy(where[:, :, :], row_f[:, :, :]).then_inc(where_ready, 1)
                step.count(nc.vector.memset(expert_f[:, :], 0.0))
                step.step(nc.vector.tensor_tensor(passed[:, :, :], first_slot[0:1, 1:E + 1].unsqueeze(1).to_broadcast([1, slots, E]),
                                                  slot_no[:, :].unsqueeze(2).to_broadcast([1, slots, E]), ALU.is_le))
                step.step(nc.vector.tensor_reduce(expert_f[:, 2:], passed[:, :, :], AX.X, ALU.add))
                step.step(nc.vector.tensor_scalar(expert_f[:, :], expert_f[:, :], float(E - 1), None, ALU.min))
                step.step(nc.vector.tensor_copy(table[:, :], expert_f[:, :]))
                if k == 2:
                    dve.wait_ge(scattered, 16 * TILES)
                    nc.vector.tensor_scalar(xn[:, :, C], home[:, :], float(B * N), None, ALU.add).then_inc(home_ready, 1)

            @block.scalar
            def _(act):
                act.wait_ge(loaded, LOADED)
                with act.Fori(0, B) as b:
                    root(nc, act, z, b)
                    act.wait_ge(z.psum_ready, b + 1)
                    copy_transposed(nc, bank, z.xT, z.xT_ready, *((ln[:, 0, :], ln[:, 1, :]) if k == 2 else ()))
                if k == 2:
                    act.wait_ge(gap_ready, 1)
                    nc.scalar.activation(share[:, 1, :], share[:, 1, :], ACT.Exp).then_inc(exp_ready, 1)

            @block.tensor
            def _(pe):
                pe.wait_ge(loaded, LOADED)
                pe.wait_ge(set_up, 2)
                with pe.Fori(0, B) as b:
                    pe.wait_ge(z.xn_ready, b * TB + TB)
                    transpose_rows(nc, pe, lambda s, c: z.xn[:, s, c * CH:(c + 1) * CH], ident, bank, z.psum_ready)
                    pe.wait_ge(z.xT_ready, b * COPIES + COPIES)
                    for s in range(TB):
                        for c in range(2):
                            out = bank[:, bass.ds(b + LOGITS, 1), s * NARROW:(s + 1) * NARROW].rearrange("p o e -> p (o e)")
                            ins = nc.tensor.matmul(out, z.xT[rows_of(c, k == 1), c, s * P:(s + 1) * P],
                                                   wr[rows_of(c, k == 1), c, :], start=(c == 0), stop=(c == 1))
                    ins.then_inc(logits_psum, 1)
                pe.wait_ge(chosen_ready, 1)
                mask = either[:, :, :].rearrange("p t e -> p (t e)")
                nc.tensor.matmul(bank[:, EARLIER, 0:TILES * E], earlier[:, :], mask, start=True, stop=True)
                nc.tensor.matmul(bank[:, TOTAL, 0:TILES * E], ones[:, :], mask, start=True, stop=True).then_inc(counted, 1)


def always(d):
    return True


def run_slots(nc, name, k, table, x_rows, y_rows, w1, w2, b2, weights_in, ident, ln):
    slots = slots_for(k)
    rows = CH if k == 2 else CH + 1
    with Memory(nc, f"{name}_slots") as m:
        x = m.sbuf("x", [P, 2, C + 1])
        stage = m.sbuf("stage", [P, 2])
        dest = m.sbuf("dest", [P, 2], I32)
        xT = m.sbuf("xT", [CH + 1, 2, 2, P])
        wide = m.sbuf("wide", [CH + 1, 2, 2, FF])
        hT = m.sbuf("hT", [P, 2, FFT, P])
        y = m.sbuf("y", [P, 2, C])
        bank = m.psum("bank", [P, 8, 512])
        UP, OUT, XT = (0, 2), 6, 7
        (ones_ready, staged, dest_ready, pool_own, wide_ready, xT_psum, xT_ready, up_psum, hT_ready, y_psum, y_ready) = m.sems(
            *"ones_ready staged dest_ready pool_own wide_ready xT_psum xT_ready up_psum hT_ready y_psum y_ready".split())
        x_in = m.sems("x_in0", "x_in1")
        y_stored = m.sems("y_stored0", "y_stored1")
        PARTS_OF_FF = ((0, 4), (4, FFT))

        def by_slot(dram, i):
            return dram[bass.ds(i * P, P), :]

        def turns(eng, turn):
            def some(p, n):
                for c in range(n):
                    i = p * 2 + c
                    turn(i, c, p, lambda d: 0 <= i + d < slots)

            some(0, 2)
            some(1, 2)
            with eng.Fori(2, slots // 2 - 1) as p:
                for c in range(2):
                    turn(p * 2 + c, c, p, always)
            some(slots // 2 - 1, 2)
            some(slots // 2, 1)

        def experts_of(engine, at, n, fixed):
            entries = table[0:1, at:at + n] if fixed else table[0:1, bass.ds(at, n)]
            return nc.values_load_multi_w_load_instructions(entries, engines=[engine], min_val=0, max_val=E - 1)[1]

        with nc.Block() as block:

            @block.sync
            def _(sp):
                def turn(i, c, p, exists):
                    if exists(0) and exists(2):
                        sp.wait_ge(xT_psum, i + 1)
                        sp.wait_ge(staged, i + 1)
                        sp.dma_start(x[:, c, :], by_slot(x_rows, i + 2)).then_inc(x_in[c], 16)

                for c in range(2):
                    sp.dma_start(x[:, c, :], by_slot(x_rows, c)).then_inc(x_in[c], 16)
                turns(sp, turn)

            @block.gpsimd
            def _(pool):
                nc.gpsimd.memset(xT[CH:CH + 1, :, :, :], 1.0).then_inc(ones_ready, 1)

                def turn(i, c, p, exists):
                    if exists(-1):
                        pool.wait_ge(y_ready, i + 1)
                        pool.wait_ge(dest_ready, i)
                        pool.sem_inc(pool_own, 1)
                        nc.gpsimd.indirect_dma_start(out=y_rows, out_offset=bass.IndirectOffsetOnAxis(ap=dest[:, 1 - c:2 - c], axis=0),
                                                     in_=y[:, 1 - c, :], in_offset=None).then_inc(y_stored[1 - c], 16)

                turns(pool, turn)
                for c in range(2):
                    pool.wait_ge(y_stored[c], 16 * (slots // 2))

            @block.vector
            def _(dve):
                dve.sem_inc(y_ready, 1)

                def copy_wide(c, e):
                    nc.vector.tensor_scalar(wide[0:rows, c, :, :], w1[0:rows, bass.ds(e, 1), :, :].rearrange("p o h f -> p (o h) f"),
                                            1.0, None, ALU.mult).then_inc(wide_ready, 1)

                following, preceding = [], []

                def turn(i, c, p, exists):
                    if c == 0 and exists(1):
                        following[:] = experts_of(mybir.EngineType.DVE, i + 3, 2 if exists(2) else 1, exists is not always)
                    if c == 0 and k == 1:
                        preceding[:] = experts_of(mybir.EngineType.DVE, i + 1, 2 if exists(0) else 1, exists is not always)
                    if exists(0):
                        dve.wait_ge(xT_psum, i + 1)
                        if exists(-2):
                            dve.wait_ge(dest_ready, i - 1)
                        nc.vector.tensor_copy(stage[:, c:c + 1], x[:, c, C:C + 1]).then_inc(staged, 1)
                    if exists(1) and exists(0):
                        if exists(-1):
                            dve.wait_ge(up_psum, i * 2)
                        copy_wide(1 - c, following[c])
                    if exists(-1):
                        dve.wait_ge(y_psum, i)
                        if exists(-3):
                            dve.wait_ge(y_stored[1 - c], (p + c - 1) * 16)
                        dve.wait_ge(staged, i)
                        nc.vector.tensor_copy(dest[:, 1 - c:2 - c], stage[:, 1 - c:2 - c]).then_inc(dest_ready, 1)
                        if k == 2:
                            ins = nc.vector.tensor_copy(y[:, 1 - c, :], bank[:, OUT, 0:C])
                        else:
                            bias = b2[:, bass.ds(preceding[c], 1), :].rearrange("p o c -> p (o c)")
                            ins = nc.vector.tensor_tensor(y[:, 1 - c, :], bank[:, OUT, 0:C], bias, ALU.add)
                        ins.then_inc(y_ready, 1)

                dve.wait_ge(*weights_in)
                copy_wide(0, experts_of(mybir.EngineType.DVE, 2, 1, True)[0])
                turns(dve, turn)

            @block.scalar
            def _(act):
                def rows_in(i, c):
                    act.wait_ge(xT_psum, i + 1)
                    for half in range(2):
                        src, dst = bank[0:CH, XT, half * P:(half + 1) * P], xT[0:CH, c, half, :]
                        if k == 2:
                            ins = nc.scalar.activation(dst, src, ACT.Identity, scale=ln[:, 0, half:half + 1], bias=ln[:, 1, half:half + 1])
                        else:
                            ins = nc.scalar.activation(dst, src, ACT.Copy)
                        ins.then_inc(xT_ready, 1)

                def turn(i, c, p, exists):
                    if exists(0):
                        for part, (f0, f1) in enumerate(PARTS_OF_FF):
                            act.wait_ge(up_psum, i * 2 + part + 1)
                            nc.scalar.activation(hT[:, c, f0:f1, :], bank[:, UP[c] + part, 0:(f1 - f0) * P].rearrange("p (f t) -> p f t", t=P),
                                                 ACT.Gelu).then_inc(hT_ready, 1)
                    if exists(1) and exists(0):
                        rows_in(i + 1, 1 - c)

                rows_in(0, 0)
                turns(act, turn)

            @block.tensor
            def _(pe):
                def transpose_x(i, c, p):
                    pe.wait_ge(x_in[c], p * 16 + 16)
                    for half in range(2):
                        ins = nc.tensor.transpose(bank[0:CH, XT, half * P:(half + 1) * P], x[:, c, half * CH:(half + 1) * CH], ident[:, :])
                    ins.then_inc(xT_psum, 1)

                def widen(i, c):
                    pe.wait_ge(wide_ready, i + 1)
                    pe.wait_ge(xT_ready, i * 2 + 2)
                    for part, (f0, f1) in enumerate(PARTS_OF_FF):
                        for f in range(f0, f1):
                            for half in range(2):
                                n = rows if half else CH
                                ins = nc.tensor.matmul(bank[:, UP[c] + part, (f - f0) * P:(f - f0 + 1) * P], wide[0:n, c, half, f * P:(f + 1) * P],
                                                       xT[0:n, c, half, :], start=(half == 0), stop=(half == 1))
                        ins.then_inc(up_psum, 1)

                def narrow(c, e):
                    for f in range(FFT):
                        ins = nc.tensor.matmul(bank[:, OUT, 0:C], hT[:, c, f, :], w2[:, bass.ds(e, 1), f, :].rearrange("p o c -> p (o c)"),
                                               start=(f == 0), stop=(f == FFT - 1))
                    ins.then_inc(y_psum, 1)

                preceding = []

                def turn(i, c, p, exists):
                    if c == 0:
                        preceding[:] = experts_of(mybir.EngineType.PE, i + 1, 2 if exists(0) else 1, exists is not always)
                    if exists(0):
                        widen(i, c)
                        if exists(1):
                            transpose_x(i + 1, 1 - c, p + c)
                    if exists(-1):
                        pe.wait_ge(hT_ready, i * 2)
                        pe.wait_ge(y_ready, i)
                        narrow(1 - c, preceding[c])

                pe.wait_ge(*weights_in)
                pe.wait_ge(ones_ready, 1)
                transpose_x(0, 0, 0)
                turns(pe, turn)


def combine(nc, name, k, h, x1, share, y_rows):
    with Memory(nc, f"{name}_combine") as m:
        found = m.sbuf("found", [P, B, k, TB, C])
        base_ready, scaled, added = m.sems("base_ready", "scaled", "added")
        found_in = m.sems(*(f"found_in{b}" for b in range(B)))
        with nc.Block() as block:

            @block.sync
            def _(sp):
                tokens = y_rows[0:k * B * N, :].rearrange("(j b s p) c -> p b j s c", j=k, b=B, p=P)
                for b in range(B):
                    for j in range(k):
                        sp.dma_start(found[:, b, j, :, :], tokens[:, b, j, :, :]).then_inc(found_in[b], 16)

            @block.vector
            def _(dve):
                done = InOrder(dve, added)
                for b in range(B):
                    rows = h[:, b * TB:(b + 1) * TB, :]
                    if k == 1:
                        dve.wait_ge(found_in[b], 16)
                        done.step(nc.vector.tensor_tensor(rows, rows, found[:, b, 0, :, :], ALU.add))
                        continue
                    dve.wait_ge(base_ready, b + 1)
                    dve.wait_ge(found_in[b], 16 * k)
                    for s in range(TB):
                        t = b * TB + s
                        done.count(nc.vector.scalar_tensor_tensor(h[:, t, :], found[:, b, 1, s, :], share[:, 1, t:t + 1], h[:, t, :],
                                                                  ALU.mult, ALU.add))
                    done.wait()
                    dve.wait_ge(scaled, (b + 1) * TB)
                    done.step(nc.vector.tensor_tensor(rows, rows, found[:, b, 0, :, :], ALU.add))

            @block.gpsimd
            def _(pool):
                if k == 2:
                    for b in range(B):
                        rows = h[:, b * TB:(b + 1) * TB, :]
                        nc.gpsimd.tensor_tensor(rows, rows, x1[:, b * TB:(b + 1) * TB, :], ALU.add).then_inc(base_ready, 1)

            @block.scalar
            def _(act):
                if k == 2:
                    for b in range(B):
                        act.wait_ge(found_in[b], 16 * k)
                        for s in range(TB):
                            t = b * TB + s
                            nc.scalar.activation(found[:, b, 0, s, :], found[:, b, 0, s, :], ACT.Copy, scale=share[:, 0, t:t + 1]).then_inc(scaled, 1)


def experts(nc, h, x1, ident, io, top2):
    name, k = ("moe", 2) if top2 else ("ffn", 1)
    slots = slots_for(k)
    x_rows, y_rows = (nc.dram_tensor(f"{name}_{r}_rows", shape, F32, kind="Internal").ap()
                      for r, shape in (("x", (slots * P, C + 1)), ("y", (k * B * N + slots * P, C))))
    with Memory(nc, name) as m:
        share = m.sbuf("share", [P, k, TILES])
        table = m.sbuf("table", [1, slots + 2], I32)
        w1 = m.sbuf("w1", [CH + 1, E, 2, FF])
        w2 = m.sbuf("w2", [P, E, FFT, C])
        b2 = m.sbuf("b2", [P, E, C]) if k == 1 else None
        ln = m.sbuf("ln_gb", [CH, 2, 2])
        weights_in, ln_in = m.sems("weights_in", "ln_in")
        weights = [(w1[0:CH, e, :, :], io[f"{name}_w1"][e]) for e in range(E)] + [(w2[:, e, :, :], io[f"{name}_w2"][e]) for e in range(E)]
        if k == 1:
            weights += [(w1[CH:CH + 1, :, :, :], io["ffn_b1"]), (b2[:, :, :], io["ffn_b2"])]
        if k == 2:
            with nc.Block() as block:

                @block.sync
                def _(sp):
                    sp.dma_start(ln[:, :, :], io["moe_ln"]).then_inc(ln_in, 16)
                    sp.wait_ge(ln_in, 16)

        route_tokens(nc, name, k, x1 if top2 else h, share, table, x_rows, weights, weights_in, ident, ln, io)
        run_slots(nc, name, k, table, x_rows, y_rows, w1, w2, b2, (weights_in, 16 * len(weights)), ident, ln)
        combine(nc, name, k, h, x1, share, y_rows)


CK = 16
NC = N // CK
CB = GH * CK
WIDTH = 6
DVE_EACH = 11
EACH = 16
STREAMS = 2 * B
PATHS = 5
SIDE = C + H + H * PATHS
SHORT, LONG = 3, 7
PAD = LONG - 1
MIX_ITEMS = 4 + TB + TB + 4 + TB + TB + 1


def mix_paths(nc, h, part, delta_weight, kq, k_rows, v_rows, ident, io):
    with Memory(nc, "mix") as m:
        z = Normed(m, "ln")
        wq = m.sbuf("wq", [CH, 2, C])
        wkv = m.sbuf("wkv", [CH, 2, 2 * C])
        wside = m.sbuf("wside", [CH + 1, 2, SIDE])
        wg1 = m.sbuf("wg1", [CH, 2, C])
        bg1 = m.sbuf("bg1", [CH, 2])
        wg2 = m.sbuf("wg2", [CH + 1, 2, NARROW])
        static = m.sbuf("static", [P, H])
        taps = m.sbuf("taps", [CH, 2, SHORT + LONG])
        mixer = m.sbuf("mixer", [CH, 2, C])
        same_dim = m.sbuf("same_dim", [CH, 2, C])
        same = m.sbuf("same", [CH, 2, C])
        kv = m.sbuf("kv", [P, TB, 2 * C])
        squares = m.sbuf("squares", [P, TB, C])
        norm = m.sbuf("norm", [P, TB, H])
        unit = m.sbuf("unit", [P, TB, C])
        side = m.sbuf("side", [P, TB, SIDE])
        vT = m.sbuf("vT", [CH, 2, PAD + N])
        fir = m.sbuf("fir", [CH, 2, 2, N])
        mixed = m.sbuf("mixed", [P, TB, 2, C])
        hidden = m.sbuf("hidden", [CH + 1, 2, N])
        top = m.sbuf("top", [P, TB, H])
        weights = m.sbuf("weights", [P, TB, H, PATHS])
        total = m.sbuf("total", [P, TB, H])
        dyn = m.sbuf("dyn", [P, TB, H])
        gate = m.sbuf("gate", [P, TB, H])
        term = m.sbuf("term", [P, TB, C])
        sum_ = m.sbuf("sum", [P, TB, C])
        bank = m.psum("bank", [P, 8, 512])
        act_banks, banks = (0, 1, 2), (3, 4, 5, 6, 7)
        (loaded, set_up, mixer_ready, static_ready, filled, taken, act_filled, act_taken, norm2_ready, norm_ready, unit_ready,
         side_ready, dyn_ready, gap_ready, exp_ready, fir_ready, gate_raw, gate_ready, rows_stored, part_ready,
         dve_own) = m.sems(*(
             "loaded set_up mixer_ready static_ready filled taken act_filled act_taken norm2_ready norm_ready unit_ready "
             "side_ready dyn_ready gap_ready exp_ready fir_ready gate_raw gate_ready rows_stored part_ready dve_own").split())
        pairs = ((wq, io["mix_wq"]), (wkv, io["mix_wkv"]), (wside, io["mix_wside"]), (wg1, io["mix_wg1"]),
                 (bg1, io["mix_bg1"]), (wg2, io["mix_wg2"]), (static, io["mix_static"]), (taps, io["mix_taps"]),
                 (mixer, io["mix_mixer"]), (same_dim, io["same_dim"]), (same, io["same"]))
        LOADED = 16 * len(pairs)

        def heads(ap):
            return ap.rearrange("p s (h d) -> p s h d", h=H)

        def per_head(ap):
            return ap.unsqueeze(3).to_broadcast([P, TB, H, D])

        def weight(p):
            return weights[:, :, :, p]

        with nc.Block() as block:

            @block.sync
            def _(sp):
                load(sp, pairs, loaded)
                with sp.Fori(0, B) as b:
                    sp.wait_ge(unit_ready, b + 1)
                    sp.wait_ge(taken, b * MIX_ITEMS + len(banks) + 4 + TB)
                    for dram, buf in ((k_rows, unit[:, :, :]), (v_rows, kv[:, :, C:])):
                        sp.dma_start(dram[bass.ds(b * N, N), :].rearrange("(s p) c -> p s c", p=P), buf).then_inc(rows_stored, 16)
                sp.wait_ge(rows_stored, 32 * B + 32)

            @block.gpsimd
            def _(pool):
                pool.sem_inc(rows_stored, 32)
                fill(nc, pool, set_up, ((vT[:, :, 0:PAD], 0.0), (z.xT[CH:CH + 1, :, :], 1.0), (hidden[CH:CH + 1, :, :], 1.0)))

            @block.vector
            def _(dve):
                setup = InOrder(dve, mixer_ready)
                dve.sem_inc(taken, len(banks))
                dve.sem_inc(part_ready, 1)
                dve.wait_ge(loaded, LOADED)
                setup.step(nc.vector.tensor_tensor(mixer[:, :, :], mixer[:, :, :], same_dim[:, :, :], ALU.mult))
                setup.step(nc.vector.tensor_tensor(mixer[:, :, :], mixer[:, :, :], same[:, :, :], ALU.add))
                dve.wait_ge(set_up, 3)
                dve.wait_ge(static_ready, 1)
                own = InOrder(dve, dve_own, MIX_DVE_STEPS)
                ring = Ring(dve, banks, filled, taken, MIX_ITEMS)
                norm_rows(nc, dve, own, z, lambda s: h[:, s, :], 0)
                with dve.Fori(0, B) as b:
                    own.turn(b, NORM_STEPS)
                    ring.turn(b)
                    for half in range(2):
                        for c in range(2):
                            slot = ring.get()
                            dst = kq[:, half, b, c * NC // 2:(c + 1) * NC // 2, CK:]
                            ring.take(nc.vector.tensor_scalar(dst, bank[0:CH, slot, 0:HALF].rearrange("p (c t) -> p c t", t=CK),
                                                              float(D) ** -0.5, None, ALU.mult))
                    dve.wait_ge(rows_stored, b * 32 + 32)
                    for s in range(TB):
                        slot = ring.get()
                        ring.take(nc.vector.tensor_copy(kv[:, s, :], bank[:, slot, 0:2 * C]))
                    ring.done()
                    own.step(nc.vector.tensor_tensor(squares[:, :, :], kv[:, :, 0:C], kv[:, :, 0:C], ALU.mult))
                    nc.vector.tensor_reduce(norm[:, :, :], heads(squares[:, :, :]), AX.X, ALU.add).then_inc(norm2_ready, 1)
                    for s in range(TB):
                        slot = ring.get()
                        ring.take(nc.vector.tensor_copy(side[:, s, :], bank[:, slot, 0:SIDE]))
                    ring.done()
                    dve.wait_ge(norm_ready, b + 1)
                    own.step(nc.vector.tensor_scalar(norm[:, :, :], norm[:, :, :], 1e-6, None, ALU.add))
                    own.step(nc.vector.reciprocal(norm[:, :, :], norm[:, :, :]))
                    nc.vector.tensor_tensor(heads(unit[:, :, :]), heads(kv[:, :, 0:C]), per_head(norm[:, :, :]),
                                            ALU.mult).then_inc(unit_ready, 1)
                    logits = side[:, :, C + H:].rearrange("p s (h q) -> p s h q", q=PATHS)
                    own.step(nc.vector.tensor_reduce(top[:, :, :], logits, AX.X, ALU.max))
                    nc.vector.tensor_tensor(weights[:, :, :, :], logits, top[:, :, :].unsqueeze(3).to_broadcast([P, TB, H, PATHS]),
                                            ALU.subtract).then_inc(gap_ready, 1)
                    for half in range(2):
                        for c in range(2):
                            slot = ring.get()
                            ring.take(nc.vector.tensor_copy(vT[:, half, PAD + c * HALF:PAD + (c + 1) * HALF], bank[0:CH, slot, 0:HALF]))
                    ring.done()
                    norm_rows(nc, dve, own, z, lambda s: h[:, following(b) * TB + s, :], b + 1)
                    for half in range(2):
                        for which, first, n_taps in ((0, 0, SHORT), (1, SHORT, LONG)):
                            dst = fir[:, which, half, :]
                            for k in range(n_taps):
                                at = PAD - (n_taps - 1) + k
                                src, tap = vT[:, half, at:at + N], taps[:, half, first + k:first + k + 1]
                                if k == 0:
                                    own.step(nc.vector.tensor_scalar(dst, src, tap, None, ALU.mult))
                                elif k < n_taps - 1:
                                    own.step(nc.vector.scalar_tensor_tensor(dst, src, tap, dst, ALU.mult, ALU.add))
                                else:
                                    nc.vector.scalar_tensor_tensor(dst, src, tap, dst, ALU.mult, ALU.add).then_inc(fir_ready, 1)
                    for s in range(TB):
                        slot = ring.get()
                        ring.take(nc.vector.tensor_copy(kq[:, :, b, s * P // CK:(s + 1) * P // CK, 0:CK],
                                                        bank[0:CH, slot, 0:2 * P].rearrange("p (z c t) -> p z c t", z=2, t=CK)))
                    slot = ring.get()
                    ring.take(nc.vector.tensor_copy(gate[:, :, :], bank[:, slot, 0:TB * NARROW].rearrange("p (s h) -> p s h", s=TB)[:, :, 0:H]))
                    dve.wait_ge(exp_ready, b + 1)
                    own.step(nc.vector.tensor_reduce(total[:, :, :], weights[:, :, :, :], AX.X, ALU.add))
                    own.step(nc.vector.reciprocal(total[:, :, :], total[:, :, :]))
                    dve.wait_ge(gate_ready, b + 1)
                    own.step(nc.vector.tensor_tensor(total[:, :, :], total[:, :, :], gate[:, :, :], ALU.mult))
                    own.step(nc.vector.tensor_tensor(weights[:, :, :, :], weights[:, :, :, :],
                                                     total[:, :, :].unsqueeze(3).to_broadcast([P, TB, H, PATHS]), ALU.mult))
                    own.count(nc.vector.tensor_copy(delta_weight[:, bass.ds(b * TB, TB), :], weight(2)))
                    dve.wait_ge(dyn_ready, b + 1)
                    own.step(nc.vector.tensor_tensor(dyn[:, :, :], dyn[:, :, :], static[:, :].unsqueeze(1).to_broadcast([P, TB, H]), ALU.mult))
                    own.step(nc.vector.tensor_tensor(dyn[:, :, :], dyn[:, :, :], weight(4), ALU.mult))
                    own.count(nc.vector.tensor_tensor(heads(sum_[:, :, :]), heads(kv[:, :, C:]), per_head(weight(3)), ALU.mult))
                    own.step(nc.vector.tensor_tensor(heads(term[:, :, :]), heads(side[:, :, 0:C]), per_head(dyn[:, :, :]), ALU.mult))
                    own.step(nc.vector.tensor_tensor(sum_[:, :, :], sum_[:, :, :], term[:, :, :], ALU.add))
                    for s in range(TB):
                        slot = ring.get()
                        ring.take(nc.vector.tensor_copy(mixed[:, s, :, :], bank[:, slot, 0:2 * C].rearrange("p (w c) -> p w c", w=2)))
                    ring.done()
                    for which in range(2):
                        own.step(nc.vector.tensor_tensor(heads(term[:, :, :]), heads(mixed[:, :, which, :]), per_head(weight(which)), ALU.mult))
                        if which == 0:
                            own.step(nc.vector.tensor_tensor(sum_[:, :, :], sum_[:, :, :], term[:, :, :], ALU.add))
                    own.step(nc.vector.tensor_tensor(part[:, bass.ds(b * TB, TB), :], sum_[:, :, :], term[:, :, :], ALU.add))
                    ring.ended()
                    own.ended()

            @block.scalar
            def _(act):
                ring = Ring(act, act_banks, act_filled, act_taken, 4)
                act.sem_inc(act_taken, len(act_banks))
                act.wait_ge(loaded, LOADED)
                nc.scalar.activation(static[:, :], static[:, :], ACT.Sigmoid).then_inc(static_ready, 1)
                root(nc, act, z, 0)
                act.wait_ge(z.psum_ready, 1)
                copy_transposed(nc, bank, z.xT, z.xT_ready)
                with act.Fori(0, B) as b:
                    ring.turn(b)
                    act.wait_ge(norm2_ready, b + 1)
                    nc.scalar.activation(norm[:, :, :], norm[:, :, :], ACT.Sqrt).then_inc(norm_ready, 1)
                    for half in range(2):
                        for c in range(2):
                            slot = ring.get()
                            ring.take(nc.scalar.activation(hidden[0:CH, half, c * HALF:(c + 1) * HALF], bank[0:CH, slot, 0:HALF],
                                                           ACT.Gelu_apprx_tanh, bias=bg1[:, half:half + 1]))
                    act.wait_ge(gap_ready, b + 1)
                    nc.scalar.activation(weights[:, :, :, :], weights[:, :, :, :], ACT.Exp).then_inc(exp_ready, 1)
                    nc.scalar.activation(dyn[:, :, :], side[:, :, C:C + H], ACT.Sigmoid).then_inc(dyn_ready, 1)
                    root(nc, act, z, b + 1)
                    act.wait_ge(z.psum_ready, b + 2)
                    copy_transposed(nc, bank, z.xT, z.xT_ready)
                    act.wait_ge(taken, b * MIX_ITEMS + len(banks) + 4 + TB + TB + 4 + TB + 1)
                    nc.scalar.activation(gate[:, :, :], gate[:, :, :], ACT.Sigmoid).then_inc(gate_ready, 1)
                    ring.ended()

            @block.tensor
            def _(pe):
                ring = Ring(pe, banks, filled, taken, MIX_ITEMS)
                up = Ring(pe, act_banks, act_filled, act_taken, 4)
                pe.wait_ge(loaded, LOADED)
                pe.wait_ge(set_up, 3)
                pe.wait_ge(mixer_ready, 2)

                def columns(ring, w, at, rows, half_tokens):
                    slot = ring.free()
                    for k in range(2):
                        ins = nc.tensor.matmul(bank[0:rows, slot, 0:HALF], w[:, k, at:at + rows],
                                               z.xT[0:CH, k, half_tokens * HALF:(half_tokens + 1) * HALF], start=(k == 0), stop=(k == 1))
                    ring.fill(ins)

                pe.wait_ge(z.xn_ready, TB)
                transpose_rows(nc, pe, lambda s, k: z.xn[:, s, k * CH:(k + 1) * CH], ident, bank, z.psum_ready)
                with pe.Fori(0, B) as b:
                    ring.restart(b)
                    up.turn(b)
                    pe.wait_ge(z.xT_ready, b * COPIES + COPIES)
                    for half in range(2):
                        for c in range(2):
                            columns(ring, wq, half * CH, CH, c)
                    for s in range(TB):
                        slot = ring.free()
                        for k in range(2):
                            ins = nc.tensor.matmul(bank[:, slot, 0:2 * C], z.xT[0:CH, k, s * P:(s + 1) * P], wkv[:, k, :], start=(k == 0), stop=(k == 1))
                        ring.fill(ins)
                    for s in range(TB):
                        slot = ring.free()
                        for k in range(2):
                            ins = nc.tensor.matmul(bank[:, slot, 0:SIDE], z.xT[rows_of(k), k, s * P:(s + 1) * P], wside[rows_of(k), k, :],
                                                   start=(k == 0), stop=(k == 1))
                        ring.fill(ins)
                    for half in range(2):
                        for c in range(2):
                            columns(up, wg1, half * CH, CH, c)
                    for half in range(2):
                        for c in range(2):
                            columns(ring, wkv, C + half * CH, CH, c)
                    up.arrived()
                    pe.wait_ge(z.xn_ready, b * TB + 2 * TB)
                    transpose_rows(nc, pe, lambda s, k: z.xn[:, s, k * CH:(k + 1) * CH], ident, bank, z.psum_ready)
                    pe.wait_ge(unit_ready, b + 1)
                    for s in range(TB):
                        slot = ring.free()
                        for k in range(2):
                            ins = nc.tensor.transpose(bank[0:CH, slot, k * P:(k + 1) * P], unit[:, s, k * CH:(k + 1) * CH], ident[:, :])
                        ring.fill(ins)
                    slot = ring.free()
                    for s in range(TB):
                        for k in range(2):
                            ins = nc.tensor.matmul(bank[:, slot, s * NARROW:(s + 1) * NARROW], hidden[rows_of(k), k, s * P:(s + 1) * P],
                                                   wg2[rows_of(k), k, :], start=(k == 0), stop=(k == 1))
                    ring.fill(ins)
                    pe.wait_ge(fir_ready, b * 4 + 4)
                    for s in range(TB):
                        slot = ring.free()
                        for which in range(2):
                            for k in range(2):
                                ins = nc.tensor.matmul(bank[:, slot, which * C:(which + 1) * C], fir[:, which, k, s * P:(s + 1) * P],
                                                       mixer[:, k, :], start=(k == 0), stop=(k == 1))
                        ring.fill(ins)
                    ring.ended()
                    up.ended()


MIX_DVE_STEPS = 46


def chunk_products(nc, kq, grams, reads, keys, values, k_rows, v_rows, mask, upto, g_dram, tt_dram):
    GROUPS = STREAMS * NC // EACH
    with Memory(nc, "gram") as m:
        k_block = m.sbuf("k_block", [CB, 2, STREAMS, GH, CK])
        a = m.sbuf("a", [GH * GROUPS, CK, EACH, CK])
        tt = m.sbuf("tt", [GH * GROUPS, CK, EACH, CK])
        product = m.sbuf("product", [GH * GROUPS, CK, EACH, CK])
        bank = m.psum("bank", [CB, 4, 512])
        (rows_in, even_ready, odd_ready, filled, taken, stored, a_in, zeroed, solved, back, dve_own, pool_own) = m.sems(
            *"rows_in even_ready odd_ready filled taken stored a_in zeroed solved back dve_own pool_own".split())
        with nc.Block() as block:

            def of_step(step, at):
                return bank[:, step * 2:step * 2 + 2, 0:B * 6 * CK].rearrange("p z (n c) -> p z n c", n=B)[:, :, :, at * 2 * CK:(at + 1) * 2 * CK]

            def k_blocks(eng, step, c):
                return eng.tensor_tensor(k_block[:, c, :, :, :], kq[:, :, step, 0:CK].unsqueeze(2).to_broadcast([CB, STREAMS, GH, CK]),
                                         mask[:, :].unsqueeze(2).unsqueeze(1).to_broadcast([CB, STREAMS, GH, CK]), ALU.mult)

            def halves(ap):
                return ap.rearrange("p (z n) c -> p z n c", z=2)

            def solve(compute, own, eng, e0, e1):
                own.step(compute.memset(tt[:, :, e0:e1, :], 0.0))
                for i in range(CK):
                    own.step(compute.memset(tt[:, i, e0:e1, i], 1.0))
                eng.wait_ge(a_in, 16 * GH)
                for j in range(CK - 1):
                    shape = [GH * GROUPS, j + 1, e1 - e0, CK - 1 - j]
                    below = product[:, 0:j + 1, e0:e1, j + 1:]
                    own.step(compute.tensor_tensor(below, a[:, j + 1:, e0:e1, j].rearrange("p k e -> p e k").unsqueeze(1).to_broadcast(shape),
                                                   tt[:, 0:j + 1, e0:e1, j].unsqueeze(3).to_broadcast(shape), ALU.mult))
                    last = compute.tensor_tensor(tt[:, 0:j + 1, e0:e1, j + 1:], tt[:, 0:j + 1, e0:e1, j + 1:], below, ALU.subtract)
                    if j < CK - 2:
                        own.step(last)
                    else:
                        last.then_inc(solved, 1)

            @block.vector
            def _(dve):
                def copy_out(step, c, at):
                    dve.wait_ge(filled, step + 1)
                    got = of_step(c, at)
                    nc.vector.tensor_copy(halves(grams[:, :, step, :]), got[:, :, :, 0:CK]).then_inc(taken, 1)
                    nc.vector.tensor_tensor(halves(reads[:, :, step, :]), got[:, :, :, CK:],
                                            upto[:, :].unsqueeze(1).unsqueeze(1).to_broadcast([CB, 2, B, CK]), ALU.mult).then_inc(taken, 1)

                k_blocks(nc.vector, 1, 1).then_inc(odd_ready, 1)
                copy_out(0, 0, 0)
                copy_out(1, 1, 1)
                with dve.Fori(1, NC // 2) as cc:
                    k_blocks(nc.vector, cc * 2 + 1, 1).then_inc(odd_ready, 1)
                    for c in range(2):
                        copy_out(cc * 2 + c, c, 2)
                solve(nc.vector, InOrder(dve, dve_own), dve, 0, DVE_EACH)

            @block.gpsimd
            def _(pool):
                k_blocks(nc.gpsimd, 0, 0).then_inc(even_ready, 1)
                with pool.Fori(1, NC // 2) as cc:
                    pool.wait_ge(filled, cc * 2 - 1)
                    k_blocks(nc.gpsimd, cc * 2, 0).then_inc(even_ready, 1)
                solve(nc.gpsimd, InOrder(pool, pool_own), pool, DVE_EACH, EACH)

            @block.tensor
            def _(pe):
                def products(step, c, first):
                    for n in range(STREAMS):
                        ins = nc.tensor.matmul(bank[:, c * 2 + n // B, (n % B) * 6 * CK:(n % B + 1) * 6 * CK],
                                               k_block[:, c, n, :, :].rearrange("p h t -> p (h t)"),
                                               kq[:, n, bass.ds(first, 3), :].rearrange("p c t -> p (c t)"), start=True, stop=True)
                    ins.then_inc(filled, 1)

                pe.wait_ge(even_ready, 1)
                products(0, 0, 0)
                pe.wait_ge(odd_ready, 1)
                products(1, 1, 0)
                with pe.Fori(1, NC // 2) as cc:
                    for c, ready in ((0, even_ready), (1, odd_ready)):
                        pe.wait_ge(ready, cc + 1)
                        pe.wait_ge(taken, cc * 4 + c * 2 - 2)
                        products(cc * 2 + c, c, cc * 2 + c - 2)

            @block.sync
            def _(sp):
                def by_row(dram):
                    return dram.rearrange("h i s j -> (h i) (s j)")

                def by_system(buf, dram, g):
                    return buf[g * GROUPS:(g + 1) * GROUPS].rearrange("p i e j -> p i (e j)"), dram[g].rearrange("i (p e) j -> p i (e j)", p=GROUPS)

                sp.wait_ge(taken, NC * 2)
                flat = grams[:, :, :, :].rearrange("p n c j -> p (n c j)")
                sp.dma_start(by_row(g_dram), flat).then_inc(stored, 16)
                sp.wait_ge(stored, 16)
                for g in range(GH):
                    dst, src = by_system(a, g_dram, g)
                    sp.dma_start(dst, src).then_inc(a_in, 16)
                sp.wait_ge(solved, 2)
                for g in range(GH):
                    src, dst = by_system(tt, tt_dram, g)
                    sp.dma_start(dst, src).then_inc(stored, 16)
                sp.wait_ge(stored, 16 * GH + 16)
                sp.dma_start(flat, by_row(tt_dram)).then_inc(back, 16)
                sp.wait_ge(back, 16)

            @block.scalar
            def _(act):
                for dram, buf in ((k_rows, keys), (v_rows, values)):
                    for half in range(2):
                        for g in range(GH):
                            act.dma_start(buf[g * CK:(g + 1) * CK, half * B:(half + 1) * B, :, :].rearrange("p b c e -> p (b c) e"),
                                          chunk_rows(dram, half, g)).then_inc(rows_in, 16)
                act.wait_ge(rows_in, 16 * 2 * H)


def chunk_rows(dram, half, g):
    at = half * CH + g * D
    return dram.rearrange("(n t) c -> t n c", t=CK)[:, :, at:at + D]


def delta_rule(nc, kq, tt, reads, keys, values, o_rows, mask):
    with Memory(nc, "delta") as m:
        state = m.sbuf("state", [CB, 2, WIDTH, CK])
        resid = m.sbuf("resid", [CB, 2, WIDTH, CK])
        update = m.sbuf("update", [CB, 2, WIDTH, CK])
        K_T, T_T, Q_T, R_T, K = range(5)
        blocks = [m.sbuf(f"block{i}", [CB, 2, STREAMS, GH, CK]) for i in range(5)]
        bank = m.psum("bank", [CB, 8, 512])
        (blocks_dve, blocks_pool, zeroed, ks_psum, resid_ready, u_psum, u_ready, s_psum, s_ready, o_psum, o_taken,
         o_stored) = m.sems(*("blocks_dve blocks_pool zeroed ks_psum resid_ready u_psum u_ready s_psum s_ready "
                              "o_psum o_taken o_stored").split())
        KS, U, SB, O = 0, 2, 4, 6

        def part(z):
            return slice(z * B, (z + 1) * B)

        def own_columns(slot):
            return bank[:, slot, 0:B * (WIDTH + 1) * CK].rearrange("p (b e) -> p b e", b=B)[:, :, 0:CK]

        def spread(ap):
            return ap.unsqueeze(2).to_broadcast([CB, STREAMS, GH, CK])

        masks = mask[:, :].unsqueeze(2).unsqueeze(1).to_broadcast([CB, STREAMS, GH, CK])

        def operands(i, c):
            return {K_T: kq[:, :, c, 0:CK], T_T: tt[:, :, c, :], Q_T: kq[:, :, c, CK:], R_T: reads[:, :, c, :], K: keys[:, :, c, :]}[i]

        with nc.Block() as block:

            @block.sync
            def _(sp):
                sp.wait_ge(o_taken, 2 * NC + 2)
                for half in range(2):
                    for g in range(GH):
                        sp.dma_start(chunk_rows(o_rows, half, g),
                                     values[g * CK:(g + 1) * CK, part(half), :, :].rearrange("p b c e -> p (b c) e")).then_inc(o_stored, 16)
                sp.wait_ge(o_stored, 16 * H)

            @block.gpsimd
            def _(pool):
                for buf in (resid, update):
                    nc.gpsimd.memset(buf[:, :, :, :], 0.0).then_inc(zeroed, 1)

                def make_blocks(step, c):
                    for i in (R_T, K):
                        nc.gpsimd.tensor_tensor(blocks[i][:, c], spread(operands(i, step)), masks, ALU.mult).then_inc(blocks_pool, 1)

                for c in range(2):
                    make_blocks(c, c)
                with pool.Fori(1, NC // 2) as cc:
                    for c in range(2):
                        pool.wait_ge(s_psum, cc * 4 + c * 2 - 2)
                        make_blocks(cc * 2 + c, c)

            @block.vector
            def _(dve):
                nc.vector.memset(state[:, :, :, :], 0.0).then_inc(s_ready, 2)
                dve.wait_ge(zeroed, 2)

                def make_block(i, step, c):
                    nc.vector.tensor_tensor(blocks[i][:, c], spread(operands(i, step)), masks, ALU.mult).then_inc(blocks_dve, 1)

                def chunk(step, c, more):
                    for z in range(2):
                        dve.wait_ge(ks_psum, step * 2 + z + 1)
                        nc.vector.tensor_tensor(resid[:, z, 0:B, :], values[:, part(z), step, :], own_columns(KS + z), ALU.subtract).then_inc(resid_ready, 1)
                    for z in range(2):
                        dve.wait_ge(u_psum, step * 2 + z + 1)
                        nc.vector.tensor_copy(update[:, z, 0:B, :], own_columns(U + z)).then_inc(u_ready, 1)
                    if more:
                        make_block(K_T, step + 1, 1 - c)
                        make_block(T_T, step + 1, 1 - c)
                    for z in range(2):
                        at = step * 2 + z + 1
                        dve.wait_ge(s_psum, at)
                        dve.wait_ge(s_ready, at)
                        nc.vector.tensor_tensor(state[:, z, 0:B, :], state[:, z, 0:B, :], own_columns(SB + z), ALU.add).then_inc(s_ready, 1)
                        if z == 0 and more:
                            make_block(Q_T, step + 1, 1 - c)

                for i in (K_T, T_T, Q_T):
                    make_block(i, 0, 0)
                with dve.Fori(0, NC // 2 - 1) as cc:
                    for c in range(2):
                        chunk(cc * 2 + c, c, True)
                chunk(NC - 2, 0, True)
                chunk(NC - 1, 1, False)

            @block.scalar
            def _(act):
                act.sem_inc(o_taken, 2)
                with act.Fori(0, NC // 2) as cc:
                    for c in range(2):
                        step = cc * 2 + c
                        for z in range(2):
                            at = step * 2 + z + 1
                            act.wait_ge(o_psum, at)
                            nc.scalar.activation(values[:, part(z), step, :], own_columns(O + z), ACT.Copy).then_inc(o_taken, 1)

            @block.tensor
            def _(pe):
                def columns(buf, z):
                    return buf[:, z, :, :].rearrange("p w e -> p (w e)")

                def product(z, dst, i, c, rhs, start, stop):
                    for n in range(B):
                        ins = nc.tensor.matmul(bank[:, dst + z, n * WIDTH * CK:(n + 1) * WIDTH * CK],
                                               blocks[i][:, c, z * B + n].rearrange("p h t -> p (h t)"), columns(rhs, z), start=start, stop=stop)
                    return ins

                with pe.Fori(0, NC // 2) as cc:
                    for c in range(2):
                        step = cc * 2 + c
                        pe.wait_ge(blocks_dve, step * 3 + 3)
                        for z in range(2):
                            pe.wait_ge(s_ready, step * 2 + z + 1)
                            product(z, KS, K_T, c, state, True, True).then_inc(ks_psum, 1)
                        for z in range(2):
                            pe.wait_ge(resid_ready, step * 2 + z + 1)
                            product(z, U, T_T, c, resid, True, True).then_inc(u_psum, 1)
                        pe.wait_ge(blocks_pool, step * 2 + 2)
                        for z in range(2):
                            at = step * 2 + z + 1
                            pe.wait_ge(u_ready, at)
                            pe.wait_ge(o_taken, at)
                            for n in range(B):
                                out = bank[:, O + z, n * WIDTH * CK:(n + 1) * WIDTH * CK]
                                at_n = z * B + n
                                nc.tensor.matmul(out, blocks[Q_T][:, c, at_n].rearrange("p h t -> p (h t)"), columns(state, z), start=True, stop=False)
                                ins = nc.tensor.matmul(out, blocks[R_T][:, c, at_n].rearrange("p h t -> p (h t)"), columns(update, z), start=False, stop=True)
                            ins.then_inc(o_psum, 1)
                            product(z, SB, K, c, update, True, True).then_inc(s_psum, 1)


def project_paths(nc, h, part, delta_weight, o_rows, ident, io):
    with Memory(nc, "proj") as m:
        delta = m.sbuf("delta", [P, TILES, C])
        context = m.sbuf("context", [P, TB, C])
        cT = m.sbuf("cT", [CH + 1, 2, N])
        wp = m.sbuf("wp", [CH + 1, 2, C])
        bank = m.psum("bank", [P, 8, 512])
        banks = (3, 4, 5, 6, 7)
        (loaded, set_up, scaled, context_ready, cT_psum, cT_ready, filled, taken) = m.sems(
            *"loaded set_up scaled context_ready cT_psum cT_ready filled taken".split())
        pairs = ((wp, io["proj_w"]),)
        LOADED = 16 * (len(pairs) + B)
        with nc.Block() as block:

            @block.sync
            def _(sp):
                load(sp, pairs, loaded)
                for b in range(B):
                    sp.dma_start(delta[:, b * TB:(b + 1) * TB, :],
                                 o_rows[b * N:(b + 1) * N, :].rearrange("(s p) c -> p s c", p=P)).then_inc(loaded, 16)

            @block.gpsimd
            def _(pool):
                nc.gpsimd.memset(cT[CH:CH + 1, :, :], 1.0).then_inc(set_up, 1)

            @block.vector
            def _(dve):
                ring = Ring(dve, banks, filled, taken, TB)
                dve.sem_inc(taken, len(banks))
                dve.wait_ge(loaded, LOADED)

                def contexts(here, n):
                    nc.vector.tensor_tensor(context[:, :, :].rearrange("p s (h d) -> p (s h) d", h=H),
                                            delta[:, here, :].rearrange("p s (h d) -> p (s h) d", h=H),
                                            delta_weight[:, here, :].rearrange("p s h -> p (s h)").unsqueeze(2).to_broadcast([P, TB * H, D]),
                                            ALU.mult).then_inc(scaled, 1)
                    dve.wait_ge(scaled, n + 1)
                    nc.vector.tensor_tensor(context[:, :, :], context[:, :, :], part[:, here, :], ALU.add).then_inc(context_ready, 1)

                contexts(slice(0, TB), 0)
                with dve.Fori(0, B) as b:
                    ring.turn(b)
                    for s in range(TB):
                        slot = ring.get()
                        row = h[:, b * TB + s, :]
                        ring.take(nc.vector.tensor_tensor(row, row, bank[:, slot, 0:C], ALU.add))
                        if s == 0:
                            contexts(bass.ds(following(b) * TB, TB), b + 1)
                    ring.ended()

            @block.scalar
            def _(act):
                with act.Fori(0, B + 1) as b:
                    act.wait_ge(cT_psum, b + 1)
                    copy_transposed(nc, bank, cT, cT_ready)

            @block.tensor
            def _(pe):
                ring = Ring(pe, banks, filled, taken, TB)
                pe.wait_ge(loaded, LOADED)
                pe.wait_ge(set_up, 1)
                pe.wait_ge(context_ready, 1)
                transpose_rows(nc, pe, lambda s, k: context[:, s, k * CH:(k + 1) * CH], ident, bank, cT_psum)
                with pe.Fori(0, B) as b:
                    ring.restart(b)
                    pe.wait_ge(cT_ready, b * COPIES + COPIES)
                    for s in range(TB):
                        slot = ring.free()
                        for k in range(2):
                            ins = nc.tensor.matmul(bank[:, slot, 0:C], cT[rows_of(k), k, s * P:(s + 1) * P], wp[rows_of(k), k, :],
                                                   start=(k == 0), stop=(k == 1))
                        ring.fill(ins)
                    pe.wait_ge(context_ready, b + 2)
                    transpose_rows(nc, pe, lambda s, k: context[:, s, k * CH:(k + 1) * CH], ident, bank, cT_psum)
                    ring.ended()


def delta_attention(nc, h, part, ident, io):
    scratch = {k: nc.dram_tensor(k, (B * N, C), F32, kind="Internal").ap() for k in ("k_rows", "v_rows", "o_rows")}
    systems = {k: nc.dram_tensor(k, (GH, CK, STREAMS * NC, CK), F32, kind="Internal").ap() for k in ("g_rows", "t_rows")}
    with Memory(nc, "l1") as m:
        delta_weight = m.sbuf("delta_weight", [P, TILES, H])
        kq = m.sbuf("kq", [CH, 2, B, NC, 2 * CK])
        mask = m.sbuf("mask", [CB, GH])
        upto = m.sbuf("upto", [CB, CK])
        masks_in = m.sem("masks_in")
        with nc.Block() as block:

            @block.sync
            def _(sp):
                sp.wait_ge(masks_in, load(sp, ((mask, io["head_mask"]), (upto, io["upto"])), masks_in))
        mix_paths(nc, h, part, delta_weight, kq, scratch["k_rows"], scratch["v_rows"], ident, io)
        by_stream = kq[:, :, :, :, :].rearrange("p z b c t -> p (z b) c t")
        with Memory(nc, "chunks") as n:
            grams = n.sbuf("grams", [CB, STREAMS, NC, CK])
            reads = n.sbuf("reads", [CB, STREAMS, NC, CK])
            keys = n.sbuf("keys", [CB, STREAMS, NC, CK])
            values = n.sbuf("values", [CB, STREAMS, NC, CK])
            chunk_products(nc, by_stream, grams, reads, keys, values, scratch["k_rows"], scratch["v_rows"], mask, upto,
                           systems["g_rows"], systems["t_rows"])
            delta_rule(nc, by_stream, grams, reads, keys, values, scratch["o_rows"], mask)
        project_paths(nc, h, part, delta_weight, scratch["o_rows"], ident, io)


def store(nc, h, out):
    with Memory(nc, "store") as m:
        stored = m.sem("stored")
        with nc.Block() as block:

            @block.sync
            def _(sp):
                rows = out.rearrange("b (s p) c -> p (b s) c", p=P)
                for b in range(B):
                    sp.dma_start(rows[:, b * TB:(b + 1) * TB, :], h[:, b * TB:(b + 1) * TB, :]).then_inc(stored, 16)
                sp.wait_ge(stored, 16 * B)


def program(nc, io, out):
    with Memory(nc, "all") as m:
        h = m.sbuf("h", [P, TILES, C])
        ident = m.sbuf("ident", [P, P])
        ident_in = m.sem("ident_in")
        with nc.Block() as block:

            @block.sync
            def _(sp):
                sp.dma_start(ident[:, :], io["ident"]).then_inc(ident_in, 16)
                sp.wait_ge(ident_in, 16)
        image_embedding(nc, h, io)
        text_embedding(nc, h, ident, io)
        performer(nc, h, ident, io)
        x1 = m.sbuf("x1", [P, TILES, C])
        with Memory(nc, "values") as n:
            v = n.sbuf("v", [P, TILES, H, DV])
            qk_rows = nc.dram_tensor("qk_rows", (B * 2 * PARTS, C, N), BF16, kind="Internal").ap()
            attention_operands(nc, h, x1, v, qk_rows, ident, io)
            softmax_attention(nc, x1, v, qk_rows, ident, io)
        experts(nc, h, x1, ident, io, True)
        delta_attention(nc, h, x1, ident, io)
        experts(nc, h, x1, ident, io, False)
        store(nc, h, out)


def layouts(i, np):
    a = {}
    flat = i["x"].reshape(B, NI, 3 * C).transpose(0, 2, 1)
    a["x"] = np.concatenate([flat[:, :512].reshape(B, 4, P, NI),
                             np.concatenate([flat[:, 512:], flat[:, 512:]], 1)[:, None]], 1).reshape(B * JC, P, NI)
    wt = i["L0_tok_W"].T.reshape(3 * C, 2 * BANDS, C)
    main = wt[:512].reshape(4, P, 2 * BANDS, C).transpose(1, 0, 2, 3).reshape(P, 8 * BANDS, C)
    last = np.concatenate([wt[512:, :BANDS], wt[512:, BANDS:]], 0)
    a["tok_w"] = np.concatenate([main, last], 1)
    a["freq"] = np.broadcast_to(i["L0_tok_freq_bands"], (P, BANDS))
    a["sincos_shift"] = np.stack([np.where(np.arange(P) < 64, 0.0, math.pi / 2), np.full(P, math.pi / 2)], 1).astype(np.float32)
    a["ident"] = np.eye(P, dtype=np.float32)
    a["ids"] = i["x_txt"].T
    a["emb"] = i["L0_txt_emb"]

    def halves(w):
        return w.reshape(w.shape[:-2] + (2, CH, w.shape[-1])).swapaxes(-3, -2)

    def biased(w, bias, columns=0):
        out = np.zeros((CH + 1, 2, max(columns, w.shape[-1])), w.dtype)
        out[:CH, :, :w.shape[-1]] = halves(w)
        if bias is not None:
            out[CH, 1, :w.shape[-1]] = bias
        return out

    def tiles(w):
        return w.reshape(LAYERS, FT, P, -1).swapaxes(1, 2)

    a["in_proj"] = halves(i["L0_txt_in_proj_w"])
    a["norm_w"] = i["L0_txt_norm_w"].reshape(LAYERS, 2, CH).swapaxes(1, 2)
    a["txt_par"] = tiles(np.concatenate([i["L0_txt_conv_w"][:, :, 0], i["L0_txt_conv_b"][..., None], i["L0_txt_dt_proj_b"][..., None],
                                         i["L0_txt_A_log"], i["L0_txt_D"][..., None]], -1))
    w = i["L0_txt_x_proj_w"]
    a["x_proj"] = tiles(np.concatenate([w[..., RANK:]] * 3 + [w[..., :RANK]], -1))
    a["dt_proj"] = i["L0_txt_dt_proj_w"]
    a["out_proj"] = tiles(i["L0_txt_out_proj_w"])
    pick = np.zeros((3, BC, BC, P), np.float32)
    pick[:, np.arange(BC), np.arange(BC)] = 1
    pick = pick.reshape(COPIED, BC, P)
    a["pick"] = pick

    def vector(v):
        return v.reshape(2, CH).T

    def blocks(w):
        out = np.zeros((GH, D, GH, w.shape[0]), w.dtype)
        for g in range(GH):
            out[g, :, g] = w.T
        return out.reshape(CH, GH * w.shape[0])

    a["perf_w"] = biased(i["L0_attn_w_qkv"].T, i["L0_attn_b_qkv"])
    a["perf_wp"] = biased(i["L0_attn_w_proj"].T, i["L0_attn_b_proj"])
    a["perf_feat"] = blocks(i["L0_attn_projection"])
    qkv = i["L0_ffn_Wqkv"].reshape(C, 3, H, D)
    a["att_wqk"] = halves(i["L0_ffn_Wqkv"][:, :2 * C])
    a["att_wv"] = halves(qkv[:, 2].reshape(C, C))
    a["att_wp"] = halves(i["L0_ffn_Wproj"])
    a["att_ln"] = np.stack([vector(i["L0_ffn_ln1_g"]), vector(i["L0_ffn_ln1_b"])], 1)
    a["home"] = np.arange(B * N, dtype=np.float32).reshape(TILES, P).T
    for name, k in (("moe", 2), ("ffn", 1)):
        rows = slots_for(k) * P
        a[f"{name}_blank"] = np.zeros((rows, C + 1), np.float32)
        a[f"{name}_blank"][:, C] = k * B * N + np.arange(rows)
    a["earlier"] = np.triu(np.ones((P, P), np.float32), 1)
    a["slot_no"] = np.arange(slots_for(2), dtype=np.float32)[None]
    a["before"] = np.broadcast_to(np.tril(np.ones((E, E), np.float32), -1), (P, E, E))
    a["moe_ln"] = np.stack([vector(i["L0_ffn_ln2_g"]), vector(i["L0_ffn_ln2_b"])], 1)
    a["moe_wr"] = biased(i["L0_ffn_Wrouter"], None, NARROW)
    a["moe_w1"] = halves(i["L0_ffn_W1"])
    a["moe_w2"] = i["L0_ffn_W2"].reshape(E, FFT, P, C).swapaxes(1, 2)
    a["ffn_wr"] = biased(i["L1_ffn_gate_w"], i["L1_ffn_gate_b"], NARROW)
    a["ffn_w1"] = halves(i["L1_ffn_w1"])
    b1 = i["L1_ffn_b1"]
    a["ffn_b1"] = np.stack([np.zeros_like(b1), b1], 1)[None]
    a["ffn_w2"] = i["L1_ffn_w2"].reshape(E, FFT, P, C).swapaxes(1, 2)
    a["ffn_b2"] = np.broadcast_to(i["L1_ffn_b2"], (P, E, C))
    w = i["L1_attn_w_qkv"]
    a["mix_wq"] = halves(w[:, :C])
    a["mix_wkv"] = halves(w[:, C:])
    a["mix_wside"] = biased(np.concatenate([i["L1_attn_w_id"], i["L1_attn_w_idgate"], i["L1_attn_w_prune"]], 1),
                            np.concatenate([np.zeros(C, np.float32), i["L1_attn_b_idgate"], i["L1_attn_b_prune"]]))
    a["mix_wg1"] = halves(i["L1_attn_w_g1"])
    a["mix_bg1"] = vector(i["L1_attn_b_g1"])
    a["mix_wg2"] = biased(i["L1_attn_w_g2"], i["L1_attn_b_g2"], NARROW)
    a["mix_static"] = np.broadcast_to(i["L1_attn_id_static_logit"], (P, H))
    a["mix_taps"] = halves(np.concatenate([i["L1_attn_fir_short_w"].reshape(C, SHORT), i["L1_attn_fir_long_w"].reshape(C, LONG)], 1))
    a["mix_mixer"] = halves(np.repeat(np.repeat(i["L1_attn_mix"], D, 0), D, 1))
    a["same_dim"] = halves(np.tile(np.eye(D, dtype=np.float32), (H, H)))
    a["same"] = halves(np.eye(C, dtype=np.float32))
    a["head_mask"] = np.repeat(np.eye(GH, dtype=np.float32), CK, 0)
    a["upto"] = np.tile(np.triu(np.ones((CK, CK), np.float32)), (GH, 1))
    a["proj_w"] = biased(i["L1_attn_w_proj"], i["L1_attn_b_proj"])
    return {k: np.ascontiguousarray(v) for k, v in a.items()}


def kernel(**inputs):
    import numpy as np
    import concourse.bacc as bacc
    from concourse.bass_utils import run_bass_kernel_spmd

    arrays = layouts({k: np.asarray(v) for k, v in inputs.items()}, np)
    nc = bacc.Bacc("TRN2", target_bir_lowering=False, num_devices=1)
    io = {k: nc.dram_tensor(f"in_{k}", v.shape, mybir.dt.from_np(v.dtype), kind="ExternalInput").ap()
          for k, v in arrays.items()}
    out = nc.dram_tensor("out", (B, N, C), F32, kind="ExternalOutput").ap()
    program(nc, io, out)
    r = run_bass_kernel_spmd(nc, [{f"in_{k}": v for k, v in arrays.items()}], core_ids=[0])
    return r.results[0]["out"]
```
